# Optimizing a Trainium2 kernel written in Bass

```python
import numpy as np
import jax
import jax.numpy as jnp

def _softmax(x, axis=-1):
    return jax.nn.softmax(x, axis=axis)

def _gelu(x):
    return jax.nn.gelu(x, approximate=True)

def _silu(x):
    return jax.nn.silu(x)

def _sigmoid(x):
    return jax.nn.sigmoid(x)

def _layernorm(x, axis=-1, eps=1e-05):
    m = jnp.mean(x, axis=axis, keepdims=True)
    v = jnp.var(x, axis=axis, keepdims=True)
    return (x - m) / jnp.sqrt(v + eps)

def _scatter_add(tgt, idx, src, axis=0):
    return tgt.at[idx].add(src)

def _segment_sum(src, seg, n):
    return jax.ops.segment_sum(src, seg, n)
kernel_name = 'mk_prb_d4_jaxref_r8_6b454a'

def setup_inputs(seed: int=0):
    np.random.seed(seed)
    _w = jnp.asarray

    def _L0_attn_setup():
        import jax, jax.numpy as jnp
        import numpy as np
        NUM_HEADS = 16
        EPS = 1e-06

        def elu_plus_one(x):
            return jax.nn.elu(x) + 1.0
        key = jax.random.key(seed)
        ks = jax.random.split(key, 9)
        B, L, E = (4, 512, 128)
        s = 1.0 / np.sqrt(E)
        return {'query': jax.random.normal(ks[0], (B, L, E), jnp.float32), 'Wq': jax.random.normal(ks[1], (E, E), jnp.float32) * s, 'bq': jax.random.normal(ks[2], (E,), jnp.float32) * 0.01, 'Wk': jax.random.normal(ks[3], (E, E), jnp.float32) * s, 'bk': jax.random.normal(ks[4], (E,), jnp.float32) * 0.01, 'Wv': jax.random.normal(ks[5], (E, E), jnp.float32) * s, 'bv': jax.random.normal(ks[6], (E,), jnp.float32) * 0.01, 'Wo': jax.random.normal(ks[7], (E, E), jnp.float32) * s, 'bo': jax.random.normal(ks[8], (E,), jnp.float32) * 0.01}
    _L0_attn_in = _L0_attn_setup()

    def _L0_ffn_setup():
        import jax, jax.numpy as jnp
        import numpy as np
        TOP_K = 2
        key = jax.random.key(seed)
        k1, k2, k3, k4 = jax.random.split(key, 4)
        B, T, D, H, E = (2, 256, 128, 256, 8)
        x = jax.random.normal(k1, (B, T, D), dtype=jnp.float32)
        w12 = jax.random.normal(k2, (E, 2 * H, D), dtype=jnp.float32) * D ** (-0.5)
        w3 = jax.random.normal(k3, (E, D, H), dtype=jnp.float32) * H ** (-0.5)
        gate_w = jax.random.normal(k4, (E, D), dtype=jnp.float32) * D ** (-0.5)
        return {'x': x, 'w12': w12, 'w3': w3, 'gate_w': gate_w}
    _L0_ffn_in = _L0_ffn_setup()

    def _L1_attn_setup():
        import jax, jax.numpy as jnp
        import numpy as np
        DIM = 128

        def _wkv_scan(k, v, u, w):
            kT = jnp.swapaxes(k, 0, 1)
            vT = jnp.swapaxes(v, 0, 1)

            def step(carry, kv_t):
                a, b = carry
                k_t, v_t = kv_t
                q = jnp.maximum(u + k_t, w)
                e1 = jnp.exp(-w - q)
                e2 = jnp.exp(u + k_t - q)
                a = e1 * a + e2 * v_t
                b = e1 * b + e2
                return ((a, b), a / b)
            B, _, d = k.shape
            init = (jnp.zeros((B, d), k.dtype), jnp.zeros((B, d), k.dtype))
            _, wkvT = jax.lax.scan(step, init, (kT, vT))
            return jnp.swapaxes(wkvT, 0, 1)
        key = jax.random.key(seed)
        ks = jax.random.split(key, 12)
        d = DIM
        B, T = (8, 512)
        s = 1.0 / np.sqrt(d)
        return {'x': jax.random.normal(ks[0], (B, T, d), dtype=jnp.float32), 'u': jnp.ones((d,), dtype=jnp.float32), 'w': jnp.ones((d,), dtype=jnp.float32), 'tmk': jnp.ones((d,), dtype=jnp.float32), 'tmv': jnp.ones((d,), dtype=jnp.float32), 'tmr': jnp.ones((d,), dtype=jnp.float32), 'Wk': jax.random.normal(ks[1], (d, d), dtype=jnp.float32) * s, 'Wv': jax.random.normal(ks[2], (d, d), dtype=jnp.float32) * s, 'Wr': jax.random.normal(ks[3], (d, d), dtype=jnp.float32) * s, 'Wo': jax.random.normal(ks[4], (d, d), dtype=jnp.float32) * s, 'bo': jnp.zeros((d,), dtype=jnp.float32)}
    _L1_attn_in = _L1_attn_setup()

    def _L1_ffn_setup():
        import jax, jax.numpy as jnp
        import numpy as np
        B, S, D, E, K = (4, 256, 128, 8, 2)
        EPS, W_THRES, TEMP = (0.0001, 0.1, 1.0)
        key = jax.random.key(seed)
        k1, k2, k3, k4, k5 = jax.random.split(key, 5)
        x = jax.random.normal(k1, (B, S, D), dtype=jnp.float32)
        gate_W = jax.random.normal(k2, (D, E), dtype=jnp.float32) * 0.02
        gate_b = jnp.zeros((E,), dtype=jnp.float32)
        expert_W = jax.random.normal(k3, (E, D, D), dtype=jnp.float32) * 0.02
        expert_b = jnp.zeros((E, D), dtype=jnp.float32)
        return {'x': x, 'gate_W': gate_W, 'gate_b': gate_b, 'expert_W': expert_W, 'expert_b': expert_b}
    _L1_ffn_in = _L1_ffn_setup()

    def _L2_attn_setup():
        import jax, jax.numpy as jnp
        import numpy as np
        B, T, DM, H, DH = (4, 256, 128, 16, 64)
        DI = H * DH
        CLIP = 1.0
        LN_EPS = 1e-05
        key = jax.random.key(seed)
        ks = jax.random.split(key, 9)

        def xav(k, shape):
            lim = float(np.sqrt(6.0 / (shape[0] + shape[1])))
            return jax.random.uniform(k, shape, jnp.float32, -lim, lim)

        def kai(k, shape):
            lim = float(1.0 / np.sqrt(shape[1]))
            return jax.random.uniform(k, shape, jnp.float32, -lim, lim)
        return {'x': jax.random.normal(ks[0], (B, T, DM), jnp.float32), 'Wq': xav(ks[1], (DI, DM)), 'Wk': xav(ks[2], (DI, DM)), 'Wv': xav(ks[3], (DI, DM)), 'Wa': kai(ks[4], (DI, DM)), 'ba': jnp.full((DI,), 3.0, jnp.float32), 'Wb': kai(ks[5], (H, DM)), 'bb': jnp.zeros((H,), jnp.float32), 'Wg': kai(ks[6], (H, DM)), 'bg': jnp.zeros((H,), jnp.float32), 'WaR': kai(ks[7], (DI, DM)), 'baR': jnp.full((DI,), 3.0, jnp.float32), 'Wo': xav(ks[8], (DM, DI)), 'ln_w': jnp.ones((DM,), jnp.float32), 'ln_b': jnp.zeros((DM,), jnp.float32)}
    _L2_attn_in = _L2_attn_setup()

    def _L2_ffn_setup():
        import jax, jax.numpy as jnp
        import numpy as np
        DIM = 128
        HEADS = 16
        HD = DIM // HEADS
        M = 32
        E = 4
        K = 2
        HID = 256
        MID = 256
        LB = 0.01
        EPS = 1.1920929e-07

        def _rms(x, w):
            return x * jax.lax.rsqrt(jnp.mean(x * x, axis=-1, keepdims=True) + EPS) * w

        def _gelu(x):
            return jax.nn.gelu(x, approximate=False)
        key = jax.random.key(seed)
        ks = jax.random.split(key, 20)
        d = DIM
        w = lambda k, s: jax.random.normal(k, s, jnp.float32) * 0.02
        return {'x': jax.random.normal(ks[0], (4, 128, d), jnp.float32), 'n1_w': jnp.ones((d,), jnp.float32), 'n2_w': jnp.ones((d,), jnp.float32), 'wq': w(ks[1], (d, d)), 'wk': w(ks[2], (d, d)), 'wv': w(ks[3], (d, d)), 'wo': w(ks[4], (d, d)), 'qn_w': jnp.ones((HD,), jnp.float32), 'kn_w': jnp.ones((HD,), jnp.float32), 'gate_w': w(ks[5], (E, d)), 'e0_up': w(ks[6], (HID, d)), 'e0_down': w(ks[7], (d, HID)), 'e1_w1': w(ks[8], (HID, d)), 'e1_w2': w(ks[9], (HID, d)), 'e1_down': w(ks[10], (d, HID)), 'e2_l1': w(ks[11], (MID, d)), 'e2_l2': w(ks[12], (HID, MID)), 'e2_l3': w(ks[13], (MID, HID)), 'e2_l4': w(ks[14], (d, MID)), 'e3_down': w(ks[15], (d, d)), 'e3_up': w(ks[16], (HID, d)), 'e3_out': w(ks[17], (d, HID))}
    _L2_ffn_in = _L2_ffn_setup()

    def _L3_attn_setup():
        import jax, jax.numpy as jnp
        import numpy as np
        B, S, HID = (2, 256, 128)
        H, D = (16, 64)
        KD = H * D
        RMS_EPS = 1e-05
        L2_EPS = 1e-12

        def _l2norm(t):
            n = jnp.sqrt(jnp.sum(t * t, axis=-1, keepdims=True))
            return t / jnp.clip(n, L2_EPS)
        key = jax.random.key(seed)
        ks = jax.random.split(key, 9)
        w = lambda k, shape: jax.random.normal(k, shape, jnp.float32) * 0.02
        return {'x': jax.random.normal(ks[0], (B, S, HID), jnp.float32), 'Wq': w(ks[1], (HID, KD)), 'Wk': w(ks[2], (HID, KD)), 'Wv': w(ks[3], (HID, KD)), 'Wf': w(ks[4], (HID, KD)), 'Wb': w(ks[5], (HID, H)), 'A_log': jnp.log(jnp.full((H,), 8.0, jnp.float32)), 'dt_bias': jnp.zeros((KD,), jnp.float32), 'Wg': w(ks[6], (HID, KD)), 'bg': jnp.zeros((KD,), jnp.float32), 'Wo': w(ks[7], (KD, HID)), 'norm_w': jnp.ones((D,), jnp.float32)}
    _L3_attn_in = _L3_attn_setup()

    def _L3_ffn_setup():
        import jax, jax.numpy as jnp
        import numpy as np
        DIM = 128
        DEPTH = 6
        HEADS = 16
        DIM_HEAD = 64
        WINDOW = 32
        INNER = HEADS * DIM_HEAD
        DIM_INNER = int(DIM * 4 * 2 / 3)
        QK_SCALE = 8.0

        def shift_tokens(t):
            a, s = jnp.split(t, 2, -1)
            s = jnp.pad(s, ((0, 0), (1, 0), (0, 0)))[:, :-1]
            return jnp.concatenate([a, s], -1)

        def l2norm(t):
            return t / jnp.maximum(jnp.linalg.norm(t, axis=-1, keepdims=True), 1e-12)

        def rotate_half(x):
            x1, x2 = jnp.split(x, 2, -1)
            return jnp.concatenate([-x2, x1], -1)

        def rotary_tables(n):
            half = jnp.arange(0, DIM_HEAD, 2, dtype=jnp.float32)
            inv_freq = 1.0 / 10000.0 ** (half / DIM_HEAD)
            t = jnp.arange(n, dtype=jnp.float32)
            freqs = t[:, None] * inv_freq[None, :]
            freqs = jnp.concatenate([freqs, freqs], -1)
            base_scale = (half + 0.4 * DIM_HEAD) / (1.4 * DIM_HEAD)
            power = (t - n // 2) / (WINDOW // 2)
            scale = base_scale[None, :] ** power[:, None]
            scale = jnp.concatenate([scale, scale], -1)
            return (freqs, scale)

        def local_attention(q, k, v):
            b, h, n, d = q.shape
            w = WINDOW
            nw = n // w
            bq = q.reshape(b, h, nw, w, d)
            bk = k.reshape(b, h, nw, w, d)
            bv = v.reshape(b, h, nw, w, d)

            def look(t):
                p = jnp.pad(t, ((0, 0), (0, 0), (1, 0), (0, 0), (0, 0)))
                return jnp.concatenate([p[:, :, :nw], p[:, :, 1:]], axis=3)
            bk2, bv2 = (look(bk), look(bv))
            seq = jnp.arange(n).reshape(nw, w)
            seq_p = jnp.pad(seq, ((1, 0), (0, 0)), constant_values=-1)
            jt = jnp.concatenate([seq_p[:nw], seq_p[1:]], axis=1)
            it = seq[:, :, None]
            jb = jt[:, None, :]
            mask = (it < jb) | (it > jb + w) | (jb == -1)
            sim = jnp.einsum('bhwie,bhwje->bhwij', bq, bk2) * QK_SCALE
            sim = jnp.where(mask, -jnp.finfo(sim.dtype).max, sim)
            attn = jax.nn.softmax(sim, -1)
            out = jnp.einsum('bhwij,bhwje->bhwie', attn, bv2)
            return out.reshape(b, h, n, d)

        def attn_layer(x, Wqkv, qs, ksc, Wo):
            b, n, _ = x.shape
            qkv = x @ Wqkv
            q, k, v = jnp.split(qkv, 3, -1)
            sh = lambda t: t.reshape(b, n, HEADS, DIM_HEAD).transpose(0, 2, 1, 3)
            q, k, v = (sh(q), sh(k), sh(v))
            q = l2norm(q) * qs
            k = l2norm(k) * ksc
            freqs, scale = rotary_tables(n)
            cos, sin = (jnp.cos(freqs), jnp.sin(freqs))
            q = q * cos * scale + rotate_half(q) * sin * scale
            inv = 1.0 / scale
            k = k * cos * inv + rotate_half(k) * sin * inv
            out = local_attention(q, k, v)
            out = out.transpose(0, 2, 1, 3).reshape(b, n, INNER)
            return out @ Wo

        def ffn_layer(x, g, bln, W1, b1, W2, b2):
            mu = x.mean(-1, keepdims=True)
            var = ((x - mu) ** 2).mean(-1, keepdims=True)
            xn = (x - mu) / jnp.sqrt(var + 1e-05) * g + bln
            hg = xn @ W1 + b1
            a, gate = jnp.split(hg, 2, -1)
            return a * jax.nn.gelu(gate, approximate=False) @ W2 + b2
        key = jax.random.key(seed)
        ks = jax.random.split(key, 8)
        B, N = (2, 256)
        init = lambda k, shape: jax.random.normal(k, shape, jnp.float32) * 0.02
        return {'x': jax.random.normal(ks[0], (B, N, DIM), jnp.float32), 'Wqkv': init(ks[1], (DEPTH, DIM, 3 * INNER)), 'q_scale': jnp.ones((DEPTH, DIM_HEAD), jnp.float32), 'k_scale': jnp.ones((DEPTH, DIM_HEAD), jnp.float32), 'Wo': init(ks[2], (DEPTH, INNER, DIM)), 'ln_g': jnp.ones((DEPTH, DIM), jnp.float32), 'ln_b': jnp.zeros((DEPTH, DIM), jnp.float32), 'W1': init(ks[3], (DEPTH, DIM, 2 * DIM_INNER)), 'b1': jnp.zeros((DEPTH, 2 * DIM_INNER), jnp.float32), 'W2': init(ks[4], (DEPTH, DIM_INNER, DIM)), 'b2': jnp.zeros((DEPTH, DIM), jnp.float32)}
    _L3_ffn_in = _L3_ffn_setup()
    _d = {'L0_attn_query': _L0_attn_in['query'], 'L0_attn_Wq': _L0_attn_in['Wq'], 'L0_attn_bq': _L0_attn_in['bq'], 'L0_attn_Wk': _L0_attn_in['Wk'], 'L0_attn_bk': _L0_attn_in['bk'], 'L0_attn_Wv': _L0_attn_in['Wv'], 'L0_attn_bv': _L0_attn_in['bv'], 'L0_attn_Wo': _L0_attn_in['Wo'], 'L0_attn_bo': _L0_attn_in['bo'], 'L0_ffn_w12': _L0_ffn_in['w12'], 'L0_ffn_w3': _L0_ffn_in['w3'], 'L0_ffn_gate_w': _L0_ffn_in['gate_w'], 'L1_attn_u': _L1_attn_in['u'], 'L1_attn_w': _L1_attn_in['w'], 'L1_attn_tmk': _L1_attn_in['tmk'], 'L1_attn_tmv': _L1_attn_in['tmv'], 'L1_attn_tmr': _L1_attn_in['tmr'], 'L1_attn_Wk': _L1_attn_in['Wk'], 'L1_attn_Wv': _L1_attn_in['Wv'], 'L1_attn_Wr': _L1_attn_in['Wr'], 'L1_attn_Wo': _L1_attn_in['Wo'], 'L1_attn_bo': _L1_attn_in['bo'], 'L1_ffn_gate_W': _L1_ffn_in['gate_W'], 'L1_ffn_gate_b': _L1_ffn_in['gate_b'], 'L1_ffn_expert_W': _L1_ffn_in['expert_W'], 'L1_ffn_expert_b': _L1_ffn_in['expert_b'], 'L2_attn_Wq': _L2_attn_in['Wq'], 'L2_attn_Wk': _L2_attn_in['Wk'], 'L2_attn_Wv': _L2_attn_in['Wv'], 'L2_attn_Wa': _L2_attn_in['Wa'], 'L2_attn_ba': _L2_attn_in['ba'], 'L2_attn_Wb': _L2_attn_in['Wb'], 'L2_attn_bb': _L2_attn_in['bb'], 'L2_attn_Wg': _L2_attn_in['Wg'], 'L2_attn_bg': _L2_attn_in['bg'], 'L2_attn_WaR': _L2_attn_in['WaR'], 'L2_attn_baR': _L2_attn_in['baR'], 'L2_attn_Wo': _L2_attn_in['Wo'], 'L2_attn_ln_w': _L2_attn_in['ln_w'], 'L2_attn_ln_b': _L2_attn_in['ln_b'], 'L2_ffn_n1_w': _L2_ffn_in['n1_w'], 'L2_ffn_n2_w': _L2_ffn_in['n2_w'], 'L2_ffn_wq': _L2_ffn_in['wq'], 'L2_ffn_wk': _L2_ffn_in['wk'], 'L2_ffn_wv': _L2_ffn_in['wv'], 'L2_ffn_wo': _L2_ffn_in['wo'], 'L2_ffn_qn_w': _L2_ffn_in['qn_w'], 'L2_ffn_kn_w': _L2_ffn_in['kn_w'], 'L2_ffn_gate_w': _L2_ffn_in['gate_w'], 'L2_ffn_e0_up': _L2_ffn_in['e0_up'], 'L2_ffn_e0_down': _L2_ffn_in['e0_down'], 'L2_ffn_e1_w1': _L2_ffn_in['e1_w1'], 'L2_ffn_e1_w2': _L2_ffn_in['e1_w2'], 'L2_ffn_e1_down': _L2_ffn_in['e1_down'], 'L2_ffn_e2_l1': _L2_ffn_in['e2_l1'], 'L2_ffn_e2_l2': _L2_ffn_in['e2_l2'], 'L2_ffn_e2_l3': _L2_ffn_in['e2_l3'], 'L2_ffn_e2_l4': _L2_ffn_in['e2_l4'], 'L2_ffn_e3_down': _L2_ffn_in['e3_down'], 'L2_ffn_e3_up': _L2_ffn_in['e3_up'], 'L2_ffn_e3_out': _L2_ffn_in['e3_out'], 'L3_attn_Wq': _L3_attn_in['Wq'], 'L3_attn_Wk': _L3_attn_in['Wk'], 'L3_attn_Wv': _L3_attn_in['Wv'], 'L3_attn_Wf': _L3_attn_in['Wf'], 'L3_attn_Wb': _L3_attn_in['Wb'], 'L3_attn_A_log': _L3_attn_in['A_log'], 'L3_attn_dt_bias': _L3_attn_in['dt_bias'], 'L3_attn_Wg': _L3_attn_in['Wg'], 'L3_attn_bg': _L3_attn_in['bg'], 'L3_attn_Wo': _L3_attn_in['Wo'], 'L3_attn_norm_w': _L3_attn_in['norm_w'], 'L3_ffn_Wqkv': _L3_ffn_in['Wqkv'], 'L3_ffn_q_scale': _L3_ffn_in['q_scale'], 'L3_ffn_k_scale': _L3_ffn_in['k_scale'], 'L3_ffn_Wo': _L3_ffn_in['Wo'], 'L3_ffn_ln_g': _L3_ffn_in['ln_g'], 'L3_ffn_ln_b': _L3_ffn_in['ln_b'], 'L3_ffn_W1': _L3_ffn_in['W1'], 'L3_ffn_b1': _L3_ffn_in['b1'], 'L3_ffn_W2': _L3_ffn_in['W2'], 'L3_ffn_b2': _L3_ffn_in['b2']}
    _x0 = _d['L0_attn_query']
    _d['L0_attn_query'] = jax.random.normal(jax.random.fold_in(jax.random.key(seed), 1), (16, 256, 128), dtype=_x0.dtype)
    del _x0
    return _d

def reference(L0_attn_query, L0_attn_Wq, L0_attn_bq, L0_attn_Wk, L0_attn_bk, L0_attn_Wv, L0_attn_bv, L0_attn_Wo, L0_attn_bo, L0_ffn_w12, L0_ffn_w3, L0_ffn_gate_w, L1_attn_u, L1_attn_w, L1_attn_tmk, L1_attn_tmv, L1_attn_tmr, L1_attn_Wk, L1_attn_Wv, L1_attn_Wr, L1_attn_Wo, L1_attn_bo, L1_ffn_gate_W, L1_ffn_gate_b, L1_ffn_expert_W, L1_ffn_expert_b, L2_attn_Wq, L2_attn_Wk, L2_attn_Wv, L2_attn_Wa, L2_attn_ba, L2_attn_Wb, L2_attn_bb, L2_attn_Wg, L2_attn_bg, L2_attn_WaR, L2_attn_baR, L2_attn_Wo, L2_attn_ln_w, L2_attn_ln_b, L2_ffn_n1_w, L2_ffn_n2_w, L2_ffn_wq, L2_ffn_wk, L2_ffn_wv, L2_ffn_wo, L2_ffn_qn_w, L2_ffn_kn_w, L2_ffn_gate_w, L2_ffn_e0_up, L2_ffn_e0_down, L2_ffn_e1_w1, L2_ffn_e1_w2, L2_ffn_e1_down, L2_ffn_e2_l1, L2_ffn_e2_l2, L2_ffn_e2_l3, L2_ffn_e2_l4, L2_ffn_e3_down, L2_ffn_e3_up, L2_ffn_e3_out, L3_attn_Wq, L3_attn_Wk, L3_attn_Wv, L3_attn_Wf, L3_attn_Wb, L3_attn_A_log, L3_attn_dt_bias, L3_attn_Wg, L3_attn_bg, L3_attn_Wo, L3_attn_norm_w, L3_ffn_Wqkv, L3_ffn_q_scale, L3_ffn_k_scale, L3_ffn_Wo, L3_ffn_ln_g, L3_ffn_ln_b, L3_ffn_W1, L3_ffn_b1, L3_ffn_W2, L3_ffn_b2):

    def _L0_attn_ref(query, Wq, bq, Wk, bk, Wv, bv, Wo, bo):
        import jax, jax.numpy as jnp
        import numpy as np
        NUM_HEADS = 16
        EPS = 1e-06

        def elu_plus_one(x):
            return jax.nn.elu(x) + 1.0
        B, L, E = query.shape
        H = NUM_HEADS
        d = E // H

        def proj(x, W, b):
            return jnp.einsum('ble,fe->blf', x, W) + b

        def heads(x):
            return x.reshape(B, L, H, d).transpose(0, 2, 1, 3)
        Q = heads(proj(query, Wq, bq))
        K = heads(proj(query, Wk, bk))
        V = heads(proj(query, Wv, bv))
        phiQ = elu_plus_one(Q)
        phiK = elu_plus_one(K)
        S = jnp.einsum('bhki,bhkj->bhij', phiK, V)
        Z = phiK.sum(axis=-2)
        num = jnp.einsum('bhqi,bhij->bhqj', phiQ, S)
        denom = jnp.einsum('bhqi,bhi->bhq', phiQ, Z)[..., None] + EPS
        context = (num / denom).transpose(0, 2, 1, 3).reshape(B, L, E)
        return jnp.einsum('ble,fe->blf', context, Wo) + bo

    def _L0_ffn_ref(x, w12, w3, gate_w):
        import jax, jax.numpy as jnp
        import numpy as np
        TOP_K = 2
        E = gate_w.shape[0]
        H = w3.shape[-1]
        scores = jnp.einsum('btd,ed->bte', x, gate_w)
        topk_scores, topk_idx = jax.lax.top_k(scores, TOP_K)
        topk_probs = jax.nn.softmax(topk_scores, axis=-1)
        total_probs = jnp.sum(jax.nn.one_hot(topk_idx, E, dtype=topk_probs.dtype) * topk_probs[..., None], axis=-2)
        h12 = jnp.einsum('btd,ehd->bteh', x, w12)
        h1, h2 = (h12[..., :H], h12[..., H:])
        hidden = jax.nn.silu(h1) * h2
        expert_out = jnp.einsum('bteh,edh->bted', hidden, w3)
        y = jnp.sum(total_probs[..., None] * expert_out, axis=-2)
        return y

    def _L1_attn_ref(x, u, w, tmk, tmv, tmr, Wk, Wv, Wr, Wo, bo):
        import jax, jax.numpy as jnp
        import numpy as np
        DIM = 128

        def _wkv_scan(k, v, u, w):
            kT = jnp.swapaxes(k, 0, 1)
            vT = jnp.swapaxes(v, 0, 1)

            def step(carry, kv_t):
                a, b = carry
                k_t, v_t = kv_t
                q = jnp.maximum(u + k_t, w)
                e1 = jnp.exp(-w - q)
                e2 = jnp.exp(u + k_t - q)
                a = e1 * a + e2 * v_t
                b = e1 * b + e2
                return ((a, b), a / b)
            B, _, d = k.shape
            init = (jnp.zeros((B, d), k.dtype), jnp.zeros((B, d), k.dtype))
            _, wkvT = jax.lax.scan(step, init, (kT, vT))
            return jnp.swapaxes(wkvT, 0, 1)
        x_sh = jnp.pad(x, ((0, 0), (1, 0), (0, 0)))[:, :-1, :]
        key = x * tmk + x_sh * (1.0 - tmk)
        value = x * tmv + x_sh * (1.0 - tmv)
        receptance = jax.nn.sigmoid(x * tmr + x_sh * (1.0 - tmr))
        k = jnp.einsum('btd,ed->bte', key, Wk)
        v = jnp.einsum('btd,ed->bte', value, Wv)
        r = jnp.einsum('btd,ed->bte', receptance, Wr)
        wkv = _wkv_scan(k, v, u, w)
        return jnp.einsum('btd,ed->bte', wkv * r, Wo) + bo

    def _L1_ffn_ref(x, gate_W, gate_b, expert_W, expert_b):
        import jax, jax.numpy as jnp
        import numpy as np
        B, S, D, E, K = (4, 256, 128, 8, 2)
        EPS, W_THRES, TEMP = (0.0001, 0.1, 1.0)
        scores = jnp.maximum((x @ gate_W + gate_b) / TEMP, EPS)
        p = jax.nn.softmax(scores, axis=-1)
        _, topk_idx = jax.lax.top_k(p, K)
        topk_mask = jax.nn.one_hot(topk_idx, E, dtype=p.dtype).sum(-2) > 0
        w = jnp.maximum(p, W_THRES)
        w_gather = jnp.take_along_axis(w, topk_idx, axis=-1)
        total = jax.lax.stop_gradient(w_gather.sum(-1, keepdims=True))
        w = w / total
        comb = jnp.where(topk_mask, w, jnp.zeros_like(w))
        y = jnp.einsum('bsd,edf->bsef', x, expert_W) + expert_b
        out = jnp.einsum('bsef,bse->bsf', y, comb) / K
        return out

    def _L2_attn_ref(x, Wq, Wk, Wv, Wa, ba, Wb, bb, Wg, bg, WaR, baR, Wo, ln_w, ln_b):
        import jax, jax.numpy as jnp
        import numpy as np
        B, T, DM, H, DH = (4, 256, 128, 16, 64)
        DI = H * DH
        CLIP = 1.0
        LN_EPS = 1e-05
        Bs, Ts, _ = x.shape
        residual = x
        mu = jnp.mean(x, -1, keepdims=True)
        var = jnp.mean((x - mu) ** 2, -1, keepdims=True)
        xn = (x - mu) / jnp.sqrt(var + LN_EPS) * ln_w + ln_b
        q = (xn @ Wq.T).reshape(Bs, Ts, H, DH)
        k = (xn @ Wk.T).reshape(Bs, Ts, H, DH)
        v = (xn @ Wv.T).reshape(Bs, Ts, H, DH)
        alpha = jax.nn.sigmoid(xn @ Wa.T + ba).reshape(Bs, Ts, H, DH)
        aR = jax.nn.sigmoid(xn @ WaR.T + baR).reshape(Bs, Ts, H, DH)
        beta = jax.nn.sigmoid(xn @ Wb.T + bb)
        gamma = jax.nn.sigmoid(xn @ Wg.T + bg)
        tm = lambda a: jnp.moveaxis(a, 1, 0)
        xs = (tm(q), tm(k), tm(v), tm(alpha), tm(aR), tm(beta), tm(gamma))
        S0 = jnp.zeros((Bs, H, DH, DH), x.dtype)

        def step(carry, inp):
            S, R = carry
            q_t, k_t, v_t, a_t, aR_t, b_t, g_t = inp
            kn = k_t / jnp.maximum(jnp.linalg.norm(k_t, axis=-1, keepdims=True), 1e-12)
            pred = jnp.einsum('bhji,bhj->bhi', S, kn)
            r = jnp.clip(v_t - pred, -CLIP, CLIP)
            S = a_t[..., None] * S
            kp = jnp.einsum('bhd,bhde->bhe', kn, S)
            S = S + b_t[..., None, None] * kn[..., None] * (v_t - kp)[..., None, :]
            o = jnp.einsum('bhji,bhj->bhi', S, q_t)
            R = aR_t[..., None] * R
            kpR = jnp.einsum('bhd,bhde->bhe', kn, R)
            R = R + g_t[..., None, None] * kn[..., None] * (r - kpR)[..., None, :]
            o = o + jnp.einsum('bhji,bhj->bhi', R, q_t)
            return ((S, R), o)
        _, os = jax.lax.scan(step, (S0, S0), xs)
        out = jnp.moveaxis(os, 0, 1).reshape(Bs, Ts, DI) @ Wo.T
        return out + residual

    def _L2_ffn_ref(x, n1_w, n2_w, wq, wk, wv, wo, qn_w, kn_w, gate_w, e0_up, e0_down, e1_w1, e1_w2, e1_down, e2_l1, e2_l2, e2_l3, e2_l4, e3_down, e3_up, e3_out):
        import jax, jax.numpy as jnp
        import numpy as np
        DIM = 128
        HEADS = 16
        HD = DIM // HEADS
        M = 32
        E = 4
        K = 2
        HID = 256
        MID = 256
        LB = 0.01
        EPS = 1.1920929e-07

        def _rms(x, w):
            return x * jax.lax.rsqrt(jnp.mean(x * x, axis=-1, keepdims=True) + EPS) * w

        def _gelu(x):
            return jax.nn.gelu(x, approximate=False)
        B, T, C = x.shape
        h = _rms(x, n1_w)
        heads = lambda w_: (h @ w_.T).reshape(B, T, HEADS, HD).transpose(0, 2, 1, 3)
        q = _rms(heads(wq), qn_w)
        k = _rms(heads(wk), kn_w)
        v = heads(wv)
        scores = jnp.einsum('bhqd,bhkd->bhqk', q, k) * HD ** (-0.5)
        causal = jnp.tril(jnp.ones((T, T), bool))
        scores = jnp.where(causal[None, None], scores, -jnp.inf)
        attn = jax.nn.softmax(scores, axis=-1)
        ao = jnp.einsum('bhqk,bhkd->bhqd', attn, v).transpose(0, 2, 1, 3).reshape(B, T, C) @ wo.T
        ao = ao.at[:, :, :M].set(0.0)
        x = x + ao
        xf = _rms(x, n2_w).reshape(-1, C)
        N = xf.shape[0]
        logits = jnp.nan_to_num(xf @ gate_w.T)
        probs = jax.nn.softmax(logits, axis=-1)
        topv, topi = jax.lax.top_k(probs, K)
        topv = topv / (topv.sum(-1, keepdims=True) + 1e-08)
        wts = jnp.zeros((N, E), x.dtype).at[jnp.arange(N)[:, None], topi].add(topv)
        o0 = _gelu(xf @ e0_up.T) @ e0_down.T
        o1 = jax.nn.silu(xf @ e1_w1.T) * (xf @ e1_w2.T) @ e1_down.T
        o2 = _gelu(_gelu(_gelu(xf @ e2_l1.T) @ e2_l2.T) @ e2_l3.T) @ e2_l4.T
        o3 = _gelu(_gelu(xf @ e3_down.T) @ e3_up.T) @ e3_out.T
        moe = wts[:, 0:1] * o0 + wts[:, 1:2] * o1 + wts[:, 2:3] * o2 + wts[:, 3:4] * o3
        moe = moe.reshape(B, T, C).at[:, :, :M].set(0.0)
        return x + moe

    def _L3_attn_ref(x, Wq, Wk, Wv, Wf, Wb, A_log, dt_bias, Wg, bg, Wo, norm_w):
        import jax, jax.numpy as jnp
        import numpy as np
        B, S, HID = (2, 256, 128)
        H, D = (16, 64)
        KD = H * D
        RMS_EPS = 1e-05
        L2_EPS = 1e-12

        def _l2norm(t):
            n = jnp.sqrt(jnp.sum(t * t, axis=-1, keepdims=True))
            return t / jnp.clip(n, L2_EPS)
        b, s, _ = x.shape
        h = A_log.shape[0]
        d = norm_w.shape[0]
        q = jax.nn.silu(x @ Wq).reshape(b, s, h, d)
        k = jax.nn.silu(x @ Wk).reshape(b, s, h, d)
        v = jax.nn.silu(x @ Wv).reshape(b, s, h, d)
        g = (x @ Wf).reshape(b, s, h, d)
        beta = jax.nn.sigmoid(x @ Wb)
        q = _l2norm(q)
        k = _l2norm(k)
        g = jax.nn.sigmoid(g - dt_bias.reshape(h, d))
        A = jnp.exp(-jnp.exp(A_log))
        qs = jnp.moveaxis(q, 1, 0)
        kss = jnp.moveaxis(k, 1, 0)
        vs = jnp.moveaxis(v, 1, 0)
        gs = jnp.moveaxis(g, 1, 0)
        bs = jnp.moveaxis(beta, 1, 0)
        state0 = jnp.zeros((b, h, d, d), x.dtype)

        def step(state, inp):
            q_t, k_t, v_t, g_t, b_t = inp
            o_t = jnp.einsum('bhd,bhde->bhe', q_t, state) * g_t
            state = A[None, :, None, None] * state + b_t[..., None, None] * (k_t[..., :, None] * v_t[..., None, :])
            return (state, o_t)
        _, o = jax.lax.scan(step, state0, (qs, kss, vs, gs, bs))
        o = jnp.moveaxis(o, 0, 1)
        o = o * jax.lax.rsqrt(jnp.mean(o * o, axis=-1, keepdims=True) + RMS_EPS) * norm_w
        gate = jax.nn.sigmoid(x @ Wg + bg).reshape(b, s, h, d)
        o = (o * gate).reshape(b, s, h * d)
        return o @ Wo

    def _L3_ffn_ref(x, Wqkv, q_scale, k_scale, Wo, ln_g, ln_b, W1, b1, W2, b2):
        import jax, jax.numpy as jnp
        import numpy as np
        DIM = 128
        DEPTH = 6
        HEADS = 16
        DIM_HEAD = 64
        WINDOW = 32
        INNER = HEADS * DIM_HEAD
        DIM_INNER = int(DIM * 4 * 2 / 3)
        QK_SCALE = 8.0

        def shift_tokens(t):
            a, s = jnp.split(t, 2, -1)
            s = jnp.pad(s, ((0, 0), (1, 0), (0, 0)))[:, :-1]
            return jnp.concatenate([a, s], -1)

        def l2norm(t):
            return t / jnp.maximum(jnp.linalg.norm(t, axis=-1, keepdims=True), 1e-12)

        def rotate_half(x):
            x1, x2 = jnp.split(x, 2, -1)
            return jnp.concatenate([-x2, x1], -1)

        def rotary_tables(n):
            half = jnp.arange(0, DIM_HEAD, 2, dtype=jnp.float32)
            inv_freq = 1.0 / 10000.0 ** (half / DIM_HEAD)
            t = jnp.arange(n, dtype=jnp.float32)
            freqs = t[:, None] * inv_freq[None, :]
            freqs = jnp.concatenate([freqs, freqs], -1)
            base_scale = (half + 0.4 * DIM_HEAD) / (1.4 * DIM_HEAD)
            power = (t - n // 2) / (WINDOW // 2)
            scale = base_scale[None, :] ** power[:, None]
            scale = jnp.concatenate([scale, scale], -1)
            return (freqs, scale)

        def local_attention(q, k, v):
            b, h, n, d = q.shape
            w = WINDOW
            nw = n // w
            bq = q.reshape(b, h, nw, w, d)
            bk = k.reshape(b, h, nw, w, d)
            bv = v.reshape(b, h, nw, w, d)

            def look(t):
                p = jnp.pad(t, ((0, 0), (0, 0), (1, 0), (0, 0), (0, 0)))
                return jnp.concatenate([p[:, :, :nw], p[:, :, 1:]], axis=3)
            bk2, bv2 = (look(bk), look(bv))
            seq = jnp.arange(n).reshape(nw, w)
            seq_p = jnp.pad(seq, ((1, 0), (0, 0)), constant_values=-1)
            jt = jnp.concatenate([seq_p[:nw], seq_p[1:]], axis=1)
            it = seq[:, :, None]
            jb = jt[:, None, :]
            mask = (it < jb) | (it > jb + w) | (jb == -1)
            sim = jnp.einsum('bhwie,bhwje->bhwij', bq, bk2) * QK_SCALE
            sim = jnp.where(mask, -jnp.finfo(sim.dtype).max, sim)
            attn = jax.nn.softmax(sim, -1)
            out = jnp.einsum('bhwij,bhwje->bhwie', attn, bv2)
            return out.reshape(b, h, n, d)

        def attn_layer(x, Wqkv, qs, ksc, Wo):
            b, n, _ = x.shape
            qkv = x @ Wqkv
            q, k, v = jnp.split(qkv, 3, -1)
            sh = lambda t: t.reshape(b, n, HEADS, DIM_HEAD).transpose(0, 2, 1, 3)
            q, k, v = (sh(q), sh(k), sh(v))
            q = l2norm(q) * qs
            k = l2norm(k) * ksc
            freqs, scale = rotary_tables(n)
            cos, sin = (jnp.cos(freqs), jnp.sin(freqs))
            q = q * cos * scale + rotate_half(q) * sin * scale
            inv = 1.0 / scale
            k = k * cos * inv + rotate_half(k) * sin * inv
            out = local_attention(q, k, v)
            out = out.transpose(0, 2, 1, 3).reshape(b, n, INNER)
            return out @ Wo

        def ffn_layer(x, g, bln, W1, b1, W2, b2):
            mu = x.mean(-1, keepdims=True)
            var = ((x - mu) ** 2).mean(-1, keepdims=True)
            xn = (x - mu) / jnp.sqrt(var + 1e-05) * g + bln
            hg = xn @ W1 + b1
            a, gate = jnp.split(hg, 2, -1)
            return a * jax.nn.gelu(gate, approximate=False) @ W2 + b2
        for i in range(DEPTH):
            x = attn_layer(shift_tokens(x), Wqkv[i], q_scale[i], k_scale[i], Wo[i]) + x
            x = ffn_layer(shift_tokens(x), ln_g[i], ln_b[i], W1[i], b1[i], W2[i], b2[i]) + x
        return x
    x = L0_attn_query
    xn = _layernorm(x, axis=-1)
    x = x + _L0_attn_ref(xn, L0_attn_Wq, L0_attn_bq, L0_attn_Wk, L0_attn_bk, L0_attn_Wv, L0_attn_bv, L0_attn_Wo, L0_attn_bo) + _L0_ffn_ref(xn, L0_ffn_w12, L0_ffn_w3, L0_ffn_gate_w)
    xn = _layernorm(x, axis=-1)
    x = x + _L1_attn_ref(xn, L1_attn_u, L1_attn_w, L1_attn_tmk, L1_attn_tmv, L1_attn_tmr, L1_attn_Wk, L1_attn_Wv, L1_attn_Wr, L1_attn_Wo, L1_attn_bo) + _L1_ffn_ref(xn, L1_ffn_gate_W, L1_ffn_gate_b, L1_ffn_expert_W, L1_ffn_expert_b)
    xn = _layernorm(x, axis=-1)
    x = x + _L2_attn_ref(xn, L2_attn_Wq, L2_attn_Wk, L2_attn_Wv, L2_attn_Wa, L2_attn_ba, L2_attn_Wb, L2_attn_bb, L2_attn_Wg, L2_attn_bg, L2_attn_WaR, L2_attn_baR, L2_attn_Wo, L2_attn_ln_w, L2_attn_ln_b) + _L2_ffn_ref(xn, L2_ffn_n1_w, L2_ffn_n2_w, L2_ffn_wq, L2_ffn_wk, L2_ffn_wv, L2_ffn_wo, L2_ffn_qn_w, L2_ffn_kn_w, L2_ffn_gate_w, L2_ffn_e0_up, L2_ffn_e0_down, L2_ffn_e1_w1, L2_ffn_e1_w2, L2_ffn_e1_down, L2_ffn_e2_l1, L2_ffn_e2_l2, L2_ffn_e2_l3, L2_ffn_e2_l4, L2_ffn_e3_down, L2_ffn_e3_up, L2_ffn_e3_out)
    xn = _layernorm(x, axis=-1)
    x = x + _L3_attn_ref(xn, L3_attn_Wq, L3_attn_Wk, L3_attn_Wv, L3_attn_Wf, L3_attn_Wb, L3_attn_A_log, L3_attn_dt_bias, L3_attn_Wg, L3_attn_bg, L3_attn_Wo, L3_attn_norm_w) + _L3_ffn_ref(xn, L3_ffn_Wqkv, L3_ffn_q_scale, L3_ffn_k_scale, L3_ffn_Wo, L3_ffn_ln_g, L3_ffn_ln_b, L3_ffn_W1, L3_ffn_b1, L3_ffn_W2, L3_ffn_b2)
    return x

_drawn_inputs = setup_inputs


def setup_inputs(seed=0):
    import zlib

    import numpy as np

    out = dict(_drawn_inputs(seed))
    spreads = {'L1_attn_u': (1.0, 0.6),
     'L1_attn_w': (1.0, 0.6),
     'L1_attn_tmk': (1.0, 0.6),
     'L1_attn_tmv': (1.0, 0.2),
     'L1_attn_tmr': (1.0, 0.2),
     'L1_attn_bo': (0.0, 0.1),
     'L1_ffn_gate_b': (0.0, 0.1),
     'L1_ffn_expert_b': (0.0, 0.1),
     'L2_attn_ba': (3.0, 0.2),
     'L2_attn_bb': (0.0, 2.0),
     'L2_attn_bg': (0.0, 0.8),
     'L2_attn_baR': (3.0, 0.6),
     'L2_attn_ln_w': (1.0, 0.2),
     'L2_attn_ln_b': (0.0, 0.1),
     'L2_ffn_n1_w': (1.0, 0.6),
     'L2_ffn_n2_w': (1.0, 0.6),
     'L2_ffn_qn_w': (1.0, 0.6),
     'L2_ffn_kn_w': (1.0, 0.6),
     'L3_attn_A_log': (2.079441547393799, 0.6),
     'L3_attn_dt_bias': (0.0, 2.0),
     'L3_attn_bg': (0.0, 2.0),
     'L3_attn_norm_w': (1.0, 0.6),
     'L3_ffn_q_scale': (1.0, 0.6),
     'L3_ffn_k_scale': (1.0, 0.6),
     'L3_ffn_ln_g': (1.0, 0.6),
     'L3_ffn_ln_b': (0.0, 0.8),
     'L3_ffn_b1': (0.0, 0.8),
     'L3_ffn_b2': (0.0, 0.708)}
    factors = {'L0_attn_Wq': 3.035,
     'L0_attn_bq': 27.15,
     'L0_attn_bk': 23.442,
     'L0_attn_bv': 4.337,
     'L0_attn_bo': 4.778,
     'L2_attn_Wa': 3.544,
     'L2_attn_WaR': 4.007,
     'L2_ffn_wq': 8.0,
     'L2_ffn_wk': 8.0,
     'L2_ffn_wv': 8.0,
     'L2_ffn_wo': 8.0,
     'L2_ffn_gate_w': 8.0,
     'L2_ffn_e0_up': 8.0,
     'L2_ffn_e0_down': 8.0,
     'L2_ffn_e1_w1': 8.0,
     'L2_ffn_e1_w2': 8.0,
     'L2_ffn_e1_down': 8.0,
     'L2_ffn_e2_l1': 8.0,
     'L2_ffn_e2_l2': 8.0,
     'L2_ffn_e2_l3': 8.0,
     'L2_ffn_e2_l4': 8.0,
     'L2_ffn_e3_down': 8.0,
     'L2_ffn_e3_up': 8.0,
     'L2_ffn_e3_out': 8.0,
     'L3_attn_Wf': 64.0,
     'L3_attn_Wb': 64.0,
     'L3_attn_Wg': 64.0,
     'L3_ffn_W1': 7.892,
     'L3_ffn_W2': 7.818,
     'L3_attn_Wq': 7.617,
     'L3_attn_Wk': 7.873,
     'L3_attn_Wv': 7.662,
     'L3_attn_Wo': 7.779}
    for name, (base, spread) in spreads.items():
        noise = np.random.default_rng([zlib.crc32(name.encode()), seed]).standard_normal(out[name].shape)
        drawn = base * np.exp(spread * noise) if base else spread * noise
        out[name] = jnp.asarray(drawn.astype(out[name].dtype))
    for name, factor in factors.items():
        out[name] = (out[name] * factor).astype(out[name].dtype)
    return out
```

```python
from contextlib import ExitStack

import concourse.bass as bass
from concourse import mybir
import numpy as np

F32 = mybir.dt.float32
U32 = mybir.dt.uint32
ALU = mybir.AluOpType
ACT = mybir.ActivationFunctionType
AX = mybir.AxisListType.X

P = 128
B, T, D = 16, 256, 128
N = B * T
BLK = 512
NBLK = N // BLK
TILES = N // P
HEADS = 16
NEG = -1.0e30
HD = 64
INNER = HEADS * HD
PAIRS = HEADS // 2


class Stage:

    def __init__(self, nc, name):
        self.nc, self.name, self.ctx = nc, name, ExitStack()
        self.sems = []

    def __enter__(self):
        return self

    def __exit__(self, *e):
        if e[0] is None:
            with self.nc.Block() as block:
                @block.sync
                def _(sp):
                    for s in self.sems:
                        self.nc.sync.sem_clear(s)
        return self.ctx.__exit__(*e)

    def sb(self, name, shape, dt=F32):
        return self.ctx.enter_context(self.nc.sbuf_tensor(f"{self.name}_{name}", shape, dt))

    def ps(self, name, shape, dt=F32):
        return self.ctx.enter_context(self.nc.psum_tensor(f"{self.name}_{name}", shape, dt))

    def sem(self, name):
        s = self.ctx.enter_context(self.nc.semaphore(f"{self.name}_{name}"))
        self.sems.append(s)
        return s


class Chain:

    def __init__(self, eng, sem, per_turn=0, turn=0):
        self.eng, self.sem, self.per_turn, self.turn, self.n = eng, sem, per_turn, turn, 0

    def link(self, ins):
        ins.then_inc(self.sem, 1)
        self.n += 1
        self.eng.wait_ge(self.sem, self.turn * self.per_turn + self.n)

    def close(self):
        assert self.n == self.per_turn, (self.n, self.per_turn)


def block(i):
    return bass.ds(i * BLK, BLK)


def bcast(ap, shape):
    return ap.to_broadcast(shape)


class Pack:

    def __init__(self):
        self.at, self.n, self.rows = {}, 0, {}

    def add(self, name, rows, cols):
        self.at[name] = (self.n, rows, cols)
        self.n += cols

    def of(self, tile, name):
        a, rows, cols = self.at[name]
        return tile[0:rows, a:a + cols]


def layout(pieces):
    p = Pack()
    for name, rows, cols in pieces:
        p.add(name, rows, cols)
    return p


def load_pack(nc, st, dram, tile, name):
    landed = st.sem(name + "_landed")
    with nc.Block() as blk:
        @blk.sync
        def _(sp):
            sp.dma_start(tile[:], dram).then_inc(landed, 16)
            sp.wait_ge(landed, 16)


def layer_norm(nc, name, src, dst, mean_w, eps_col, gain=None, shift=None):
    with Stage(nc, name) as st:
        sq = st.sb("sq", [P, N])
        mean_ps = st.ps("mean", [P, 2, BLK])
        var_ps = st.ps("var", [P, 2, BLK])
        std = st.sb("std", [P, 2, BLK])
        mean_ready, centered, squared = st.sem("mean_ready"), st.sem("centered"), st.sem("squared")
        var_ready, std_ready, normed = st.sem("var_ready"), st.sem("std_ready"), st.sem("normed")
        dve_step = st.sem("dve_step")
        extra = 1 if gain is not None else 0

        with nc.Block() as blk:
            @blk.tensor
            def _(pe):
                with pe.Fori(0, NBLK // 2) as i:
                    for k in range(2):
                        pe.wait_ge(centered, 2 * i + k + 1)
                        nc.tensor.matmul(mean_ps[:, k, :], mean_w, src[:, block(2 * i + k)],
                                         start=True, stop=True).then_inc(mean_ready, 1)
                with pe.Fori(0, NBLK // 2) as i:
                    for k in range(2):
                        pe.wait_ge(squared, 2 * i + k + 1)
                        pe.wait_ge(std_ready, 2 * i + k + 1)
                        nc.tensor.matmul(var_ps[:, k, :], mean_w, sq[:, block(2 * i + k)],
                                         start=True, stop=True).then_inc(var_ready, 1)

            @blk.vector
            def _(dve):
                nc.vector.sem_inc(centered, 2)
                with dve.Fori(0, NBLK // 2) as i:
                    for k in range(2):
                        dve.wait_ge(mean_ready, 2 * i + k + 1)
                        nc.vector.tensor_tensor(dst[:, block(2 * i + k)], src[:, block(2 * i + k)],
                                                mean_ps[:, k, :], ALU.subtract).then_inc(centered, 1)
                nc.vector.sem_inc(normed, 2)
                with dve.Fori(0, NBLK // 2) as i:
                    c = Chain(dve, dve_step, 2 + 2 * extra, i)
                    for k in range(2):
                        dve.wait_ge(std_ready, 2 * i + k + 3)
                        c.link(nc.vector.reciprocal(std[:, k, :], std[:, k, :]))
                        cols = dst[:, block(2 * i + k)]
                        if gain is None:
                            nc.vector.tensor_tensor(cols, cols, std[:, k, :], ALU.mult).then_inc(normed, 1)
                        else:
                            c.link(nc.vector.tensor_tensor(cols, cols, std[:, k, :], ALU.mult))
                            nc.vector.tensor_scalar(cols, cols, gain, shift, ALU.mult, ALU.add).then_inc(normed, 1)
                    c.close()

            @blk.scalar
            def _(act):
                with act.Fori(0, NBLK // 2) as i:
                    for k in range(2):
                        act.wait_ge(centered, 2 * i + k + 3)
                        nc.scalar.activation(sq[:, block(2 * i + k)], dst[:, block(2 * i + k)],
                                             ACT.Square).then_inc(squared, 1)
                nc.scalar.sem_inc(std_ready, 2)
                with act.Fori(0, NBLK // 2) as i:
                    for k in range(2):
                        act.wait_ge(var_ready, 2 * i + k + 1)
                        act.wait_ge(normed, 2 * i + k + 1)
                        nc.scalar.activation(std[:, k, :], var_ps[:, k, :], ACT.Sqrt,
                                             bias=eps_col).then_inc(std_ready, 1)


L0 = layout([("wq", P, D), ("wkv", P, 2 * D), ("wo", P, D), ("bq", P, 1), ("bo", P, 1), ("bkv", 1, 2 * D),
             ("gate", P, 8), ("w12", P, 8 * 512), ("w3", P, 8 * 2 * D)])


def linear_attention(nc, g, w):
    W = lambda n: L0.of(w, n)
    with Stage(nc, "l0a") as st:
        xb = st.sb("xb", [P, T])
        kv = st.sb("kv", [P, 2, 2 * D + 2])
        neg, pos = st.sb("neg", [P, 2, D]), st.sb("pos", [P, 2, D])
        qneg, phiq = st.sb("qneg", [P, T]), st.sb("phiq", [P, T])
        qpos = st.sb("qpos", [P, T])
        sm, zm = st.sb("sm", [P, D]), st.sb("zm", [P, D])
        rden, ctx = st.sb("rden", [P, T]), st.sb("ctx", [P, T])
        kv_ps = st.ps("kv_ps", [P, 2, 2 * D])
        q_ps, s_ps = st.ps("q_ps", [P, T]), st.ps("s_ps", [P, D + 1])
        num_ps, den_ps, o_ps = st.ps("num_ps", [P, T]), st.ps("den_ps", [P, T]), st.ps("o_ps", [P, T])
        ones_set, xb_ready, qkv_ready, min_ready = (st.sem(n) for n in ("ones_set", "xb_ready", "qkv_ready", "min_ready"))
        exp_ready, phi_ready, s_ready, masked = (st.sem(n) for n in ("exp_ready", "phi_ready", "s_ready", "masked"))
        numden_ready, ctx_ready, o_ready, added, dve_step = (
            st.sem(n) for n in ("numden_ready", "ctx_ready", "o_ready", "added", "dve_step"))

        with nc.Block() as blk:
            @blk.tensor
            def _(pe):
                with pe.Fori(0, B) as b:
                    pe.wait_ge(xb_ready, b + 1)
                    nc.tensor.matmul(q_ps[:], W("wq"), xb[:], start=True, stop=True)
                    for t in range(2):
                        nc.tensor.matmul(kv_ps[:, t, :], xb[:, t * P:(t + 1) * P], W("wkv"), start=True, stop=False)
                        mm = nc.tensor.matmul(kv_ps[:, t, :], g.ones_row, W("bkv"), start=False, stop=True)
                    mm.then_inc(qkv_ready, 1)
                    pe.wait_ge(phi_ready, b + 1)
                    for t in range(2):
                        mm = nc.tensor.matmul(s_ps[:], kv[:, t, 0:D], kv[:, t, D:2 * D + 1], start=(t == 0), stop=(t == 1))
                    mm.then_inc(s_ready, 1)
                    pe.wait_ge(masked, b + 1)
                    nc.tensor.matmul(num_ps[:], sm[:], phiq[:], start=True, stop=True)
                    nc.tensor.matmul(den_ps[:], zm[:], phiq[:], start=True, stop=True).then_inc(numden_ready, 1)
                    pe.wait_ge(ctx_ready, b + 1)
                    nc.tensor.matmul(o_ps[:], W("wo"), ctx[:], start=True, stop=True).then_inc(o_ready, 1)

            @blk.scalar
            def _(act):
                with act.Fori(0, B) as b:
                    act.wait_ge(added, b + 1)
                    nc.scalar.activation(xb[:], g.xn[:, bass.ds(b * T, T)], ACT.Copy).then_inc(xb_ready, 1)
                    act.wait_ge(min_ready, b + 1)
                    nc.scalar.activation(qpos[:], q_ps[:], ACT.Relu, bias=W("bq"))
                    nc.scalar.activation(pos[:], kv_ps[:, :, 0:D], ACT.Relu)
                    nc.scalar.activation(kv[:, :, D:2 * D], kv_ps[:, :, D:2 * D], ACT.Copy)
                    nc.scalar.activation(qneg[:], qneg[:], ACT.Exp)
                    nc.scalar.activation(neg[:], neg[:], ACT.Exp).then_inc(exp_ready, 1)

            @blk.vector
            def _(dve):
                nc.vector.memset(kv[:, :, 2 * D:2 * D + 1], 1.0).then_inc(ones_set, 1)
                nc.vector.sem_inc(added, 1)
                dve.wait_ge(ones_set, 1)
                with dve.Fori(0, B) as b:
                    c = Chain(dve, dve_step, 3, b)
                    dve.wait_ge(qkv_ready, b + 1)
                    nc.vector.tensor_scalar(qneg[:], q_ps[:], W("bq"), 0.0, ALU.add, ALU.min)
                    nc.vector.tensor_scalar(neg[:], kv_ps[:, :, 0:D], 0.0, None, ALU.min).then_inc(min_ready, 1)
                    dve.wait_ge(exp_ready, b + 1)
                    nc.vector.tensor_tensor(phiq[:], qneg[:], qpos[:], ALU.add)
                    nc.vector.tensor_tensor(kv[:, :, 0:D], neg[:], pos[:], ALU.add).then_inc(phi_ready, 1)
                    dve.wait_ge(s_ready, b + 1)
                    nc.vector.tensor_tensor(sm[:], s_ps[:, 0:D], g.c("mask8"), ALU.mult)
                    nc.vector.tensor_scalar(zm[:], g.c("mask8"), s_ps[:, D:D + 1], None, ALU.mult).then_inc(masked, 1)
                    dve.wait_ge(numden_ready, b + 1)
                    c.link(nc.vector.tensor_scalar(rden[:], den_ps[:], 1e-6, None, ALU.add))
                    c.link(nc.vector.reciprocal(rden[:], rden[:]))
                    nc.vector.tensor_tensor(ctx[:], rden[:], num_ps[:], ALU.mult).then_inc(ctx_ready, 1)
                    dve.wait_ge(o_ready, b + 1)
                    xs = g.x[:, bass.ds(b * T, T)]
                    c.link(nc.vector.scalar_tensor_tensor(out=xs, in0=o_ps[:], scalar=W("bo"), in1=xs,
                                                          op0=ALU.add, op1=ALU.add))
                    nc.vector.sem_inc(added, 1)
                    c.close()


def top2(nc, g, c, s, mask, E, tmp_gt, tmp_eq, rank):
    sh = [P, TILES, E, E]
    sj, se = s.unsqueeze(2).to_broadcast(sh), s.unsqueeze(3).to_broadcast(sh)
    before = g.c("before%d" % E).rearrange("p (a e) -> p a e", a=1).to_broadcast([P, TILES, E * E])
    flat = "p t e j -> p t (e j)"
    c.link(nc.vector.tensor_tensor(tmp_gt[:], sj, se, ALU.is_gt))
    c.link(nc.vector.tensor_tensor(tmp_eq[:], sj, se, ALU.is_equal))
    c.link(nc.vector.tensor_tensor(tmp_eq[:].rearrange(flat), tmp_eq[:].rearrange(flat), before, ALU.mult))
    c.link(nc.vector.tensor_tensor(tmp_gt[:], tmp_gt[:], tmp_eq[:], ALU.add))
    c.link(nc.vector.tensor_reduce(rank[:], tmp_gt[:], AX, ALU.add))
    c.link(nc.vector.tensor_scalar(mask[:], rank[:], 1.5, None, ALU.is_lt))


TOP2_LINKS = 6


def gate(nc, g, name, act_t, wgate, bias_row, E, weigh, prob_t):
    with Stage(nc, name) as st:
        s_ps = st.ps("s_ps", [P, TILES, E])
        s, mask = st.sb("s", [P, TILES, E]), st.sb("mask", [P, TILES, E])
        prob = st.sb("prob", [P, TILES, E])
        t_gt, t_eq = st.sb("t_gt", [P, TILES, E, E]), st.sb("t_eq", [P, TILES, E, E])
        rank, one = st.sb("rank", [P, TILES, E]), st.sb("one", [P, TILES, 1])
        p_ps = st.ps("p_ps", [E, 4, BLK])
        scores_ready, exp_in, exp_out = st.sem("scores_ready"), st.sem("exp_in"), st.sem("exp_out")
        prob_ready, turned, moved, dve_step = st.sem("prob_ready"), st.sem("turned"), st.sem("moved"), st.sem("dve_step")
        with nc.Block() as blk:
            @blk.tensor
            def _(pe):
                for t in range(TILES):
                    mm = nc.tensor.matmul(s_ps[:, t, :], act_t[:, t * P:(t + 1) * P], wgate, start=True,
                                          stop=bias_row is None)
                    if bias_row is not None:
                        mm = nc.tensor.matmul(s_ps[:, t, :], g.ones_row, bias_row, start=False, stop=True)
                mm.then_inc(scores_ready, 1)
                pe.wait_ge(prob_ready, 1)
                for t in range(TILES):
                    if t == 16:
                        pe.wait_ge(moved, 1)
                    mm = nc.tensor.transpose(p_ps[:, t // 4 % 4, (t % 4) * P:(t % 4 + 1) * P], prob[:, t, :], g.c("ident"))
                    if t % 16 == 15:
                        mm.then_inc(turned, 1)

            @blk.scalar
            def _(act):
                act.wait_ge(exp_in, 1)
                nc.scalar.activation(s[:], s[:], ACT.Exp).then_inc(exp_out, 1)

            @blk.vector
            def _(dve):
                c = Chain(dve, dve_step)
                c.link(nc.vector.memset(prob_t[:], 0.0))
                dve.wait_ge(scores_ready, 1)
                weigh(dve, c, s_ps, s, mask, prob, t_gt, t_eq, rank, one, exp_in, exp_out)
                nc.vector.sem_inc(prob_ready, 1)
                for half in range(2):
                    dve.wait_ge(turned, half + 1)
                    nc.vector.tensor_copy(prob_t[0:E, half * 2048:(half + 1) * 2048].rearrange("p (a n) -> p a n", a=4),
                                          p_ps[:]).then_inc(moved, 1)


def l0_weigh(nc, g):
    def weigh(dve, c, s_ps, s, mask, prob, t_gt, t_eq, rank, one, exp_in, exp_out):
        sh = [P, TILES, 8]
        c.link(nc.vector.tensor_copy(s[:], s_ps[:]))
        top2(nc, g, c, s[:], mask, 8, t_gt, t_eq, rank)
        c.link(nc.vector.tensor_reduce(one[:], s[:].unsqueeze(2), AX, ALU.max))
        c.link(nc.vector.tensor_tensor(s[:], s[:], one[:].to_broadcast(sh), ALU.subtract))
        nc.vector.sem_inc(exp_in, 1)
        dve.wait_ge(exp_out, 1)
        c.link(nc.vector.tensor_tensor(prob[:], s[:], mask[:], ALU.mult))
        c.link(nc.vector.tensor_reduce(one[:], prob[:].unsqueeze(2), AX, ALU.add))
        c.link(nc.vector.reciprocal(one[:], one[:]))
        c.link(nc.vector.tensor_tensor(prob[:], prob[:], one[:].to_broadcast(sh), ALU.mult))
    return weigh


def swiglu_experts(nc, g, w, prob_t):
    W12 = L0.of(w, "w12").rearrange("p (e h c n) -> p e h c n", e=8, h=2, c=2)
    W3 = L0.of(w, "w3").rearrange("p (e c n) -> p e c n", e=8, c=2)
    UNITS = 16
    with Stage(nc, "l0f") as st:
        h_ps = st.ps("h_ps", [P, 2, 2, BLK])
        pr_ps = st.ps("pr_ps", [P, 2, BLK])
        o_ps = st.ps("o_ps", [P, BLK])
        sil, hid = st.sb("sil", [P, 2, BLK]), st.sb("hid", [P, 2, BLK])
        tmp = st.sb("tmp", [P, 2, BLK])
        up_ready, silu_ready, hid_ready = (st.sem(n) for n in ("up_ready", "silu_ready", "hid_ready"))
        out_used, hid_used, dve_step = st.sem("out_used"), st.sem("hid_used"), st.sem("dve_step")
        with nc.Block() as blk:
            @blk.tensor
            def _(pe):
                nc.tensor.sem_inc(hid_used, 2)
                with pe.Fori(0, NBLK) as i:
                    xs = g.xn[:, block(i)]

                    def up(u):
                        e, c = divmod(u, 2)
                        pe.wait_ge(hid_ready, i * UNITS + u + 1)
                        if c == 0:
                            nc.tensor.matmul(pr_ps[:, e % 2, :], g.c("pick8").rearrange("k (e m) -> k e m", e=8)[:, e, :],
                                             prob_t[:, block(i)], start=True, stop=True)
                        nc.tensor.matmul(h_ps[:, u % 2, 0, :], W12[:, e, 0, c, :], xs, start=True, stop=True)
                        nc.tensor.matmul(h_ps[:, u % 2, 1, :], W12[:, e, 1, c, :], xs, start=True, stop=True).then_inc(up_ready, 1)

                    up(0)
                    pe.wait_ge(out_used, i + 1)
                    for u in range(UNITS):
                        if u + 1 < UNITS:
                            up(u + 1)
                        pe.wait_ge(hid_ready, i * UNITS + u + 3)
                        mm = nc.tensor.matmul(o_ps[:], W3[:, u // 2, u % 2, :], hid[:, u % 2, :],
                                              start=(u == 0), stop=(u == UNITS - 1))
                        mm.then_inc(hid_used, 1)

            @blk.scalar
            def _(act):
                with act.Fori(0, NBLK) as i:
                    for u in range(UNITS):
                        act.wait_ge(up_ready, i * UNITS + u + 1)
                        act.wait_ge(hid_ready, i * UNITS + u + 1)
                        nc.scalar.activation(sil[:, u % 2, :], h_ps[:, u % 2, 0, :], ACT.Silu).then_inc(silu_ready, 1)

            @blk.vector
            def _(dve):
                nc.vector.sem_inc(hid_ready, 2)
                nc.vector.sem_inc(out_used, 1)
                with dve.Fori(0, NBLK) as i:
                    c = Chain(dve, dve_step, UNITS + 1, i)
                    for u in range(UNITS):
                        dve.wait_ge(silu_ready, i * UNITS + u + 1)
                        c.link(nc.vector.tensor_tensor(tmp[:, u % 2, :], sil[:, u % 2, :], h_ps[:, u % 2, 1, :], ALU.mult))
                        dve.wait_ge(hid_used, i * UNITS + u + 1)
                        nc.vector.tensor_tensor(hid[:, u % 2, :], tmp[:, u % 2, :], pr_ps[:, u // 2 % 2, :],
                                                ALU.mult).then_inc(hid_ready, 1)
                    dve.wait_ge(hid_used, i * UNITS + UNITS + 2)
                    c.link(nc.vector.tensor_tensor(g.x[:, block(i)], g.x[:, block(i)], o_ps[:], ALU.add))
                    nc.vector.sem_inc(out_used, 1)
                    c.close()


L1 = layout([("wk", P, D), ("wv", P, D), ("wr", P, D), ("wo", P, D), ("bo", P, 1), ("u", P, 1), ("w", P, 1),
             ("tmk", P, 1), ("tmv", P, 1), ("tmr", P, 1), ("gate", P, 8), ("gate_b", 1, 8),
             ("ew", P, 8 * D), ("eb", P, D)])


def wkv_attention(nc, g, w):
    W = lambda n: L1.of(w, n)
    with Stage(nc, "l1a") as st:
        xs, om = st.sb("xs", [P, T]), st.sb("om", [P, 3])
        mix = st.sb("mix", [P, 3, T])
        mixs = st.sb("mixs", [P, 3, T])
        kvr_ps, o_ps = st.ps("kvr_ps", [P, 3, BLK]), st.ps("o_ps", [P, T])
        kk, q, e1, e2 = (st.sb(n, [P, T]) for n in ("kk", "q", "e1", "e2"))
        e1x, e2x, ev = (st.sb(n, [P, T]) for n in ("e1x", "e2x", "ev"))
        a, b_, wr = (st.sb(n, [P, T]) for n in ("a", "b", "wr"))
        mixed, sig_done, kvr_ready, args_ready, exps_ready, wr_ready, o_ready, dve_step = (
            st.sem(n) for n in ("mixed", "sig_done", "kvr_ready", "args_ready", "exps_ready", "wr_ready", "o_ready", "dve_step"))
        with nc.Block() as blk:
            @blk.tensor
            def _(pe):
                with pe.Fori(0, B) as i:
                    pe.wait_ge(mixed, i + 1)
                    pe.wait_ge(sig_done, i + 1)
                    for n, wn in enumerate(("wk", "wv", "wr")):
                        mm = nc.tensor.matmul(kvr_ps[:, n, 0:T], W(wn), mixs[:, n, :] if n == 2 else mix[:, n, :],
                                              start=True, stop=True)
                    mm.then_inc(kvr_ready, 1)
                    pe.wait_ge(wr_ready, i + 1)
                    nc.tensor.matmul(o_ps[:], W("wo"), wr[:], start=True, stop=True).then_inc(o_ready, 1)

            @blk.scalar
            def _(act):
                with act.Fori(0, B) as i:
                    act.wait_ge(mixed, i + 1)
                    nc.scalar.activation(mixs[:, 2, :], mix[:, 2, :], ACT.Sigmoid).then_inc(sig_done, 1)
                    act.wait_ge(args_ready, i + 1)
                    nc.scalar.activation(e1[:], e1x[:], ACT.Exp)
                    nc.scalar.activation(e2[:], e2x[:], ACT.Exp).then_inc(exps_ready, 1)

            @blk.vector
            def _(dve):
                for n, t in enumerate(("tmk", "tmv", "tmr")):
                    nc.vector.tensor_scalar(om[:, n:n + 1], W(t), -1.0, 1.0, ALU.mult, ALU.add)
                nc.vector.memset(xs[:, 0:1], 0.0)
                nc.vector.drain()
                with dve.Fori(0, B) as i:
                    c = Chain(dve, dve_step, 13, i)
                    c.link(nc.vector.tensor_copy(xs[:, 1:T], g.xn[:, bass.ds(i * T, T - 1)]))
                    for n in range(3):
                        c.link(nc.vector.tensor_scalar(mix[:, n, :], xs[:], om[:, n:n + 1], None, ALU.mult))
                    for n, t in enumerate(("tmk", "tmv", "tmr")):
                        ins = nc.vector.scalar_tensor_tensor(out=mix[:, n, :], in0=g.xn[:, bass.ds(i * T, T)], scalar=W(t),
                                                             in1=mix[:, n, :], op0=ALU.mult, op1=ALU.add)
                    ins.then_inc(mixed, 1)
                    dve.wait_ge(kvr_ready, i + 1)
                    c.link(nc.vector.tensor_scalar(kk[:], kvr_ps[:, 0, 0:T], W("u"), None, ALU.add))
                    c.link(nc.vector.tensor_scalar(q[:], kk[:], W("w"), None, ALU.max))
                    nc.vector.tensor_scalar(e1x[:], q[:], -1.0, W("w"), ALU.mult, ALU.subtract)
                    nc.vector.tensor_tensor(e2x[:], kk[:], q[:], ALU.subtract).then_inc(args_ready, 1)
                    dve.wait_ge(exps_ready, i + 1)
                    c.link(nc.vector.tensor_tensor(ev[:], e2[:], kvr_ps[:, 1, 0:T], ALU.mult))
                    c.link(nc.vector.tensor_tensor_scan(a[:], e1[:], ev[:], 0.0, ALU.mult, ALU.add))
                    c.link(nc.vector.tensor_tensor_scan(b_[:], e1[:], e2[:], 0.0, ALU.mult, ALU.add))
                    c.link(nc.vector.reciprocal(b_[:], b_[:]))
                    c.link(nc.vector.tensor_tensor(a[:], a[:], b_[:], ALU.mult))
                    c.link(nc.vector.tensor_tensor(wr[:], a[:], kvr_ps[:, 2, 0:T], ALU.mult))
                    nc.vector.sem_inc(wr_ready, 1)
                    dve.wait_ge(o_ready, i + 1)
                    xc = g.x[:, bass.ds(i * T, T)]
                    c.link(nc.vector.scalar_tensor_tensor(out=xc, in0=o_ps[:], scalar=W("bo"), in1=xc,
                                                          op0=ALU.add, op1=ALU.add))
                    c.close()


def l1_weigh(nc, g):
    def weigh(dve, c, s_ps, s, mask, prob, t_gt, t_eq, rank, one, exp_in, exp_out):
        sh = [P, TILES, 8]
        c.link(nc.vector.tensor_scalar(s[:], s_ps[:], 1e-4, None, ALU.max))
        c.link(nc.vector.tensor_reduce(one[:], s[:].unsqueeze(2), AX, ALU.max))
        c.link(nc.vector.tensor_tensor(s[:], s[:], one[:].to_broadcast(sh), ALU.subtract))
        nc.vector.sem_inc(exp_in, 1)
        dve.wait_ge(exp_out, 1)
        c.link(nc.vector.tensor_reduce(one[:], s[:].unsqueeze(2), AX, ALU.add))
        c.link(nc.vector.reciprocal(one[:], one[:]))
        c.link(nc.vector.tensor_tensor(s[:], s[:], one[:].to_broadcast(sh), ALU.mult))
        top2(nc, g, c, s[:], mask, 8, t_gt, t_eq, rank)
        c.link(nc.vector.tensor_scalar(prob[:], s[:], 0.1, None, ALU.max))
        c.link(nc.vector.tensor_tensor(prob[:], prob[:], mask[:], ALU.mult))
        c.link(nc.vector.tensor_reduce(one[:], prob[:].unsqueeze(2), AX, ALU.add))
        c.link(nc.vector.reciprocal(one[:], one[:]))
        c.link(nc.vector.tensor_scalar(one[:], one[:], 0.5, None, ALU.mult))
        c.link(nc.vector.tensor_tensor(prob[:], prob[:], one[:].to_broadcast(sh), ALU.mult))
    return weigh


def linear_experts(nc, g, w, prob_t):
    EW = L1.of(w, "ew").rearrange("p (e n) -> p e n", e=8)
    with Stage(nc, "l1f") as st:
        pr_ps, o_ps = st.ps("pr_ps", [P, 2, BLK]), st.ps("o_ps", [P, BLK])
        xc = st.sb("xc", [P, 2, BLK])
        comb_ready, scaled, used, out_used, dve_step = (
            st.sem(n) for n in ("comb_ready", "scaled", "used", "out_used", "dve_step"))
        with nc.Block() as blk:
            @blk.tensor
            def _(pe):
                nc.tensor.sem_inc(used, 2)
                with pe.Fori(0, NBLK) as i:
                    pb = prob_t[:, block(i)]

                    def spread(e):
                        pe.wait_ge(scaled, i * 8 + e + 1)
                        nc.tensor.matmul(pr_ps[:, e % 2, :], g.c("pick8").rearrange("k (e m) -> k e m", e=8)[:, e, :], pb,
                                         start=True, stop=True).then_inc(comb_ready, 1)

                    spread(0)
                    pe.wait_ge(out_used, i + 1)
                    nc.tensor.matmul(o_ps[:], L1.of(w, "eb"), pb, start=True, stop=False)
                    for e in range(8):
                        if e < 7:
                            spread(e + 1)
                        pe.wait_ge(scaled, i * 8 + e + 3)
                        nc.tensor.matmul(o_ps[:], EW[:, e, :], xc[:, e % 2, :], start=False, stop=(e == 7)).then_inc(used, 1)

            @blk.vector
            def _(dve):
                nc.vector.sem_inc(scaled, 2)
                nc.vector.sem_inc(out_used, 1)
                with dve.Fori(0, NBLK) as i:
                    c = Chain(dve, dve_step, 1, i)
                    for e in range(8):
                        dve.wait_ge(comb_ready, i * 8 + e + 1)
                        dve.wait_ge(used, i * 8 + e + 1)
                        nc.vector.tensor_tensor(xc[:, e % 2, :], g.xn[:, block(i)], pr_ps[:, e % 2, :],
                                                ALU.mult).then_inc(scaled, 1)
                    dve.wait_ge(used, i * 8 + 8 + 2)
                    c.link(nc.vector.tensor_tensor(g.x[:, block(i)], g.x[:, block(i)], o_ps[:], ALU.add))
                    nc.vector.sem_inc(out_used, 1)
                    c.close()


L2A = layout([("wk", P, INNER), ("wq", P, INNER), ("wv", P, INNER), ("wa", P, INNER), ("war", P, INNER),
              ("wbg", P, 2 * HEADS), ("wo", P, PAIRS * D), ("lnw", P, 1), ("lnb", P, 1),
              ("ba", 1, INNER), ("bar", 1, INNER), ("bbg", 1, 2 * HEADS),
              ("cum", P, P), ("ends", P, 8), ("keep", P, 4 * P), ("keep_r", P, 3 * P)])
CH = 32
GB = P // CH
NG, NCH = B // GB, T // CH


def delta_attention(nc, g, dram):
    kept = nc.dram_tensor("xn_kept", (P, N), F32).ap()
    I32 = mybir.dt.int32
    with Stage(nc, "l2d") as st:
        w = st.sb("w", [P, L2A.n])
        W = lambda n: L2A.of(w, n)
        load_pack(nc, st, dram["l2a"], w, "l2a")
        saved = st.sem("saved")
        with nc.Block() as blk:
            @blk.sync
            def _(sp):
                sp.dma_start(kept, g.xn[:]).then_inc(saved, 16)
                sp.wait_ge(saved, 16)

            @blk.vector
            def _(dve):
                nc.vector.tensor_tensor(g.x[:], g.x[:], g.xn[:], ALU.add)
        layer_norm(nc, "l2dn", g.xn, g.xn, g.c("mean"), g.c("eps5"), W("lnw"), W("lnb"))

        xt = st.sb("xt", [P, P])
        arena = st.sb("arena", [P, 9 * INNER])
        at = lambda n: arena[:, n * INNER:(n + 1) * INNER]
        kp, k0, qp, ez, sp_, ep, em, kn, q = (at(n) for n in range(9))
        Y = arena[:, 0:4 * INNER].rearrange("p (f c n) -> p f c n", f=PAIRS, c=4)
        X, U, UR = at(4), at(5), at(6)
        OT = at(7).rearrange("p (f n) -> p f n", f=PAIRS)
        O = at(8)
        v = st.sb("v", [P, INNER])
        km, kmr = st.sb("km", [P, INNER]), st.sb("kmr", [P, INNER])
        TS = st.sb("TS", [P, PAIRS, 4, P])
        TR = st.sb("TR", [P, PAIRS, 3, P])
        A, AR = st.sb("A", [P, HEADS, 2, P]), st.sb("AR", [P, HEADS, P])
        NL = st.sb("NL", [P, 2, 2, 4, P])
        SS, RR = st.sb("SS", [P, GB, PAIRS, HD]), st.sb("RR", [P, GB, PAIRS, HD])
        bgm, neg = st.sb("bgm", [P, 2, HEADS]), st.sb("neg", [P, 2, HEADS])
        ss = st.sb("ss", [P, HEADS])
        er = st.sb("er", [P, 2, PAIRS, GB, 2])
        fac, last = st.sb("fac", [P, 2, GB, PAIRS]), st.sb("last", [P, 2, GB, PAIRS])
        big = st.ps("big", [P, 8, BLK])
        wide = lambda a: big[:, a:a + 2, :].rearrange("p c n -> p (c n)")
        heads = lambda ap: ap.rearrange("p (h d) -> p h d", h=HEADS)
        by_head = lambda ap: ap.unsqueeze(2).to_broadcast([P, HEADS, HD])
        keep = W("keep").bitcast(I32).rearrange("p (m n) -> p m n", m=4)
        keep_r = W("keep_r").bitcast(I32).rearrange("p (m n) -> p m n", m=3)
        names = ("xt_ready", "proj_ready", "act_used", "dve_used", "small_ready", "small_used", "squared", "summed", "root",
                 "kn_ready", "exp_done", "ln_ready", "e_ready", "ends_ready", "ends_used", "dve_made", "pool_made", "flipped", "flip_used",
                 "mats_ready", "masked", "y_start", "lev_ready", "nl_moved", "y_added", "scaled", "s1", "x_ready", "s2", "u_ready",
                 "s3", "r_ready", "s4", "xr_ready", "s5", "ur_ready", "s6", "o_ready", "s7", "s_added", "s8", "r_added",
                 "o_flipped", "ot_ready", "y_ready", "added", "dve_step", "zeroed", "pe_go", "dve_go")
        S = {n: st.sem(n) for n in names}
        split = lambda ap: ap.rearrange("p (f q d) -> p q f d", q=2, d=HD)
        even_odd = lambda a: big[:, a:a + 2, :].rearrange("p q (f d) -> p q f d", d=HD)
        time = lambda tile_, gi, ci: tile_.rearrange("p (b t) -> p b t", t=T)[:, bass.ds(gi * GB, GB), bass.ds(ci * CH, CH)]

        def tensor_tile(pe, t):
            pe.wait_ge(S["xt_ready"], t + 1)

            def wide_product(u, lhs, wn, bias=None):
                for c in range(2):
                    out, cols = big[:, 2 * (u % 2) + c, :], slice(c * BLK, (c + 1) * BLK)
                    mm = nc.tensor.matmul(out, lhs, wn[:, cols], start=True, stop=bias is None)
                    if bias is not None:
                        mm = nc.tensor.matmul(out, g.ones_row, bias[:, cols], start=False, stop=True)
                mm.then_inc(S["proj_ready"], 1)

            def ends(s):
                for f in range(PAIRS):
                    mm = nc.tensor.matmul(big[:, 7, 64 * s + 8 * f:64 * s + 8 * f + 8], sp_[:, f * P:(f + 1) * P], W("ends"), start=True, stop=True)
                mm.then_inc(S["ends_ready"], 1)

            def flip(n, made, count, src):
                pe.wait_ge(S[made], count)
                pe.wait_ge(S["flip_used"], 7 * t + n + 1)
                for f in range(PAIRS):
                    mm = nc.tensor.transpose(big[:, 4 + f // 4, (f % 4) * P:(f % 4 + 1) * P], src[:, f * P:(f + 1) * P], g.c("ident"))
                mm.then_inc(S["flipped"], 1)

            wide_product(0, xt[:], W("wk"))
            wide_product(1, xt[:], W("wq"))
            nc.tensor.matmul(big[:, 6, 0:2 * HEADS], xt[:], W("wbg"), start=True, stop=False)
            nc.tensor.matmul(big[:, 6, 0:2 * HEADS], g.ones_row, W("bbg"), start=False, stop=True).then_inc(S["small_ready"], 1)
            pe.wait_ge(S["act_used"], 3 * t + 1)
            wide_product(2, xt[:], W("wv"))
            pe.wait_ge(S["act_used"], 3 * t + 2)
            wide_product(3, xt[:], W("wa"), W("ba"))
            pe.wait_ge(S["act_used"], 3 * t + 3)
            pe.wait_ge(S["ln_ready"], 2 * t + 1)
            wide_product(4, W("cum"), sp_)
            ends(0)
            pe.wait_ge(S["dve_used"], 4 * t + 1)
            wide_product(5, xt[:], W("war"), W("bar"))
            flip(0, "dve_made", 3 * t + 1, k0)
            flip(1, "dve_made", 3 * t + 2, kp)
            flip(2, "pool_made", 4 * t + 1, km[:])
            flip(3, "pool_made", 4 * t + 2, qp)
            pe.wait_ge(S["dve_used"], 4 * t + 2)
            pe.wait_ge(S["ln_ready"], 2 * t + 2)
            wide_product(6, W("cum"), sp_)
            ends(1)
            flip(4, "dve_made", 3 * t + 3, kp)
            flip(5, "pool_made", 4 * t + 3, kmr[:])
            flip(6, "pool_made", 4 * t + 4, qp)

            pe.wait_ge(S["flip_used"], 7 * t + 8)
            pe.wait_ge(S["small_used"], t + 1)
            pe.wait_ge(S["ends_used"], 2 * t + 2)
            for p_ in range(PAIRS // 2):
                if p_:
                    pe.wait_ge(S["y_added"], 32 * t + 8 * p_)
                    pe.wait_ge(S["nl_moved"], 32 * t + 8 * p_)
                for wv in range(2):
                    f = 2 * p_ + wv
                    for par in range(2):
                        rows = slice(par * HD, (par + 1) * HD)
                        a, b = big[:, 4 * wv + par, :], big[:, 4 * wv + 2 + par, :]
                        nc.tensor.matmul(a[:, 0:3 * P], TS[rows, f, 3, :], TS[rows, f, 0:3, :], start=True, stop=True)
                        nc.tensor.matmul(a[:, 3 * P:4 * P], TS[rows, f, 0, :], TS[rows, f, 3, :], start=True, stop=True)
                        nc.tensor.matmul(b[:, 0:2 * P], TR[rows, f, 2, :], TR[rows, f, 0:2, :], start=True, stop=True)
                        mm = nc.tensor.matmul(b[:, 2 * P:3 * P], TR[rows, f, 0, :], TR[rows, f, 2, :], start=True, stop=True)
                    mm.then_inc(S["mats_ready"], 1)
                pe.wait_ge(S["masked"], 8 * t + 2 * p_ + 2)
                for l in range(5):
                    for wv in range(2):
                        f = 2 * p_ + wv
                        if l >= 1:
                            pe.wait_ge(S["nl_moved"], 32 * t + 8 * p_ + 2 * (l - 1) + wv + 1)
                            if l == 1:
                                pe.wait_ge(S["y_start"], 8 * t + 2 * p_ + wv + 1)
                            else:
                                pe.wait_ge(S["y_added"], 32 * t + 8 * p_ + 2 * (l - 2) + wv + 1)
                        for ch in range(4):
                            Nm, Lm = NL[:, wv, 0, ch, :], NL[:, wv, 1, ch, :]
                            cols = slice(ch * P, (ch + 1) * P)
                            if l <= 2:
                                mm = nc.tensor.matmul(big[:, 3 * wv, cols], Lm, Nm, start=True, stop=True)
                            if l >= 1:
                                mm = nc.tensor.matmul(big[:, 3 * wv + 2, cols], Lm, Y[:, f, ch, :], start=True, stop=True)
                            if l <= 3:
                                mm = nc.tensor.matmul(big[:, 3 * wv + 1, cols], Nm, Lm, start=True, stop=True)
                        mm.then_inc(S["lev_ready"], 1)

            def by_batch(bank0, h, src, m, state, stop):
                f, par = divmod(h, 2)
                rows = slice(par * HD, (par + 1) * HD)
                for b in range(GB):
                    mm = nc.tensor.matmul(big[32 * b:32 * b + 32, bank0 + par, f * HD:(f + 1) * HD], src[rows, f, m, 32 * b:32 * b + 32],
                                          state[rows, b, f, :], start=stop != "add", stop=stop == "alone")
                return mm

            def whole(bank0, h, lhs, rhs, stop):
                f, par = divmod(h, 2)
                return nc.tensor.matmul(big[:, bank0 + par, f * HD:(f + 1) * HD], lhs, rhs[:, h * HD:(h + 1) * HD], start=False, stop=stop)

            def solve(chain0, out):
                for h in range(HEADS):
                    f, par = divmod(h, 2)
                    mm = nc.tensor.matmul(big[:, 2 + h // 8, (h % 8) * HD:(h % 8 + 1) * HD], Y[:, f, chain0 + par, :], X[:, h * HD:(h + 1) * HD],
                                          start=True, stop=True)
                mm.then_inc(S[out], 1)

            pe.wait_ge(S["y_added"], 32 * t + 32)
            pe.wait_ge(S["scaled"], t + 1)
            nc.tensor.sem_inc(S["pe_go"], 1)
            for h in range(HEADS):
                mm = by_batch(0, h, TS, 0, SS, "alone")
            mm.then_inc(S["s1"], 1)
            pe.wait_ge(S["x_ready"], t + 1)
            solve(0, "s2")
            pe.wait_ge(S["u_ready"], t + 1)
            nc.tensor.sem_inc(S["pe_go"], 1)
            for h in range(HEADS):
                by_batch(4, h, TS, 2, SS, "open")
                mm = whole(4, h, A[:, h, 1, :], U, True)
            mm.then_inc(S["s3"], 1)
            for h in range(HEADS):
                mm = by_batch(0, h, TR, 0, RR, "alone")
            mm.then_inc(S["s4"], 1)
            pe.wait_ge(S["xr_ready"], t + 1)
            solve(2, "s5")
            pe.wait_ge(S["ur_ready"], t + 1)
            nc.tensor.sem_inc(S["pe_go"], 1)
            for h in range(HEADS):
                by_batch(4, h, TS, 1, SS, "open")
                whole(4, h, A[:, h, 0, :], U, False)
                by_batch(4, h, TR, 1, RR, "add")
                mm = whole(4, h, AR[:, h, :], UR, True)
            mm.then_inc(S["s6"], 1)

            def update(k_, u_, out):
                for h in range(HEADS):
                    f, par = divmod(h, 2)
                    for b in range(GB):
                        rows, cols = slice(32 * b, 32 * b + 32), slice(h * HD, (h + 1) * HD)
                        mm = nc.tensor.matmul(big[par * HD:(par + 1) * HD, b, f * HD:(f + 1) * HD], k_[rows, cols], u_[rows, cols],
                                              start=True, stop=True)
                mm.then_inc(S[out], 1)

            update(km, U, "s7")
            pe.wait_ge(S["s_added"], t + 1)
            nc.tensor.sem_inc(S["pe_go"], 1)
            update(kmr, UR, "s8")
            pe.wait_ge(S["o_ready"], t + 1)
            for f in range(PAIRS):
                mm = nc.tensor.transpose(big[:, 6 + f // 4, (f % 4) * P:(f % 4 + 1) * P], O[:, f * P:(f + 1) * P], g.c("ident"))
            mm.then_inc(S["o_flipped"], 1)
            pe.wait_ge(S["ot_ready"], t + 1)
            for f in range(PAIRS):
                mm = nc.tensor.matmul(big[:, 6, 0:P], W("wo")[:, f * D:(f + 1) * D], OT[:, f, :], start=(f == 0), stop=(f == PAIRS - 1))
            mm.then_inc(S["y_ready"], 1)

        def scalar_tile(act, t, gi, ci):
            act.wait_ge(S["added"], t + 1)
            nc.scalar.activation(xt[:].rearrange("p (b t) -> p b t", t=CH), time(g.xn[:], gi, ci), ACT.Copy).then_inc(S["xt_ready"], 1)
            for u, dst in enumerate((kn, q, v[:])):
                act.wait_ge(S["proj_ready"], 7 * t + u + 1)
                nc.scalar.activation(dst, wide(2 * (u % 2)), ACT.Copy).then_inc(S["act_used"], 1)
                if u == 0:
                    act.wait_ge(S["act_used"], 3 * t + 1)
                    nc.scalar.activation(ep, kn, ACT.Square).then_inc(S["squared"], 1)
                    act.wait_ge(S["summed"], t + 1)
                    nc.scalar.activation(ss[:], ss[:], ACT.Sqrt).then_inc(S["root"], 1)
                    act.wait_ge(S["small_ready"], t + 1)
                    nc.scalar.activation(bgm[:].rearrange("p a h -> p (a h)"), big[:, 6, 0:2 * HEADS], ACT.Sigmoid).then_inc(S["small_used"], 1)

            def decays(s):
                act.wait_ge(S["dve_used"], 4 * t + 2 * s + 1)
                nc.scalar.activation(ez, ez, ACT.Exp).then_inc(S["exp_done"], 1)
                act.wait_ge(S["exp_done"], 2 * t + s + 1)
                nc.scalar.activation(sp_, ez, ACT.Ln, bias=1.0).then_inc(S["ln_ready"], 1)
                act.wait_ge(S["dve_used"], 4 * t + 2 * s + 2)
                nc.scalar.activation(em, ep, ACT.Exp, scale=-1.0)
                nc.scalar.activation(ep, ep, ACT.Exp).then_inc(S["e_ready"], 1)
                act.wait_ge(S["ends_ready"], 2 * t + s + 1)
                nc.scalar.activation(er[:, s].rearrange("p f b k -> p (f b k)"), big[:, 7, 64 * s:64 * s + 64], ACT.Exp,
                                     scale=-1.0).then_inc(S["ends_used"], 1)

            def flips(n0, dsts):
                for n, dst in enumerate(dsts):
                    act.wait_ge(S["flipped"], 7 * t + n0 + n + 1)
                    nc.scalar.activation(dst, big[:, 4:6, :].rearrange("p c (f n) -> p (c f) n", n=P), ACT.Copy).then_inc(S["flip_used"], 1)

            decays(0)
            flips(0, (TS[:, :, 2, :], TS[:, :, 0, :], TS[:, :, 3, :], TS[:, :, 1, :]))
            decays(1)
            flips(4, (TR[:, :, 0, :], TR[:, :, 2, :], TR[:, :, 1, :]))
            for p_ in range(PAIRS // 2):
                for l in range(4):
                    for wv in range(2):
                        act.wait_ge(S["lev_ready"], 40 * t + 10 * p_ + 2 * l + wv + 1)
                        if l == 0:
                            act.wait_ge(S["y_start"], 8 * t + 2 * p_ + wv + 1)
                        if l < 3:
                            src, dst = big[:, 3 * wv:3 * wv + 2, :], NL[:, wv].rearrange("p m c n -> p m (c n)")
                        else:
                            src, dst = big[:, 3 * wv + 1, :], NL[:, wv, 1].rearrange("p c n -> p (c n)")
                        nc.scalar.activation(dst, src, ACT.Copy).then_inc(S["nl_moved"], 1)
            act.wait_ge(S["s2"], t + 1)
            nc.scalar.activation(U, wide(2), ACT.Copy).then_inc(S["u_ready"], 1)
            act.wait_ge(S["s5"], t + 1)
            nc.scalar.activation(UR, wide(2), ACT.Copy).then_inc(S["ur_ready"], 1)
            act.wait_ge(S["s6"], t + 1)
            for par in range(2):
                ins = nc.scalar.activation(split(O)[:, par], even_odd(4)[:, par], ACT.Copy)
            ins.then_inc(S["o_ready"], 1)
            act.wait_ge(S["o_flipped"], t + 1)
            nc.scalar.activation(OT, big[:, 6:8, :].rearrange("p c (f n) -> p (c f) n", n=P), ACT.Copy).then_inc(S["ot_ready"], 1)

        def pool_tile(pool, t):
            pool.wait_ge(S["kn_ready"], t + 1)
            for s, (k_, wait_flip) in enumerate(((km, None), (kmr, 7 * t + 4))):
                pool.wait_ge(S["e_ready"], 2 * t + s + 1)
                nc.gpsimd.tensor_tensor(k_[:], kn, em, ALU.mult).then_inc(S["pool_made"], 1)
                if s == 1:
                    pool.wait_ge(S["flipped"], wait_flip)
                nc.gpsimd.tensor_tensor(qp, q, ep, ALU.mult).then_inc(S["pool_made"], 1)

        def vector_tile(dve, t, gi, ci):
            c = Chain(dve, S["dve_step"], LINKS, t)
            dve.wait_ge(S["squared"], t + 1)
            nc.vector.tensor_reduce(ss[:], heads(ep), AX, ALU.add).then_inc(S["summed"], 1)
            dve.wait_ge(S["root"], t + 1)
            c.link(nc.vector.tensor_scalar(ss[:], ss[:], 1e-12, None, ALU.max))
            c.link(nc.vector.reciprocal(ss[:], ss[:]))
            c.link(nc.vector.tensor_tensor(heads(kn), heads(kn), by_head(ss[:]), ALU.mult))
            nc.vector.sem_inc(S["kn_ready"], 1)
            dve.wait_ge(S["small_used"], t + 1)
            c.link(nc.vector.tensor_scalar(neg[:], bgm[:], -1.0, None, ALU.mult))
            for s in range(2):
                dve.wait_ge(S["proj_ready"], 7 * t + 4 + 2 * s)
                nc.vector.tensor_scalar(ez, wide(2), -1.0, 40.0, ALU.mult, ALU.min).then_inc(S["dve_used"], 1)
                dve.wait_ge(S["proj_ready"], 7 * t + 5 + 2 * s)
                if s == 1:
                    dve.wait_ge(S["pool_made"], 4 * t + 2)
                nc.vector.tensor_scalar(ep, wide(0), 80.0, -80.0, ALU.min, ALU.max).then_inc(S["dve_used"], 1)
                dve.wait_ge(S["e_ready"], 2 * t + s + 1)
                if s == 1:
                    dve.wait_ge(S["flipped"], 7 * t + 2)
                c.link(nc.vector.tensor_tensor(kp, kn, ep, ALU.mult))
                if s == 0:
                    nc.vector.scalar_tensor_tensor(out=k0, in0=ez, scalar=1.0, in1=kp, op0=ALU.add, op1=ALU.mult).then_inc(S["dve_made"], 1)
                    dve.wait_ge(S["dve_made"], 3 * t + 1)
                nc.vector.tensor_tensor(heads(kp), heads(kp), by_head(neg[:, s, :]), ALU.mult).then_inc(S["dve_made"], 1)
            dve.wait_ge(S["ends_used"], 2 * t + 2)
            for s, state in enumerate((SS, RR)):
                er_b = er[:, s].rearrange("p f b k -> p b f k")
                c.link(nc.vector.tensor_tensor(fac[:, s], last[:, s], er_b[:, :, :, 0], ALU.mult))
                c.link(nc.vector.tensor_copy(last[:, s], er_b[:, :, :, 1]))
                flat = state[:].rearrange("p b f d -> p (b f) d")
                ins = nc.vector.tensor_tensor(flat, flat, fac[:, s].rearrange("p b f -> p (b f)").unsqueeze(2).to_broadcast([P, 32, HD]), ALU.mult)
            ins.then_inc(S["scaled"], 1)
            nc.vector.tensor_tensor(heads(X), heads(v[:]), by_head(bgm[:, 0, :]), ALU.mult)
            for p_ in range(PAIRS // 2):
                for wv in range(2):
                    f = 2 * p_ + wv
                    dve.wait_ge(S["mats_ready"], 8 * t + f + 1)
                    nc.vector.sem_inc(S["dve_go"], 1)
                    for par in range(2):
                        h = 2 * f + par
                        a = big[:, 4 * wv + par, :].rearrange("p (m n) -> p m n", n=P)
                        b = big[:, 4 * wv + 2 + par, 0:3 * P].rearrange("p (m n) -> p m n", n=P)
                        nc.vector.copy_predicated(NL[:, wv, :, par, :], keep[:, 0:4:3, :], a[:, 0:4:3, :])
                        nc.vector.copy_predicated(NL[:, wv, :, 2 + par, :], keep_r[:, 0:3:2, :], b[:, 0:3:2, :])
                        nc.vector.copy_predicated(A[:, h], keep[:, 1:3, :], a[:, 1:3, :])
                        ins = nc.vector.copy_predicated(AR[:, h, :], keep_r[:, 1, :], b[:, 1, :])
                    ins.then_inc(S["masked"], 1)
                    dve.wait_ge(S["masked"], 8 * t + f + 1)
                    nc.vector.tensor_tensor(Y[:, f], NL[:, wv, 0], g.c("ident").unsqueeze(1).to_broadcast([P, 4, P]), ALU.add).then_inc(S["y_start"], 1)
                for l in range(1, 5):
                    for wv in range(2):
                        f = 2 * p_ + wv
                        dve.wait_ge(S["lev_ready"], 40 * t + 10 * p_ + 2 * l + wv + 1)
                        yf = Y[:, f].rearrange("p c n -> p (c n)")
                        nc.vector.tensor_tensor(yf, yf, big[:, 3 * wv + 2, :], ALU.add).then_inc(S["y_added"], 1)
            dve.wait_ge(S["s1"], t + 1)
            nc.vector.tensor_tensor(split(X), split(X), even_odd(0), ALU.add).then_inc(S["x_ready"], 1)
            dve.wait_ge(S["s3"], t + 1)
            c.link(nc.vector.tensor_tensor(split(X), split(v[:]), even_odd(4), ALU.subtract))
            c.link(nc.vector.tensor_scalar(X, X, 1.0, -1.0, ALU.min, ALU.max))
            c.link(nc.vector.tensor_tensor(heads(X), heads(X), by_head(bgm[:, 1, :]), ALU.mult))
            dve.wait_ge(S["s4"], t + 1)
            nc.vector.tensor_tensor(split(X), split(X), even_odd(0), ALU.add).then_inc(S["xr_ready"], 1)
            for state, ready, done in ((SS, "s7", "s_added"), (RR, "s8", "r_added")):
                dve.wait_ge(S[ready], t + 1)
                flat = state[:].rearrange("p b f d -> p (b f d)")
                nc.vector.tensor_tensor(flat, flat, big[:, 0:4, :].rearrange("p c n -> p (c n)"), ALU.add).then_inc(S[done], 1)
            dve.wait_ge(S["y_ready"], t + 1)
            xs = time(g.x[:], gi, ci)
            c.link(nc.vector.tensor_tensor(xs, xs, big[:, 6, 0:P].rearrange("p (b t) -> p b t", t=CH), ALU.add))
            nc.vector.sem_inc(S["added"], 1)
            c.close()

        LINKS = 4 + 2 + 4 + 3 + 1
        with nc.Block() as blk:
            @blk.tensor
            def _(pe):
                pe.wait_ge(S["zeroed"], 1)
                with pe.Fori(0, NG) as gi:
                    with pe.Fori(0, NCH) as ci:
                        tensor_tile(pe, gi * NCH + ci)

            @blk.scalar
            def _(act):
                nc.scalar.sem_inc(S["flip_used"], 1)
                with act.Fori(0, NG) as gi:
                    with act.Fori(0, NCH) as ci:
                        scalar_tile(act, gi * NCH + ci, gi, ci)

            @blk.gpsimd
            def _(pool):
                with pool.Fori(0, NG) as gi:
                    with pool.Fori(0, NCH) as ci:
                        pool_tile(pool, gi * NCH + ci)

            @blk.vector
            def _(dve):
                for buf in (A, AR, NL):
                    ins = nc.vector.memset(buf[:], 0.0)
                nc.vector.sem_inc(S["added"], 1)
                ins.then_inc(S["zeroed"], 1)
                with dve.Fori(0, NG) as gi:
                    nc.vector.memset(SS[:], 0.0)
                    nc.vector.memset(RR[:], 0.0)
                    nc.vector.memset(last[:], 1.0)
                    with dve.Fori(0, NCH) as ci:
                        vector_tile(dve, gi * NCH + ci, gi, ci)
        back = st.sem("back")
        with nc.Block() as blk:
            @blk.sync
            def _(sp):
                sp.dma_start(g.xn[:], kept).then_inc(back, 16)
                sp.wait_ge(back, 16)


L2F = layout([("n1", P, 1), ("n2", P, 1), ("wq", P, 4 * P), ("wk", P, 4 * P), ("wv", P, D), ("qn", P, 1), ("kn", P, 1),
              ("wo", P, 4 * D), ("gate", P, 4), ("e0u", P, 2 * P), ("e0d", P, 2 * D), ("e1a", P, 2 * P), ("e1b", P, 2 * P),
              ("e1d", P, 2 * D), ("e2a", P, 2 * P), ("e2b", P, 4 * P), ("e2c", P, 4 * P), ("e2d", P, 2 * D),
              ("e3a", P, P), ("e3b", P, 2 * P), ("e3d", P, 2 * D)])
QUADS = HEADS // 4


def rms_norm(nc, name, src, dst, mean_w, eps_col, weight):
    with Stage(nc, name) as st:
        sq, root = st.sb("sq", [P, 2, BLK]), st.sb("root", [P, 2, BLK])
        ms_ps = st.ps("ms", [P, 2, BLK])
        squared, ms_ready, root_ready, normed, step = (st.sem(n) for n in ("squared", "ms_ready", "root_ready", "normed", "step"))
        with nc.Block() as blk:
            @blk.tensor
            def _(pe):
                with pe.Fori(0, NBLK // 2) as i:
                    for k in range(2):
                        pe.wait_ge(squared, 2 * i + k + 1)
                        pe.wait_ge(root_ready, 2 * i + k + 1)
                        nc.tensor.matmul(ms_ps[:, k, :], mean_w, sq[:, k, :], start=True, stop=True).then_inc(ms_ready, 1)

            @blk.scalar
            def _(act):
                nc.scalar.sem_inc(root_ready, 2)
                with act.Fori(0, NBLK // 2) as i:
                    for k in range(2):
                        nc.scalar.activation(sq[:, k, :], src[:, block(2 * i + k)], ACT.Square).then_inc(squared, 1)
                    for k in range(2):
                        act.wait_ge(ms_ready, 2 * i + k + 1)
                        act.wait_ge(normed, 2 * i + k + 1)
                        nc.scalar.activation(root[:, k, :], ms_ps[:, k, :], ACT.Sqrt, bias=eps_col).then_inc(root_ready, 1)

            @blk.vector
            def _(dve):
                nc.vector.sem_inc(normed, 2)
                with dve.Fori(0, NBLK // 2) as i:
                    c = Chain(dve, step, 2, i)
                    for k in range(2):
                        dve.wait_ge(root_ready, 2 * i + k + 3)
                        c.link(nc.vector.reciprocal(root[:, k, :], root[:, k, :]))
                        nc.vector.scalar_tensor_tensor(out=dst[:, block(2 * i + k)], in0=src[:, block(2 * i + k)], scalar=weight,
                                                       in1=root[:, k, :], op0=ALU.mult, op1=ALU.mult).then_inc(normed, 1)
                    c.close()


def causal_attention(nc, g, w, h):
    W = lambda n: L2F.of(w, n)
    with Stage(nc, "l2h") as st:
        hb = st.sb("hb", [P, T])
        raw = st.sb("raw", [P, 2, 2 * T])
        sq, root = st.sb("sq", [P, 2, 2 * T]), st.sb("root", [P, 2, 2 * T])
        qk = st.sb("qk", [P, QUADS, 2, T])
        v = st.sb("v", [P, 2, HEADS, 32])
        mx = st.sb("mx", [P, 4, 2])
        e = st.sb("e", [P, 4, 3 * P])
        et = st.sb("et", [P, 2, 3 * P])
        raw_o, rden = st.sb("raw_o", [P, T]), st.sb("rden", [P, T])
        ctxt = st.sb("ctxt", [P, QUADS, T])
        identb, maskb = st.sb("identb", [P, P], mybir.dt.bfloat16), st.sb("maskb", [P, P], mybir.dt.bfloat16)
        big = st.ps("big", [P, 8, BLK])
        names = ("setup", "hb_ready", "v_ready", "v_moved", "raw_ready", "squared", "ms_ready", "root_ready", "normed", "moved",
                 "s_ready", "max_ready", "exp_ready", "e_turned", "et_ready", "mixed", "o_moved", "den_ready", "ctx_ready",
                 "y_ready", "added", "dve_step")
        S = {n: st.sem(n) for n in names}
        with nc.Block() as blk:
            @blk.tensor
            def _(pe):
                pe.wait_ge(S["setup"], 1)
                with pe.Fori(0, B) as b:
                    pe.wait_ge(S["hb_ready"], b + 1)
                    for t in range(2):
                        mm = nc.tensor.matmul(big[:, 7, t * P:(t + 1) * P], hb[:, t * P:(t + 1) * P], W("wv"), start=True, stop=True)
                    mm.then_inc(S["v_ready"], 1)
                    for j in range(QUADS):
                        if j >= 2:
                            pe.wait_ge(S["moved"], QUADS * b + j - 1)
                        for n, wn in enumerate(("wq", "wk")):
                            mm = nc.tensor.matmul(big[:, j % 2, n * T:(n + 1) * T], W(wn)[:, j * P:(j + 1) * P], hb[:], start=True, stop=True)
                        mm.then_inc(S["raw_ready"], 1)
                        pe.wait_ge(S["squared"], QUADS * b + j + 1)
                        if j >= 2:
                            pe.wait_ge(S["root_ready"], QUADS * b + j - 1)
                        nc.tensor.matmul(big[:, 2 + j % 2, :], g.c("mean32"), sq[:, j % 2, :], start=True, stop=True).then_inc(S["ms_ready"], 1)
                    pe.wait_ge(S["normed"], QUADS * b + QUADS)
                    pe.wait_ge(S["v_moved"], b + 1)

                    def scores(n):
                        j, r = divmod(n, 4)
                        rows = slice(32 * r, 32 * r + 32)
                        if n >= 4:
                            pe.wait_ge(S["exp_ready"], HEADS * b + n - 3)
                        nc.tensor.matmul(big[:, r, 0:P], qk[rows, j, 0, 0:P], qk[rows, j, 1, 0:P], start=True, stop=False, tile_position=(32 * r, 0))
                        nc.tensor.matmul(big[:, r, 0:P], identb[:], maskb[:], start=False, stop=True)
                        nc.tensor.matmul(big[:, r, P:2 * P], qk[rows, j, 0, P:T], qk[rows, j, 1, 0:P], start=True, stop=True, tile_position=(32 * r, 0))
                        nc.tensor.matmul(big[:, r, 2 * P:3 * P], qk[rows, j, 0, P:T], qk[rows, j, 1, P:T], start=True, stop=False, tile_position=(32 * r, 0))
                        nc.tensor.matmul(big[:, r, 2 * P:3 * P], identb[:], maskb[:], start=False, stop=True).then_inc(S["s_ready"], 1)

                    def turn(n):
                        pe.wait_ge(S["exp_ready"], HEADS * b + n + 1)
                        if n >= 2:
                            pe.wait_ge(S["et_ready"], HEADS * b + n - 1)
                        for k in range(3):
                            mm = nc.tensor.transpose(big[:, 4 + n % 2, k * P:(k + 1) * P], e[:, n % 4, k * P:(k + 1) * P], g.c("ident"))
                        mm.then_inc(S["e_turned"], 1)

                    def mix(n):
                        j, r = divmod(n, 4)
                        out = big[32 * r:32 * r + 32, 6, :]
                        if n >= 4 and r == 0:
                            pe.wait_ge(S["ctx_ready"], QUADS * b + j)
                        pe.wait_ge(S["et_ready"], HEADS * b + n + 1)
                        nc.tensor.matmul(out[:, 0:T], v[:, 0, n, :], et[:, n % 2, 0:T], start=True, stop=False)
                        mm = nc.tensor.matmul(out[:, P:T], v[:, 1, n, :], et[:, n % 2, T:3 * P], start=False, stop=True)
                        mm.then_inc(S["mixed"], 1)
                        if r == 3:
                            pe.wait_ge(S["o_moved"], QUADS * b + j + 1)
                            nc.tensor.matmul(big[:, 6, T:2 * T], g.c("sum32"), raw_o[:], start=True, stop=True).then_inc(S["den_ready"], 1)

                    scores(0)
                    for n in range(HEADS):
                        if n + 1 < HEADS:
                            scores(n + 1)
                        turn(n)
                        if n >= 1:
                            mix(n - 1)
                    mix(HEADS - 1)
                    pe.wait_ge(S["ctx_ready"], QUADS * b + QUADS)
                    for j in range(QUADS):
                        mm = nc.tensor.matmul(big[:, 7, 0:T], W("wo")[:, j * D:(j + 1) * D], ctxt[:, j, :], start=(j == 0), stop=(j == QUADS - 1))
                    mm.then_inc(S["y_ready"], 1)

            @blk.scalar
            def _(act):
                with act.Fori(0, B) as b:
                    act.wait_ge(S["added"], b + 1)
                    nc.scalar.activation(hb[:], h[:, bass.ds(b * T, T)], ACT.Copy).then_inc(S["hb_ready"], 1)
                    act.wait_ge(S["v_ready"], b + 1)
                    nc.scalar.activation(v[:, :, :, 0:8], big[:, 7, 0:2 * P].rearrange("p (t h d) -> p t h d", t=2, d=8),
                                         ACT.Copy).then_inc(S["v_moved"], 1)
                    for j in range(QUADS):
                        act.wait_ge(S["raw_ready"], QUADS * b + j + 1)
                        if j >= 2:
                            act.wait_ge(S["normed"], QUADS * b + j - 1)
                        nc.scalar.activation(raw[:, j % 2, :], big[:, j % 2, :], ACT.Copy).then_inc(S["moved"], 1)
                        act.wait_ge(S["moved"], QUADS * b + j + 1)
                        nc.scalar.activation(sq[:, j % 2, :], raw[:, j % 2, :], ACT.Square).then_inc(S["squared"], 1)
                        act.wait_ge(S["ms_ready"], QUADS * b + j + 1)
                        nc.scalar.activation(root[:, j % 2, :], big[:, 2 + j % 2, :], ACT.Sqrt, bias=g.c("eps_rms")).then_inc(S["root_ready"], 1)
                    for n in range(HEADS):
                        act.wait_ge(S["max_ready"], HEADS * b + n + 1)
                        if n >= 4:
                            act.wait_ge(S["e_turned"], HEADS * b + n - 3)
                        nc.scalar.activation(e[:, n % 4, 0:P], big[:, n % 4, 0:P], ACT.Exp, bias=mx[:, n % 4, 0:1], scale=8 ** -0.5)
                        nc.scalar.activation(e[:, n % 4, P:3 * P], big[:, n % 4, P:3 * P], ACT.Exp, bias=mx[:, n % 4, 1:2],
                                             scale=8 ** -0.5).then_inc(S["exp_ready"], 1)
                        act.wait_ge(S["e_turned"], HEADS * b + n + 1)
                        if n >= 2:
                            act.wait_ge(S["mixed"], HEADS * b + n - 1)
                        nc.scalar.activation(et[:, n % 2, :], big[:, 4 + n % 2, 0:3 * P], ACT.Copy).then_inc(S["et_ready"], 1)

            @blk.vector
            def _(dve):
                nc.vector.sem_inc(S["added"], 1)
                nc.vector.memset(v[:, :, :, 9:32], 0.0)
                nc.vector.memset(v[:, :, :, 8:9], 1.0)
                nc.vector.tensor_copy(identb[:], g.c("ident"))
                nc.vector.tensor_copy(maskb[:], g.c("causal")).then_inc(S["setup"], 1)
                with dve.Fori(0, B) as b:
                    c = Chain(dve, S["dve_step"], QUADS + 2 * HEADS + QUADS + 1, b)
                    for j in range(QUADS):
                        dve.wait_ge(S["root_ready"], QUADS * b + j + 1)
                        c.link(nc.vector.reciprocal(root[:, j % 2, :], root[:, j % 2, :]))
                        for n, wn in enumerate(("qn", "kn")):
                            cols = slice(n * T, (n + 1) * T)
                            ins = nc.vector.scalar_tensor_tensor(out=qk[:, j, n, :], in0=raw[:, j % 2, cols], scalar=W(wn),
                                                                 in1=root[:, j % 2, cols], op0=ALU.mult, op1=ALU.mult)
                        ins.then_inc(S["normed"], 1)

                    def finish(j):
                        dve.wait_ge(S["mixed"], HEADS * b + 4 * j + 4)
                        nc.vector.tensor_copy(raw_o[:], big[:, 6, 0:T]).then_inc(S["o_moved"], 1)
                        dve.wait_ge(S["den_ready"], QUADS * b + j + 1)
                        c.link(nc.vector.reciprocal(rden[:], big[:, 6, T:2 * T]))
                        nc.vector.tensor_tensor(ctxt[:, j, :], raw_o[:], rden[:], ALU.mult).then_inc(S["ctx_ready"], 1)

                    for n in range(HEADS):
                        r = n % 4
                        dve.wait_ge(S["s_ready"], HEADS * b + n + 1)
                        if n >= 4:
                            dve.wait_ge(S["exp_ready"], HEADS * b + n - 3)
                        nc.vector.tensor_reduce(mx[:, r, 0:1], big[:, r, 0:P], AX, ALU.max)
                        c.link(nc.vector.tensor_reduce(mx[:, r, 1:2], big[:, r, P:3 * P], AX, ALU.max))
                        c.link(nc.vector.tensor_scalar(mx[:, r, :], mx[:, r, :], -(8 ** -0.5), None, ALU.mult))
                        nc.vector.sem_inc(S["max_ready"], 1)
                        if n % 4 == 1 and n > 4:
                            finish(n // 4 - 1)
                    finish(QUADS - 1)
                    dve.wait_ge(S["y_ready"], b + 1)
                    for r in range(32, P, 32):
                        xs = g.xn[r:r + 32, bass.ds(b * T, T)]
                        ins = nc.vector.tensor_tensor(xs, xs, big[r:r + 32, 7, 0:T], ALU.add)
                    c.link(ins)
                    nc.vector.sem_inc(S["added"], 1)
                    c.close()


def l2_weigh(nc, g):
    def weigh(dve, c, s_ps, s, mask, prob, t_gt, t_eq, rank, one, exp_in, exp_out):
        sh = [P, TILES, 4]
        c.link(nc.vector.tensor_scalar(s[:], s_ps[:], 3.4028235e38, -3.4028235e38, ALU.min, ALU.max))
        c.link(nc.vector.tensor_reduce(one[:], s[:].unsqueeze(2), AX, ALU.max))
        c.link(nc.vector.tensor_tensor(s[:], s[:], one[:].to_broadcast(sh), ALU.subtract))
        nc.vector.sem_inc(exp_in, 1)
        dve.wait_ge(exp_out, 1)
        c.link(nc.vector.tensor_reduce(one[:], s[:].unsqueeze(2), AX, ALU.add))
        c.link(nc.vector.reciprocal(one[:], one[:]))
        c.link(nc.vector.tensor_tensor(s[:], s[:], one[:].to_broadcast(sh), ALU.mult))
        top2(nc, g, c, s[:], mask, 4, t_gt, t_eq, rank)
        c.link(nc.vector.tensor_tensor(prob[:], s[:], mask[:], ALU.mult))
        c.link(nc.vector.tensor_reduce(one[:], prob[:].unsqueeze(2), AX, ALU.add))
        c.link(nc.vector.tensor_scalar(one[:], one[:], 1e-8, None, ALU.add))
        c.link(nc.vector.reciprocal(one[:], one[:]))
        c.link(nc.vector.tensor_tensor(prob[:], prob[:], one[:].to_broadcast(sh), ALU.mult))
    return weigh


def mixed_experts(nc, g, w, xf, prob_t):
    W = lambda n: L2F.of(w, n)
    part = lambda n, k: W(n)[:, k * P:(k + 1) * P]
    CHUNKS = [
        ("a0", [("e0u", 0, None)], 0, ("e0d", 0)), ("a1", [("e0u", 1, None)], 0, ("e0d", 1)),
        ("b0", [("e1a", 0, None)], 1, ("e1d", 0)), ("b1", [("e1a", 1, None)], 1, ("e1d", 1)),
        ("c0", [("e2a", 0, None)], None, None), ("c1", [("e2a", 1, None)], None, None),
        ("d0", [("e3a", 0, None)], None, None),
        ("f0", [("e2b", 0, "c0"), ("e2b", 2, "c1")], None, None), ("f1", [("e2b", 1, "c0"), ("e2b", 3, "c1")], None, None),
        ("h0", [("e3b", 0, "d0")], 3, ("e3d", 0)), ("h1", [("e3b", 1, "d0")], 3, ("e3d", 1)),
        ("i0", [("e2c", 0, "f0"), ("e2c", 2, "f1")], 2, ("e2d", 0)), ("i1", [("e2c", 1, "f0"), ("e2c", 3, "f1")], 2, ("e2d", 1)),
    ]
    at = {c[0]: n for n, c in enumerate(CHUNKS)}
    OUTS = [n for n, c in enumerate(CHUNKS) if c[3]]
    NC, NO = len(CHUNKS), len(OUTS)
    RING = 4
    with Stage(nc, "l2m") as st:
        hid = st.sb("hid", [P, NC, BLK])
        big = st.ps("big", [P, 8, BLK])
        up_ready, hid_ready, scaled, used, spread, out_used, step = (
            st.sem(n) for n in ("up_ready", "hid_ready", "scaled", "used", "spread", "out_used", "step"))
        with nc.Block() as blk:
            @blk.tensor
            def _(pe):
                with pe.Fori(0, NBLK) as i:
                    def up(n):
                        name, products, expert, out = CHUNKS[n]
                        pe.wait_ge(hid_ready, NC * i + n + 1)
                        if name == "b0":
                            nc.tensor.matmul(big[:, 4, :], part("e1b", 0), xf[:, block(i)], start=True, stop=True)
                        if name == "b1":
                            pe.wait_ge(scaled, NO * i + 3)
                            nc.tensor.matmul(big[:, 4, :], part("e1b", 1), xf[:, block(i)], start=True, stop=True)
                        for m, (wn, k, source) in enumerate(products):
                            if source:
                                pe.wait_ge(hid_ready, NC * i + at[source] + 5)
                            rhs = hid[:, at[source], :] if source else xf[:, block(i)]
                            mm = nc.tensor.matmul(big[:, n % RING, :], part(wn, k), rhs, start=(m == 0), stop=(m == len(products) - 1))
                        mm.then_inc(up_ready, 1)
                        if n in OUTS and OUTS.index(n) % 2 == 0:
                            e = OUTS.index(n) // 2
                            if e >= 2:
                                pe.wait_ge(scaled, NO * i + 2 * (e - 1))
                            nc.tensor.matmul(big[:, 6 + e % 2, :], g.c("pick8").rearrange("k (e m) -> k e m", e=8)[:, expert, :],
                                             prob_t[:, block(i)], start=True, stop=True).then_inc(spread, 1)

                    def down(m):
                        wn, k = CHUNKS[OUTS[m]][3]
                        if m == 0:
                            pe.wait_ge(out_used, i + 1)
                        pe.wait_ge(scaled, NO * i + m + 1)
                        nc.tensor.matmul(big[:, 5, :], part(wn, k), hid[:, OUTS[m], :], start=(m == 0), stop=(m == NO - 1)).then_inc(used, 1)

                    m = 0
                    for n in range(NC):
                        up(n)
                        while m < NO and OUTS[m] < n:
                            down(m)
                            m += 1
                    while m < NO:
                        down(m)
                        m += 1

            @blk.scalar
            def _(act):
                nc.scalar.sem_inc(hid_ready, RING)
                with act.Fori(0, NBLK) as i:
                    for n, (name, products, expert, out) in enumerate(CHUNKS):
                        act.wait_ge(up_ready, NC * i + n + 1)
                        if n == 0:
                            act.wait_ge(out_used, i + 1)
                        nc.scalar.activation(hid[:, n, :], big[:, n % RING, :], ACT.Silu if expert == 1 else ACT.Gelu).then_inc(hid_ready, 1)

            @blk.vector
            def _(dve):
                nc.vector.sem_inc(out_used, 1)
                with dve.Fori(0, NBLK) as i:
                    c = Chain(dve, step, 2 + 1 + 1, i)
                    xs = g.x[:, block(i)]
                    for m, n in enumerate(OUTS):
                        dve.wait_ge(hid_ready, NC * i + n + 1 + RING)
                        dve.wait_ge(spread, 4 * i + m // 2 + 1)
                        if CHUNKS[n][2] == 1:
                            c.link(nc.vector.tensor_tensor(hid[:, n, :], hid[:, n, :], big[:, 4, :], ALU.mult))
                        nc.vector.tensor_tensor(hid[:, n, :], hid[:, n, :], big[:, 6 + m // 2 % 2, :], ALU.mult).then_inc(scaled, 1)
                    c.link(nc.vector.tensor_tensor(xs, xs, g.xn[:, block(i)], ALU.add))
                    dve.wait_ge(used, NO * i + NO)
                    for r in range(32, P, 32):
                        xr = g.x[r:r + 32, block(i)]
                        ins = nc.vector.tensor_tensor(xr, xr, big[r:r + 32, 5, :], ALU.add)
                    c.link(ins)
                    nc.vector.sem_inc(out_used, 1)
                    c.close()


DEPTH = 6
WINDOW = 32
HALF = 341
L3A = layout([("wq", P, INNER), ("wk", P, INNER), ("wv", P, INNER), ("wf", P, INNER), ("wg", P, INNER),
              ("wb", P, HEADS), ("wo", P, PAIRS * D), ("dt", 1, INNER), ("bg", 1, INNER), ("a_log", P, HEADS),
              ("norm_w", P, 1)])
L3W = layout([("wq", P, INNER), ("wqr", P, INNER), ("wk", P, INNER), ("wkr", P, INNER), ("wv", P, INNER),
              ("wo", P, PAIRS * D), ("qs", P, 2), ("ks", P, 2)])
L3F = layout([("w1", P, 6 * P), ("b1", P, 6), ("w2", P, 3 * D), ("b2", P, 1), ("g", P, 1), ("b", P, 1)])


def decay_attention(nc, g, w):
    W = lambda n: L3A.of(w, n)
    with Stage(nc, "l3a") as st:
        dmask = st.sb("dmask", [P, HEADS, 3 * P])
        ealog = st.sb("ealog", [P, HEADS])
        xb = st.sb("xb", [P, T])
        qk = st.sb("qk", [P, 2, PAIRS, T])
        sq = st.sb("sq", [P, 2, T])
        v, gt, gate_s = (st.sb(n, [P, 2, INNER]) for n in ("v", "gt", "gate"))
        nrm = st.sb("nrm", [P, 2, 2, HEADS])
        beta = st.sb("beta", [P, 2, HEADS])
        kb = st.sb("kb", [P, 2, HEADS])
        sc = st.sb("sc", [P, 2, 3 * P])
        o, osq = st.sb("o", [P, INNER]), st.sb("osq", [P, INNER])
        ms = st.sb("ms", [P, HEADS])
        ot = st.sb("ot", [P, PAIRS, T])
        big = st.ps("big", [P, 8, BLK])
        nrm_ps = big[:, 4, 0:64].rearrange("p (t q h) -> p t q h", t=2, q=2)
        beta_ps = big[:, 5, 0:2 * HEADS].rearrange("p (t h) -> p t h", t=2)
        names = ("mask_arg", "mask_exp", "mask_done", "xb_ready", "proj_ready", "silu_ready", "sq_ready", "sq_used",
                 "nb_ready", "tok_ready", "tok_moved", "sqrt_ready", "scaled", "s_ready", "s_masked", "s_used",
                 "o_gated", "o_squared", "rms_arg", "rms_root", "o_normed", "turned", "ot_ready", "y_ready", "added",
                 "dve_step")
        S = {n: st.sem(n) for n in names}
        def norms(pe, b, f):
            pe.wait_ge(S["sq_ready"], b * PAIRS + f + 1)
            for n in range(2):
                for t in range(2):
                    mm = nc.tensor.matmul(nrm_ps[:, t, n, 2 * f:2 * f + 2], sq[:, n, t * P:(t + 1) * P],
                                          g.c("pair"), start=True, stop=True)
            mm.then_inc(S["sq_used"], 1)

        def sums(pe, b, t, h):
            pe.wait_ge(S["s_masked"], 32 * b + t * HEADS + h + 3)
            for j in range(t + 1):
                mm = nc.tensor.matmul(big[:, 6 + h // 8, (h % 8) * HD:(h % 8 + 1) * HD], sc[:, h % 2, j * P:(j + 1) * P],
                                      v[:, j, h * HD:(h + 1) * HD], start=(j == 0), stop=(j == t))
            mm.then_inc(S["s_used"], 1)

        with nc.Block() as blk:
            @blk.tensor
            def _(pe):
                nc.tensor.sem_inc(S["s_used"], 2)
                nc.tensor.sem_inc(S["turned"], 1)
                with pe.Fori(0, B) as b:
                    pe.wait_ge(S["xb_ready"], b + 1)
                    for f in range(PAIRS):
                        pe.wait_ge(S["silu_ready"], b * PAIRS + f + 1)
                        for n, wn in enumerate(("wq", "wk")):
                            mm = nc.tensor.matmul(big[:, f % 2, n * T:(n + 1) * T], W(wn)[:, f * P:(f + 1) * P], xb[:],
                                                  start=True, stop=True)
                        mm.then_inc(S["proj_ready"], 1)
                        if f >= 1:
                            norms(pe, b, f - 1)
                    norms(pe, b, PAIRS - 1)
                    for t in range(2):
                        mm = nc.tensor.matmul(beta_ps[:, t, :], xb[:, t * P:(t + 1) * P], W("wb"), start=True, stop=True)
                    mm.then_inc(S["nb_ready"], 1)
                    for t in range(2):
                        for n, (wn, sign, bias) in enumerate((("wv", None, None), ("wf", g.c("minus_row"), "dt"), ("wg", g.c("ones_row"), "bg"))):
                            u = t * 3 + n
                            pe.wait_ge(S["tok_moved"], b * 6 + u + 1)
                            for c in range(2):
                                cols = slice(c * BLK, (c + 1) * BLK)
                                mm = nc.tensor.matmul(big[:, 6 + c, :], xb[:, t * P:(t + 1) * P], W(wn)[:, cols],
                                                      start=True, stop=bias is None)
                                if bias:
                                    mm = nc.tensor.matmul(big[:, 6 + c, :], sign[:, 0:P], W(bias)[:, cols], start=False, stop=True)
                            mm.then_inc(S["tok_ready"], 1)
                    pe.wait_ge(S["scaled"], b + 1)
                    for t in range(2):
                        if t == 0:
                            pe.wait_ge(S["tok_moved"], b * 6 + 7)
                        else:
                            pe.wait_ge(S["o_gated"], 2 * b + 1)
                        for h in range(HEADS):
                            n = t * HEADS + h
                            r, f = (h % 2) * HD, h // 2
                            rows = slice(r, r + HD)
                            pe.wait_ge(S["s_masked"], 32 * b + n + 1)
                            for j in range(t + 1):
                                mm = nc.tensor.matmul(big[:, h % 2, j * P:(j + 1) * P], qk[rows, 1, f, j * P:(j + 1) * P],
                                                      qk[rows, 0, f, t * P:(t + 1) * P], start=True, stop=True)
                            mm.then_inc(S["s_ready"], 1)
                            if h >= 1:
                                sums(pe, b, t, h - 1)
                        sums(pe, b, t, HEADS - 1)
                        pe.wait_ge(S["o_normed"], 2 * b + t + 1)
                        for f in range(PAIRS):
                            mm = nc.tensor.transpose(big[:, 2 + f // 4, (f % 4) * P:(f % 4 + 1) * P], o[:, f * P:(f + 1) * P], g.c("ident"))
                        mm.then_inc(S["turned"], 1)
                        pe.wait_ge(S["ot_ready"], 2 * b + t + 1)
                    for f in range(PAIRS):
                        mm = nc.tensor.matmul(big[:, 2, 0:T], W("wo")[:, f * D:(f + 1) * D], ot[:, f, :],
                                              start=(f == 0), stop=(f == PAIRS - 1))
                    mm.then_inc(S["y_ready"], 1)

            @blk.scalar
            def _(act):
                nc.scalar.activation(ealog[:], W("a_log"), ACT.Exp).then_inc(S["mask_arg"], 1)
                for h in range(HEADS):
                    act.wait_ge(S["mask_exp"], h + 1)
                    nc.scalar.activation(dmask[:, h, :], dmask[:, h, :], ACT.Exp).then_inc(S["mask_done"], 1)
                nc.scalar.sem_inc(S["tok_moved"], 1)
                nc.scalar.sem_inc(S["silu_ready"], 2)
                with act.Fori(0, B) as b:
                    act.wait_ge(S["added"], b + 1)
                    nc.scalar.activation(xb[:], g.xn[:, bass.ds(b * T, T)], ACT.Copy).then_inc(S["xb_ready"], 1)
                    for f in range(PAIRS):
                        act.wait_ge(S["proj_ready"], b * PAIRS + f + 1)
                        nc.scalar.activation(qk[:, :, f, :], big[:, f % 2, :].rearrange("p (n t) -> p n t", n=2),
                                             ACT.Silu).then_inc(S["silu_ready"], 1)
                        act.wait_ge(S["silu_ready"], b * PAIRS + f + 3)
                        act.wait_ge(S["sq_used"], b * PAIRS + f + 1)
                        nc.scalar.activation(sq[:], qk[:, :, f, :], ACT.Square).then_inc(S["sq_ready"], 1)
                    act.wait_ge(S["nb_ready"], b + 1)
                    nc.scalar.activation(nrm[:], nrm_ps, ACT.Sqrt)
                    nc.scalar.activation(beta[:], beta_ps, ACT.Sigmoid).then_inc(S["sqrt_ready"], 1)
                    for t in range(2):
                        for n, (dst, fn) in enumerate(((v, ACT.Silu), (gt, ACT.Sigmoid), (gate_s, ACT.Sigmoid))):
                            act.wait_ge(S["tok_ready"], b * 6 + t * 3 + n + 1)
                            nc.scalar.activation(dst[:, t, :], big[:, 6:8, :].rearrange("p c n -> p (c n)"), fn).then_inc(S["tok_moved"], 1)
                    for t in range(2):
                        act.wait_ge(S["o_gated"], 2 * b + t + 1)
                        nc.scalar.activation(osq[:], o[:], ACT.Square).then_inc(S["o_squared"], 1)
                        act.wait_ge(S["rms_arg"], 2 * b + t + 1)
                        nc.scalar.activation(ms[:], ms[:], ACT.Sqrt, bias=g.c("eps5"), scale=1.0 / HD).then_inc(S["rms_root"], 1)
                        act.wait_ge(S["turned"], 2 * b + t + 2)
                        nc.scalar.activation(ot[:, :, t * P:(t + 1) * P], big[:, 2:4, :].rearrange("p c (f n) -> p (c f) n", f=4),
                                             ACT.Copy).then_inc(S["ot_ready"], 1)

            @blk.vector
            def _(dve):
                nc.vector.sem_inc(S["added"], 1)
                nc.vector.sem_inc(S["sq_used"], 1)
                nc.vector.sem_inc(S["s_masked"], 2)
                nc.vector.tensor_scalar(W("wo"), W("wo"), W("norm_w"), None, ALU.mult)
                dve.wait_ge(S["mask_arg"], 1)
                for h in range(HEADS):
                    nc.vector.tensor_scalar(dmask[:, h, :], g.c("lag"), ealog[:, h:h + 1], None, ALU.mult).then_inc(S["mask_exp"], 1)
                for h in range(HEADS):
                    dve.wait_ge(S["mask_done"], h + 1)
                    ins = nc.vector.tensor_tensor(dmask[:, h, :], dmask[:, h, :], g.c("earlier"), ALU.mult)
                setup = Chain(dve, st.sem("setup_done"))
                setup.link(ins)
                with dve.Fori(0, B) as b:
                    c = Chain(dve, S["dve_step"], 4 + 2 * 2 + 1, b)
                    dve.wait_ge(S["sqrt_ready"], b + 1)
                    c.link(nc.vector.tensor_scalar(nrm[:], nrm[:], 1e-12, None, ALU.max))
                    c.link(nc.vector.reciprocal(nrm[:], nrm[:]))
                    c.link(nc.vector.tensor_tensor(kb[:], nrm[:, :, 1, :], beta[:], ALU.mult))
                    dve.wait_ge(S["tok_moved"], b * 6 + 7)
                    vv = v[:].rearrange("p t (h d) -> p (t h) d", h=HEADS)
                    gg = gt[:].rearrange("p t (h d) -> p (t h) d", h=HEADS)
                    nc.vector.tensor_tensor(vv, vv, kb[:].rearrange("p t h -> p (t h)").unsqueeze(2).to_broadcast([P, 32, HD]),
                                            ALU.mult).then_inc(S["scaled"], 1)
                    for t in range(2):
                        ins = nc.vector.tensor_tensor(gt[:, t, :].rearrange("p (h d) -> p h d", h=HEADS),
                                                      gt[:, t, :].rearrange("p (h d) -> p h d", h=HEADS),
                                                      nrm[:, t, 0, :].unsqueeze(2).to_broadcast([P, HEADS, HD]), ALU.mult)
                    c.link(ins)
                    for t in range(2):
                        for h in range(HEADS):
                            n = t * HEADS + h
                            dve.wait_ge(S["s_ready"], 32 * b + n + 1)
                            dve.wait_ge(S["s_used"], 32 * b + n + 1)
                            mk = dmask[:, h, 0:P] if t == 0 else dmask[:, h, P:3 * P]
                            nc.vector.tensor_tensor(sc[:, h % 2, 0:(t + 1) * P], big[:, h % 2, 0:(t + 1) * P], mk,
                                                    ALU.mult).then_inc(S["s_masked"], 1)
                        dve.wait_ge(S["s_used"], 32 * b + t * HEADS + HEADS + 2)
                        dve.wait_ge(S["turned"], 2 * b + t + 1)
                        nc.vector.tensor_tensor(o[:], big[:, 6:8, :].rearrange("p c n -> p (c n)"), gt[:, t, :],
                                                ALU.mult).then_inc(S["o_gated"], 1)
                        dve.wait_ge(S["o_squared"], 2 * b + t + 1)
                        nc.vector.tensor_reduce(ms[:], osq[:].rearrange("p (h d) -> p h d", h=HEADS), AX,
                                                ALU.add).then_inc(S["rms_arg"], 1)
                        dve.wait_ge(S["rms_root"], 2 * b + t + 1)
                        c.link(nc.vector.reciprocal(ms[:], ms[:]))
                        o3 = o[:].rearrange("p (h d) -> p h d", h=HEADS)
                        c.link(nc.vector.tensor_tensor(o3, o3, ms[:].unsqueeze(2).to_broadcast([P, HEADS, HD]), ALU.mult))
                        nc.vector.tensor_tensor(o[:], o[:], gate_s[:, t, :], ALU.mult).then_inc(S["o_normed"], 1)
                    dve.wait_ge(S["y_ready"], b + 1)
                    xs = g.x[:, bass.ds(b * T, T)]
                    c.link(nc.vector.tensor_tensor(xs, xs, big[:, 2, 0:T], ALU.add))
                    nc.vector.sem_inc(S["added"], 1)
                    c.close()


def shift_copy(eng, dst, y, sem):
    d3, y3 = dst.rearrange("p (b t) -> p b t", t=T), y.rearrange("p (b t) -> p b t", t=T)
    eng.tensor_copy(d3[0:HD], y3[0:HD])
    eng.tensor_copy(d3[HD:P, :, 1:T], y3[HD:P, :, 0:T - 1])
    eng.memset(d3[HD:P, :, 0:1], 0.0).then_inc(sem, 1)


QT = (0, 96, 160)
KT = (0, 64, 128)
QN = 96


def window_attention(nc, g, w, layer):
    W = lambda n: L3W.of(w, n)
    y = g.xn
    GROUPS = 4
    with Stage(nc, "l3w") as st:
        tab = st.sb("tab", [P, 2, 2, T])
        xb = st.sb("xb", [P, T])
        rot = st.sb("rot", [P, 2, 2, 2, T])
        sq = st.sb("sq", [P, 2, 2, T])
        qf, kf = st.sb("qf", [P, PAIRS, T]), st.sb("kf", [P, PAIRS, T])
        kn = st.sb("kn", [P, 2, T])
        v = st.sb("v", [P, 3, INNER])
        qn = st.sb("qn", [P, 3, HEADS])
        mx, nb = st.sb("mx", [P, 2, GROUPS]), st.sb("nb", [P, 2, GROUPS])
        sm = st.sb("sm", [P, 2, GROUPS])
        rs = st.sb("rs", [P, HEADS])
        pr = st.sb("pr", [P, 2, GROUPS, P])
        pt = st.sb("pt", [P, 2, GROUPS, QN])
        o, ot = st.sb("o", [P, INNER]), st.sb("ot", [P, PAIRS, T])
        identb, maskb = st.sb("identb", [P, QN], mybir.dt.bfloat16), st.sb("maskb", [P, 2, P], mybir.dt.bfloat16)
        big = st.ps("big", [P, 8, BLK])
        qn_ps = big[:, 6, 0:3 * HEADS].rearrange("p (t h) -> p t h", t=3)
        names = ("tab_ready", "xb_ready", "qk_ready", "rot_done", "sq_ready", "kn_ready", "kn_root", "added2", "k_done", "sq_used",
                 "qn_ready", "v_ready", "v_moved", "qn_root", "scale_ready", "s_ready", "max_ready", "exp_done", "p_turned",
                 "pt_ready", "pt_used", "o_scaled", "o_turned", "ot_ready", "y_ready", "added", "dve_step", "pool_step", "sum_ready")
        S = {n: st.sem(n) for n in names}
        def k_root(act, b, f):
            act.wait_ge(S["kn_ready"], b * PAIRS + f + 1)
            if f >= 2:
                act.wait_ge(S["added2"], b * PAIRS + f - 1)
            nc.scalar.activation(kn[:, f % 2, :], big[:, 4 + f % 2, 0:T], ACT.Sqrt).then_inc(S["kn_root"], 1)

        def move_o(act, b, t):
            act.wait_ge(S["o_turned"], 3 * b + t + 1)
            nc.scalar.activation(ot[:, :, QT[t]:QT[t] + QN].rearrange("p (c f) n -> p c f n", c=2),
                                 big[:, 6:8, 0:4 * QN].rearrange("p c (f n) -> p c f n", f=4), ACT.Copy).then_inc(S["ot_ready"], 1)

        with nc.Block() as blk:
            @blk.tensor
            def _(pe):
                pe.wait_ge(S["tab_ready"], 1)
                with pe.Fori(0, B) as b:
                    pe.wait_ge(S["xb_ready"], b + 1)

                    def k_norm(f):
                        pe.wait_ge(S["sq_ready"], b * PAIRS + f + 1)
                        pe.wait_ge(S["kn_root"], b * PAIRS + f + 1)
                        nc.tensor.matmul(big[:, 4 + f % 2, 0:T], g.c("head64"), sq[:, f % 2, 1, :], start=True, stop=True)
                        for t in range(3):
                            mm = nc.tensor.matmul(qn_ps[0:QN, t, 2 * f:2 * f + 2], sq[:, f % 2, 0, QT[t]:QT[t] + QN], g.c("pair"),
                                                  start=True, stop=True)
                        mm.then_inc(S["kn_ready"], 1)

                    for f in range(PAIRS):
                        if f >= 2:
                            pe.wait_ge(S["sq_ready"], b * PAIRS + f - 1)
                        for n, (wa, wb) in enumerate((("wq", "wqr"), ("wk", "wkr"))):
                            nc.tensor.matmul(big[:, 2 * (f % 2) + n, 0:T], W(wa)[:, f * P:(f + 1) * P], xb[:], start=True, stop=True)
                            mm = nc.tensor.matmul(big[:, 2 * (f % 2) + n, T:2 * T], W(wb)[:, f * P:(f + 1) * P], xb[:], start=True, stop=True)
                        mm.then_inc(S["qk_ready"], 1)
                        if f >= 1:
                            k_norm(f - 1)
                    k_norm(PAIRS - 1)
                    for t in range(3):
                        for c in range(2):
                            n = 2 * t + c
                            bank = 7 if n % 2 else 0
                            if n == 0:
                                pe.wait_ge(S["sq_ready"], b * PAIRS + PAIRS)
                            if n >= 2:
                                pe.wait_ge(S["v_moved"], 6 * b + n - 1)
                            nc.tensor.matmul(big[:, bank, :], xb[:, KT[t]:KT[t] + P], W("wv")[:, c * BLK:(c + 1) * BLK],
                                             start=True, stop=True).then_inc(S["v_ready"], 1)
                    pe.wait_ge(S["v_moved"], 6 * b + 6)
                    pe.wait_ge(S["k_done"], b + 1)

                    def scores(u):
                        t, q4 = divmod(u, 4)
                        par, half = q4 % 2, q4 // 2
                        rows = slice(par * HD, (par + 1) * HD)
                        if u >= 2:
                            pe.wait_ge(S["exp_done"], 12 * b + u - 1)
                        for i in range(GROUPS):
                            f = half * GROUPS + i
                            cols = slice(i * P, (i + 1) * P)
                            nc.tensor.matmul(big[0:QN, par, cols], qf[rows, f, QT[t]:QT[t] + QN], kf[rows, f, KT[t]:KT[t] + P],
                                             start=True, stop=False)
                            mm = nc.tensor.matmul(big[0:QN, par, cols], identb[0:QN, :], maskb[0:QN, min(t, 1), :], start=False, stop=True)
                        mm.then_inc(S["s_ready"], 1)

                    def turn(u):
                        pe.wait_ge(S["exp_done"], 12 * b + u + 1)
                        if u >= 2:
                            pe.wait_ge(S["pt_ready"], 12 * b + u - 1)
                        for i in range(GROUPS):
                            mm = nc.tensor.transpose(big[:, 2 + u % 2, i * QN:(i + 1) * QN], pr[0:QN, u % 2, i, :], g.c("ident")[0:QN, 0:QN])
                        mm.then_inc(S["p_turned"], 1)

                    def mix(u):
                        t, q4 = divmod(u, 4)
                        par, half = q4 % 2, q4 // 2
                        if q4 == 0 and t >= 1:
                            pe.wait_ge(S["o_scaled"], 3 * b + t)
                        pe.wait_ge(S["pt_ready"], 12 * b + u + 1)
                        for i in range(GROUPS):
                            h = 2 * (half * GROUPS + i) + par
                            mm = nc.tensor.matmul(big[0:QN, 4 + h // 8, (h % 8) * HD:(h % 8 + 1) * HD], pt[:, u % 2, i, :],
                                                  v[:, t, h * HD:(h + 1) * HD], start=True, stop=True)
                        mm.then_inc(S["pt_used"], 1)

                    def turn_o(t):
                        pe.wait_ge(S["o_scaled"], 3 * b + t + 1)
                        if t >= 1:
                            pe.wait_ge(S["ot_ready"], 3 * b + t)
                        for f in range(PAIRS):
                            mm = nc.tensor.transpose(big[:, 6 + f // 4, (f % 4) * QN:(f % 4 + 1) * QN], o[0:QN, f * P:(f + 1) * P], g.c("ident")[0:QN, 0:QN])
                        mm.then_inc(S["o_turned"], 1)

                    scores(0)
                    for u in range(12):
                        if u + 1 < 12:
                            scores(u + 1)
                        turn(u)
                        if u >= 1:
                            mix(u - 1)
                        if u % 4 == 2 and u > 4:
                            turn_o(u // 4 - 1)
                    mix(11)
                    turn_o(2)
                    pe.wait_ge(S["ot_ready"], 3 * b + 3)
                    for f in range(PAIRS):
                        mm = nc.tensor.matmul(big[:, 6, 0:T], W("wo")[:, f * D:(f + 1) * D], ot[:, f, :],
                                              start=(f == 0), stop=(f == PAIRS - 1))
                    mm.then_inc(S["y_ready"], 1)

            @blk.scalar
            def _(act):
                with act.Fori(0, B) as b:
                    act.wait_ge(S["added"], b + 1)
                    nc.scalar.activation(xb[0:HD, :], y[0:HD, bass.ds(b * T, T)], ACT.Copy)
                    nc.scalar.activation(xb[HD:P, 1:T], y[HD:P, bass.ds(b * T, T - 1)], ACT.Copy).then_inc(S["xb_ready"], 1)
                    for f in range(PAIRS):
                        act.wait_ge(S["rot_done"], b * PAIRS + f + 1)
                        if f >= 2:
                            act.wait_ge(S["kn_ready"], b * PAIRS + f - 1)
                        nc.scalar.activation(sq[:, f % 2], big[:, 2 * (f % 2):2 * (f % 2) + 2, 0:T], ACT.Square).then_inc(S["sq_ready"], 1)
                        if f >= 1:
                            k_root(act, b, f - 1)
                    k_root(act, b, PAIRS - 1)
                    nc.scalar.activation(qn[0:QN], qn_ps[0:QN], ACT.Sqrt).then_inc(S["qn_root"], 1)
                    for n in range(6):
                        act.wait_ge(S["v_ready"], 6 * b + n + 1)
                        nc.scalar.activation(v[:, n // 2, (n % 2) * BLK:(n % 2 + 1) * BLK], big[:, 7 if n % 2 else 0, :],
                                             ACT.Copy).then_inc(S["v_moved"], 1)
                    for u in range(12):
                        t, q4 = divmod(u, 4)
                        par, half = q4 % 2, q4 // 2
                        act.wait_ge(S["max_ready"], 12 * b + u + 1)
                        if u >= 2:
                            act.wait_ge(S["p_turned"], 12 * b + u - 1)
                        for i in range(GROUPS):
                            h = 2 * (half * GROUPS + i) + par
                            ins = nc.scalar.activation(pr[0:QN, u % 2, i, :], big[0:QN, par, i * P:(i + 1) * P], ACT.Exp,
                                                       bias=nb[0:QN, u % 2, i:i + 1], scale=qn[0:QN, t, h:h + 1],
                                                       accum_out=sm[0:QN, u % 2, i:i + 1])
                        ins.then_inc(S["exp_done"], 1)
                        act.wait_ge(S["p_turned"], 12 * b + u + 1)
                        if u >= 2:
                            act.wait_ge(S["pt_used"], 12 * b + u - 1)
                        nc.scalar.activation(pt[:, u % 2], big[:, 2 + u % 2, 0:GROUPS * QN].rearrange("p (i n) -> p i n", n=QN),
                                             ACT.Copy).then_inc(S["pt_ready"], 1)
                        if u % 4 == 3 and u > 4:
                            move_o(act, b, u // 4 - 1)
                    move_o(act, b, 2)

            @blk.gpsimd
            def _(pool):
                with pool.Fori(0, B) as b:
                    for f in range(PAIRS):
                        pool.wait_ge(S["rot_done"], b * PAIRS + f + 1)
                        nc.gpsimd.tensor_tensor(qf[:, f, :], rot[:, f % 2, 0, 0, :], rot[:, f % 2, 0, 1, :], ALU.add)
                        nc.gpsimd.tensor_tensor(kf[:, f, :], rot[:, f % 2, 1, 0, :], rot[:, f % 2, 1, 1, :], ALU.add).then_inc(S["sum_ready"], 1)

            @blk.vector
            def _(dve):
                nc.vector.sem_inc(S["added"], 1)
                nc.vector.sem_inc(S["kn_root"], 2)
                nc.vector.memset(xb[HD:P, 0:1], 0.0)
                for n, s in enumerate(("qs", "ks")):
                    for m in range(2):
                        nc.vector.tensor_scalar(tab[:, n, m, :], g.c(("rot_q", "rot_k")[n])[:, m * T:(m + 1) * T], W(s)[:, m:m + 1], None, ALU.mult)
                nc.vector.tensor_copy(identb[:], g.c("ident")[:, 0:QN])
                nc.vector.tensor_copy(maskb[:], g.c("window").rearrange("p (a n) -> p a n", a=2)).then_inc(S["tab_ready"], 1)
                dve.wait_ge(S["tab_ready"], 1)
                with dve.Fori(0, B) as b:
                    c = Chain(dve, S["dve_step"], PAIRS * 2 + 2 + 12 * 1 + 3 + 1, b)

                    def k_scale(f):
                        dve.wait_ge(S["kn_root"], b * PAIRS + f + 3)
                        c.link(nc.vector.tensor_scalar(kn[:, f % 2, :], kn[:, f % 2, :], 1e-12, None, ALU.max))
                        c.link(nc.vector.reciprocal(kn[:, f % 2, :], kn[:, f % 2, :]))
                        dve.wait_ge(S["sum_ready"], b * PAIRS + f + 1)
                        ins = nc.vector.tensor_tensor(kf[:, f, :], kf[:, f, :], kn[:, f % 2, :], ALU.mult)
                        ins.then_inc(S["added2"], 1)

                    for f in range(PAIRS):
                        dve.wait_ge(S["qk_ready"], b * PAIRS + f + 1)
                        if f >= 2:
                            dve.wait_ge(S["sum_ready"], b * PAIRS + f - 1)
                        nc.vector.tensor_tensor(rot[:, f % 2].rearrange("p a b t -> p a (b t)"), big[:, 2 * (f % 2):2 * (f % 2) + 2, :],
                                                tab[:].rearrange("p a b t -> p a (b t)"), ALU.mult).then_inc(S["rot_done"], 1)
                        if f >= 2:
                            k_scale(f - 2)
                    k_scale(PAIRS - 2)
                    k_scale(PAIRS - 1)
                    dve.wait_ge(S["added2"], b * PAIRS + PAIRS)
                    nc.vector.sem_inc(S["k_done"], 1)
                    dve.wait_ge(S["qn_root"], b + 1)
                    c.link(nc.vector.tensor_scalar(qn[0:QN], qn[0:QN], 1e-12, None, ALU.max))
                    c.link(nc.vector.reciprocal(qn[0:QN], qn[0:QN]))
                    nc.vector.tensor_scalar(qn[0:QN], qn[0:QN], 8.0, None, ALU.mult).then_inc(S["scale_ready"], 1)
                    dve.wait_ge(S["scale_ready"], b + 1)

                    def sums_inv(u):
                        t, q4 = divmod(u, 4)
                        par, half = q4 % 2, q4 // 2
                        dve.wait_ge(S["exp_done"], 12 * b + u + 1)
                        hs = rs[:].rearrange("p (f two) -> p f two", two=2)[0:QN, half * GROUPS:(half + 1) * GROUPS, par]
                        return nc.vector.reciprocal(hs, sm[0:QN, u % 2, :])

                    def scale_o(t):
                        dve.wait_ge(S["pt_used"], 12 * b + 4 * t + 4)
                        if t >= 1:
                            dve.wait_ge(S["o_turned"], 3 * b + t)
                        nc.vector.tensor_tensor(o[0:QN, :].rearrange("p (h d) -> p h d", h=HEADS),
                                                big[0:QN, 4:6, :].rearrange("p c (h d) -> p (c h) d", h=8),
                                                rs[0:QN, :].unsqueeze(2).to_broadcast([QN, HEADS, HD]), ALU.mult).then_inc(S["o_scaled"], 1)

                    for u in range(12):
                        t, q4 = divmod(u, 4)
                        par, half = q4 % 2, q4 // 2
                        dve.wait_ge(S["s_ready"], 12 * b + u + 1)
                        c.link(nc.vector.tensor_reduce(mx[0:QN, u % 2, :], big[0:QN, par, :].rearrange("p (i n) -> p i n", n=P), AX, ALU.max))
                        if u >= 2:
                            dve.wait_ge(S["exp_done"], 12 * b + u - 1)
                        scale = qn[:].rearrange("p t (f two) -> p t f two", two=2)[0:QN, t, half * GROUPS:(half + 1) * GROUPS, par]
                        nc.vector.scalar_tensor_tensor(out=nb[0:QN, u % 2, :], in0=mx[0:QN, u % 2, :], scalar=-1.0, in1=scale,
                                                       op0=ALU.mult, op1=ALU.mult).then_inc(S["max_ready"], 1)
                        if u >= 1:
                            ins = sums_inv(u - 1)
                            if u % 4 == 0:
                                c.link(ins)
                                scale_o(u // 4 - 1)
                    c.link(sums_inv(11))
                    scale_o(2)
                    dve.wait_ge(S["y_ready"], b + 1)
                    ys = y[:, bass.ds(b * T, T)]
                    c.link(nc.vector.tensor_tensor(ys, ys, big[:, 6, 0:T], ALU.add))
                    nc.vector.sem_inc(S["added"], 1)
                    c.close()


def gated_mlp(nc, g, w, layer):
    W = lambda n: L3F.of(w, n)
    y = g.xn
    ROWS = (P, P, HALF - 2 * P)
    with Stage(nc, "l3f") as st:
        xs = st.sb("xs", [P, N])
        shifted = st.sem("shifted")
        with nc.Block() as blk:
            @blk.vector
            def _(dve):
                shift_copy(nc.vector, xs[:], y[:], shifted)
        layer_norm(nc, "l3n", xs, xs, g.c("mean"), g.c("eps5"), W("g"), W("b"))
        h_ps, o_ps = st.ps("h_ps", [P, 3, 2, BLK]), st.ps("o_ps", [P, BLK])
        ge, hid = st.sb("ge", [P, 3, BLK]), st.sb("hid", [P, 3, BLK])
        up_ready, gelu_ready, hid_ready, hid_used, out_used, step = (
            st.sem(n) for n in ("up_ready", "gelu_ready", "hid_ready", "hid_used", "out_used", "step"))
        def down(pe, i, c):
            if c == 0:
                pe.wait_ge(out_used, i + 1)
            pe.wait_ge(hid_ready, 3 * i + c + 4)
            nc.tensor.matmul(o_ps[:], W("w2")[0:ROWS[c], c * D:(c + 1) * D], hid[0:ROWS[c], c, :],
                             start=(c == 0), stop=(c == 2)).then_inc(hid_used, 1)

        with nc.Block() as blk:
            @blk.tensor
            def _(pe):
                with pe.Fori(0, NBLK) as i:
                    def up(c):
                        pe.wait_ge(hid_ready, 3 * i + c + 1)
                        for m in range(2):
                            at = (3 * m + c) * P
                            mm = nc.tensor.matmul(h_ps[0:ROWS[c], c, m, :], W("w1")[:, at:at + ROWS[c]], xs[:, block(i)],
                                                  start=True, stop=True)
                        mm.then_inc(up_ready, 1)

                    for c in range(3):
                        up(c)
                        if c >= 1:
                            down(pe, i, c - 1)
                    down(pe, i, 2)

            @blk.scalar
            def _(act):
                with act.Fori(0, NBLK) as i:
                    for c in range(3):
                        act.wait_ge(up_ready, 3 * i + c + 1)
                        act.wait_ge(hid_ready, 3 * i + c + 1)
                        r = ROWS[c]
                        nc.scalar.activation(ge[0:r, c, :], h_ps[0:r, c, 1, :], ACT.Gelu,
                                             bias=W("b1")[0:r, 3 + c:4 + c]).then_inc(gelu_ready, 1)

            @blk.vector
            def _(dve):
                nc.vector.sem_inc(hid_ready, 3)
                nc.vector.sem_inc(out_used, 1)
                nc.vector.sem_inc(hid_used, 3)
                with dve.Fori(0, NBLK) as i:
                    c_ = Chain(dve, step, 1, i)
                    for c in range(3):
                        r = ROWS[c]
                        dve.wait_ge(gelu_ready, 3 * i + c + 1)
                        dve.wait_ge(hid_used, 3 * i + c + 1)
                        nc.vector.scalar_tensor_tensor(out=hid[0:r, c, :], in0=h_ps[0:r, c, 0, :], scalar=W("b1")[0:r, c:c + 1],
                                                       in1=ge[0:r, c, :], op0=ALU.add, op1=ALU.mult).then_inc(hid_ready, 1)
                    dve.wait_ge(hid_used, 3 * i + 3 + 3)
                    ys = y[:, block(i)]
                    c_.link(nc.vector.scalar_tensor_tensor(out=ys, in0=o_ps[:], scalar=W("b2"), in1=ys, op0=ALU.add, op1=ALU.add))
                    nc.vector.sem_inc(out_used, 1)
                    c_.close()


CONST = layout([("ident", P, P), ("mean", P, P), ("mask8", P, P), ("before8", P, 64), ("before4", P, 16),
                ("pick8", P, 8 * P), ("ones_row", 1, 512), ("eps5", P, 1),
                ("mean32", P, P), ("sum32", P, P), ("causal", P, P), ("eps_rms", P, 1)])
CONST3 = layout([("minus_row", 1, P), ("pair", P, 2), ("head64", P, P), ("lag", P, 3 * P), ("earlier", P, 3 * P),
                 ("rot_q", P, 2 * T), ("rot_k", P, 2 * T), ("window", P, 2 * P)])


def constants():
    i = np.arange(P)
    pick8 = np.zeros((P, 8, P), np.float32)
    pick8[np.arange(8), np.arange(8), :] = 1
    key, query = i[:, None], np.concatenate([i, i + P, i])[None]
    lag = query - 1 - key
    q96 = i[:, None]
    window0 = (i[None] <= q96) & (i[None] >= q96 - WINDOW)
    window1 = (i[None] <= q96 + WINDOW) & (i[None] >= q96)
    half = np.arange(0, HD, 2, dtype=np.float32)
    t = np.arange(T, dtype=np.float32)
    freqs = t[:, None] * (np.float32(1) / np.float32(10000) ** (half / np.float32(HD)))[None]
    base = (half + np.float32(0.4 * HD)) / np.float32(1.4 * HD)
    scale = base[None] ** ((t - T // 2) / np.float32(WINDOW // 2))[:, None]
    cos, sin = np.cos(freqs), np.sin(freqs)

    def rotation(s):
        c4 = np.concatenate([cos * s] * 4, 1).T
        s4 = np.concatenate([-sin * s, sin * s] * 2, 1).T
        return np.concatenate([c4, s4], 1)

    made = {
        "ident": np.eye(P), "mean": np.full((P, P), 1.0 / P), "mask8": (i[:, None] // 8 == i[None] // 8),
        "before8": np.tile(np.tril(np.ones((8, 8)), -1).reshape(1, 64), (P, 1)),
        "before4": np.tile(np.tril(np.ones((4, 4)), -1).reshape(1, 16), (P, 1)),
        "pick8": pick8.reshape(P, 8 * P), "ones_row": np.ones((1, 512)), "eps5": np.full((P, 1), 1e-5),
        "minus_row": np.full((1, P), -1.0), "pair": (i[:, None] // HD == np.arange(2)[None]),
        "head64": (i[:, None] // HD == i[None] // HD), "lag": np.where(lag >= 0, -lag, 0), "earlier": lag >= 0,
        "rot_q": rotation(scale), "rot_k": rotation(np.float32(1) / scale),
        "mean32": (i[:, None] // 32 == i[None] // 32) / 8.0,
        "sum32": (i[:, None] // 32 == i[None] // 32) * (i[:, None] % 32 == 8),
        "causal": np.where(i[None] <= i[:, None], 0, NEG), "eps_rms": np.full((P, 1), 1.1920929e-07),
        "window": np.concatenate([np.where(window0, 0, NEG), np.where(window1, 0, NEG)], 1),
    }
    return made


class Shared:
    pass


def program(nc, dram, out):
    ctx = ExitStack()
    with ctx:
        g = Shared()
        g.x = ctx.enter_context(nc.sbuf_tensor("x", [P, N], F32))
        g.xn = ctx.enter_context(nc.sbuf_tensor("xn", [P, N], F32))
        const = ctx.enter_context(nc.sbuf_tensor("const", [P, CONST.n], F32))
        g.c = lambda n: CONST.of(const, n) if n in CONST.at else CONST3.of(g.const3, n)
        g.ones_row = CONST.of(const, "ones_row")[:, 0:P]
        in_landed = ctx.enter_context(nc.semaphore("in_landed"))
        with nc.Block() as blk:
            @blk.sync
            def _(sp):
                sp.dma_start(g.x[:], dram["x"]).then_inc(in_landed, 16)
                sp.dma_start(const[:], dram["const"]).then_inc(in_landed, 16)
                sp.wait_ge(in_landed, 32)
        if 0 in STAGES:
            with Stage(nc, "l0") as st:
                w, prob_t = st.sb("w", [P, L0.n]), st.sb("prob_t", [P, N])
                load_pack(nc, st, dram["l0"], w, "l0")
                layer_norm(nc, "ln0", g.x, g.xn, g.c("mean"), g.c("eps5"))
                linear_attention(nc, g, w)
                gate(nc, g, "l0g", g.xn, L0.of(w, "gate"), None, 8, l0_weigh(nc, g), prob_t)
                swiglu_experts(nc, g, w, prob_t)
        if 1 in STAGES:
            with Stage(nc, "l1") as st:
                w, prob_t = st.sb("w", [P, L1.n]), st.sb("prob_t", [P, N])
                load_pack(nc, st, dram["l1"], w, "l1")
                layer_norm(nc, "ln1", g.x, g.xn, g.c("mean"), g.c("eps5"))
                wkv_attention(nc, g, w)
                gate(nc, g, "l1g", g.xn, L1.of(w, "gate"), L1.of(w, "gate_b"), 8, l1_weigh(nc, g), prob_t)
                linear_experts(nc, g, w, prob_t)
        if 2 in STAGES:
            layer_norm(nc, "ln2", g.x, g.xn, g.c("mean"), g.c("eps5"))
            if "a" in SUB:
                delta_attention(nc, g, dram)
            if "f" in SUB:
                with Stage(nc, "l2") as st:
                    w, prob_t = st.sb("w", [P, L2F.n]), st.sb("prob_t", [P, N])
                    h = st.sb("h", [P, N])
                    load_pack(nc, st, dram["l2f"], w, "l2f")
                    rms_norm(nc, "l2n1", g.xn, h, g.c("mean"), g.c("eps_rms"), L2F.of(w, "n1"))
                    causal_attention(nc, g, w, h)
                    rms_norm(nc, "l2n2", g.xn, h, g.c("mean"), g.c("eps_rms"), L2F.of(w, "n2"))
                    gate(nc, g, "l2g", h, L2F.of(w, "gate"), None, 4, l2_weigh(nc, g), prob_t)
                    mixed_experts(nc, g, w, h, prob_t)
        if 3 in STAGES:
            g.const3 = ctx.enter_context(nc.sbuf_tensor("const3", [P, CONST3.n], F32))
            with Stage(nc, "c3") as st:
                load_pack(nc, st, dram["const3"], g.const3, "const3")
            layer_norm(nc, "ln3", g.x, g.xn, g.c("mean"), g.c("eps5"))
            if "a" in SUB:
                with Stage(nc, "l3") as st:
                    w = st.sb("w", [P, L3A.n])
                    load_pack(nc, st, dram["l3a"], w, "l3a")
                    decay_attention(nc, g, w)
            if "f" in SUB:
                with Stage(nc, "l3deep") as st:
                    wa, wf = st.sb("wa", [P, L3W.n]), st.sb("wf", [P, L3F.n])
                    with nc.Fori(0, DEPTH) as layer:
                        with Stage(nc, "l3load") as ld:
                            load_pack(nc, ld, dram["l3w"][bass.ds(layer, 1)].rearrange("l p n -> (l p) n"), wa, "l3w")
                            load_pack(nc, ld, dram["l3f"][bass.ds(layer, 1)].rearrange("l p n -> (l p) n"), wf, "l3f")
                        window_attention(nc, g, wa, layer)
                        gated_mlp(nc, g, wf, layer)
                    done = st.sem("done")
                    with nc.Block() as blk:
                        @blk.vector
                        def _(dve):
                            nc.vector.tensor_tensor(g.x[:], g.x[:], g.xn[:], ALU.add).then_inc(done, 1)
        stored = ctx.enter_context(nc.semaphore("stored"))
        with nc.Block() as blk:
            @blk.sync
            def _(sp):
                sp.dma_start(out, g.x[:]).then_inc(stored, 16)
                sp.wait_ge(stored, 16)


STAGES = (0, 1, 2, 3)
SUB = "af"


def fill(pack, pieces):
    a = np.zeros((P, pack.n), np.float32)
    for name, (at, rows, cols) in pack.at.items():
        piece = np.asarray(pieces[name], np.float32)
        assert piece.shape == (rows, cols), (name, piece.shape, rows, cols)
        a[:rows, at:at + cols] = piece
    return a


def pad_rows(a):
    return np.concatenate([a, np.zeros((P - a.shape[0], a.shape[1]), a.dtype)], 0)


def col(v):
    return np.asarray(v).reshape(-1, 1)


def row(v):
    return np.asarray(v).reshape(1, -1)


def host_layout(i):
    i = {k: np.asarray(v) for k, v in i.items()}
    packs = {"x": np.ascontiguousarray(i["L0_attn_query"].reshape(N, D).T), "const": fill(CONST, constants()), "const3": fill(CONST3, constants())}
    a = "L0_attn_"
    packs["l0"] = fill(L0, {
        "wq": i[a + "Wq"].T, "wkv": np.concatenate([i[a + "Wk"].T, i[a + "Wv"].T], 1), "wo": i[a + "Wo"].T,
        "bq": col(i[a + "bq"]), "bo": col(i[a + "bo"]), "bkv": row(np.concatenate([i[a + "bk"], i[a + "bv"]])),
        "gate": i["L0_ffn_gate_w"].T,
        "w12": i["L0_ffn_w12"].transpose(2, 0, 1).reshape(D, -1),
        "w3": i["L0_ffn_w3"].reshape(8, D, 2, P).transpose(3, 0, 2, 1).reshape(P, -1)})
    a, f = "L1_attn_", "L1_ffn_"
    packs["l1"] = fill(L1, {
        "wk": i[a + "Wk"].T, "wv": i[a + "Wv"].T, "wr": i[a + "Wr"].T, "wo": i[a + "Wo"].T,
        **{n: col(i[a + n]) for n in ("bo", "u", "w", "tmk", "tmv", "tmr")},
        "gate": i[f + "gate_W"], "gate_b": row(i[f + "gate_b"]),
        "ew": i[f + "expert_W"].transpose(1, 0, 2).reshape(D, -1), "eb": pad_rows(i[f + "expert_b"])})
    a = "L2_attn_"
    by_pair = lambda wo: wo.reshape(PAIRS, P, D).transpose(1, 0, 2).reshape(P, -1)
    n = np.arange(P)
    b_, t_ = n // CH, n % CH
    same = b_[:, None] == b_[None]
    row_t, col_t = t_[:, None], t_[None]
    upto, before = same & (row_t <= col_t), same & (row_t < col_t)
    after = same & (row_t > col_t)
    first = same & (row_t < CH // 2)
    ends = np.stack([(b_[:, None] == np.arange(GB)) & (row_t < CH // 2), (b_[:, None] == np.arange(GB)) & (row_t >= CH // 2)], -1)
    packs["l2a"] = fill(L2A, {
        **{n_: i[a + "W" + n_[1:]].T for n_ in ("wk", "wq", "wv", "wa")}, "war": i[a + "WaR"].T,
        "wbg": np.concatenate([i[a + "Wb"].T, i[a + "Wg"].T], 1), "wo": by_pair(i[a + "Wo"].T),
        "lnw": col(i[a + "ln_w"]), "lnb": col(i[a + "ln_b"]), "ba": row(i[a + "ba"]), "bar": row(i[a + "baR"]),
        "bbg": row(np.concatenate([i[a + "bb"], i[a + "bg"]])),
        "cum": first.astype(np.float32) - upto, "ends": ends.reshape(P, 8),
        "keep": np.concatenate([before, upto, before, after], 1), "keep_r": np.concatenate([before, upto, after], 1)})
    f = "L2_ffn_"

    def spread32(wt):
        out = np.zeros((D, HEADS, 32), np.float32)
        out[:, :, :8] = wt.reshape(D, HEADS, 8)
        return out.reshape(D, -1)

    def head_col(v):
        out = np.zeros((4, 32), np.float32)
        out[:, :8] = v
        return out.reshape(P, 1)

    up = lambda n: i[f + n].T
    tall = lambda n: i[f + n].T.reshape(2, P, -1).transpose(1, 0, 2).reshape(P, -1)
    packs["l2f"] = fill(L2F, {
        "n1": col(i[f + "n1_w"]), "n2": col(i[f + "n2_w"]), "wq": spread32(up("wq")), "wk": spread32(up("wk")), "wv": up("wv"),
        "qn": head_col(i[f + "qn_w"]), "kn": head_col(i[f + "kn_w"]),
        "wo": spread32(i[f + "wo"]).T.reshape(4, P, D).transpose(1, 0, 2).reshape(P, -1), "gate": up("gate_w"),
        "e0u": up("e0_up"), "e0d": tall("e0_down"), "e1a": up("e1_w1"), "e1b": up("e1_w2"), "e1d": tall("e1_down"),
        "e2a": up("e2_l1"), "e2b": tall("e2_l2"), "e2c": tall("e2_l3"), "e2d": tall("e2_l4"),
        "e3a": up("e3_down"), "e3b": up("e3_up"), "e3d": tall("e3_out")})
    a = "L3_attn_"
    by_pair = lambda wo: wo.reshape(PAIRS, P, D).transpose(1, 0, 2).reshape(P, -1)
    packs["l3a"] = fill(L3A, {
        **{n: i[a + "W" + n[1:]] for n in ("wq", "wk", "wv", "wf", "wg", "wb")}, "wo": by_pair(i[a + "Wo"]),
        "dt": row(i[a + "dt_bias"]), "bg": row(i[a + "bg"]), "a_log": np.tile(row(i[a + "A_log"]), (P, 1)),
        "norm_w": col(np.tile(i[a + "norm_w"], 2))})
    a = "L3_ffn_"
    swap = np.arange(INNER).reshape(HEADS, 2, HD // 2)[:, ::-1].reshape(-1)
    deep_w, deep_f = [], []
    for l in range(DEPTH):
        wq, wk, wv = np.split(i[a + "Wqkv"][l], 3, -1)
        qs, ks = (np.tile(i[a + s][l], 2) for s in ("q_scale", "k_scale"))
        deep_w.append(fill(L3W, {
            "wq": wq, "wqr": wq[:, swap], "wk": wk, "wkr": wk[:, swap], "wv": wv, "wo": by_pair(i[a + "Wo"][l]),
            "qs": np.stack([qs, qs[swap[:P]]], 1), "ks": np.stack([ks, ks[swap[:P]]], 1)}))
        w1 = np.zeros((D, 2, 3 * P), np.float32)
        w1[:, :, :HALF] = i[a + "W1"][l].reshape(D, 2, HALF)
        b1 = np.zeros((2, 3 * P), np.float32)
        b1[:, :HALF] = i[a + "b1"][l].reshape(2, HALF)
        w2 = np.zeros((3 * P, D), np.float32)
        w2[:HALF] = i[a + "W2"][l]
        deep_f.append(fill(L3F, {
            "w1": w1.reshape(D, -1), "b1": b1.reshape(6, P).T, "w2": w2.reshape(3, P, D).transpose(1, 0, 2).reshape(P, -1),
            "b2": col(i[a + "b2"][l]), "g": col(i[a + "ln_g"][l]), "b": col(i[a + "ln_b"][l])}))
    packs["l3w"], packs["l3f"] = np.stack(deep_w), np.stack(deep_f)
    return packs


def kernel(**inputs):
    import concourse.bacc as _bacc
    from concourse.bass_utils import run_bass_kernel_spmd as _run

    arrays = {k + "_dram": v for k, v in host_layout(inputs).items()}
    nc = _bacc.Bacc("TRN2", target_bir_lowering=False, num_devices=1)
    dram = {k[:-5]: nc.dram_tensor(k, v.shape, F32, kind="ExternalInput").ap() for k, v in arrays.items()}
    out = nc.dram_tensor("out_dram", (P, N), F32, kind="ExternalOutput").ap()
    program(nc, dram, out)
    r = _run(nc, [arrays], core_ids=[0])
    return np.ascontiguousarray(r.results[0]["out_dram"].T).reshape(B, T, D)
```

```python
from contextlib import ExitStack

import concourse.bass as bass
from concourse import mybir
import numpy as np

F32 = mybir.dt.float32
U32 = mybir.dt.uint32
ALU = mybir.AluOpType
ACT = mybir.ActivationFunctionType
AX = mybir.AxisListType.X

P = 128
B, T, D = 16, 256, 128
N = B * T
BLK = 512
NBLK = N // BLK
TILES = N // P
HEADS = 16
NEG = -1.0e30
HD = 64
INNER = HEADS * HD
PAIRS = HEADS // 2


class Stage:

    def __init__(self, nc, name):
        self.nc, self.name, self.ctx = nc, name, ExitStack()
        self.sems = []

    def __enter__(self):
        return self

    def __exit__(self, *e):
        if e[0] is None:
            with self.nc.Block() as block:
                @block.sync
                def _(sp):
                    for s in self.sems:
                        self.nc.sync.sem_clear(s)
        return self.ctx.__exit__(*e)

    def sb(self, name, shape, dt=F32):
        return self.ctx.enter_context(self.nc.sbuf_tensor(f"{self.name}_{name}", shape, dt))

    def ps(self, name, shape, dt=F32):
        return self.ctx.enter_context(self.nc.psum_tensor(f"{self.name}_{name}", shape, dt))

    def sem(self, name):
        s = self.ctx.enter_context(self.nc.semaphore(f"{self.name}_{name}"))
        self.sems.append(s)
        return s


class Chain:

    def __init__(self, eng, sem, per_turn=0, turn=0):
        self.eng, self.sem, self.per_turn, self.turn, self.n = eng, sem, per_turn, turn, 0

    def link(self, ins):
        ins.then_inc(self.sem, 1)
        self.n += 1
        self.eng.wait_ge(self.sem, self.turn * self.per_turn + self.n)

    def close(self):
        assert self.n == self.per_turn, (self.n, self.per_turn)


def block(i):
    return bass.ds(i * BLK, BLK)


def bcast(ap, shape):
    return ap.to_broadcast(shape)


class Pack:

    def __init__(self):
        self.at, self.n, self.rows = {}, 0, {}

    def add(self, name, rows, cols):
        self.at[name] = (self.n, rows, cols)
        self.n += cols

    def of(self, tile, name):
        a, rows, cols = self.at[name]
        return tile[0:rows, a:a + cols]


def layout(pieces):
    p = Pack()
    for name, rows, cols in pieces:
        p.add(name, rows, cols)
    return p


def load_pack(nc, st, dram, tile, name):
    landed = st.sem(name + "_landed")
    with nc.Block() as blk:
        @blk.sync
        def _(sp):
            sp.dma_start(tile[:], dram).then_inc(landed, 16)
            sp.wait_ge(landed, 16)


def layer_norm(nc, name, src, dst, mean_w, eps_col, gain=None, shift=None):
    with Stage(nc, name) as st:
        sq = st.sb("sq", [P, N])
        mean_ps = st.ps("mean", [P, 2, BLK])
        var_ps = st.ps("var", [P, 2, BLK])
        std = st.sb("std", [P, 2, BLK])
        mean_ready, centered, squared = st.sem("mean_ready"), st.sem("centered"), st.sem("squared")
        var_ready, std_ready, normed = st.sem("var_ready"), st.sem("std_ready"), st.sem("normed")
        dve_step = st.sem("dve_step")
        extra = 1 if gain is not None else 0

        with nc.Block() as blk:
            @blk.tensor
            def _(pe):
                with pe.Fori(0, NBLK // 2) as i:
                    for k in range(2):
                        pe.wait_ge(centered, 2 * i + k + 1)
                        nc.tensor.matmul(mean_ps[:, k, :], mean_w, src[:, block(2 * i + k)],
                                         start=True, stop=True).then_inc(mean_ready, 1)
                with pe.Fori(0, NBLK // 2) as i:
                    for k in range(2):
                        pe.wait_ge(squared, 2 * i + k + 1)
                        pe.wait_ge(std_ready, 2 * i + k + 1)
                        nc.tensor.matmul(var_ps[:, k, :], mean_w, sq[:, block(2 * i + k)],
                                         start=True, stop=True).then_inc(var_ready, 1)

            @blk.vector
            def _(dve):
                nc.vector.sem_inc(centered, 2)
                with dve.Fori(0, NBLK // 2) as i:
                    for k in range(2):
                        dve.wait_ge(mean_ready, 2 * i + k + 1)
                        nc.vector.tensor_tensor(dst[:, block(2 * i + k)], src[:, block(2 * i + k)],
                                                mean_ps[:, k, :], ALU.subtract).then_inc(centered, 1)
                nc.vector.sem_inc(normed, 2)
                with dve.Fori(0, NBLK // 2) as i:
                    c = Chain(dve, dve_step, 2 + 2 * extra, i)
                    for k in range(2):
                        dve.wait_ge(std_ready, 2 * i + k + 3)
                        c.link(nc.vector.reciprocal(std[:, k, :], std[:, k, :]))
                        cols = dst[:, block(2 * i + k)]
                        if gain is None:
                            nc.vector.tensor_tensor(cols, cols, std[:, k, :], ALU.mult).then_inc(normed, 1)
                        else:
                            c.link(nc.vector.tensor_tensor(cols, cols, std[:, k, :], ALU.mult))
                            nc.vector.tensor_scalar(cols, cols, gain, shift, ALU.mult, ALU.add).then_inc(normed, 1)
                    c.close()

            @blk.scalar
            def _(act):
                with act.Fori(0, NBLK // 2) as i:
                    for k in range(2):
                        act.wait_ge(centered, 2 * i + k + 3)
                        nc.scalar.activation(sq[:, block(2 * i + k)], dst[:, block(2 * i + k)],
                                             ACT.Square).then_inc(squared, 1)
                nc.scalar.sem_inc(std_ready, 2)
                with act.Fori(0, NBLK // 2) as i:
                    for k in range(2):
                        act.wait_ge(var_ready, 2 * i + k + 1)
                        act.wait_ge(normed, 2 * i + k + 1)
                        nc.scalar.activation(std[:, k, :], var_ps[:, k, :], ACT.Sqrt,
                                             bias=eps_col).then_inc(std_ready, 1)


L0 = layout([("wq", P, D), ("wkv", P, 2 * D), ("wo", P, D), ("bq", P, 1), ("bo", P, 1), ("bkv", 1, 2 * D),
             ("gate", P, 8), ("w12", P, 8 * 512), ("w3", P, 8 * 2 * D)])


def linear_attention(nc, g, w):
    W = lambda n: L0.of(w, n)
    with Stage(nc, "l0a") as st:
        xb = st.sb("xb", [P, T])
        kv = st.sb("kv", [P, 2, 2 * D + 2])
        neg, pos = st.sb("neg", [P, 2, D]), st.sb("pos", [P, 2, D])
        qneg, phiq = st.sb("qneg", [P, T]), st.sb("phiq", [P, T])
        qpos = st.sb("qpos", [P, T])
        sm, zm = st.sb("sm", [P, D]), st.sb("zm", [P, D])
        rden, ctx = st.sb("rden", [P, T]), st.sb("ctx", [P, T])
        kv_ps = st.ps("kv_ps", [P, 2, 2 * D])
        q_ps, s_ps = st.ps("q_ps", [P, T]), st.ps("s_ps", [P, D + 1])
        num_ps, den_ps, o_ps = st.ps("num_ps", [P, T]), st.ps("den_ps", [P, T]), st.ps("o_ps", [P, T])
        ones_set, xb_ready, qkv_ready, min_ready = (st.sem(n) for n in ("ones_set", "xb_ready", "qkv_ready", "min_ready"))
        exp_ready, phi_ready, s_ready, masked = (st.sem(n) for n in ("exp_ready", "phi_ready", "s_ready", "masked"))
        numden_ready, ctx_ready, o_ready, added, dve_step = (
            st.sem(n) for n in ("numden_ready", "ctx_ready", "o_ready", "added", "dve_step"))

        with nc.Block() as blk:
            @blk.tensor
            def _(pe):
                with pe.Fori(0, B) as b:
                    pe.wait_ge(xb_ready, b + 1)
                    nc.tensor.matmul(q_ps[:], W("wq"), xb[:], start=True, stop=True)
                    for t in range(2):
                        nc.tensor.matmul(kv_ps[:, t, :], xb[:, t * P:(t + 1) * P], W("wkv"), start=True, stop=False)
                        mm = nc.tensor.matmul(kv_ps[:, t, :], g.ones_row, W("bkv"), start=False, stop=True)
                    mm.then_inc(qkv_ready, 1)
                    pe.wait_ge(phi_ready, b + 1)
                    for t in range(2):
                        mm = nc.tensor.matmul(s_ps[:], kv[:, t, 0:D], kv[:, t, D:2 * D + 1], start=(t == 0), stop=(t == 1))
                    mm.then_inc(s_ready, 1)
                    pe.wait_ge(masked, b + 1)
                    nc.tensor.matmul(num_ps[:], sm[:], phiq[:], start=True, stop=True)
                    nc.tensor.matmul(den_ps[:], zm[:], phiq[:], start=True, stop=True).then_inc(numden_ready, 1)
                    pe.wait_ge(ctx_ready, b + 1)
                    nc.tensor.matmul(o_ps[:], W("wo"), ctx[:], start=True, stop=True).then_inc(o_ready, 1)

            @blk.scalar
            def _(act):
                with act.Fori(0, B) as b:
                    act.wait_ge(added, b + 1)
                    nc.scalar.activation(xb[:], g.xn[:, bass.ds(b * T, T)], ACT.Copy).then_inc(xb_ready, 1)
                    act.wait_ge(min_ready, b + 1)
                    nc.scalar.activation(qpos[:], q_ps[:], ACT.Relu, bias=W("bq"))
                    nc.scalar.activation(pos[:], kv_ps[:, :, 0:D], ACT.Relu)
                    nc.scalar.activation(kv[:, :, D:2 * D], kv_ps[:, :, D:2 * D], ACT.Copy)
                    nc.scalar.activation(qneg[:], qneg[:], ACT.Exp)
                    nc.scalar.activation(neg[:], neg[:], ACT.Exp).then_inc(exp_ready, 1)

            @blk.vector
            def _(dve):
                nc.vector.memset(kv[:, :, 2 * D:2 * D + 1], 1.0).then_inc(ones_set, 1)
                nc.vector.sem_inc(added, 1)
                dve.wait_ge(ones_set, 1)
                with dve.Fori(0, B) as b:
                    c = Chain(dve, dve_step, 3, b)
                    dve.wait_ge(qkv_ready, b + 1)
                    nc.vector.tensor_scalar(qneg[:], q_ps[:], W("bq"), 0.0, ALU.add, ALU.min)
                    nc.vector.tensor_scalar(neg[:], kv_ps[:, :, 0:D], 0.0, None, ALU.min).then_inc(min_ready, 1)
                    dve.wait_ge(exp_ready, b + 1)
                    nc.vector.tensor_tensor(phiq[:], qneg[:], qpos[:], ALU.add)
                    nc.vector.tensor_tensor(kv[:, :, 0:D], neg[:], pos[:], ALU.add).then_inc(phi_ready, 1)
                    dve.wait_ge(s_ready, b + 1)
                    nc.vector.tensor_tensor(sm[:], s_ps[:, 0:D], g.c("mask8"), ALU.mult)
                    nc.vector.tensor_scalar(zm[:], g.c("mask8"), s_ps[:, D:D + 1], None, ALU.mult).then_inc(masked, 1)
                    dve.wait_ge(numden_ready, b + 1)
                    c.link(nc.vector.tensor_scalar(rden[:], den_ps[:], 1e-6, None, ALU.add))
                    c.link(nc.vector.reciprocal(rden[:], rden[:]))
                    nc.vector.tensor_tensor(ctx[:], rden[:], num_ps[:], ALU.mult).then_inc(ctx_ready, 1)
                    dve.wait_ge(o_ready, b + 1)
                    xs = g.x[:, bass.ds(b * T, T)]
                    c.link(nc.vector.scalar_tensor_tensor(out=xs, in0=o_ps[:], scalar=W("bo"), in1=xs,
                                                          op0=ALU.add, op1=ALU.add))
                    nc.vector.sem_inc(added, 1)
                    c.close()


def top2(nc, g, c, s, mask, E, tmp_gt, tmp_eq, rank):
    sh = [P, TILES, E, E]
    sj, se = s.unsqueeze(2).to_broadcast(sh), s.unsqueeze(3).to_broadcast(sh)
    before = g.c("before%d" % E).rearrange("p (a e) -> p a e", a=1).to_broadcast([P, TILES, E * E])
    flat = "p t e j -> p t (e j)"
    c.link(nc.vector.tensor_tensor(tmp_gt[:], sj, se, ALU.is_gt))
    c.link(nc.vector.tensor_tensor(tmp_eq[:], sj, se, ALU.is_equal))
    c.link(nc.vector.tensor_tensor(tmp_eq[:].rearrange(flat), tmp_eq[:].rearrange(flat), before, ALU.mult))
    c.link(nc.vector.tensor_tensor(tmp_gt[:], tmp_gt[:], tmp_eq[:], ALU.add))
    c.link(nc.vector.tensor_reduce(rank[:], tmp_gt[:], AX, ALU.add))
    c.link(nc.vector.tensor_scalar(mask[:], rank[:], 1.5, None, ALU.is_lt))


TOP2_LINKS = 6


def gate(nc, g, name, act_t, wgate, bias_row, E, weigh, prob_t):
    with Stage(nc, name) as st:
        s_ps = st.ps("s_ps", [P, TILES, E])
        s, mask = st.sb("s", [P, TILES, E]), st.sb("mask", [P, TILES, E])
        prob = st.sb("prob", [P, TILES, E])
        t_gt, t_eq = st.sb("t_gt", [P, TILES, E, E]), st.sb("t_eq", [P, TILES, E, E])
        rank, one = st.sb("rank", [P, TILES, E]), st.sb("one", [P, TILES, 1])
        p_ps = st.ps("p_ps", [E, 4, BLK])
        scores_ready, exp_in, exp_out = st.sem("scores_ready"), st.sem("exp_in"), st.sem("exp_out")
        prob_ready, turned, moved, dve_step = st.sem("prob_ready"), st.sem("turned"), st.sem("moved"), st.sem("dve_step")
        with nc.Block() as blk:
            @blk.tensor
            def _(pe):
                for t in range(TILES):
                    mm = nc.tensor.matmul(s_ps[:, t, :], act_t[:, t * P:(t + 1) * P], wgate, start=True,
                                          stop=bias_row is None)
                    if bias_row is not None:
                        mm = nc.tensor.matmul(s_ps[:, t, :], g.ones_row, bias_row, start=False, stop=True)
                mm.then_inc(scores_ready, 1)
                pe.wait_ge(prob_ready, 1)
                for t in range(TILES):
                    if t == 16:
                        pe.wait_ge(moved, 1)
                    mm = nc.tensor.transpose(p_ps[:, t // 4 % 4, (t % 4) * P:(t % 4 + 1) * P], prob[:, t, :], g.c("ident"))
                    if t % 16 == 15:
                        mm.then_inc(turned, 1)

            @blk.scalar
            def _(act):
                act.wait_ge(exp_in, 1)
                nc.scalar.activation(s[:], s[:], ACT.Exp).then_inc(exp_out, 1)

            @blk.vector
            def _(dve):
                c = Chain(dve, dve_step)
                c.link(nc.vector.memset(prob_t[:], 0.0))
                dve.wait_ge(scores_ready, 1)
                weigh(dve, c, s_ps, s, mask, prob, t_gt, t_eq, rank, one, exp_in, exp_out)
                nc.vector.sem_inc(prob_ready, 1)
                for half in range(2):
                    dve.wait_ge(turned, half + 1)
                    nc.vector.tensor_copy(prob_t[0:E, half * 2048:(half + 1) * 2048].rearrange("p (a n) -> p a n", a=4),
                                          p_ps[:]).then_inc(moved, 1)


def l0_weigh(nc, g):
    def weigh(dve, c, s_ps, s, mask, prob, t_gt, t_eq, rank, one, exp_in, exp_out):
        sh = [P, TILES, 8]
        c.link(nc.vector.tensor_copy(s[:], s_ps[:]))
        top2(nc, g, c, s[:], mask, 8, t_gt, t_eq, rank)
        c.link(nc.vector.tensor_reduce(one[:], s[:].unsqueeze(2), AX, ALU.max))
        c.link(nc.vector.tensor_tensor(s[:], s[:], one[:].to_broadcast(sh), ALU.subtract))
        nc.vector.sem_inc(exp_in, 1)
        dve.wait_ge(exp_out, 1)
        c.link(nc.vector.tensor_tensor(prob[:], s[:], mask[:], ALU.mult))
        c.link(nc.vector.tensor_reduce(one[:], prob[:].unsqueeze(2), AX, ALU.add))
        c.link(nc.vector.reciprocal(one[:], one[:]))
        c.link(nc.vector.tensor_tensor(prob[:], prob[:], one[:].to_broadcast(sh), ALU.mult))
    return weigh


def swiglu_experts(nc, g, w, prob_t):
    W12 = L0.of(w, "w12").rearrange("p (e h c n) -> p e h c n", e=8, h=2, c=2)
    W3 = L0.of(w, "w3").rearrange("p (e c n) -> p e c n", e=8, c=2)
    UNITS = 16
    with Stage(nc, "l0f") as st:
        h_ps = st.ps("h_ps", [P, 2, 2, BLK])
        pr_ps = st.ps("pr_ps", [P, 2, BLK])
        o_ps = st.ps("o_ps", [P, BLK])
        sil, hid = st.sb("sil", [P, 2, BLK]), st.sb("hid", [P, 2, BLK])
        tmp = st.sb("tmp", [P, 2, BLK])
        up_ready, silu_ready, hid_ready = (st.sem(n) for n in ("up_ready", "silu_ready", "hid_ready"))
        out_used, hid_used, dve_step = st.sem("out_used"), st.sem("hid_used"), st.sem("dve_step")
        with nc.Block() as blk:
            @blk.tensor
            def _(pe):
                nc.tensor.sem_inc(hid_used, 2)
                with pe.Fori(0, NBLK) as i:
                    xs = g.xn[:, block(i)]

                    def up(u):
                        e, c = divmod(u, 2)
                        pe.wait_ge(hid_ready, i * UNITS + u + 1)
                        if c == 0:
                            nc.tensor.matmul(pr_ps[:, e % 2, :], g.c("pick8").rearrange("k (e m) -> k e m", e=8)[:, e, :],
                                             prob_t[:, block(i)], start=True, stop=True)
                        nc.tensor.matmul(h_ps[:, u % 2, 0, :], W12[:, e, 0, c, :], xs, start=True, stop=True)
                        nc.tensor.matmul(h_ps[:, u % 2, 1, :], W12[:, e, 1, c, :], xs, start=True, stop=True).then_inc(up_ready, 1)

                    up(0)
                    pe.wait_ge(out_used, i + 1)
                    for u in range(UNITS):
                        if u + 1 < UNITS:
                            up(u + 1)
                        pe.wait_ge(hid_ready, i * UNITS + u + 3)
                        mm = nc.tensor.matmul(o_ps[:], W3[:, u // 2, u % 2, :], hid[:, u % 2, :],
                                              start=(u == 0), stop=(u == UNITS - 1))
                        mm.then_inc(hid_used, 1)

            @blk.scalar
            def _(act):
                with act.Fori(0, NBLK) as i:
                    for u in range(UNITS):
                        act.wait_ge(up_ready, i * UNITS + u + 1)
                        act.wait_ge(hid_ready, i * UNITS + u + 1)
                        nc.scalar.activation(sil[:, u % 2, :], h_ps[:, u % 2, 0, :], ACT.Silu).then_inc(silu_ready, 1)

            @blk.vector
            def _(dve):
                nc.vector.sem_inc(hid_ready, 2)
                nc.vector.sem_inc(out_used, 1)
                with dve.Fori(0, NBLK) as i:
                    c = Chain(dve, dve_step, UNITS + 1, i)
                    for u in range(UNITS):
                        dve.wait_ge(silu_ready, i * UNITS + u + 1)
                        c.link(nc.vector.tensor_tensor(tmp[:, u % 2, :], sil[:, u % 2, :], h_ps[:, u % 2, 1, :], ALU.mult))
                        dve.wait_ge(hid_used, i * UNITS + u + 1)
                        nc.vector.tensor_tensor(hid[:, u % 2, :], tmp[:, u % 2, :], pr_ps[:, u // 2 % 2, :],
                                                ALU.mult).then_inc(hid_ready, 1)
                    dve.wait_ge(hid_used, i * UNITS + UNITS + 2)
                    c.link(nc.vector.tensor_tensor(g.x[:, block(i)], g.x[:, block(i)], o_ps[:], ALU.add))
                    nc.vector.sem_inc(out_used, 1)
                    c.close()


L1 = layout([("wk", P, D), ("wv", P, D), ("wr", P, D), ("wo", P, D), ("bo", P, 1), ("u", P, 1), ("w", P, 1),
             ("tmk", P, 1), ("tmv", P, 1), ("tmr", P, 1), ("gate", P, 8), ("gate_b", 1, 8),
             ("ew", P, 8 * D), ("eb", P, D)])


def wkv_attention(nc, g, w):
    W = lambda n: L1.of(w, n)
    with Stage(nc, "l1a") as st:
        xs, om = st.sb("xs", [P, T]), st.sb("om", [P, 3])
        mix = st.sb("mix", [P, 3, T])
        mixs = st.sb("mixs", [P, 3, T])
        kvr_ps, o_ps = st.ps("kvr_ps", [P, 3, BLK]), st.ps("o_ps", [P, T])
        kk, q, e1, e2 = (st.sb(n, [P, T]) for n in ("kk", "q", "e1", "e2"))
        e1x, e2x, ev = (st.sb(n, [P, T]) for n in ("e1x", "e2x", "ev"))
        a, b_, wr = (st.sb(n, [P, T]) for n in ("a", "b", "wr"))
        mixed, sig_done, kvr_ready, args_ready, exps_ready, wr_ready, o_ready, dve_step = (
            st.sem(n) for n in ("mixed", "sig_done", "kvr_ready", "args_ready", "exps_ready", "wr_ready", "o_ready", "dve_step"))
        with nc.Block() as blk:
            @blk.tensor
            def _(pe):
                with pe.Fori(0, B) as i:
                    pe.wait_ge(mixed, i + 1)
                    pe.wait_ge(sig_done, i + 1)
                    for n, wn in enumerate(("wk", "wv", "wr")):
                        mm = nc.tensor.matmul(kvr_ps[:, n, 0:T], W(wn), mixs[:, n, :] if n == 2 else mix[:, n, :],
                                              start=True, stop=True)
                    mm.then_inc(kvr_ready, 1)
                    pe.wait_ge(wr_ready, i + 1)
                    nc.tensor.matmul(o_ps[:], W("wo"), wr[:], start=True, stop=True).then_inc(o_ready, 1)

            @blk.scalar
            def _(act):
                with act.Fori(0, B) as i:
                    act.wait_ge(mixed, i + 1)
                    nc.scalar.activation(mixs[:, 2, :], mix[:, 2, :], ACT.Sigmoid).then_inc(sig_done, 1)
                    act.wait_ge(args_ready, i + 1)
                    nc.scalar.activation(e1[:], e1x[:], ACT.Exp)
                    nc.scalar.activation(e2[:], e2x[:], ACT.Exp).then_inc(exps_ready, 1)

            @blk.vector
            def _(dve):
                for n, t in enumerate(("tmk", "tmv", "tmr")):
                    nc.vector.tensor_scalar(om[:, n:n + 1], W(t), -1.0, 1.0, ALU.mult, ALU.add)
                nc.vector.memset(xs[:, 0:1], 0.0)
                nc.vector.drain()
                with dve.Fori(0, B) as i:
                    c = Chain(dve, dve_step, 13, i)
                    c.link(nc.vector.tensor_copy(xs[:, 1:T], g.xn[:, bass.ds(i * T, T - 1)]))
                    for n in range(3):
                        c.link(nc.vector.tensor_scalar(mix[:, n, :], xs[:], om[:, n:n + 1], None, ALU.mult))
                    for n, t in enumerate(("tmk", "tmv", "tmr")):
                        ins = nc.vector.scalar_tensor_tensor(out=mix[:, n, :], in0=g.xn[:, bass.ds(i * T, T)], scalar=W(t),
                                                             in1=mix[:, n, :], op0=ALU.mult, op1=ALU.add)
                    ins.then_inc(mixed, 1)
                    dve.wait_ge(kvr_ready, i + 1)
                    c.link(nc.vector.tensor_scalar(kk[:], kvr_ps[:, 0, 0:T], W("u"), None, ALU.add))
                    c.link(nc.vector.tensor_scalar(q[:], kk[:], W("w"), None, ALU.max))
                    nc.vector.tensor_scalar(e1x[:], q[:], -1.0, W("w"), ALU.mult, ALU.subtract)
                    nc.vector.tensor_tensor(e2x[:], kk[:], q[:], ALU.subtract).then_inc(args_ready, 1)
                    dve.wait_ge(exps_ready, i + 1)
                    c.link(nc.vector.tensor_tensor(ev[:], e2[:], kvr_ps[:, 1, 0:T], ALU.mult))
                    c.link(nc.vector.tensor_tensor_scan(a[:], e1[:], ev[:], 0.0, ALU.mult, ALU.add))
                    c.link(nc.vector.tensor_tensor_scan(b_[:], e1[:], e2[:], 0.0, ALU.mult, ALU.add))
                    c.link(nc.vector.reciprocal(b_[:], b_[:]))
                    c.link(nc.vector.tensor_tensor(a[:], a[:], b_[:], ALU.mult))
                    c.link(nc.vector.tensor_tensor(wr[:], a[:], kvr_ps[:, 2, 0:T], ALU.mult))
                    nc.vector.sem_inc(wr_ready, 1)
                    dve.wait_ge(o_ready, i + 1)
                    xc = g.x[:, bass.ds(i * T, T)]
                    c.link(nc.vector.scalar_tensor_tensor(out=xc, in0=o_ps[:], scalar=W("bo"), in1=xc,
                                                          op0=ALU.add, op1=ALU.add))
                    c.close()


def l1_weigh(nc, g):
    def weigh(dve, c, s_ps, s, mask, prob, t_gt, t_eq, rank, one, exp_in, exp_out):
        sh = [P, TILES, 8]
        c.link(nc.vector.tensor_scalar(s[:], s_ps[:], 1e-4, None, ALU.max))
        c.link(nc.vector.tensor_reduce(one[:], s[:].unsqueeze(2), AX, ALU.max))
        c.link(nc.vector.tensor_tensor(s[:], s[:], one[:].to_broadcast(sh), ALU.subtract))
        nc.vector.sem_inc(exp_in, 1)
        dve.wait_ge(exp_out, 1)
        c.link(nc.vector.tensor_reduce(one[:], s[:].unsqueeze(2), AX, ALU.add))
        c.link(nc.vector.reciprocal(one[:], one[:]))
        c.link(nc.vector.tensor_tensor(s[:], s[:], one[:].to_broadcast(sh), ALU.mult))
        top2(nc, g, c, s[:], mask, 8, t_gt, t_eq, rank)
        c.link(nc.vector.tensor_scalar(prob[:], s[:], 0.1, None, ALU.max))
        c.link(nc.vector.tensor_tensor(prob[:], prob[:], mask[:], ALU.mult))
        c.link(nc.vector.tensor_reduce(one[:], prob[:].unsqueeze(2), AX, ALU.add))
        c.link(nc.vector.reciprocal(one[:], one[:]))
        c.link(nc.vector.tensor_scalar(one[:], one[:], 0.5, None, ALU.mult))
        c.link(nc.vector.tensor_tensor(prob[:], prob[:], one[:].to_broadcast(sh), ALU.mult))
    return weigh


def linear_experts(nc, g, w, prob_t):
    EW = L1.of(w, "ew").rearrange("p (e n) -> p e n", e=8)
    with Stage(nc, "l1f") as st:
        pr_ps, o_ps = st.ps("pr_ps", [P, 2, BLK]), st.ps("o_ps", [P, BLK])
        xc = st.sb("xc", [P, 2, BLK])
        comb_ready, scaled, used, out_used, dve_step = (
            st.sem(n) for n in ("comb_ready", "scaled", "used", "out_used", "dve_step"))
        with nc.Block() as blk:
            @blk.tensor
            def _(pe):
                nc.tensor.sem_inc(used, 2)
                with pe.Fori(0, NBLK) as i:
                    pb = prob_t[:, block(i)]

                    def spread(e):
                        pe.wait_ge(scaled, i * 8 + e + 1)
                        nc.tensor.matmul(pr_ps[:, e % 2, :], g.c("pick8").rearrange("k (e m) -> k e m", e=8)[:, e, :], pb,
                                         start=True, stop=True).then_inc(comb_ready, 1)

                    spread(0)
                    pe.wait_ge(out_used, i + 1)
                    nc.tensor.matmul(o_ps[:], L1.of(w, "eb"), pb, start=True, stop=False)
                    for e in range(8):
                        if e < 7:
                            spread(e + 1)
                        pe.wait_ge(scaled, i * 8 + e + 3)
                        nc.tensor.matmul(o_ps[:], EW[:, e, :], xc[:, e % 2, :], start=False, stop=(e == 7)).then_inc(used, 1)

            @blk.vector
            def _(dve):
                nc.vector.sem_inc(scaled, 2)
                nc.vector.sem_inc(out_used, 1)
                with dve.Fori(0, NBLK) as i:
                    c = Chain(dve, dve_step, 1, i)
                    for e in range(8):
                        dve.wait_ge(comb_ready, i * 8 + e + 1)
                        dve.wait_ge(used, i * 8 + e + 1)
                        nc.vector.tensor_tensor(xc[:, e % 2, :], g.xn[:, block(i)], pr_ps[:, e % 2, :],
                                                ALU.mult).then_inc(scaled, 1)
                    dve.wait_ge(used, i * 8 + 8 + 2)
                    c.link(nc.vector.tensor_tensor(g.x[:, block(i)], g.x[:, block(i)], o_ps[:], ALU.add))
                    nc.vector.sem_inc(out_used, 1)
                    c.close()


L2A = layout([("wk", P, INNER), ("wq", P, INNER), ("wv", P, INNER), ("wa", P, INNER), ("war", P, INNER),
              ("wbg", P, 2 * HEADS), ("wo", P, PAIRS * D), ("lnw", P, 1), ("lnb", P, 1),
              ("ba", 1, INNER), ("bar", 1, INNER), ("bbg", 1, 2 * HEADS),
              ("cum", P, P), ("ends", P, 8), ("keep", P, 4 * P), ("keep_r", P, 3 * P)])
CH = 32
GB = P // CH
NG, NCH = B // GB, T // CH


def delta_attention(nc, g, dram):
    kept = nc.dram_tensor("xn_kept", (P, N), F32).ap()
    I32 = mybir.dt.int32
    with Stage(nc, "l2d") as st:
        w = st.sb("w", [P, L2A.n])
        W = lambda n: L2A.of(w, n)
        load_pack(nc, st, dram["l2a"], w, "l2a")
        saved = st.sem("saved")
        with nc.Block() as blk:
            @blk.sync
            def _(sp):
                sp.dma_start(kept, g.xn[:]).then_inc(saved, 16)
                sp.wait_ge(saved, 16)

            @blk.vector
            def _(dve):
                nc.vector.tensor_tensor(g.x[:], g.x[:], g.xn[:], ALU.add)
        layer_norm(nc, "l2dn", g.xn, g.xn, g.c("mean"), g.c("eps5"), W("lnw"), W("lnb"))

        xt = st.sb("xt", [P, P])
        arena = st.sb("arena", [P, 9 * INNER])
        at = lambda n: arena[:, n * INNER:(n + 1) * INNER]
        kp, k0, qp, ez, sp_, ep, em, kn, q = (at(n) for n in range(9))
        Y = arena[:, 0:4 * INNER].rearrange("p (f c n) -> p f c n", f=PAIRS, c=4)
        X, U, UR = at(4), at(5), at(6)
        OT = at(7).rearrange("p (f n) -> p f n", f=PAIRS)
        O = at(8)
        v = st.sb("v", [P, INNER])
        km, kmr = st.sb("km", [P, INNER]), st.sb("kmr", [P, INNER])
        TS = st.sb("TS", [P, PAIRS, 4, P])
        TR = st.sb("TR", [P, PAIRS, 3, P])
        A, AR = st.sb("A", [P, HEADS, 2, P]), st.sb("AR", [P, HEADS, P])
        NL = st.sb("NL", [P, 2, 2, 4, P])
        SS, RR = st.sb("SS", [P, GB, PAIRS, HD]), st.sb("RR", [P, GB, PAIRS, HD])
        bgm, neg = st.sb("bgm", [P, 2, HEADS]), st.sb("neg", [P, 2, HEADS])
        ss = st.sb("ss", [P, HEADS])
        er = st.sb("er", [P, 2, PAIRS, GB, 2])
        fac, last = st.sb("fac", [P, 2, GB, PAIRS]), st.sb("last", [P, 2, GB, PAIRS])
        big = st.ps("big", [P, 8, BLK])
        wide = lambda a: big[:, a:a + 2, :].rearrange("p c n -> p (c n)")
        heads = lambda ap: ap.rearrange("p (h d) -> p h d", h=HEADS)
        by_head = lambda ap: ap.unsqueeze(2).to_broadcast([P, HEADS, HD])
        keep = W("keep").bitcast(I32).rearrange("p (m n) -> p m n", m=4)
        keep_r = W("keep_r").bitcast(I32).rearrange("p (m n) -> p m n", m=3)
        names = ("xt_ready", "proj_ready", "act_used", "dve_used", "small_ready", "small_used", "squared", "summed", "root",
                 "kn_ready", "exp_done", "ln_ready", "e_ready", "ends_ready", "ends_used", "dve_made", "pool_made", "flipped", "flip_used",
                 "mats_ready", "masked", "y_start", "lev_ready", "nl_moved", "y_added", "scaled", "s1", "x_ready", "s2", "u_ready",
                 "s3", "r_ready", "s4", "xr_ready", "s5", "ur_ready", "s6", "o_ready", "s7", "s_added", "s8", "r_added",
                 "o_flipped", "ot_ready", "y_ready", "added", "dve_step", "zeroed", "pe_go", "dve_go")
        S = {n: st.sem(n) for n in names}
        split = lambda ap: ap.rearrange("p (f q d) -> p q f d", q=2, d=HD)
        even_odd = lambda a: big[:, a:a + 2, :].rearrange("p q (f d) -> p q f d", d=HD)
        time = lambda tile_, gi, ci: tile_.rearrange("p (b t) -> p b t", t=T)[:, bass.ds(gi * GB, GB), bass.ds(ci * CH, CH)]

        def tensor_tile(pe, t):
            pe.wait_ge(S["xt_ready"], t + 1)

            def wide_product(u, lhs, wn, bias=None):
                for c in range(2):
                    out, cols = big[:, 2 * (u % 2) + c, :], slice(c * BLK, (c + 1) * BLK)
                    mm = nc.tensor.matmul(out, lhs, wn[:, cols], start=True, stop=bias is None)
                    if bias is not None:
                        mm = nc.tensor.matmul(out, g.ones_row, bias[:, cols], start=False, stop=True)
                mm.then_inc(S["proj_ready"], 1)

            def ends(s):
                for f in range(PAIRS):
                    mm = nc.tensor.matmul(big[:, 7, 64 * s + 8 * f:64 * s + 8 * f + 8], sp_[:, f * P:(f + 1) * P], W("ends"), start=True, stop=True)
                mm.then_inc(S["ends_ready"], 1)

            def flip(n, made, count, src):
                pe.wait_ge(S[made], count)
                pe.wait_ge(S["flip_used"], 7 * t + n + 1)
                for f in range(PAIRS):
                    mm = nc.tensor.transpose(big[:, 4 + f // 4, (f % 4) * P:(f % 4 + 1) * P], src[:, f * P:(f + 1) * P], g.c("ident"))
                mm.then_inc(S["flipped"], 1)

            wide_product(0, xt[:], W("wk"))
            wide_product(1, xt[:], W("wq"))
            nc.tensor.matmul(big[:, 6, 0:2 * HEADS], xt[:], W("wbg"), start=True, stop=False)
            nc.tensor.matmul(big[:, 6, 0:2 * HEADS], g.ones_row, W("bbg"), start=False, stop=True).then_inc(S["small_ready"], 1)
            pe.wait_ge(S["act_used"], 3 * t + 1)
            wide_product(2, xt[:], W("wv"))
            pe.wait_ge(S["act_used"], 3 * t + 2)
            wide_product(3, xt[:], W("wa"), W("ba"))
            pe.wait_ge(S["act_used"], 3 * t + 3)
            pe.wait_ge(S["ln_ready"], 2 * t + 1)
            wide_product(4, W("cum"), sp_)
            ends(0)
            pe.wait_ge(S["dve_used"], 4 * t + 1)
            wide_product(5, xt[:], W("war"), W("bar"))
            flip(0, "dve_made", 3 * t + 1, k0)
            flip(1, "dve_made", 3 * t + 2, kp)
            flip(2, "pool_made", 4 * t + 1, km[:])
            flip(3, "pool_made", 4 * t + 2, qp)
            pe.wait_ge(S["dve_used"], 4 * t + 2)
            pe.wait_ge(S["ln_ready"], 2 * t + 2)
            wide_product(6, W("cum"), sp_)
            ends(1)
            flip(4, "dve_made", 3 * t + 3, kp)
            flip(5, "pool_made", 4 * t + 3, kmr[:])
            flip(6, "pool_made", 4 * t + 4, qp)

            pe.wait_ge(S["flip_used"], 7 * t + 8)
            pe.wait_ge(S["small_used"], t + 1)
            pe.wait_ge(S["ends_used"], 2 * t + 2)
            for p_ in range(PAIRS // 2):
                if p_:
                    pe.wait_ge(S["y_added"], 32 * t + 8 * p_)
                    pe.wait_ge(S["nl_moved"], 32 * t + 8 * p_)
                for wv in range(2):
                    f = 2 * p_ + wv
                    for par in range(2):
                        rows = slice(par * HD, (par + 1) * HD)
                        a, b = big[:, 4 * wv + par, :], big[:, 4 * wv + 2 + par, :]
                        nc.tensor.matmul(a[:, 0:3 * P], TS[rows, f, 3, :], TS[rows, f, 0:3, :], start=True, stop=True)
                        nc.tensor.matmul(a[:, 3 * P:4 * P], TS[rows, f, 0, :], TS[rows, f, 3, :], start=True, stop=True)
                        nc.tensor.matmul(b[:, 0:2 * P], TR[rows, f, 2, :], TR[rows, f, 0:2, :], start=True, stop=True)
                        mm = nc.tensor.matmul(b[:, 2 * P:3 * P], TR[rows, f, 0, :], TR[rows, f, 2, :], start=True, stop=True)
                    mm.then_inc(S["mats_ready"], 1)
                pe.wait_ge(S["masked"], 8 * t + 2 * p_ + 2)
                for l in range(5):
                    for wv in range(2):
                        f = 2 * p_ + wv
                        if l >= 1:
                            pe.wait_ge(S["nl_moved"], 32 * t + 8 * p_ + 2 * (l - 1) + wv + 1)
                            if l == 1:
                                pe.wait_ge(S["y_start"], 8 * t + 2 * p_ + wv + 1)
                            else:
                                pe.wait_ge(S["y_added"], 32 * t + 8 * p_ + 2 * (l - 2) + wv + 1)
                        for ch in range(4):
                            Nm, Lm = NL[:, wv, 0, ch, :], NL[:, wv, 1, ch, :]
                            cols = slice(ch * P, (ch + 1) * P)
                            if l <= 2:
                                mm = nc.tensor.matmul(big[:, 3 * wv, cols], Lm, Nm, start=True, stop=True)
                            if l >= 1:
                                mm = nc.tensor.matmul(big[:, 3 * wv + 2, cols], Lm, Y[:, f, ch, :], start=True, stop=True)
                            if l <= 3:
                                mm = nc.tensor.matmul(big[:, 3 * wv + 1, cols], Nm, Lm, start=True, stop=True)
                        mm.then_inc(S["lev_ready"], 1)

            def by_batch(bank0, h, src, m, state, stop):
                f, par = divmod(h, 2)
                rows = slice(par * HD, (par + 1) * HD)
                for b in range(GB):
                    mm = nc.tensor.matmul(big[32 * b:32 * b + 32, bank0 + par, f * HD:(f + 1) * HD], src[rows, f, m, 32 * b:32 * b + 32],
                                          state[rows, b, f, :], start=stop != "add", stop=stop == "alone")
                return mm

            def whole(bank0, h, lhs, rhs, stop):
                f, par = divmod(h, 2)
                return nc.tensor.matmul(big[:, bank0 + par, f * HD:(f + 1) * HD], lhs, rhs[:, h * HD:(h + 1) * HD], start=False, stop=stop)

            def solve(chain0, out):
                for h in range(HEADS):
                    f, par = divmod(h, 2)
                    mm = nc.tensor.matmul(big[:, 2 + h // 8, (h % 8) * HD:(h % 8 + 1) * HD], Y[:, f, chain0 + par, :], X[:, h * HD:(h + 1) * HD],
                                          start=True, stop=True)
                mm.then_inc(S[out], 1)

            pe.wait_ge(S["y_added"], 32 * t + 32)
            pe.wait_ge(S["scaled"], t + 1)
            nc.tensor.sem_inc(S["pe_go"], 1)
            for h in range(HEADS):
                mm = by_batch(0, h, TS, 0, SS, "alone")
            mm.then_inc(S["s1"], 1)
            pe.wait_ge(S["x_ready"], t + 1)
            solve(0, "s2")
            pe.wait_ge(S["u_ready"], t + 1)
            nc.tensor.sem_inc(S["pe_go"], 1)
            for h in range(HEADS):
                by_batch(4, h, TS, 2, SS, "open")
                mm = whole(4, h, A[:, h, 1, :], U, True)
            mm.then_inc(S["s3"], 1)
            for h in range(HEADS):
                mm = by_batch(0, h, TR, 0, RR, "alone")
            mm.then_inc(S["s4"], 1)
            pe.wait_ge(S["xr_ready"], t + 1)
            solve(2, "s5")
            pe.wait_ge(S["ur_ready"], t + 1)
            nc.tensor.sem_inc(S["pe_go"], 1)
            for h in range(HEADS):
                by_batch(4, h, TS, 1, SS, "open")
                whole(4, h, A[:, h, 0, :], U, False)
                by_batch(4, h, TR, 1, RR, "add")
                mm = whole(4, h, AR[:, h, :], UR, True)
            mm.then_inc(S["s6"], 1)

            def update(k_, u_, out):
                for h in range(HEADS):
                    f, par = divmod(h, 2)
                    for b in range(GB):
                        rows, cols = slice(32 * b, 32 * b + 32), slice(h * HD, (h + 1) * HD)
                        mm = nc.tensor.matmul(big[par * HD:(par + 1) * HD, b, f * HD:(f + 1) * HD], k_[rows, cols], u_[rows, cols],
                                              start=True, stop=True)
                mm.then_inc(S[out], 1)

            update(km, U, "s7")
            pe.wait_ge(S["s_added"], t + 1)
            nc.tensor.sem_inc(S["pe_go"], 1)
            update(kmr, UR, "s8")
            pe.wait_ge(S["o_ready"], t + 1)
            for f in range(PAIRS):
                mm = nc.tensor.transpose(big[:, 6 + f // 4, (f % 4) * P:(f % 4 + 1) * P], O[:, f * P:(f + 1) * P], g.c("ident"))
            mm.then_inc(S["o_flipped"], 1)
            pe.wait_ge(S["ot_ready"], t + 1)
            for f in range(PAIRS):
                mm = nc.tensor.matmul(big[:, 6, 0:P], W("wo")[:, f * D:(f + 1) * D], OT[:, f, :], start=(f == 0), stop=(f == PAIRS - 1))
            mm.then_inc(S["y_ready"], 1)

        def scalar_tile(act, t, gi, ci):
            act.wait_ge(S["added"], t + 1)
            nc.scalar.activation(xt[:].rearrange("p (b t) -> p b t", t=CH), time(g.xn[:], gi, ci), ACT.Copy).then_inc(S["xt_ready"], 1)
            for u, dst in enumerate((kn, q, v[:])):
                act.wait_ge(S["proj_ready"], 7 * t + u + 1)
                nc.scalar.activation(dst, wide(2 * (u % 2)), ACT.Copy).then_inc(S["act_used"], 1)
                if u == 0:
                    act.wait_ge(S["act_used"], 3 * t + 1)
                    nc.scalar.activation(ep, kn, ACT.Square).then_inc(S["squared"], 1)
                    act.wait_ge(S["summed"], t + 1)
                    nc.scalar.activation(ss[:], ss[:], ACT.Sqrt).then_inc(S["root"], 1)
                    act.wait_ge(S["small_ready"], t + 1)
                    nc.scalar.activation(bgm[:].rearrange("p a h -> p (a h)"), big[:, 6, 0:2 * HEADS], ACT.Sigmoid).then_inc(S["small_used"], 1)

            def decays(s):
                act.wait_ge(S["dve_used"], 4 * t + 2 * s + 1)
                nc.scalar.activation(ez, ez, ACT.Exp).then_inc(S["exp_done"], 1)
                act.wait_ge(S["exp_done"], 2 * t + s + 1)
                nc.scalar.activation(sp_, ez, ACT.Ln, bias=1.0).then_inc(S["ln_ready"], 1)
                act.wait_ge(S["dve_used"], 4 * t + 2 * s + 2)
                nc.scalar.activation(em, ep, ACT.Exp, scale=-1.0)
                nc.scalar.activation(ep, ep, ACT.Exp).then_inc(S["e_ready"], 1)
                act.wait_ge(S["ends_ready"], 2 * t + s + 1)
                nc.scalar.activation(er[:, s].rearrange("p f b k -> p (f b k)"), big[:, 7, 64 * s:64 * s + 64], ACT.Exp,
                                     scale=-1.0).then_inc(S["ends_used"], 1)

            def flips(n0, dsts):
                for n, dst in enumerate(dsts):
                    act.wait_ge(S["flipped"], 7 * t + n0 + n + 1)
                    nc.scalar.activation(dst, big[:, 4:6, :].rearrange("p c (f n) -> p (c f) n", n=P), ACT.Copy).then_inc(S["flip_used"], 1)

            decays(0)
            flips(0, (TS[:, :, 2, :], TS[:, :, 0, :], TS[:, :, 3, :], TS[:, :, 1, :]))
            decays(1)
            flips(4, (TR[:, :, 0, :], TR[:, :, 2, :], TR[:, :, 1, :]))
            for p_ in range(PAIRS // 2):
                for l in range(4):
                    for wv in range(2):
                        act.wait_ge(S["lev_ready"], 40 * t + 10 * p_ + 2 * l + wv + 1)
                        if l == 0:
                            act.wait_ge(S["y_start"], 8 * t + 2 * p_ + wv + 1)
                        if l < 3:
                            src, dst = big[:, 3 * wv:3 * wv + 2, :], NL[:, wv].rearrange("p m c n -> p m (c n)")
                        else:
                            src, dst = big[:, 3 * wv + 1, :], NL[:, wv, 1].rearrange("p c n -> p (c n)")
                        nc.scalar.activation(dst, src, ACT.Copy).then_inc(S["nl_moved"], 1)
            act.wait_ge(S["s2"], t + 1)
            nc.scalar.activation(U, wide(2), ACT.Copy).then_inc(S["u_ready"], 1)
            act.wait_ge(S["s5"], t + 1)
            nc.scalar.activation(UR, wide(2), ACT.Copy).then_inc(S["ur_ready"], 1)
            act.wait_ge(S["s6"], t + 1)
            for par in range(2):
                ins = nc.scalar.activation(split(O)[:, par], even_odd(4)[:, par], ACT.Copy)
            ins.then_inc(S["o_ready"], 1)
            act.wait_ge(S["o_flipped"], t + 1)
            nc.scalar.activation(OT, big[:, 6:8, :].rearrange("p c (f n) -> p (c f) n", n=P), ACT.Copy).then_inc(S["ot_ready"], 1)

        def pool_tile(pool, t):
            pool.wait_ge(S["kn_ready"], t + 1)
            for s, (k_, wait_flip) in enumerate(((km, None), (kmr, 7 * t + 4))):
                pool.wait_ge(S["e_ready"], 2 * t + s + 1)
                nc.gpsimd.tensor_tensor(k_[:], kn, em, ALU.mult).then_inc(S["pool_made"], 1)
                if s == 1:
                    pool.wait_ge(S["flipped"], wait_flip)
                nc.gpsimd.tensor_tensor(qp, q, ep, ALU.mult).then_inc(S["pool_made"], 1)

        def vector_tile(dve, t, gi, ci):
            c = Chain(dve, S["dve_step"], LINKS, t)
            dve.wait_ge(S["squared"], t + 1)
            nc.vector.tensor_reduce(ss[:], heads(ep), AX, ALU.add).then_inc(S["summed"], 1)
            dve.wait_ge(S["root"], t + 1)
            c.link(nc.vector.tensor_scalar(ss[:], ss[:], 1e-12, None, ALU.max))
            c.link(nc.vector.reciprocal(ss[:], ss[:]))
            c.link(nc.vector.tensor_tensor(heads(kn), heads(kn), by_head(ss[:]), ALU.mult))
            nc.vector.sem_inc(S["kn_ready"], 1)
            dve.wait_ge(S["small_used"], t + 1)
            c.link(nc.vector.tensor_scalar(neg[:], bgm[:], -1.0, None, ALU.mult))
            for s in range(2):
                dve.wait_ge(S["proj_ready"], 7 * t + 4 + 2 * s)
                nc.vector.tensor_scalar(ez, wide(2), -1.0, 40.0, ALU.mult, ALU.min).then_inc(S["dve_used"], 1)
                dve.wait_ge(S["proj_ready"], 7 * t + 5 + 2 * s)
                if s == 1:
                    dve.wait_ge(S["pool_made"], 4 * t + 2)
                nc.vector.tensor_scalar(ep, wide(0), 80.0, -80.0, ALU.min, ALU.max).then_inc(S["dve_used"], 1)
                dve.wait_ge(S["e_ready"], 2 * t + s + 1)
                if s == 1:
                    dve.wait_ge(S["flipped"], 7 * t + 2)
                c.link(nc.vector.tensor_tensor(kp, kn, ep, ALU.mult))
                if s == 0:
                    nc.vector.scalar_tensor_tensor(out=k0, in0=ez, scalar=1.0, in1=kp, op0=ALU.add, op1=ALU.mult).then_inc(S["dve_made"], 1)
                    dve.wait_ge(S["dve_made"], 3 * t + 1)
                nc.vector.tensor_tensor(heads(kp), heads(kp), by_head(neg[:, s, :]), ALU.mult).then_inc(S["dve_made"], 1)
            dve.wait_ge(S["ends_used"], 2 * t + 2)
            for s, state in enumerate((SS, RR)):
                er_b = er[:, s].rearrange("p f b k -> p b f k")
                c.link(nc.vector.tensor_tensor(fac[:, s], last[:, s], er_b[:, :, :, 0], ALU.mult))
                c.link(nc.vector.tensor_copy(last[:, s], er_b[:, :, :, 1]))
                flat = state[:].rearrange("p b f d -> p (b f) d")
                ins = nc.vector.tensor_tensor(flat, flat, fac[:, s].rearrange("p b f -> p (b f)").unsqueeze(2).to_broadcast([P, 32, HD]), ALU.mult)
            ins.then_inc(S["scaled"], 1)
            nc.vector.tensor_tensor(heads(X), heads(v[:]), by_head(bgm[:, 0, :]), ALU.mult)
            for p_ in range(PAIRS // 2):
                for wv in range(2):
                    f = 2 * p_ + wv
                    dve.wait_ge(S["mats_ready"], 8 * t + f + 1)
                    nc.vector.sem_inc(S["dve_go"], 1)
                    for par in range(2):
                        h = 2 * f + par
                        a = big[:, 4 * wv + par, :].rearrange("p (m n) -> p m n", n=P)
                        b = big[:, 4 * wv + 2 + par, 0:3 * P].rearrange("p (m n) -> p m n", n=P)
                        nc.vector.copy_predicated(NL[:, wv, :, par, :], keep[:, 0:4:3, :], a[:, 0:4:3, :])
                        nc.vector.copy_predicated(NL[:, wv, :, 2 + par, :], keep_r[:, 0:3:2, :], b[:, 0:3:2, :])
                        nc.vector.copy_predicated(A[:, h], keep[:, 1:3, :], a[:, 1:3, :])
                        ins = nc.vector.copy_predicated(AR[:, h, :], keep_r[:, 1, :], b[:, 1, :])
                    ins.then_inc(S["masked"], 1)
                    dve.wait_ge(S["masked"], 8 * t + f + 1)
                    nc.vector.tensor_tensor(Y[:, f], NL[:, wv, 0], g.c("ident").unsqueeze(1).to_broadcast([P, 4, P]), ALU.add).then_inc(S["y_start"], 1)
                for l in range(1, 5):
                    for wv in range(2):
                        f = 2 * p_ + wv
                        dve.wait_ge(S["lev_ready"], 40 * t + 10 * p_ + 2 * l + wv + 1)
                        yf = Y[:, f].rearrange("p c n -> p (c n)")
                        nc.vector.tensor_tensor(yf, yf, big[:, 3 * wv + 2, :], ALU.add).then_inc(S["y_added"], 1)
            dve.wait_ge(S["s1"], t + 1)
            nc.vector.tensor_tensor(split(X), split(X), even_odd(0), ALU.add).then_inc(S["x_ready"], 1)
            dve.wait_ge(S["s3"], t + 1)
            c.link(nc.vector.tensor_tensor(split(X), split(v[:]), even_odd(4), ALU.subtract))
            c.link(nc.vector.tensor_scalar(X, X, 1.0, -1.0, ALU.min, ALU.max))
            c.link(nc.vector.tensor_tensor(heads(X), heads(X), by_head(bgm[:, 1, :]), ALU.mult))
            dve.wait_ge(S["s4"], t + 1)
            nc.vector.tensor_tensor(split(X), split(X), even_odd(0), ALU.add).then_inc(S["xr_ready"], 1)
            for state, ready, done in ((SS, "s7", "s_added"), (RR, "s8", "r_added")):
                dve.wait_ge(S[ready], t + 1)
                flat = state[:].rearrange("p b f d -> p (b f d)")
                nc.vector.tensor_tensor(flat, flat, big[:, 0:4, :].rearrange("p c n -> p (c n)"), ALU.add).then_inc(S[done], 1)
            dve.wait_ge(S["y_ready"], t + 1)
            xs = time(g.x[:], gi, ci)
            c.link(nc.vector.tensor_tensor(xs, xs, big[:, 6, 0:P].rearrange("p (b t) -> p b t", t=CH), ALU.add))
            nc.vector.sem_inc(S["added"], 1)
            c.close()

        LINKS = 4 + 2 + 4 + 3 + 1
        with nc.Block() as blk:
            @blk.tensor
            def _(pe):
                pe.wait_ge(S["zeroed"], 1)
                with pe.Fori(0, NG) as gi:
                    with pe.Fori(0, NCH) as ci:
                        tensor_tile(pe, gi * NCH + ci)

            @blk.scalar
            def _(act):
                nc.scalar.sem_inc(S["flip_used"], 1)
                with act.Fori(0, NG) as gi:
                    with act.Fori(0, NCH) as ci:
                        scalar_tile(act, gi * NCH + ci, gi, ci)

            @blk.gpsimd
            def _(pool):
                with pool.Fori(0, NG) as gi:
                    with pool.Fori(0, NCH) as ci:
                        pool_tile(pool, gi * NCH + ci)

            @blk.vector
            def _(dve):
                for buf in (A, AR, NL):
                    ins = nc.vector.memset(buf[:], 0.0)
                nc.vector.sem_inc(S["added"], 1)
                ins.then_inc(S["zeroed"], 1)
                with dve.Fori(0, NG) as gi:
                    nc.vector.memset(SS[:], 0.0)
                    nc.vector.memset(RR[:], 0.0)
                    nc.vector.memset(last[:], 1.0)
                    with dve.Fori(0, NCH) as ci:
                        vector_tile(dve, gi * NCH + ci, gi, ci)
        back = st.sem("back")
        with nc.Block() as blk:
            @blk.sync
            def _(sp):
                sp.dma_start(g.xn[:], kept).then_inc(back, 16)
                sp.wait_ge(back, 16)


L2F = layout([("n1", P, 1), ("n2", P, 1), ("wq", P, 4 * P), ("wk", P, 4 * P), ("wv", P, D), ("qn", P, 1), ("kn", P, 1),
              ("wo", P, 4 * D), ("gate", P, 4), ("e0u", P, 2 * P), ("e0d", P, 2 * D), ("e1a", P, 2 * P), ("e1b", P, 2 * P),
              ("e1d", P, 2 * D), ("e2a", P, 2 * P), ("e2b", P, 4 * P), ("e2c", P, 4 * P), ("e2d", P, 2 * D),
              ("e3a", P, P), ("e3b", P, 2 * P), ("e3d", P, 2 * D)])
QUADS = HEADS // 4


def rms_norm(nc, name, src, dst, mean_w, eps_col, weight):
    with Stage(nc, name) as st:
        sq, root = st.sb("sq", [P, 2, BLK]), st.sb("root", [P, 2, BLK])
        ms_ps = st.ps("ms", [P, 2, BLK])
        squared, ms_ready, root_ready, normed, step = (st.sem(n) for n in ("squared", "ms_ready", "root_ready", "normed", "step"))
        with nc.Block() as blk:
            @blk.tensor
            def _(pe):
                with pe.Fori(0, NBLK // 2) as i:
                    for k in range(2):
                        pe.wait_ge(squared, 2 * i + k + 1)
                        pe.wait_ge(root_ready, 2 * i + k + 1)
                        nc.tensor.matmul(ms_ps[:, k, :], mean_w, sq[:, k, :], start=True, stop=True).then_inc(ms_ready, 1)

            @blk.scalar
            def _(act):
                nc.scalar.sem_inc(root_ready, 2)
                with act.Fori(0, NBLK // 2) as i:
                    for k in range(2):
                        nc.scalar.activation(sq[:, k, :], src[:, block(2 * i + k)], ACT.Square).then_inc(squared, 1)
                    for k in range(2):
                        act.wait_ge(ms_ready, 2 * i + k + 1)
                        act.wait_ge(normed, 2 * i + k + 1)
                        nc.scalar.activation(root[:, k, :], ms_ps[:, k, :], ACT.Sqrt, bias=eps_col).then_inc(root_ready, 1)

            @blk.vector
            def _(dve):
                nc.vector.sem_inc(normed, 2)
                with dve.Fori(0, NBLK // 2) as i:
                    c = Chain(dve, step, 2, i)
                    for k in range(2):
                        dve.wait_ge(root_ready, 2 * i + k + 3)
                        c.link(nc.vector.reciprocal(root[:, k, :], root[:, k, :]))
                        nc.vector.scalar_tensor_tensor(out=dst[:, block(2 * i + k)], in0=src[:, block(2 * i + k)], scalar=weight,
                                                       in1=root[:, k, :], op0=ALU.mult, op1=ALU.mult).then_inc(normed, 1)
                    c.close()


def causal_attention(nc, g, w, h):
    W = lambda n: L2F.of(w, n)
    with Stage(nc, "l2h") as st:
        hb = st.sb("hb", [P, T])
        raw = st.sb("raw", [P, 2, 2 * T])
        sq, root = st.sb("sq", [P, 2, 2 * T]), st.sb("root", [P, 2, 2 * T])
        qk = st.sb("qk", [P, QUADS, 2, T])
        v = st.sb("v", [P, 2, HEADS, 32])
        mx = st.sb("mx", [P, 4, 2])
        e = st.sb("e", [P, 4, 3 * P])
        et = st.sb("et", [P, 2, 3 * P])
        raw_o, rden = st.sb("raw_o", [P, T]), st.sb("rden", [P, T])
        ctxt = st.sb("ctxt", [P, QUADS, T])
        identb, maskb = st.sb("identb", [P, P], mybir.dt.bfloat16), st.sb("maskb", [P, P], mybir.dt.bfloat16)
        big = st.ps("big", [P, 8, BLK])
        names = ("setup", "hb_ready", "v_ready", "v_moved", "raw_ready", "squared", "ms_ready", "root_ready", "normed", "moved",
                 "s_ready", "max_ready", "exp_ready", "e_turned", "et_ready", "mixed", "o_moved", "den_ready", "ctx_ready",
                 "y_ready", "added", "dve_step")
        S = {n: st.sem(n) for n in names}
        with nc.Block() as blk:
            @blk.tensor
            def _(pe):
                pe.wait_ge(S["setup"], 1)
                with pe.Fori(0, B) as b:
                    pe.wait_ge(S["hb_ready"], b + 1)
                    for t in range(2):
                        mm = nc.tensor.matmul(big[:, 7, t * P:(t + 1) * P], hb[:, t * P:(t + 1) * P], W("wv"), start=True, stop=True)
                    mm.then_inc(S["v_ready"], 1)
                    for j in range(QUADS):
                        if j >= 2:
                            pe.wait_ge(S["moved"], QUADS * b + j - 1)
                        for n, wn in enumerate(("wq", "wk")):
                            mm = nc.tensor.matmul(big[:, j % 2, n * T:(n + 1) * T], W(wn)[:, j * P:(j + 1) * P], hb[:], start=True, stop=True)
                        mm.then_inc(S["raw_ready"], 1)
                        pe.wait_ge(S["squared"], QUADS * b + j + 1)
                        if j >= 2:
                            pe.wait_ge(S["root_ready"], QUADS * b + j - 1)
                        nc.tensor.matmul(big[:, 2 + j % 2, :], g.c("mean32"), sq[:, j % 2, :], start=True, stop=True).then_inc(S["ms_ready"], 1)
                    pe.wait_ge(S["normed"], QUADS * b + QUADS)
                    pe.wait_ge(S["v_moved"], b + 1)

                    def scores(n):
                        j, r = divmod(n, 4)
                        rows = slice(32 * r, 32 * r + 32)
                        if n >= 4:
                            pe.wait_ge(S["exp_ready"], HEADS * b + n - 3)
                        nc.tensor.matmul(big[:, r, 0:P], qk[rows, j, 0, 0:P], qk[rows, j, 1, 0:P], start=True, stop=False, tile_position=(32 * r, 0))
                        nc.tensor.matmul(big[:, r, 0:P], identb[:], maskb[:], start=False, stop=True)
                        nc.tensor.matmul(big[:, r, P:2 * P], qk[rows, j, 0, P:T], qk[rows, j, 1, 0:P], start=True, stop=True, tile_position=(32 * r, 0))
                        nc.tensor.matmul(big[:, r, 2 * P:3 * P], qk[rows, j, 0, P:T], qk[rows, j, 1, P:T], start=True, stop=False, tile_position=(32 * r, 0))
                        nc.tensor.matmul(big[:, r, 2 * P:3 * P], identb[:], maskb[:], start=False, stop=True).then_inc(S["s_ready"], 1)

                    def turn(n):
                        pe.wait_ge(S["exp_ready"], HEADS * b + n + 1)
                        if n >= 2:
                            pe.wait_ge(S["et_ready"], HEADS * b + n - 1)
                        for k in range(3):
                            mm = nc.tensor.transpose(big[:, 4 + n % 2, k * P:(k + 1) * P], e[:, n % 4, k * P:(k + 1) * P], g.c("ident"))
                        mm.then_inc(S["e_turned"], 1)

                    def mix(n):
                        j, r = divmod(n, 4)
                        out = big[32 * r:32 * r + 32, 6, :]
                        if n >= 4 and r == 0:
                            pe.wait_ge(S["ctx_ready"], QUADS * b + j)
                        pe.wait_ge(S["et_ready"], HEADS * b + n + 1)
                        nc.tensor.matmul(out[:, 0:T], v[:, 0, n, :], et[:, n % 2, 0:T], start=True, stop=False)
                        mm = nc.tensor.matmul(out[:, P:T], v[:, 1, n, :], et[:, n % 2, T:3 * P], start=False, stop=True)
                        mm.then_inc(S["mixed"], 1)
                        if r == 3:
                            pe.wait_ge(S["o_moved"], QUADS * b + j + 1)
                            nc.tensor.matmul(big[:, 6, T:2 * T], g.c("sum32"), raw_o[:], start=True, stop=True).then_inc(S["den_ready"], 1)

                    scores(0)
                    for n in range(HEADS):
                        if n + 1 < HEADS:
                            scores(n + 1)
                        turn(n)
                        if n >= 1:
                            mix(n - 1)
                    mix(HEADS - 1)
                    pe.wait_ge(S["ctx_ready"], QUADS * b + QUADS)
                    for j in range(QUADS):
                        mm = nc.tensor.matmul(big[:, 7, 0:T], W("wo")[:, j * D:(j + 1) * D], ctxt[:, j, :], start=(j == 0), stop=(j == QUADS - 1))
                    mm.then_inc(S["y_ready"], 1)

            @blk.scalar
            def _(act):
                with act.Fori(0, B) as b:
                    act.wait_ge(S["added"], b + 1)
                    nc.scalar.activation(hb[:], h[:, bass.ds(b * T, T)], ACT.Copy).then_inc(S["hb_ready"], 1)
                    act.wait_ge(S["v_ready"], b + 1)
                    nc.scalar.activation(v[:, :, :, 0:8], big[:, 7, 0:2 * P].rearrange("p (t h d) -> p t h d", t=2, d=8),
                                         ACT.Copy).then_inc(S["v_moved"], 1)
                    for j in range(QUADS):
                        act.wait_ge(S["raw_ready"], QUADS * b + j + 1)
                        if j >= 2:
                            act.wait_ge(S["normed"], QUADS * b + j - 1)
                        nc.scalar.activation(raw[:, j % 2, :], big[:, j % 2, :], ACT.Copy).then_inc(S["moved"], 1)
                        act.wait_ge(S["moved"], QUADS * b + j + 1)
                        nc.scalar.activation(sq[:, j % 2, :], raw[:, j % 2, :], ACT.Square).then_inc(S["squared"], 1)
                        act.wait_ge(S["ms_ready"], QUADS * b + j + 1)
                        nc.scalar.activation(root[:, j % 2, :], big[:, 2 + j % 2, :], ACT.Sqrt, bias=g.c("eps_rms")).then_inc(S["root_ready"], 1)
                    for n in range(HEADS):
                        act.wait_ge(S["max_ready"], HEADS * b + n + 1)
                        if n >= 4:
                            act.wait_ge(S["e_turned"], HEADS * b + n - 3)
                        nc.scalar.activation(e[:, n % 4, 0:P], big[:, n % 4, 0:P], ACT.Exp, bias=mx[:, n % 4, 0:1], scale=8 ** -0.5)
                        nc.scalar.activation(e[:, n % 4, P:3 * P], big[:, n % 4, P:3 * P], ACT.Exp, bias=mx[:, n % 4, 1:2],
                                             scale=8 ** -0.5).then_inc(S["exp_ready"], 1)
                        act.wait_ge(S["e_turned"], HEADS * b + n + 1)
                        if n >= 2:
                            act.wait_ge(S["mixed"], HEADS * b + n - 1)
                        nc.scalar.activation(et[:, n % 2, :], big[:, 4 + n % 2, 0:3 * P], ACT.Copy).then_inc(S["et_ready"], 1)

            @blk.vector
            def _(dve):
                nc.vector.sem_inc(S["added"], 1)
                nc.vector.memset(v[:, :, :, 9:32], 0.0)
                nc.vector.memset(v[:, :, :, 8:9], 1.0)
                nc.vector.tensor_copy(identb[:], g.c("ident"))
                nc.vector.tensor_copy(maskb[:], g.c("causal")).then_inc(S["setup"], 1)
                with dve.Fori(0, B) as b:
                    c = Chain(dve, S["dve_step"], QUADS + 2 * HEADS + QUADS + 1, b)
                    for j in range(QUADS):
                        dve.wait_ge(S["root_ready"], QUADS * b + j + 1)
                        c.link(nc.vector.reciprocal(root[:, j % 2, :], root[:, j % 2, :]))
                        for n, wn in enumerate(("qn", "kn")):
                            cols = slice(n * T, (n + 1) * T)
                            ins = nc.vector.scalar_tensor_tensor(out=qk[:, j, n, :], in0=raw[:, j % 2, cols], scalar=W(wn),
                                                                 in1=root[:, j % 2, cols], op0=ALU.mult, op1=ALU.mult)
                        ins.then_inc(S["normed"], 1)

                    def finish(j):
                        dve.wait_ge(S["mixed"], HEADS * b + 4 * j + 4)
                        nc.vector.tensor_copy(raw_o[:], big[:, 6, 0:T]).then_inc(S["o_moved"], 1)
                        dve.wait_ge(S["den_ready"], QUADS * b + j + 1)
                        c.link(nc.vector.reciprocal(rden[:], big[:, 6, T:2 * T]))
                        nc.vector.tensor_tensor(ctxt[:, j, :], raw_o[:], rden[:], ALU.mult).then_inc(S["ctx_ready"], 1)

                    for n in range(HEADS):
                        r = n % 4
                        dve.wait_ge(S["s_ready"], HEADS * b + n + 1)
                        if n >= 4:
                            dve.wait_ge(S["exp_ready"], HEADS * b + n - 3)
                        nc.vector.tensor_reduce(mx[:, r, 0:1], big[:, r, 0:P], AX, ALU.max)
                        c.link(nc.vector.tensor_reduce(mx[:, r, 1:2], big[:, r, P:3 * P], AX, ALU.max))
                        c.link(nc.vector.tensor_scalar(mx[:, r, :], mx[:, r, :], -(8 ** -0.5), None, ALU.mult))
                        nc.vector.sem_inc(S["max_ready"], 1)
                        if n % 4 == 1 and n > 4:
                            finish(n // 4 - 1)
                    finish(QUADS - 1)
                    dve.wait_ge(S["y_ready"], b + 1)
                    for r in range(32, P, 32):
                        xs = g.xn[r:r + 32, bass.ds(b * T, T)]
                        ins = nc.vector.tensor_tensor(xs, xs, big[r:r + 32, 7, 0:T], ALU.add)
                    c.link(ins)
                    nc.vector.sem_inc(S["added"], 1)
                    c.close()


def l2_weigh(nc, g):
    def weigh(dve, c, s_ps, s, mask, prob, t_gt, t_eq, rank, one, exp_in, exp_out):
        sh = [P, TILES, 4]
        c.link(nc.vector.tensor_scalar(s[:], s_ps[:], 3.4028235e38, -3.4028235e38, ALU.min, ALU.max))
        c.link(nc.vector.tensor_reduce(one[:], s[:].unsqueeze(2), AX, ALU.max))
        c.link(nc.vector.tensor_tensor(s[:], s[:], one[:].to_broadcast(sh), ALU.subtract))
        nc.vector.sem_inc(exp_in, 1)
        dve.wait_ge(exp_out, 1)
        c.link(nc.vector.tensor_reduce(one[:], s[:].unsqueeze(2), AX, ALU.add))
        c.link(nc.vector.reciprocal(one[:], one[:]))
        c.link(nc.vector.tensor_tensor(s[:], s[:], one[:].to_broadcast(sh), ALU.mult))
        top2(nc, g, c, s[:], mask, 4, t_gt, t_eq, rank)
        c.link(nc.vector.tensor_tensor(prob[:], s[:], mask[:], ALU.mult))
        c.link(nc.vector.tensor_reduce(one[:], prob[:].unsqueeze(2), AX, ALU.add))
        c.link(nc.vector.tensor_scalar(one[:], one[:], 1e-8, None, ALU.add))
        c.link(nc.vector.reciprocal(one[:], one[:]))
        c.link(nc.vector.tensor_tensor(prob[:], prob[:], one[:].to_broadcast(sh), ALU.mult))
    return weigh


def mixed_experts(nc, g, w, xf, prob_t):
    W = lambda n: L2F.of(w, n)
    part = lambda n, k: W(n)[:, k * P:(k + 1) * P]
    CHUNKS = [
        ("a0", [("e0u", 0, None)], 0, ("e0d", 0)), ("a1", [("e0u", 1, None)], 0, ("e0d", 1)),
        ("b0", [("e1a", 0, None)], 1, ("e1d", 0)), ("b1", [("e1a", 1, None)], 1, ("e1d", 1)),
        ("c0", [("e2a", 0, None)], None, None), ("c1", [("e2a", 1, None)], None, None),
        ("d0", [("e3a", 0, None)], None, None),
        ("f0", [("e2b", 0, "c0"), ("e2b", 2, "c1")], None, None), ("f1", [("e2b", 1, "c0"), ("e2b", 3, "c1")], None, None),
        ("h0", [("e3b", 0, "d0")], 3, ("e3d", 0)), ("h1", [("e3b", 1, "d0")], 3, ("e3d", 1)),
        ("i0", [("e2c", 0, "f0"), ("e2c", 2, "f1")], 2, ("e2d", 0)), ("i1", [("e2c", 1, "f0"), ("e2c", 3, "f1")], 2, ("e2d", 1)),
    ]
    at = {c[0]: n for n, c in enumerate(CHUNKS)}
    OUTS = [n for n, c in enumerate(CHUNKS) if c[3]]
    NC, NO = len(CHUNKS), len(OUTS)
    RING = 4
    with Stage(nc, "l2m") as st:
        hid = st.sb("hid", [P, NC, BLK])
        big = st.ps("big", [P, 8, BLK])
        up_ready, hid_ready, scaled, used, spread, out_used, step = (
            st.sem(n) for n in ("up_ready", "hid_ready", "scaled", "used", "spread", "out_used", "step"))
        with nc.Block() as blk:
            @blk.tensor
            def _(pe):
                with pe.Fori(0, NBLK) as i:
                    def up(n):
                        name, products, expert, out = CHUNKS[n]
                        pe.wait_ge(hid_ready, NC * i + n + 1)
                        if name == "b0":
                            nc.tensor.matmul(big[:, 4, :], part("e1b", 0), xf[:, block(i)], start=True, stop=True)
                        if name == "b1":
                            pe.wait_ge(scaled, NO * i + 3)
                            nc.tensor.matmul(big[:, 4, :], part("e1b", 1), xf[:, block(i)], start=True, stop=True)
                        for m, (wn, k, source) in enumerate(products):
                            if source:
                                pe.wait_ge(hid_ready, NC * i + at[source] + 5)
                            rhs = hid[:, at[source], :] if source else xf[:, block(i)]
                            mm = nc.tensor.matmul(big[:, n % RING, :], part(wn, k), rhs, start=(m == 0), stop=(m == len(products) - 1))
                        mm.then_inc(up_ready, 1)
                        if n in OUTS and OUTS.index(n) % 2 == 0:
                            e = OUTS.index(n) // 2
                            if e >= 2:
                                pe.wait_ge(scaled, NO * i + 2 * (e - 1))
                            nc.tensor.matmul(big[:, 6 + e % 2, :], g.c("pick8").rearrange("k (e m) -> k e m", e=8)[:, expert, :],
                                             prob_t[:, block(i)], start=True, stop=True).then_inc(spread, 1)

                    def down(m):
                        wn, k = CHUNKS[OUTS[m]][3]
                        if m == 0:
                            pe.wait_ge(out_used, i + 1)
                        pe.wait_ge(scaled, NO * i + m + 1)
                        nc.tensor.matmul(big[:, 5, :], part(wn, k), hid[:, OUTS[m], :], start=(m == 0), stop=(m == NO - 1)).then_inc(used, 1)

                    m = 0
                    for n in range(NC):
                        up(n)
                        while m < NO and OUTS[m] < n:
                            down(m)
                            m += 1
                    while m < NO:
                        down(m)
                        m += 1

            @blk.scalar
            def _(act):
                nc.scalar.sem_inc(hid_ready, RING)
                with act.Fori(0, NBLK) as i:
                    for n, (name, products, expert, out) in enumerate(CHUNKS):
                        act.wait_ge(up_ready, NC * i + n + 1)
                        if n == 0:
                            act.wait_ge(out_used, i + 1)
                        nc.scalar.activation(hid[:, n, :], big[:, n % RING, :], ACT.Silu if expert == 1 else ACT.Gelu).then_inc(hid_ready, 1)

            @blk.vector
            def _(dve):
                nc.vector.sem_inc(out_used, 1)
                with dve.Fori(0, NBLK) as i:
                    c = Chain(dve, step, 2 + 1 + 1, i)
                    xs = g.x[:, block(i)]
                    for m, n in enumerate(OUTS):
                        dve.wait_ge(hid_ready, NC * i + n + 1 + RING)
                        dve.wait_ge(spread, 4 * i + m // 2 + 1)
                        if CHUNKS[n][2] == 1:
                            c.link(nc.vector.tensor_tensor(hid[:, n, :], hid[:, n, :], big[:, 4, :], ALU.mult))
                        nc.vector.tensor_tensor(hid[:, n, :], hid[:, n, :], big[:, 6 + m // 2 % 2, :], ALU.mult).then_inc(scaled, 1)
                    c.link(nc.vector.tensor_tensor(xs, xs, g.xn[:, block(i)], ALU.add))
                    dve.wait_ge(used, NO * i + NO)
                    for r in range(32, P, 32):
                        xr = g.x[r:r + 32, block(i)]
                        ins = nc.vector.tensor_tensor(xr, xr, big[r:r + 32, 5, :], ALU.add)
                    c.link(ins)
                    nc.vector.sem_inc(out_used, 1)
                    c.close()


DEPTH = 6
WINDOW = 32
HALF = 341
L3A = layout([("wq", P, INNER), ("wk", P, INNER), ("wv", P, INNER), ("wf", P, INNER), ("wg", P, INNER),
              ("wb", P, HEADS), ("wo", P, PAIRS * D), ("dt", 1, INNER), ("bg", 1, INNER), ("a_log", P, HEADS),
              ("norm_w", P, 1)])
L3W = layout([("wq", P, INNER), ("wqr", P, INNER), ("wk", P, INNER), ("wkr", P, INNER), ("wv", P, INNER),
              ("wo", P, PAIRS * D), ("qs", P, 2), ("ks", P, 2)])
L3F = layout([("w1", P, 6 * P), ("b1", P, 6), ("w2", P, 3 * D), ("b2", P, 1), ("g", P, 1), ("b", P, 1)])


def decay_attention(nc, g, w):
    W = lambda n: L3A.of(w, n)
    with Stage(nc, "l3a") as st:
        dmask = st.sb("dmask", [P, HEADS, 3 * P])
        ealog = st.sb("ealog", [P, HEADS])
        xb = st.sb("xb", [P, T])
        qk = st.sb("qk", [P, 2, PAIRS, T])
        sq = st.sb("sq", [P, 2, T])
        v, gt, gate_s = (st.sb(n, [P, 2, INNER]) for n in ("v", "gt", "gate"))
        nrm = st.sb("nrm", [P, 2, 2, HEADS])
        beta = st.sb("beta", [P, 2, HEADS])
        kb = st.sb("kb", [P, 2, HEADS])
        sc = st.sb("sc", [P, 2, 3 * P])
        o, osq = st.sb("o", [P, INNER]), st.sb("osq", [P, INNER])
        ms = st.sb("ms", [P, HEADS])
        ot = st.sb("ot", [P, PAIRS, T])
        big = st.ps("big", [P, 8, BLK])
        nrm_ps = big[:, 4, 0:64].rearrange("p (t q h) -> p t q h", t=2, q=2)
        beta_ps = big[:, 5, 0:2 * HEADS].rearrange("p (t h) -> p t h", t=2)
        names = ("mask_arg", "mask_exp", "mask_done", "xb_ready", "proj_ready", "silu_ready", "sq_ready", "sq_used",
                 "nb_ready", "tok_ready", "tok_moved", "sqrt_ready", "scaled", "s_ready", "s_masked", "s_used",
                 "o_gated", "o_squared", "rms_arg", "rms_root", "o_normed", "turned", "ot_ready", "y_ready", "added",
                 "dve_step")
        S = {n: st.sem(n) for n in names}
        def norms(pe, b, f):
            pe.wait_ge(S["sq_ready"], b * PAIRS + f + 1)
            for n in range(2):
                for t in range(2):
                    mm = nc.tensor.matmul(nrm_ps[:, t, n, 2 * f:2 * f + 2], sq[:, n, t * P:(t + 1) * P],
                                          g.c("pair"), start=True, stop=True)
            mm.then_inc(S["sq_used"], 1)

        def sums(pe, b, t, h):
            pe.wait_ge(S["s_masked"], 32 * b + t * HEADS + h + 3)
            for j in range(t + 1):
                mm = nc.tensor.matmul(big[:, 6 + h // 8, (h % 8) * HD:(h % 8 + 1) * HD], sc[:, h % 2, j * P:(j + 1) * P],
                                      v[:, j, h * HD:(h + 1) * HD], start=(j == 0), stop=(j == t))
            mm.then_inc(S["s_used"], 1)

        with nc.Block() as blk:
            @blk.tensor
            def _(pe):
                nc.tensor.sem_inc(S["s_used"], 2)
                nc.tensor.sem_inc(S["turned"], 1)
                with pe.Fori(0, B) as b:
                    pe.wait_ge(S["xb_ready"], b + 1)
                    for f in range(PAIRS):
                        pe.wait_ge(S["silu_ready"], b * PAIRS + f + 1)
                        for n, wn in enumerate(("wq", "wk")):
                            mm = nc.tensor.matmul(big[:, f % 2, n * T:(n + 1) * T], W(wn)[:, f * P:(f + 1) * P], xb[:],
                                                  start=True, stop=True)
                        mm.then_inc(S["proj_ready"], 1)
                        if f >= 1:
                            norms(pe, b, f - 1)
                    norms(pe, b, PAIRS - 1)
                    for t in range(2):
                        mm = nc.tensor.matmul(beta_ps[:, t, :], xb[:, t * P:(t + 1) * P], W("wb"), start=True, stop=True)
                    mm.then_inc(S["nb_ready"], 1)
                    for t in range(2):
                        for n, (wn, sign, bias) in enumerate((("wv", None, None), ("wf", g.c("minus_row"), "dt"), ("wg", g.c("ones_row"), "bg"))):
                            u = t * 3 + n
                            pe.wait_ge(S["tok_moved"], b * 6 + u + 1)
                            for c in range(2):
                                cols = slice(c * BLK, (c + 1) * BLK)
                                mm = nc.tensor.matmul(big[:, 6 + c, :], xb[:, t * P:(t + 1) * P], W(wn)[:, cols],
                                                      start=True, stop=bias is None)
                                if bias:
                                    mm = nc.tensor.matmul(big[:, 6 + c, :], sign[:, 0:P], W(bias)[:, cols], start=False, stop=True)
                            mm.then_inc(S["tok_ready"], 1)
                    pe.wait_ge(S["scaled"], b + 1)
                    for t in range(2):
                        if t == 0:
                            pe.wait_ge(S["tok_moved"], b * 6 + 7)
                        else:
                            pe.wait_ge(S["o_gated"], 2 * b + 1)
                        for h in range(HEADS):
                            n = t * HEADS + h
                            r, f = (h % 2) * HD, h // 2
                            rows = slice(r, r + HD)
                            pe.wait_ge(S["s_masked"], 32 * b + n + 1)
                            for j in range(t + 1):
                                mm = nc.tensor.matmul(big[:, h % 2, j * P:(j + 1) * P], qk[rows, 1, f, j * P:(j + 1) * P],
                                                      qk[rows, 0, f, t * P:(t + 1) * P], start=True, stop=True)
                            mm.then_inc(S["s_ready"], 1)
                            if h >= 1:
                                sums(pe, b, t, h - 1)
                        sums(pe, b, t, HEADS - 1)
                        pe.wait_ge(S["o_normed"], 2 * b + t + 1)
                        for f in range(PAIRS):
                            mm = nc.tensor.transpose(big[:, 2 + f // 4, (f % 4) * P:(f % 4 + 1) * P], o[:, f * P:(f + 1) * P], g.c("ident"))
                        mm.then_inc(S["turned"], 1)
                        pe.wait_ge(S["ot_ready"], 2 * b + t + 1)
                    for f in range(PAIRS):
                        mm = nc.tensor.matmul(big[:, 2, 0:T], W("wo")[:, f * D:(f + 1) * D], ot[:, f, :],
                                              start=(f == 0), stop=(f == PAIRS - 1))
                    mm.then_inc(S["y_ready"], 1)

            @blk.scalar
            def _(act):
                nc.scalar.activation(ealog[:], W("a_log"), ACT.Exp).then_inc(S["mask_arg"], 1)
                for h in range(HEADS):
                    act.wait_ge(S["mask_exp"], h + 1)
                    nc.scalar.activation(dmask[:, h, :], dmask[:, h, :], ACT.Exp).then_inc(S["mask_done"], 1)
                nc.scalar.sem_inc(S["tok_moved"], 1)
                nc.scalar.sem_inc(S["silu_ready"], 2)
                with act.Fori(0, B) as b:
                    act.wait_ge(S["added"], b + 1)
                    nc.scalar.activation(xb[:], g.xn[:, bass.ds(b * T, T)], ACT.Copy).then_inc(S["xb_ready"], 1)
                    for f in range(PAIRS):
                        act.wait_ge(S["proj_ready"], b * PAIRS + f + 1)
                        nc.scalar.activation(qk[:, :, f, :], big[:, f % 2, :].rearrange("p (n t) -> p n t", n=2),
                                             ACT.Silu).then_inc(S["silu_ready"], 1)
                        act.wait_ge(S["silu_ready"], b * PAIRS + f + 3)
                        act.wait_ge(S["sq_used"], b * PAIRS + f + 1)
                        nc.scalar.activation(sq[:], qk[:, :, f, :], ACT.Square).then_inc(S["sq_ready"], 1)
                    act.wait_ge(S["nb_ready"], b + 1)
                    nc.scalar.activation(nrm[:], nrm_ps, ACT.Sqrt)
                    nc.scalar.activation(beta[:], beta_ps, ACT.Sigmoid).then_inc(S["sqrt_ready"], 1)
                    for t in range(2):
                        for n, (dst, fn) in enumerate(((v, ACT.Silu), (gt, ACT.Sigmoid), (gate_s, ACT.Sigmoid))):
                            act.wait_ge(S["tok_ready"], b * 6 + t * 3 + n + 1)
                            nc.scalar.activation(dst[:, t, :], big[:, 6:8, :].rearrange("p c n -> p (c n)"), fn).then_inc(S["tok_moved"], 1)
                    for t in range(2):
                        act.wait_ge(S["o_gated"], 2 * b + t + 1)
                        nc.scalar.activation(osq[:], o[:], ACT.Square).then_inc(S["o_squared"], 1)
                        act.wait_ge(S["rms_arg"], 2 * b + t + 1)
                        nc.scalar.activation(ms[:], ms[:], ACT.Sqrt, bias=g.c("eps5"), scale=1.0 / HD).then_inc(S["rms_root"], 1)
                        act.wait_ge(S["turned"], 2 * b + t + 2)
                        nc.scalar.activation(ot[:, :, t * P:(t + 1) * P], big[:, 2:4, :].rearrange("p c (f n) -> p (c f) n", f=4),
                                             ACT.Copy).then_inc(S["ot_ready"], 1)

            @blk.vector
            def _(dve):
                nc.vector.sem_inc(S["added"], 1)
                nc.vector.sem_inc(S["sq_used"], 1)
                nc.vector.sem_inc(S["s_masked"], 2)
                nc.vector.tensor_scalar(W("wo"), W("wo"), W("norm_w"), None, ALU.mult)
                dve.wait_ge(S["mask_arg"], 1)
                for h in range(HEADS):
                    nc.vector.tensor_scalar(dmask[:, h, :], g.c("lag"), ealog[:, h:h + 1], None, ALU.mult).then_inc(S["mask_exp"], 1)
                for h in range(HEADS):
                    dve.wait_ge(S["mask_done"], h + 1)
                    ins = nc.vector.tensor_tensor(dmask[:, h, :], dmask[:, h, :], g.c("earlier"), ALU.mult)
                setup = Chain(dve, st.sem("setup_done"))
                setup.link(ins)
                with dve.Fori(0, B) as b:
                    c = Chain(dve, S["dve_step"], 4 + 2 * 2 + 1, b)
                    dve.wait_ge(S["sqrt_ready"], b + 1)
                    c.link(nc.vector.tensor_scalar(nrm[:], nrm[:], 1e-12, None, ALU.max))
                    c.link(nc.vector.reciprocal(nrm[:], nrm[:]))
                    c.link(nc.vector.tensor_tensor(kb[:], nrm[:, :, 1, :], beta[:], ALU.mult))
                    dve.wait_ge(S["tok_moved"], b * 6 + 7)
                    vv = v[:].rearrange("p t (h d) -> p (t h) d", h=HEADS)
                    gg = gt[:].rearrange("p t (h d) -> p (t h) d", h=HEADS)
                    nc.vector.tensor_tensor(vv, vv, kb[:].rearrange("p t h -> p (t h)").unsqueeze(2).to_broadcast([P, 32, HD]),
                                            ALU.mult).then_inc(S["scaled"], 1)
                    for t in range(2):
                        ins = nc.vector.tensor_tensor(gt[:, t, :].rearrange("p (h d) -> p h d", h=HEADS),
                                                      gt[:, t, :].rearrange("p (h d) -> p h d", h=HEADS),
                                                      nrm[:, t, 0, :].unsqueeze(2).to_broadcast([P, HEADS, HD]), ALU.mult)
                    c.link(ins)
                    for t in range(2):
                        for h in range(HEADS):
                            n = t * HEADS + h
                            dve.wait_ge(S["s_ready"], 32 * b + n + 1)
                            dve.wait_ge(S["s_used"], 32 * b + n + 1)
                            mk = dmask[:, h, 0:P] if t == 0 else dmask[:, h, P:3 * P]
                            nc.vector.tensor_tensor(sc[:, h % 2, 0:(t + 1) * P], big[:, h % 2, 0:(t + 1) * P], mk,
                                                    ALU.mult).then_inc(S["s_masked"], 1)
                        dve.wait_ge(S["s_used"], 32 * b + t * HEADS + HEADS + 2)
                        dve.wait_ge(S["turned"], 2 * b + t + 1)
                        nc.vector.tensor_tensor(o[:], big[:, 6:8, :].rearrange("p c n -> p (c n)"), gt[:, t, :],
                                                ALU.mult).then_inc(S["o_gated"], 1)
                        dve.wait_ge(S["o_squared"], 2 * b + t + 1)
                        nc.vector.tensor_reduce(ms[:], osq[:].rearrange("p (h d) -> p h d", h=HEADS), AX,
                                                ALU.add).then_inc(S["rms_arg"], 1)
                        dve.wait_ge(S["rms_root"], 2 * b + t + 1)
                        c.link(nc.vector.reciprocal(ms[:], ms[:]))
                        o3 = o[:].rearrange("p (h d) -> p h d", h=HEADS)
                        c.link(nc.vector.tensor_tensor(o3, o3, ms[:].unsqueeze(2).to_broadcast([P, HEADS, HD]), ALU.mult))
                        nc.vector.tensor_tensor(o[:], o[:], gate_s[:, t, :], ALU.mult).then_inc(S["o_normed"], 1)
                    dve.wait_ge(S["y_ready"], b + 1)
                    xs = g.x[:, bass.ds(b * T, T)]
                    c.link(nc.vector.tensor_tensor(xs, xs, big[:, 2, 0:T], ALU.add))
                    nc.vector.sem_inc(S["added"], 1)
                    c.close()


def shift_copy(eng, dst, y, sem):
    d3, y3 = dst.rearrange("p (b t) -> p b t", t=T), y.rearrange("p (b t) -> p b t", t=T)
    eng.tensor_copy(d3[0:HD], y3[0:HD])
    eng.tensor_copy(d3[HD:P, :, 1:T], y3[HD:P, :, 0:T - 1])
    eng.memset(d3[HD:P, :, 0:1], 0.0).then_inc(sem, 1)


QT = (0, 96, 160)
KT = (0, 64, 128)
QN = 96


def wait_for(eng, sem, count):
    if not isinstance(count, int) or count > 0:
        eng.wait_ge(sem, count)


def window_attention(nc, g, w, layer):
    W = lambda n: L3W.of(w, n)
    y = g.xn
    HG = 4
    GROUPS = 3 * HEADS // HG
    PER_TILE = HEADS // HG
    with Stage(nc, "l3w") as st:
        tab = st.sb("tab", [P, 2, 2, T])
        xb = st.sb("xb", [P, 2, T])
        rot = st.sb("rot", [P, 2, 2, 2, T])
        sq = st.sb("sq", [P, 2, 2, T])
        ss, rn, unit = (st.sb(n, [P, 2, 2, T]) for n in ("ss", "rn", "unit"))
        ks = st.sb("ks", [P, 4, T])
        qf, kz = st.sb("qf", [P, 2, PAIRS, T]), st.sb("kz", [P, 2, PAIRS, 2, T])
        v = st.sb("v", [P, 2, 3, INNER])
        nb, sm, rs = (st.sb(n, [P, 2, HG]) for n in ("nb", "sm", "rs"))
        pr, pt = st.sb("pr", [P, 2, HG, P]), st.sb("pt", [P, 2, HG, QN])
        ot = st.sb("ot", [P, PAIRS, T])
        identb, maskb = st.sb("identb", [P, QN], mybir.dt.bfloat16), st.sb("maskb", [P, 2, HG, P], mybir.dt.bfloat16)
        big = st.ps("big", [P, 8, BLK])
        names = ("tab_ready", "xb_ready", "qk_ready", "rot_done", "sq_ready", "norm_ready", "clamped", "ln_ready", "root_ready",
                 "summed", "scaled", "v_ready", "v_moved", "s_ready", "max_ready", "exp_done", "inv_ready", "p_ready", "p_turned",
                 "pt_ready", "pt_used", "ot_ready", "y_ready", "added",
                 "pool_step", "unit_ready", "refined")
        S = {n: st.sem(n) for n in names}

        def pe_qk(pe, b, par, f):
            if f == 0:
                wait_for(pe, S["xb_ready"], b + 1)
                wait_for(pe, S["v_moved"], 6 * b)
            wait_for(pe, S["sq_ready"], PAIRS * b + f)
            for n, (wa, wb) in enumerate((("wq", "wqr"), ("wk", "wkr"))):
                nc.tensor.matmul(big[:, n, 0:T], W(wa)[:, f * P:(f + 1) * P], xb[:, par, :], start=True, stop=True)
                mm = nc.tensor.matmul(big[:, n, T:2 * T], W(wb)[:, f * P:(f + 1) * P], xb[:, par, :], start=True, stop=True)
            mm.then_inc(S["qk_ready"], 1)

        def pe_norm(pe, b, f):
            wait_for(pe, S["sq_ready"], PAIRS * b + f + 1)
            wait_for(pe, S["clamped"], PAIRS * b + f)
            nc.tensor.matmul(big[:, 2, :], g.c("head64"), sq[:, f % 2].rearrange("p n t -> p (n t)"),
                             start=True, stop=True).then_inc(S["norm_ready"], 1)

        def pe_v(pe, b, par, n):
            t, c = divmod(n, 2)
            if n < 2:
                wait_for(pe, S["sq_ready"], PAIRS * b + PAIRS)
            else:
                wait_for(pe, S["v_moved"], 6 * b + n - 1)
            nc.tensor.matmul(big[:, c, :], xb[:, par, KT[t]:KT[t] + P], W("wv")[:, c * BLK:(c + 1) * BLK],
                             start=True, stop=True).then_inc(S["v_ready"], 1)

        def pe_scores(pe, a, par, u):
            t, grp = divmod(u, PER_TILE)
            if u == 0:
                wait_for(pe, S["scaled"], PAIRS * a + PAIRS)
            wait_for(pe, S["exp_done"], GROUPS * a + u - 1)
            bank = big[0:QN, 3 + u % 2, :]
            nc.tensor.matmul(bank, identb[:], maskb[:, min(t, 1)].rearrange("p i n -> p (i n)"), start=True, stop=False)
            for i in range(HG // 2):
                f = grp * HG // 2 + i
                mm = nc.tensor.matmul(bank[:, 2 * i * P:2 * (i + 1) * P], qf[:, par, f, QT[t]:QT[t] + QN],
                                      kz[:, par, f, :, KT[t]:KT[t] + P], start=False, stop=i == HG // 2 - 1)
            mm.then_inc(S["s_ready"], 1)

        def pe_turn(pe, a, u):
            wait_for(pe, S["p_ready"], GROUPS * a + u + 1)
            wait_for(pe, S["pt_ready"], GROUPS * a + u)
            for i in range(HG):
                mm = nc.tensor.matmul(big[:, 5, i * QN:(i + 1) * QN], pr[:, u % 2, i, :], g.c("ident")[:, 0:QN], start=True, stop=True)
            mm.then_inc(S["p_turned"], 1)

        def pe_mix(pe, a, par, u):
            t, grp = divmod(u, PER_TILE)
            j = grp // 2
            if u == 0:
                wait_for(pe, S["v_moved"], 6 * a + 6)
            if grp % 2 == 0:
                wait_for(pe, S["ot_ready"], 6 * a + 2 * t + j - 1)
                if t == 0 and j == 1:
                    wait_for(pe, S["added"], a)
            wait_for(pe, S["pt_ready"], GROUPS * a + u + 1)
            for i in range(HG):
                h = grp * HG + i
                f, odd = divmod(h, 2)
                mm = nc.tensor.matmul(big[odd * HD:(odd + 1) * HD, 6 + j, (f % 4) * QN:(f % 4 + 1) * QN],
                                      v[:, par, t, h * HD:(h + 1) * HD], pt[:, u % 2, i, :], start=True, stop=True)
            mm.then_inc(S["pt_used"], 1)

        def pe_out(pe, a):
            wait_for(pe, S["ot_ready"], 6 * a + 6)
            for f in range(PAIRS):
                mm = nc.tensor.matmul(big[:, 7, 0:T], W("wo")[:, f * D:(f + 1) * D], ot[:, f, :],
                                      start=(f == 0), stop=(f == PAIRS - 1))
            mm.then_inc(S["y_ready"], 1)

        def pe_project(pe, b, par, s):
            if s < PAIRS:
                pe_qk(pe, b, par, s)
            if 1 <= s <= PAIRS:
                pe_norm(pe, b, s - 1)
            if PAIRS <= s < PAIRS + 3:
                pe_v(pe, b, par, 2 * (s - PAIRS))
                pe_v(pe, b, par, 2 * (s - PAIRS) + 1)

        def pe_turn_of(pe, a, par, first=False, last=False):
            pe_scores(pe, a, par, 0)
            for u in range(GROUPS):
                if u + 1 < GROUPS:
                    pe_scores(pe, a, par, u + 1)
                if not last:
                    pe_project(pe, a + 1, 1 - par, u)
                if u == 1 and not first:
                    pe_out(pe, a - 1)
                pe_turn(pe, a, u)
                if u >= 1:
                    pe_mix(pe, a, par, u - 1)
            pe_mix(pe, a, par, GROUPS - 1)

        def act_input(act, b, par):
            nc.scalar.activation(xb[0:HD, par, :], y[0:HD, bass.ds(b * T, T)], ACT.Copy)
            nc.scalar.activation(xb[HD:P, par, 1:T], y[HD:P, bass.ds(b * T, T - 1)], ACT.Copy).then_inc(S["xb_ready"], 1)

        def act_square(act, b, f):
            wait_for(act, S["rot_done"], PAIRS * b + f + 1)
            wait_for(act, S["norm_ready"], PAIRS * b + f - 1)
            nc.scalar.activation(sq[:, f % 2], big[:, 0:2, 0:T], ACT.Square).then_inc(S["sq_ready"], 1)

        def act_root(act, b, f):
            wait_for(act, S["clamped"], PAIRS * b + f + 1)
            nc.scalar.activation(rn[:, f % 2], ss[:, f % 2], ACT.Ln).then_inc(S["ln_ready"], 1)
            wait_for(act, S["ln_ready"], PAIRS * b + f + 1)
            nc.scalar.activation(rn[:, f % 2], rn[:, f % 2], ACT.Exp, scale=-0.5).then_inc(S["root_ready"], 1)

        def act_v(act, b, par, n):
            if n == 0:
                wait_for(act, S["pt_used"], GROUPS * (b - 1))
            wait_for(act, S["v_ready"], 6 * b + n + 1)
            nc.scalar.activation(v[:, par, n // 2, (n % 2) * BLK:(n % 2 + 1) * BLK], big[:, n % 2, :],
                                 ACT.Copy).then_inc(S["v_moved"], 1)

        def act_exp(act, a, u):
            wait_for(act, S["max_ready"], GROUPS * a + u + 1)
            wait_for(act, S["p_turned"], GROUPS * a + u - 1)
            for i in range(HG):
                ins = nc.scalar.activation(pr[0:QN, u % 2, i, :], big[0:QN, 3 + u % 2, i * P:(i + 1) * P], ACT.Exp,
                                           bias=nb[0:QN, u % 2, i:i + 1], accum_out=sm[0:QN, u % 2, i:i + 1])
            ins.then_inc(S["exp_done"], 1)

        def act_turned(act, a, u):
            wait_for(act, S["p_turned"], GROUPS * a + u + 1)
            wait_for(act, S["pt_used"], GROUPS * a + u - 1)
            nc.scalar.activation(pt[:, u % 2], big[:, 5, 0:HG * QN].rearrange("p (i n) -> p i n", n=QN),
                                 ACT.Copy).then_inc(S["pt_ready"], 1)

        def act_sums(act, a, m):
            t, j = divmod(m, 2)
            skip = QT[1] + QN - QT[2] if t == 2 else 0
            wait_for(act, S["pt_used"], GROUPS * a + PER_TILE * t + 2 * j + 2)
            if m == 0:
                wait_for(act, S["y_ready"], a)
            nc.scalar.activation(ot[:, 4 * j:4 * j + 4, QT[t] + skip:QT[t] + QN],
                                 big[:, 6 + j, 0:4 * QN].rearrange("p (f n) -> p f n", f=4)[:, :, skip:QN],
                                 ACT.Copy).then_inc(S["ot_ready"], 1)

        def act_project_1(act, b, par, s):
            if s < PAIRS:
                act_square(act, b, s)
            if PAIRS <= s < PAIRS + 3:
                act_v(act, b, par, 2 * (s - PAIRS))
                act_v(act, b, par, 2 * (s - PAIRS) + 1)

        def act_project_2(act, b, s):
            if 1 <= s <= PAIRS:
                act_root(act, b, s - 1)

        def act_turn_of(act, a, par, last=False):
            for u in range(GROUPS):
                if u == 0 and not last:
                    act_input(act, a + 1, 1 - par)
                act_exp(act, a, u)
                if not last:
                    act_project_1(act, a + 1, 1 - par, u)
                act_turned(act, a, u)
                if not last:
                    act_project_2(act, a + 1, u)
                if u >= 2 and u % 2 == 0:
                    act_sums(act, a, u // 2 - 1)
            act_sums(act, a, 5)

        def dve_rotate(dve, b, f):
            wait_for(dve, S["qk_ready"], PAIRS * b + f + 1)
            wait_for(dve, S["summed"], PAIRS * b + f - 1)
            nc.vector.tensor_tensor(rot[:, f % 2].rearrange("p a b t -> p a (b t)"), big[:, 0:2, :],
                                    tab[:].rearrange("p a b t -> p a (b t)"), ALU.mult).then_inc(S["rot_done"], 1)

        def dve_clamp(dve, b, f):
            wait_for(dve, S["norm_ready"], PAIRS * b + f + 1)
            wait_for(dve, S["scaled"], PAIRS * b + f - 1)
            nc.vector.tensor_scalar(ss[:, f % 2].rearrange("p n t -> p (n t)"), big[:, 2, :], 1e-24, 65536.0,
                                    ALU.max, ALU.mult).then_inc(S["clamped"], 1)

        def dve_scale(dve, b, par, f):
            wait_for(dve, S["unit_ready"], PAIRS * b + f + 1)
            r = rn[:, f % 2]
            nc.vector.scalar_tensor_tensor(out=r, in0=unit[:, f % 2], scalar=-3.0, in1=r, op0=ALU.add, op1=ALU.mult).then_inc(S["refined"], 1)
            wait_for(dve, S["refined"], PAIRS * b + f + 1)
            if f == 0:
                wait_for(dve, S["s_ready"], GROUPS * (b - 1))
            nc.vector.scalar_tensor_tensor(out=qf[:, par, f, :], in0=qf[:, par, f, :], scalar=-128.0, in1=rn[:, f % 2, 0, :],
                                           op0=ALU.mult, op1=ALU.mult)
            for odd in range(2):
                rows = slice(odd * HD, (odd + 1) * HD)
                ins = nc.vector.scalar_tensor_tensor(out=kz[rows, par, f, odd, :], in0=ks[rows, f % 4, :], scalar=-128.0,
                                                     in1=rn[rows, f % 2, 1, :], op0=ALU.mult, op1=ALU.mult)
            ins.then_inc(S["scaled"], 1)

        def dve_max(dve, a, u):
            wait_for(dve, S["s_ready"], GROUPS * a + u + 1)
            wait_for(dve, S["exp_done"], GROUPS * a + u - 1)
            nc.vector.tensor_reduce(nb[0:QN, u % 2, :], big[0:QN, 3 + u % 2, :].rearrange("p (i n) -> p i n", n=P), AX, ALU.max,
                                    negate=True).then_inc(S["max_ready"], 1)

        def dve_probs(dve, a, u):
            wait_for(dve, S["exp_done"], GROUPS * a + u + 1)
            nc.vector.reciprocal(rs[0:QN, u % 2, :], sm[0:QN, u % 2, :]).then_inc(S["inv_ready"], 1)
            wait_for(dve, S["inv_ready"], GROUPS * a + u + 1)
            nc.vector.tensor_tensor(pr[0:QN, u % 2], pr[0:QN, u % 2], rs[0:QN, u % 2, :].unsqueeze(2).to_broadcast([QN, HG, P]),
                                    ALU.mult).then_inc(S["p_ready"], 1)

        def dve_add(dve, a):
            wait_for(dve, S["y_ready"], a + 1)
            ys = y[:, bass.ds(a * T, T)]
            nc.vector.tensor_tensor(ys, ys, big[:, 7, 0:T], ALU.add).then_inc(S["added"], 1)

        def dve_project(dve, b, par, s):
            if s < PAIRS:
                dve_rotate(dve, b, s)
            if 1 <= s <= PAIRS:
                dve_clamp(dve, b, s - 1)
            if 2 <= s <= PAIRS + 1:
                dve_scale(dve, b, par, s - 2)

        def dve_turn_of(dve, a, par, first=False, last=False):
            dve_max(dve, a, 0)
            for u in range(GROUPS):
                if u + 1 < GROUPS:
                    dve_max(dve, a, u + 1)
                dve_probs(dve, a, u)
                if not last:
                    dve_project(dve, a + 1, 1 - par, u)
                if u == 1 and not first:
                    dve_add(dve, a - 1)

        def pool_units(pool, b, f):
            wait_for(pool, S["root_ready"], PAIRS * b + f + 1)
            nc.gpsimd.tensor_tensor(unit[:, f % 2], ss[:, f % 2], rn[:, f % 2], ALU.mult).then_inc(S["pool_step"], 1)
            wait_for(pool, S["pool_step"], PAIRS * b + f + 1)
            nc.gpsimd.tensor_tensor(unit[:, f % 2], unit[:, f % 2], rn[:, f % 2], ALU.mult).then_inc(S["unit_ready"], 1)

        def pool_sums(pool, b, par):
            for f in range(PAIRS):
                wait_for(pool, S["rot_done"], PAIRS * b + f + 1)
                wait_for(pool, S["scaled"], PAIRS * b + f - 3)
                if f == 0:
                    wait_for(pool, S["s_ready"], GROUPS * (b - 1))
                nc.gpsimd.tensor_tensor(qf[:, par, f, :], rot[:, f % 2, 0, 0, :], rot[:, f % 2, 0, 1, :], ALU.add)
                nc.gpsimd.tensor_tensor(ks[:, f % 4, :], rot[:, f % 2, 1, 0, :], rot[:, f % 2, 1, 1, :], ALU.add).then_inc(S["summed"], 1)
                if f >= 1:
                    pool_units(pool, b, f - 1)
            pool_units(pool, b, PAIRS - 1)

        with nc.Block() as blk:
            @blk.tensor
            def _(pe):
                pe.wait_ge(S["tab_ready"], 1)
                for s in range(PAIRS + 3):
                    pe_project(pe, 0, 0, s)
                pe_turn_of(pe, 0, 0, first=True)
                with pe.Fori(0, (B - 2) // 2) as i:
                    pe_turn_of(pe, 2 * i + 1, 1)
                    pe_turn_of(pe, 2 * i + 2, 0)
                pe_turn_of(pe, B - 1, 1, last=True)
                pe_out(pe, B - 1)

            @blk.scalar
            def _(act):
                nc.scalar.preload_act_table_set("natural_log_exp_and_others")
                nc.scalar.preload_act_table_set("natural_log_exp_and_others")
                act_input(act, 0, 0)
                for s in range(PAIRS + 3):
                    act_project_1(act, 0, 0, s)
                    act_project_2(act, 0, s)
                act_turn_of(act, 0, 0)
                with act.Fori(0, (B - 2) // 2) as i:
                    act_turn_of(act, 2 * i + 1, 1)
                    act_turn_of(act, 2 * i + 2, 0)
                act_turn_of(act, B - 1, 1, last=True)

            @blk.gpsimd
            def _(pool):
                pool_sums(pool, 0, 0)
                pool_sums(pool, 1, 1)
                with pool.Fori(0, (B - 2) // 2) as i:
                    pool_sums(pool, 2 * i + 2, 0)
                    pool_sums(pool, 2 * i + 3, 1)

            @blk.vector
            def _(dve):
                nc.vector.memset(xb[HD:P, :, 0:1], 0.0)
                nc.vector.memset(kz[0:HD, :, :, 1, :], 0.0)
                nc.vector.memset(kz[HD:P, :, :, 0, :], 0.0)
                nc.vector.memset(pr[QN:P], 0.0)
                for n, s in enumerate(("qs", "ks")):
                    for m in range(2):
                        nc.vector.tensor_scalar(tab[:, n, m, :], g.c(("rot_q", "rot_k")[n])[:, m * T:(m + 1) * T], W(s)[:, m:m + 1], None, ALU.mult)
                nc.vector.tensor_copy(identb[:], g.c("ident")[:, 0:QN])
                for m in range(HG):
                    ins = nc.vector.tensor_copy(maskb[:, :, m, :], g.c("window").rearrange("p (a n) -> p a n", a=2))
                ins.then_inc(S["tab_ready"], 1)
                dve.wait_ge(S["tab_ready"], 1)
                for s in range(PAIRS + 2):
                    dve_project(dve, 0, 0, s)
                dve_turn_of(dve, 0, 0, first=True)
                with dve.Fori(0, (B - 2) // 2) as i:
                    dve_turn_of(dve, 2 * i + 1, 1)
                    dve_turn_of(dve, 2 * i + 2, 0)
                dve_turn_of(dve, B - 1, 1, last=True)
                dve_add(dve, B - 1)


def gated_mlp(nc, g, w, layer):
    W = lambda n: L3F.of(w, n)
    y = g.xn
    ROWS = (P, P, HALF - 2 * P)
    with Stage(nc, "l3f") as st:
        xs = st.sb("xs", [P, N])
        shifted = st.sem("shifted")
        with nc.Block() as blk:
            @blk.vector
            def _(dve):
                shift_copy(nc.vector, xs[:], y[:], shifted)
        layer_norm(nc, "l3n", xs, xs, g.c("mean"), g.c("eps5"), W("g"), W("b"))
        h_ps, o_ps = st.ps("h_ps", [P, 3, 2, BLK]), st.ps("o_ps", [P, BLK])
        ge, hid = st.sb("ge", [P, 3, BLK]), st.sb("hid", [P, 3, BLK])
        up_ready, gelu_ready, hid_ready, hid_used, out_used, step = (
            st.sem(n) for n in ("up_ready", "gelu_ready", "hid_ready", "hid_used", "out_used", "step"))
        def down(pe, i, c):
            if c == 0:
                pe.wait_ge(out_used, i + 1)
            pe.wait_ge(hid_ready, 3 * i + c + 4)
            nc.tensor.matmul(o_ps[:], W("w2")[0:ROWS[c], c * D:(c + 1) * D], hid[0:ROWS[c], c, :],
                             start=(c == 0), stop=(c == 2)).then_inc(hid_used, 1)

        with nc.Block() as blk:
            @blk.tensor
            def _(pe):
                with pe.Fori(0, NBLK) as i:
                    def up(c):
                        pe.wait_ge(hid_ready, 3 * i + c + 1)
                        for m in range(2):
                            at = (3 * m + c) * P
                            mm = nc.tensor.matmul(h_ps[0:ROWS[c], c, m, :], W("w1")[:, at:at + ROWS[c]], xs[:, block(i)],
                                                  start=True, stop=True)
                        mm.then_inc(up_ready, 1)

                    for c in range(3):
                        up(c)
                        if c >= 1:
                            down(pe, i, c - 1)
                    down(pe, i, 2)

            @blk.scalar
            def _(act):
                with act.Fori(0, NBLK) as i:
                    for c in range(3):
                        act.wait_ge(up_ready, 3 * i + c + 1)
                        act.wait_ge(hid_ready, 3 * i + c + 1)
                        r = ROWS[c]
                        nc.scalar.activation(ge[0:r, c, :], h_ps[0:r, c, 1, :], ACT.Gelu,
                                             bias=W("b1")[0:r, 3 + c:4 + c]).then_inc(gelu_ready, 1)

            @blk.vector
            def _(dve):
                nc.vector.sem_inc(hid_ready, 3)
                nc.vector.sem_inc(out_used, 1)
                nc.vector.sem_inc(hid_used, 3)
                with dve.Fori(0, NBLK) as i:
                    c_ = Chain(dve, step, 1, i)
                    for c in range(3):
                        r = ROWS[c]
                        dve.wait_ge(gelu_ready, 3 * i + c + 1)
                        dve.wait_ge(hid_used, 3 * i + c + 1)
                        nc.vector.scalar_tensor_tensor(out=hid[0:r, c, :], in0=h_ps[0:r, c, 0, :], scalar=W("b1")[0:r, c:c + 1],
                                                       in1=ge[0:r, c, :], op0=ALU.add, op1=ALU.mult).then_inc(hid_ready, 1)
                    dve.wait_ge(hid_used, 3 * i + 3 + 3)
                    ys = y[:, block(i)]
                    c_.link(nc.vector.scalar_tensor_tensor(out=ys, in0=o_ps[:], scalar=W("b2"), in1=ys, op0=ALU.add, op1=ALU.add))
                    nc.vector.sem_inc(out_used, 1)
                    c_.close()


CONST = layout([("ident", P, P), ("mean", P, P), ("mask8", P, P), ("before8", P, 64), ("before4", P, 16),
                ("pick8", P, 8 * P), ("ones_row", 1, 512), ("eps5", P, 1),
                ("mean32", P, P), ("sum32", P, P), ("causal", P, P), ("eps_rms", P, 1)])
CONST3 = layout([("minus_row", 1, P), ("pair", P, 2), ("head64", P, P), ("lag", P, 3 * P), ("earlier", P, 3 * P),
                 ("rot_q", P, 2 * T), ("rot_k", P, 2 * T), ("window", P, 2 * P)])


def constants():
    i = np.arange(P)
    pick8 = np.zeros((P, 8, P), np.float32)
    pick8[np.arange(8), np.arange(8), :] = 1
    key, query = i[:, None], np.concatenate([i, i + P, i])[None]
    lag = query - 1 - key
    q96 = i[:, None]
    window0 = (i[None] <= q96) & (i[None] >= q96 - WINDOW)
    window1 = (i[None] <= q96 + WINDOW) & (i[None] >= q96)
    half = np.arange(0, HD, 2, dtype=np.float32)
    t = np.arange(T, dtype=np.float32)
    freqs = t[:, None] * (np.float32(1) / np.float32(10000) ** (half / np.float32(HD)))[None]
    base = (half + np.float32(0.4 * HD)) / np.float32(1.4 * HD)
    scale = base[None] ** ((t - T // 2) / np.float32(WINDOW // 2))[:, None]
    cos, sin = np.cos(freqs), np.sin(freqs)

    def rotation(s):
        c4 = np.concatenate([cos * s] * 4, 1).T
        s4 = np.concatenate([-sin * s, sin * s] * 2, 1).T
        return np.concatenate([c4, s4], 1)

    made = {
        "ident": np.eye(P), "mean": np.full((P, P), 1.0 / P), "mask8": (i[:, None] // 8 == i[None] // 8),
        "before8": np.tile(np.tril(np.ones((8, 8)), -1).reshape(1, 64), (P, 1)),
        "before4": np.tile(np.tril(np.ones((4, 4)), -1).reshape(1, 16), (P, 1)),
        "pick8": pick8.reshape(P, 8 * P), "ones_row": np.ones((1, 512)), "eps5": np.full((P, 1), 1e-5),
        "minus_row": np.full((1, P), -1.0), "pair": (i[:, None] // HD == np.arange(2)[None]),
        "head64": (i[:, None] // HD == i[None] // HD), "lag": np.where(lag >= 0, -lag, 0), "earlier": lag >= 0,
        "rot_q": rotation(8 * scale), "rot_k": rotation(np.float32(1) / scale),
        "mean32": (i[:, None] // 32 == i[None] // 32) / 8.0,
        "sum32": (i[:, None] // 32 == i[None] // 32) * (i[:, None] % 32 == 8),
        "causal": np.where(i[None] <= i[:, None], 0, NEG), "eps_rms": np.full((P, 1), 1.1920929e-07),
        "window": np.concatenate([np.where(window0, 0, NEG), np.where(window1, 0, NEG)], 1),
    }
    return made


class Shared:
    pass


def program(nc, dram, out):
    ctx = ExitStack()
    with ctx:
        g = Shared()
        g.x = ctx.enter_context(nc.sbuf_tensor("x", [P, N], F32))
        g.xn = ctx.enter_context(nc.sbuf_tensor("xn", [P, N], F32))
        const = ctx.enter_context(nc.sbuf_tensor("const", [P, CONST.n], F32))
        g.c = lambda n: CONST.of(const, n) if n in CONST.at else CONST3.of(g.const3, n)
        g.ones_row = CONST.of(const, "ones_row")[:, 0:P]
        in_landed = ctx.enter_context(nc.semaphore("in_landed"))
        with nc.Block() as blk:
            @blk.sync
            def _(sp):
                sp.dma_start(g.x[:], dram["x"]).then_inc(in_landed, 16)
                sp.dma_start(const[:], dram["const"]).then_inc(in_landed, 16)
                sp.wait_ge(in_landed, 32)
        if 0 in STAGES:
            with Stage(nc, "l0") as st:
                w, prob_t = st.sb("w", [P, L0.n]), st.sb("prob_t", [P, N])
                load_pack(nc, st, dram["l0"], w, "l0")
                layer_norm(nc, "ln0", g.x, g.xn, g.c("mean"), g.c("eps5"))
                linear_attention(nc, g, w)
                gate(nc, g, "l0g", g.xn, L0.of(w, "gate"), None, 8, l0_weigh(nc, g), prob_t)
                swiglu_experts(nc, g, w, prob_t)
        if 1 in STAGES:
            with Stage(nc, "l1") as st:
                w, prob_t = st.sb("w", [P, L1.n]), st.sb("prob_t", [P, N])
                load_pack(nc, st, dram["l1"], w, "l1")
                layer_norm(nc, "ln1", g.x, g.xn, g.c("mean"), g.c("eps5"))
                wkv_attention(nc, g, w)
                gate(nc, g, "l1g", g.xn, L1.of(w, "gate"), L1.of(w, "gate_b"), 8, l1_weigh(nc, g), prob_t)
                linear_experts(nc, g, w, prob_t)
        if 2 in STAGES:
            layer_norm(nc, "ln2", g.x, g.xn, g.c("mean"), g.c("eps5"))
            if "a" in SUB:
                delta_attention(nc, g, dram)
            if "f" in SUB:
                with Stage(nc, "l2") as st:
                    w, prob_t = st.sb("w", [P, L2F.n]), st.sb("prob_t", [P, N])
                    h = st.sb("h", [P, N])
                    load_pack(nc, st, dram["l2f"], w, "l2f")
                    rms_norm(nc, "l2n1", g.xn, h, g.c("mean"), g.c("eps_rms"), L2F.of(w, "n1"))
                    causal_attention(nc, g, w, h)
                    rms_norm(nc, "l2n2", g.xn, h, g.c("mean"), g.c("eps_rms"), L2F.of(w, "n2"))
                    gate(nc, g, "l2g", h, L2F.of(w, "gate"), None, 4, l2_weigh(nc, g), prob_t)
                    mixed_experts(nc, g, w, h, prob_t)
        if 3 in STAGES:
            g.const3 = ctx.enter_context(nc.sbuf_tensor("const3", [P, CONST3.n], F32))
            with Stage(nc, "c3") as st:
                load_pack(nc, st, dram["const3"], g.const3, "const3")
            layer_norm(nc, "ln3", g.x, g.xn, g.c("mean"), g.c("eps5"))
            if "a" in SUB:
                with Stage(nc, "l3") as st:
                    w = st.sb("w", [P, L3A.n])
                    load_pack(nc, st, dram["l3a"], w, "l3a")
                    decay_attention(nc, g, w)
            if "f" in SUB:
                with Stage(nc, "l3deep") as st:
                    wa, wf = st.sb("wa", [P, L3W.n]), st.sb("wf", [P, L3F.n])
                    with nc.Fori(0, DEPTH) as layer:
                        with Stage(nc, "l3load") as ld:
                            load_pack(nc, ld, dram["l3w"][bass.ds(layer, 1)].rearrange("l p n -> (l p) n"), wa, "l3w")
                            load_pack(nc, ld, dram["l3f"][bass.ds(layer, 1)].rearrange("l p n -> (l p) n"), wf, "l3f")
                        window_attention(nc, g, wa, layer)
                        gated_mlp(nc, g, wf, layer)
                    done = st.sem("done")
                    with nc.Block() as blk:
                        @blk.vector
                        def _(dve):
                            nc.vector.tensor_tensor(g.x[:], g.x[:], g.xn[:], ALU.add).then_inc(done, 1)
        stored = ctx.enter_context(nc.semaphore("stored"))
        with nc.Block() as blk:
            @blk.sync
            def _(sp):
                sp.dma_start(out, g.x[:]).then_inc(stored, 16)
                sp.wait_ge(stored, 16)


STAGES = (0, 1, 2, 3)
SUB = "af"


def fill(pack, pieces):
    a = np.zeros((P, pack.n), np.float32)
    for name, (at, rows, cols) in pack.at.items():
        piece = np.asarray(pieces[name], np.float32)
        assert piece.shape == (rows, cols), (name, piece.shape, rows, cols)
        a[:rows, at:at + cols] = piece
    return a


def pad_rows(a):
    return np.concatenate([a, np.zeros((P - a.shape[0], a.shape[1]), a.dtype)], 0)


def col(v):
    return np.asarray(v).reshape(-1, 1)


def row(v):
    return np.asarray(v).reshape(1, -1)


def host_layout(i):
    i = {k: np.asarray(v) for k, v in i.items()}
    packs = {"x": np.ascontiguousarray(i["L0_attn_query"].reshape(N, D).T), "const": fill(CONST, constants()), "const3": fill(CONST3, constants())}
    a = "L0_attn_"
    packs["l0"] = fill(L0, {
        "wq": i[a + "Wq"].T, "wkv": np.concatenate([i[a + "Wk"].T, i[a + "Wv"].T], 1), "wo": i[a + "Wo"].T,
        "bq": col(i[a + "bq"]), "bo": col(i[a + "bo"]), "bkv": row(np.concatenate([i[a + "bk"], i[a + "bv"]])),
        "gate": i["L0_ffn_gate_w"].T,
        "w12": i["L0_ffn_w12"].transpose(2, 0, 1).reshape(D, -1),
        "w3": i["L0_ffn_w3"].reshape(8, D, 2, P).transpose(3, 0, 2, 1).reshape(P, -1)})
    a, f = "L1_attn_", "L1_ffn_"
    packs["l1"] = fill(L1, {
        "wk": i[a + "Wk"].T, "wv": i[a + "Wv"].T, "wr": i[a + "Wr"].T, "wo": i[a + "Wo"].T,
        **{n: col(i[a + n]) for n in ("bo", "u", "w", "tmk", "tmv", "tmr")},
        "gate": i[f + "gate_W"], "gate_b": row(i[f + "gate_b"]),
        "ew": i[f + "expert_W"].transpose(1, 0, 2).reshape(D, -1), "eb": pad_rows(i[f + "expert_b"])})
    a = "L2_attn_"
    by_pair = lambda wo: wo.reshape(PAIRS, P, D).transpose(1, 0, 2).reshape(P, -1)
    n = np.arange(P)
    b_, t_ = n // CH, n % CH
    same = b_[:, None] == b_[None]
    row_t, col_t = t_[:, None], t_[None]
    upto, before = same & (row_t <= col_t), same & (row_t < col_t)
    after = same & (row_t > col_t)
    first = same & (row_t < CH // 2)
    ends = np.stack([(b_[:, None] == np.arange(GB)) & (row_t < CH // 2), (b_[:, None] == np.arange(GB)) & (row_t >= CH // 2)], -1)
    packs["l2a"] = fill(L2A, {
        **{n_: i[a + "W" + n_[1:]].T for n_ in ("wk", "wq", "wv", "wa")}, "war": i[a + "WaR"].T,
        "wbg": np.concatenate([i[a + "Wb"].T, i[a + "Wg"].T], 1), "wo": by_pair(i[a + "Wo"].T),
        "lnw": col(i[a + "ln_w"]), "lnb": col(i[a + "ln_b"]), "ba": row(i[a + "ba"]), "bar": row(i[a + "baR"]),
        "bbg": row(np.concatenate([i[a + "bb"], i[a + "bg"]])),
        "cum": first.astype(np.float32) - upto, "ends": ends.reshape(P, 8),
        "keep": np.concatenate([before, upto, before, after], 1), "keep_r": np.concatenate([before, upto, after], 1)})
    f = "L2_ffn_"

    def spread32(wt):
        out = np.zeros((D, HEADS, 32), np.float32)
        out[:, :, :8] = wt.reshape(D, HEADS, 8)
        return out.reshape(D, -1)

    def head_col(v):
        out = np.zeros((4, 32), np.float32)
        out[:, :8] = v
        return out.reshape(P, 1)

    up = lambda n: i[f + n].T
    tall = lambda n: i[f + n].T.reshape(2, P, -1).transpose(1, 0, 2).reshape(P, -1)
    packs["l2f"] = fill(L2F, {
        "n1": col(i[f + "n1_w"]), "n2": col(i[f + "n2_w"]), "wq": spread32(up("wq")), "wk": spread32(up("wk")), "wv": up("wv"),
        "qn": head_col(i[f + "qn_w"]), "kn": head_col(i[f + "kn_w"]),
        "wo": spread32(i[f + "wo"]).T.reshape(4, P, D).transpose(1, 0, 2).reshape(P, -1), "gate": up("gate_w"),
        "e0u": up("e0_up"), "e0d": tall("e0_down"), "e1a": up("e1_w1"), "e1b": up("e1_w2"), "e1d": tall("e1_down"),
        "e2a": up("e2_l1"), "e2b": tall("e2_l2"), "e2c": tall("e2_l3"), "e2d": tall("e2_l4"),
        "e3a": up("e3_down"), "e3b": up("e3_up"), "e3d": tall("e3_out")})
    a = "L3_attn_"
    by_pair = lambda wo: wo.reshape(PAIRS, P, D).transpose(1, 0, 2).reshape(P, -1)
    packs["l3a"] = fill(L3A, {
        **{n: i[a + "W" + n[1:]] for n in ("wq", "wk", "wv", "wf", "wg", "wb")}, "wo": by_pair(i[a + "Wo"]),
        "dt": row(i[a + "dt_bias"]), "bg": row(i[a + "bg"]), "a_log": np.tile(row(i[a + "A_log"]), (P, 1)),
        "norm_w": col(np.tile(i[a + "norm_w"], 2))})
    a = "L3_ffn_"
    swap = np.arange(INNER).reshape(HEADS, 2, HD // 2)[:, ::-1].reshape(-1)
    deep_w, deep_f = [], []
    for l in range(DEPTH):
        wq, wk, wv = np.split(i[a + "Wqkv"][l], 3, -1)
        qs, ks = (np.tile(i[a + s][l], 2) for s in ("q_scale", "k_scale"))
        deep_w.append(fill(L3W, {
            "wq": wq, "wqr": wq[:, swap], "wk": wk, "wkr": wk[:, swap], "wv": wv, "wo": by_pair(i[a + "Wo"][l]),
            "qs": np.stack([qs, qs[swap[:P]]], 1), "ks": np.stack([ks, ks[swap[:P]]], 1)}))
        w1 = np.zeros((D, 2, 3 * P), np.float32)
        w1[:, :, :HALF] = i[a + "W1"][l].reshape(D, 2, HALF)
        b1 = np.zeros((2, 3 * P), np.float32)
        b1[:, :HALF] = i[a + "b1"][l].reshape(2, HALF)
        w2 = np.zeros((3 * P, D), np.float32)
        w2[:HALF] = i[a + "W2"][l]
        deep_f.append(fill(L3F, {
            "w1": w1.reshape(D, -1), "b1": b1.reshape(6, P).T, "w2": w2.reshape(3, P, D).transpose(1, 0, 2).reshape(P, -1),
            "b2": col(i[a + "b2"][l]), "g": col(i[a + "ln_g"][l]), "b": col(i[a + "ln_b"][l])}))
    packs["l3w"], packs["l3f"] = np.stack(deep_w), np.stack(deep_f)
    return packs


def kernel(**inputs):
    import concourse.bacc as _bacc
    from concourse.bass_utils import run_bass_kernel_spmd as _run

    arrays = {k + "_dram": v for k, v in host_layout(inputs).items()}
    nc = _bacc.Bacc("TRN2", target_bir_lowering=False, num_devices=1)
    dram = {k[:-5]: nc.dram_tensor(k, v.shape, F32, kind="ExternalInput").ap() for k, v in arrays.items()}
    out = nc.dram_tensor("out_dram", (P, N), F32, kind="ExternalOutput").ap()
    program(nc, dram, out)
    r = _run(nc, [arrays], core_ids=[0])
    return np.ascontiguousarray(r.results[0]["out_dram"].T).reshape(B, T, D)
```

```python
from contextlib import ExitStack

import concourse.bass as bass
from concourse import mybir
import numpy as np

F32 = mybir.dt.float32
U32 = mybir.dt.uint32
ALU = mybir.AluOpType
ACT = mybir.ActivationFunctionType
AX = mybir.AxisListType.X

P = 128
B, T, D = 16, 256, 128
N = B * T
BLK = 512
NBLK = N // BLK
TILES = N // P
HEADS = 16
NEG = -1.0e30
HD = 64
INNER = HEADS * HD
PAIRS = HEADS // 2


class Stage:

    def __init__(self, nc, name):
        self.nc, self.name, self.ctx = nc, name, ExitStack()
        self.sems = []

    def __enter__(self):
        return self

    def __exit__(self, *e):
        if e[0] is None:
            with self.nc.Block() as block:
                @block.sync
                def _(sp):
                    for s in self.sems:
                        self.nc.sync.sem_clear(s)
        return self.ctx.__exit__(*e)

    def sb(self, name, shape, dt=F32):
        return self.ctx.enter_context(self.nc.sbuf_tensor(f"{self.name}_{name}", shape, dt))

    def ps(self, name, shape, dt=F32):
        return self.ctx.enter_context(self.nc.psum_tensor(f"{self.name}_{name}", shape, dt))

    def sem(self, name):
        s = self.ctx.enter_context(self.nc.semaphore(f"{self.name}_{name}"))
        self.sems.append(s)
        return s


class Chain:

    def __init__(self, eng, sem, per_turn=0, turn=0):
        self.eng, self.sem, self.per_turn, self.turn, self.n = eng, sem, per_turn, turn, 0

    def link(self, ins):
        ins.then_inc(self.sem, 1)
        self.n += 1
        self.eng.wait_ge(self.sem, self.turn * self.per_turn + self.n)

    def close(self):
        assert self.n == self.per_turn, (self.n, self.per_turn)


def wait_for(eng, sem, count):
    if not isinstance(count, int) or count > 0:
        eng.wait_ge(sem, count)


def block(i):
    return bass.ds(i * BLK, BLK)


def bcast(ap, shape):
    return ap.to_broadcast(shape)


class Pack:

    def __init__(self):
        self.at, self.n, self.rows = {}, 0, {}

    def add(self, name, rows, cols):
        self.at[name] = (self.n, rows, cols)
        self.n += cols

    def of(self, tile, name):
        a, rows, cols = self.at[name]
        return tile[0:rows, a:a + cols]


def layout(pieces):
    p = Pack()
    for name, rows, cols in pieces:
        p.add(name, rows, cols)
    return p


def load_pack(nc, st, dram, tile, name):
    landed = st.sem(name + "_landed")
    with nc.Block() as blk:
        @blk.sync
        def _(sp):
            sp.dma_start(tile[:], dram).then_inc(landed, 16)
            sp.wait_ge(landed, 16)


def layer_norm(nc, name, src, dst, mean_w, eps_col, gain=None, shift=None):
    with Stage(nc, name) as st:
        sq = st.sb("sq", [P, N])
        mean_ps = st.ps("mean", [P, 2, BLK])
        var_ps = st.ps("var", [P, 2, BLK])
        std = st.sb("std", [P, 2, BLK])
        mean_ready, centered, squared = st.sem("mean_ready"), st.sem("centered"), st.sem("squared")
        var_ready, std_ready, normed = st.sem("var_ready"), st.sem("std_ready"), st.sem("normed")
        dve_step = st.sem("dve_step")
        extra = 1 if gain is not None else 0

        with nc.Block() as blk:
            @blk.tensor
            def _(pe):
                with pe.Fori(0, NBLK // 2) as i:
                    for k in range(2):
                        pe.wait_ge(centered, 2 * i + k + 1)
                        nc.tensor.matmul(mean_ps[:, k, :], mean_w, src[:, block(2 * i + k)],
                                         start=True, stop=True).then_inc(mean_ready, 1)
                with pe.Fori(0, NBLK // 2) as i:
                    for k in range(2):
                        pe.wait_ge(squared, 2 * i + k + 1)
                        pe.wait_ge(std_ready, 2 * i + k + 1)
                        nc.tensor.matmul(var_ps[:, k, :], mean_w, sq[:, block(2 * i + k)],
                                         start=True, stop=True).then_inc(var_ready, 1)

            @blk.vector
            def _(dve):
                nc.vector.sem_inc(centered, 2)
                with dve.Fori(0, NBLK // 2) as i:
                    for k in range(2):
                        dve.wait_ge(mean_ready, 2 * i + k + 1)
                        nc.vector.tensor_tensor(dst[:, block(2 * i + k)], src[:, block(2 * i + k)],
                                                mean_ps[:, k, :], ALU.subtract).then_inc(centered, 1)
                nc.vector.sem_inc(normed, 2)
                with dve.Fori(0, NBLK // 2) as i:
                    c = Chain(dve, dve_step, 2 + 2 * extra, i)
                    for k in range(2):
                        dve.wait_ge(std_ready, 2 * i + k + 3)
                        c.link(nc.vector.reciprocal(std[:, k, :], std[:, k, :]))
                        cols = dst[:, block(2 * i + k)]
                        if gain is None:
                            nc.vector.tensor_tensor(cols, cols, std[:, k, :], ALU.mult).then_inc(normed, 1)
                        else:
                            c.link(nc.vector.tensor_tensor(cols, cols, std[:, k, :], ALU.mult))
                            nc.vector.tensor_scalar(cols, cols, gain, shift, ALU.mult, ALU.add).then_inc(normed, 1)
                    c.close()

            @blk.scalar
            def _(act):
                with act.Fori(0, NBLK // 2) as i:
                    for k in range(2):
                        act.wait_ge(centered, 2 * i + k + 3)
                        nc.scalar.activation(sq[:, block(2 * i + k)], dst[:, block(2 * i + k)],
                                             ACT.Square).then_inc(squared, 1)
                nc.scalar.sem_inc(std_ready, 2)
                with act.Fori(0, NBLK // 2) as i:
                    for k in range(2):
                        act.wait_ge(var_ready, 2 * i + k + 1)
                        act.wait_ge(normed, 2 * i + k + 1)
                        nc.scalar.activation(std[:, k, :], var_ps[:, k, :], ACT.Sqrt,
                                             bias=eps_col).then_inc(std_ready, 1)


L0 = layout([("wq", P, D), ("wkv", P, 2 * D), ("wo", P, D), ("bq", P, 1), ("bo", P, 1), ("bkv", P, 2 * D),
             ("gate", P, 8), ("w12", P, 8 * 512), ("w3", P, 8 * 2 * D)])


def linear_attention(nc, g, w):
    W = lambda n: L0.of(w, n)
    with Stage(nc, "l0a") as st:
        xb = st.sb("xb", [P, T])
        kv = st.sb("kv", [P, 2, 2 * D + 2])
        neg, pos = st.sb("neg", [P, 2, D]), st.sb("pos", [P, 2, D])
        qneg, phiq = st.sb("qneg", [P, T]), st.sb("phiq", [P, T])
        qpos = st.sb("qpos", [P, T])
        sm, zm = st.sb("sm", [P, D]), st.sb("zm", [P, D])
        rden, ctx = st.sb("rden", [P, T]), st.sb("ctx", [P, T])
        kv_ps = st.ps("kv_ps", [P, 2, 2 * D])
        q_ps, s_ps = st.ps("q_ps", [P, T]), st.ps("s_ps", [P, D + 1])
        num_ps, den_ps, o_ps = st.ps("num_ps", [P, T]), st.ps("den_ps", [P, T]), st.ps("o_ps", [P, T])
        ones_set, xb_ready, qkv_ready, min_ready = (st.sem(n) for n in ("ones_set", "xb_ready", "qkv_ready", "min_ready"))
        exp_ready, phi_ready, s_ready, masked = (st.sem(n) for n in ("exp_ready", "phi_ready", "s_ready", "masked"))
        numden_ready, ctx_ready, o_ready, added, dve_step = (
            st.sem(n) for n in ("numden_ready", "ctx_ready", "o_ready", "added", "dve_step"))

        with nc.Block() as blk:
            @blk.tensor
            def _(pe):
                with pe.Fori(0, B) as b:
                    pe.wait_ge(xb_ready, b + 1)
                    nc.tensor.matmul(q_ps[:], W("wq"), xb[:], start=True, stop=True)
                    for t in range(2):
                        nc.tensor.matmul(kv_ps[:, t, :], xb[:, t * P:(t + 1) * P], W("wkv"), start=True, stop=False)
                        mm = nc.tensor.matmul(kv_ps[:, t, :], g.ones_row, W("bkv"), start=False, stop=True)
                    mm.then_inc(qkv_ready, 1)
                    pe.wait_ge(phi_ready, b + 1)
                    for t in range(2):
                        mm = nc.tensor.matmul(s_ps[:], kv[:, t, 0:D], kv[:, t, D:2 * D + 1], start=(t == 0), stop=(t == 1))
                    mm.then_inc(s_ready, 1)
                    pe.wait_ge(masked, b + 1)
                    nc.tensor.matmul(num_ps[:], sm[:], phiq[:], start=True, stop=True)
                    nc.tensor.matmul(den_ps[:], zm[:], phiq[:], start=True, stop=True).then_inc(numden_ready, 1)
                    pe.wait_ge(ctx_ready, b + 1)
                    nc.tensor.matmul(o_ps[:], W("wo"), ctx[:], start=True, stop=True).then_inc(o_ready, 1)

            @blk.scalar
            def _(act):
                with act.Fori(0, B) as b:
                    act.wait_ge(added, b + 1)
                    nc.scalar.activation(xb[:], g.xn[:, bass.ds(b * T, T)], ACT.Copy).then_inc(xb_ready, 1)
                    act.wait_ge(min_ready, b + 1)
                    nc.scalar.activation(qpos[:], q_ps[:], ACT.Relu, bias=W("bq"))
                    nc.scalar.activation(pos[:], kv_ps[:, :, 0:D], ACT.Relu)
                    nc.scalar.activation(kv[:, :, D:2 * D], kv_ps[:, :, D:2 * D], ACT.Copy)
                    nc.scalar.activation(qneg[:], qneg[:], ACT.Exp)
                    nc.scalar.activation(neg[:], neg[:], ACT.Exp).then_inc(exp_ready, 1)

            @blk.vector
            def _(dve):
                nc.vector.memset(kv[:, :, 2 * D:2 * D + 1], 1.0).then_inc(ones_set, 1)
                nc.vector.sem_inc(added, 1)
                dve.wait_ge(ones_set, 1)
                with dve.Fori(0, B) as b:
                    c = Chain(dve, dve_step, 3, b)
                    dve.wait_ge(qkv_ready, b + 1)
                    nc.vector.tensor_scalar(qneg[:], q_ps[:], W("bq"), 0.0, ALU.add, ALU.min)
                    nc.vector.tensor_scalar(neg[:], kv_ps[:, :, 0:D], 0.0, None, ALU.min).then_inc(min_ready, 1)
                    dve.wait_ge(exp_ready, b + 1)
                    nc.vector.tensor_tensor(phiq[:], qneg[:], qpos[:], ALU.add)
                    nc.vector.tensor_tensor(kv[:, :, 0:D], neg[:], pos[:], ALU.add).then_inc(phi_ready, 1)
                    dve.wait_ge(s_ready, b + 1)
                    nc.vector.tensor_tensor(sm[:], s_ps[:, 0:D], g.c("mask8"), ALU.mult)
                    nc.vector.tensor_scalar(zm[:], g.c("mask8"), s_ps[:, D:D + 1], None, ALU.mult).then_inc(masked, 1)
                    dve.wait_ge(numden_ready, b + 1)
                    c.link(nc.vector.tensor_scalar(rden[:], den_ps[:], 1e-6, None, ALU.add))
                    c.link(nc.vector.reciprocal(rden[:], rden[:]))
                    nc.vector.tensor_tensor(ctx[:], rden[:], num_ps[:], ALU.mult).then_inc(ctx_ready, 1)
                    dve.wait_ge(o_ready, b + 1)
                    xs = g.x[:, bass.ds(b * T, T)]
                    c.link(nc.vector.scalar_tensor_tensor(out=xs, in0=o_ps[:], scalar=W("bo"), in1=xs,
                                                          op0=ALU.add, op1=ALU.add))
                    nc.vector.sem_inc(added, 1)
                    c.close()


def top2(nc, g, c, s, mask, E, tmp_gt, tmp_eq, rank):
    sh = [P, TILES, E, E]
    sj, se = s.unsqueeze(2).to_broadcast(sh), s.unsqueeze(3).to_broadcast(sh)
    before = g.c("before%d" % E).rearrange("p (a e) -> p a e", a=1).to_broadcast([P, TILES, E * E])
    flat = "p t e j -> p t (e j)"
    c.link(nc.vector.tensor_tensor(tmp_gt[:], sj, se, ALU.is_gt))
    c.link(nc.vector.tensor_tensor(tmp_eq[:], sj, se, ALU.is_equal))
    c.link(nc.vector.tensor_tensor(tmp_eq[:].rearrange(flat), tmp_eq[:].rearrange(flat), before, ALU.mult))
    c.link(nc.vector.tensor_tensor(tmp_gt[:], tmp_gt[:], tmp_eq[:], ALU.add))
    c.link(nc.vector.tensor_reduce(rank[:], tmp_gt[:], AX, ALU.add))
    c.link(nc.vector.tensor_scalar(mask[:], rank[:], 1.5, None, ALU.is_lt))


TOP2_LINKS = 6


def gate(nc, g, name, act_t, wgate, bias_row, E, weigh, prob_t):
    with Stage(nc, name) as st:
        s_ps = st.ps("s_ps", [P, TILES, E])
        s, mask = st.sb("s", [P, TILES, E]), st.sb("mask", [P, TILES, E])
        prob = st.sb("prob", [P, TILES, E])
        t_gt, t_eq = st.sb("t_gt", [P, TILES, E, E]), st.sb("t_eq", [P, TILES, E, E])
        rank, one = st.sb("rank", [P, TILES, E]), st.sb("one", [P, TILES, 1])
        p_ps = st.ps("p_ps", [E, 4, BLK])
        scores_ready, exp_in, exp_out = st.sem("scores_ready"), st.sem("exp_in"), st.sem("exp_out")
        prob_ready, turned, moved, dve_step = st.sem("prob_ready"), st.sem("turned"), st.sem("moved"), st.sem("dve_step")
        with nc.Block() as blk:
            @blk.tensor
            def _(pe):
                for t in range(TILES):
                    mm = nc.tensor.matmul(s_ps[:, t, :], act_t[:, t * P:(t + 1) * P], wgate, start=True,
                                          stop=bias_row is None)
                    if bias_row is not None:
                        mm = nc.tensor.matmul(s_ps[:, t, :], g.ones_row, bias_row, start=False, stop=True)
                mm.then_inc(scores_ready, 1)
                pe.wait_ge(prob_ready, 1)
                for t in range(TILES):
                    if t == 16:
                        pe.wait_ge(moved, 1)
                    mm = nc.tensor.transpose(p_ps[:, t // 4 % 4, (t % 4) * P:(t % 4 + 1) * P], prob[:, t, :], g.c("ident"))
                    if t % 16 == 15:
                        mm.then_inc(turned, 1)

            @blk.scalar
            def _(act):
                act.wait_ge(exp_in, 1)
                nc.scalar.activation(s[:], s[:], ACT.Exp).then_inc(exp_out, 1)

            @blk.vector
            def _(dve):
                c = Chain(dve, dve_step)
                c.link(nc.vector.memset(prob_t[:], 0.0))
                dve.wait_ge(scores_ready, 1)
                weigh(dve, c, s_ps, s, mask, prob, t_gt, t_eq, rank, one, exp_in, exp_out)
                nc.vector.sem_inc(prob_ready, 1)
                for half in range(2):
                    dve.wait_ge(turned, half + 1)
                    nc.vector.tensor_copy(prob_t[0:E, half * 2048:(half + 1) * 2048].rearrange("p (a n) -> p a n", a=4),
                                          p_ps[:]).then_inc(moved, 1)


def l0_weigh(nc, g):
    def weigh(dve, c, s_ps, s, mask, prob, t_gt, t_eq, rank, one, exp_in, exp_out):
        sh = [P, TILES, 8]
        c.link(nc.vector.tensor_copy(s[:], s_ps[:]))
        top2(nc, g, c, s[:], mask, 8, t_gt, t_eq, rank)
        c.link(nc.vector.tensor_reduce(one[:], s[:].unsqueeze(2), AX, ALU.max))
        c.link(nc.vector.tensor_tensor(s[:], s[:], one[:].to_broadcast(sh), ALU.subtract))
        nc.vector.sem_inc(exp_in, 1)
        dve.wait_ge(exp_out, 1)
        c.link(nc.vector.tensor_tensor(prob[:], s[:], mask[:], ALU.mult))
        c.link(nc.vector.tensor_reduce(one[:], prob[:].unsqueeze(2), AX, ALU.add))
        c.link(nc.vector.reciprocal(one[:], one[:]))
        c.link(nc.vector.tensor_tensor(prob[:], prob[:], one[:].to_broadcast(sh), ALU.mult))
    return weigh


def swiglu_experts(nc, g, w, prob_t):
    W12 = L0.of(w, "w12").rearrange("p (e h c n) -> p e h c n", e=8, h=2, c=2)
    W3 = L0.of(w, "w3").rearrange("p (e c n) -> p e c n", e=8, c=2)
    UNITS = 16
    with Stage(nc, "l0f") as st:
        h_ps = st.ps("h_ps", [P, 2, 2, BLK])
        pr_ps = st.ps("pr_ps", [P, 2, BLK])
        o_ps = st.ps("o_ps", [P, BLK])
        sil, hid = st.sb("sil", [P, 2, BLK]), st.sb("hid", [P, 2, BLK])
        tmp = st.sb("tmp", [P, 2, BLK])
        up_ready, silu_ready, hid_ready = (st.sem(n) for n in ("up_ready", "silu_ready", "hid_ready"))
        out_used, hid_used, dve_step = st.sem("out_used"), st.sem("hid_used"), st.sem("dve_step")
        with nc.Block() as blk:
            @blk.tensor
            def _(pe):
                nc.tensor.sem_inc(hid_used, 2)
                with pe.Fori(0, NBLK) as i:
                    xs = g.xn[:, block(i)]

                    def up(u):
                        e, c = divmod(u, 2)
                        pe.wait_ge(hid_ready, i * UNITS + u + 1)
                        if c == 0:
                            nc.tensor.matmul(pr_ps[:, e % 2, :], g.c("pick8").rearrange("k (e m) -> k e m", e=8)[:, e, :],
                                             prob_t[:, block(i)], start=True, stop=True)
                        nc.tensor.matmul(h_ps[:, u % 2, 0, :], W12[:, e, 0, c, :], xs, start=True, stop=True)
                        nc.tensor.matmul(h_ps[:, u % 2, 1, :], W12[:, e, 1, c, :], xs, start=True, stop=True).then_inc(up_ready, 1)

                    up(0)
                    pe.wait_ge(out_used, i + 1)
                    for u in range(UNITS):
                        if u + 1 < UNITS:
                            up(u + 1)
                        pe.wait_ge(hid_ready, i * UNITS + u + 3)
                        mm = nc.tensor.matmul(o_ps[:], W3[:, u // 2, u % 2, :], hid[:, u % 2, :],
                                              start=(u == 0), stop=(u == UNITS - 1))
                        mm.then_inc(hid_used, 1)

            @blk.scalar
            def _(act):
                with act.Fori(0, NBLK) as i:
                    for u in range(UNITS):
                        act.wait_ge(up_ready, i * UNITS + u + 1)
                        act.wait_ge(hid_ready, i * UNITS + u + 1)
                        nc.scalar.activation(sil[:, u % 2, :], h_ps[:, u % 2, 0, :], ACT.Silu).then_inc(silu_ready, 1)

            @blk.vector
            def _(dve):
                nc.vector.sem_inc(hid_ready, 2)
                nc.vector.sem_inc(out_used, 1)
                with dve.Fori(0, NBLK) as i:
                    c = Chain(dve, dve_step, UNITS + 1, i)
                    for u in range(UNITS):
                        dve.wait_ge(silu_ready, i * UNITS + u + 1)
                        c.link(nc.vector.tensor_tensor(tmp[:, u % 2, :], sil[:, u % 2, :], h_ps[:, u % 2, 1, :], ALU.mult))
                        dve.wait_ge(hid_used, i * UNITS + u + 1)
                        nc.vector.tensor_tensor(hid[:, u % 2, :], tmp[:, u % 2, :], pr_ps[:, u // 2 % 2, :],
                                                ALU.mult).then_inc(hid_ready, 1)
                    dve.wait_ge(hid_used, i * UNITS + UNITS + 2)
                    c.link(nc.vector.tensor_tensor(g.x[:, block(i)], g.x[:, block(i)], o_ps[:], ALU.add))
                    nc.vector.sem_inc(out_used, 1)
                    c.close()


L1 = layout([("wk", P, D), ("wv", P, D), ("wr", P, D), ("wo", P, D), ("bo", P, 1), ("u", P, 1), ("w", P, 1),
             ("tmk", P, 1), ("tmv", P, 1), ("tmr", P, 1), ("gate", P, 8), ("gate_b", P, 8),
             ("ew", P, 8 * D), ("eb", P, D)])


def wkv_attention(nc, g, w):
    W = lambda n: L1.of(w, n)
    with Stage(nc, "l1a") as st:
        xs, om = st.sb("xs", [P, T]), st.sb("om", [P, 3])
        mix = st.sb("mix", [P, 3, T])
        mixs = st.sb("mixs", [P, 3, T])
        kvr_ps, o_ps = st.ps("kvr_ps", [P, 3, BLK]), st.ps("o_ps", [P, T])
        kk, q, e1, e2 = (st.sb(n, [P, T]) for n in ("kk", "q", "e1", "e2"))
        e1x, e2x, ev = (st.sb(n, [P, T]) for n in ("e1x", "e2x", "ev"))
        a, b_, wr = (st.sb(n, [P, T]) for n in ("a", "b", "wr"))
        mixed, sig_done, kvr_ready, args_ready, exps_ready, wr_ready, o_ready, dve_step = (
            st.sem(n) for n in ("mixed", "sig_done", "kvr_ready", "args_ready", "exps_ready", "wr_ready", "o_ready", "dve_step"))
        with nc.Block() as blk:
            @blk.tensor
            def _(pe):
                with pe.Fori(0, B) as i:
                    pe.wait_ge(mixed, i + 1)
                    pe.wait_ge(sig_done, i + 1)
                    for n, wn in enumerate(("wk", "wv", "wr")):
                        mm = nc.tensor.matmul(kvr_ps[:, n, 0:T], W(wn), mixs[:, n, :] if n == 2 else mix[:, n, :],
                                              start=True, stop=True)
                    mm.then_inc(kvr_ready, 1)
                    pe.wait_ge(wr_ready, i + 1)
                    nc.tensor.matmul(o_ps[:], W("wo"), wr[:], start=True, stop=True).then_inc(o_ready, 1)

            @blk.scalar
            def _(act):
                with act.Fori(0, B) as i:
                    act.wait_ge(mixed, i + 1)
                    nc.scalar.activation(mixs[:, 2, :], mix[:, 2, :], ACT.Sigmoid).then_inc(sig_done, 1)
                    act.wait_ge(args_ready, i + 1)
                    nc.scalar.activation(e1[:], e1x[:], ACT.Exp)
                    nc.scalar.activation(e2[:], e2x[:], ACT.Exp).then_inc(exps_ready, 1)

            @blk.vector
            def _(dve):
                for n, t in enumerate(("tmk", "tmv", "tmr")):
                    nc.vector.tensor_scalar(om[:, n:n + 1], W(t), -1.0, 1.0, ALU.mult, ALU.add)
                nc.vector.memset(xs[:, 0:1], 0.0)
                nc.vector.drain()
                with dve.Fori(0, B) as i:
                    c = Chain(dve, dve_step, 13, i)
                    c.link(nc.vector.tensor_copy(xs[:, 1:T], g.xn[:, bass.ds(i * T, T - 1)]))
                    for n in range(3):
                        c.link(nc.vector.tensor_scalar(mix[:, n, :], xs[:], om[:, n:n + 1], None, ALU.mult))
                    for n, t in enumerate(("tmk", "tmv", "tmr")):
                        ins = nc.vector.scalar_tensor_tensor(out=mix[:, n, :], in0=g.xn[:, bass.ds(i * T, T)], scalar=W(t),
                                                             in1=mix[:, n, :], op0=ALU.mult, op1=ALU.add)
                    ins.then_inc(mixed, 1)
                    dve.wait_ge(kvr_ready, i + 1)
                    c.link(nc.vector.tensor_scalar(kk[:], kvr_ps[:, 0, 0:T], W("u"), None, ALU.add))
                    c.link(nc.vector.tensor_scalar(q[:], kk[:], W("w"), None, ALU.max))
                    nc.vector.tensor_scalar(e1x[:], q[:], -1.0, W("w"), ALU.mult, ALU.subtract)
                    nc.vector.tensor_tensor(e2x[:], kk[:], q[:], ALU.subtract).then_inc(args_ready, 1)
                    dve.wait_ge(exps_ready, i + 1)
                    c.link(nc.vector.tensor_tensor(ev[:], e2[:], kvr_ps[:, 1, 0:T], ALU.mult))
                    c.link(nc.vector.tensor_tensor_scan(a[:], e1[:], ev[:], 0.0, ALU.mult, ALU.add))
                    c.link(nc.vector.tensor_tensor_scan(b_[:], e1[:], e2[:], 0.0, ALU.mult, ALU.add))
                    c.link(nc.vector.reciprocal(b_[:], b_[:]))
                    c.link(nc.vector.tensor_tensor(a[:], a[:], b_[:], ALU.mult))
                    c.link(nc.vector.tensor_tensor(wr[:], a[:], kvr_ps[:, 2, 0:T], ALU.mult))
                    nc.vector.sem_inc(wr_ready, 1)
                    dve.wait_ge(o_ready, i + 1)
                    xc = g.x[:, bass.ds(i * T, T)]
                    c.link(nc.vector.scalar_tensor_tensor(out=xc, in0=o_ps[:], scalar=W("bo"), in1=xc,
                                                          op0=ALU.add, op1=ALU.add))
                    c.close()


def l1_weigh(nc, g):
    def weigh(dve, c, s_ps, s, mask, prob, t_gt, t_eq, rank, one, exp_in, exp_out):
        sh = [P, TILES, 8]
        c.link(nc.vector.tensor_scalar(s[:], s_ps[:], 1e-4, None, ALU.max))
        c.link(nc.vector.tensor_reduce(one[:], s[:].unsqueeze(2), AX, ALU.max))
        c.link(nc.vector.tensor_tensor(s[:], s[:], one[:].to_broadcast(sh), ALU.subtract))
        nc.vector.sem_inc(exp_in, 1)
        dve.wait_ge(exp_out, 1)
        c.link(nc.vector.tensor_reduce(one[:], s[:].unsqueeze(2), AX, ALU.add))
        c.link(nc.vector.reciprocal(one[:], one[:]))
        c.link(nc.vector.tensor_tensor(s[:], s[:], one[:].to_broadcast(sh), ALU.mult))
        top2(nc, g, c, s[:], mask, 8, t_gt, t_eq, rank)
        c.link(nc.vector.tensor_scalar(prob[:], s[:], 0.1, None, ALU.max))
        c.link(nc.vector.tensor_tensor(prob[:], prob[:], mask[:], ALU.mult))
        c.link(nc.vector.tensor_reduce(one[:], prob[:].unsqueeze(2), AX, ALU.add))
        c.link(nc.vector.reciprocal(one[:], one[:]))
        c.link(nc.vector.tensor_scalar(one[:], one[:], 0.5, None, ALU.mult))
        c.link(nc.vector.tensor_tensor(prob[:], prob[:], one[:].to_broadcast(sh), ALU.mult))
    return weigh


def linear_experts(nc, g, w, prob_t):
    EW = L1.of(w, "ew").rearrange("p (e n) -> p e n", e=8)
    with Stage(nc, "l1f") as st:
        pr_ps, o_ps = st.ps("pr_ps", [P, 2, BLK]), st.ps("o_ps", [P, BLK])
        xc = st.sb("xc", [P, 2, BLK])
        comb_ready, scaled, used, out_used, dve_step = (
            st.sem(n) for n in ("comb_ready", "scaled", "used", "out_used", "dve_step"))
        with nc.Block() as blk:
            @blk.tensor
            def _(pe):
                nc.tensor.sem_inc(used, 2)
                with pe.Fori(0, NBLK) as i:
                    pb = prob_t[:, block(i)]

                    def spread(e):
                        pe.wait_ge(scaled, i * 8 + e + 1)
                        nc.tensor.matmul(pr_ps[:, e % 2, :], g.c("pick8").rearrange("k (e m) -> k e m", e=8)[:, e, :], pb,
                                         start=True, stop=True).then_inc(comb_ready, 1)

                    spread(0)
                    pe.wait_ge(out_used, i + 1)
                    nc.tensor.matmul(o_ps[:], L1.of(w, "eb"), pb, start=True, stop=False)
                    for e in range(8):
                        if e < 7:
                            spread(e + 1)
                        pe.wait_ge(scaled, i * 8 + e + 3)
                        nc.tensor.matmul(o_ps[:], EW[:, e, :], xc[:, e % 2, :], start=False, stop=(e == 7)).then_inc(used, 1)

            @blk.vector
            def _(dve):
                nc.vector.sem_inc(scaled, 2)
                nc.vector.sem_inc(out_used, 1)
                with dve.Fori(0, NBLK) as i:
                    c = Chain(dve, dve_step, 1, i)
                    for e in range(8):
                        dve.wait_ge(comb_ready, i * 8 + e + 1)
                        dve.wait_ge(used, i * 8 + e + 1)
                        nc.vector.tensor_tensor(xc[:, e % 2, :], g.xn[:, block(i)], pr_ps[:, e % 2, :],
                                                ALU.mult).then_inc(scaled, 1)
                    dve.wait_ge(used, i * 8 + 8 + 2)
                    c.link(nc.vector.tensor_tensor(g.x[:, block(i)], g.x[:, block(i)], o_ps[:], ALU.add))
                    nc.vector.sem_inc(out_used, 1)
                    c.close()


L2A = layout([("wk", P, INNER), ("wq", P, INNER), ("wv", P, INNER), ("wa", P, INNER), ("war", P, INNER),
              ("wbg", P, 2 * HEADS), ("wo", P, PAIRS * D), ("lnw", P, 1), ("lnb", P, 1),
              ("ba", P, INNER), ("bbg", P, 2 * HEADS),
              ("cum", P, P), ("ends", P, 8), ("keep", P, 4 * P), ("keep_r", P, 3 * P)])
CH = 32
GB = P // CH
NG, NCH = B // GB, T // CH


def delta_attention(nc, g, dram):
    kept, x_kept = (nc.dram_tensor(n, (P, N), F32).ap() for n in ("xn_kept", "x_kept"))
    I32 = mybir.dt.int32
    with Stage(nc, "l2d") as st:
        w = st.sb("w", [P, L2A.n])
        W = lambda n: L2A.of(w, n)
        load_pack(nc, st, dram["l2a"], w, "l2a")
        saved, summed_up = st.sem("saved"), st.sem("summed_up")
        with nc.Block() as blk:
            @blk.vector
            def _(dve):
                nc.vector.tensor_tensor(g.x[:], g.x[:], g.xn[:], ALU.add).then_inc(summed_up, 1)

            @blk.sync
            def _(sp):
                sp.dma_start(kept, g.xn[:]).then_inc(saved, 16)
                sp.wait_ge(saved, 16)
                sp.wait_ge(summed_up, 1)
                sp.dma_start(x_kept, g.x[:]).then_inc(saved, 16)
                sp.wait_ge(saved, 32)

        layer_norm(nc, "l2dn", g.xn, g.x, g.c("mean"), g.c("eps5"), W("lnw"), W("lnb"))
        by_batch_of = lambda ap, gi: ap.rearrange("p (g b c t) -> p g b c t", g=NG, b=GB, t=CH)[:, gi]
        by_tile_of = lambda ap, gi: ap.rearrange("p (g c b t) -> p g b c t", g=NG, b=GB, t=CH)[:, gi]
        with nc.Block() as blk:
            @blk.vector
            def _(dve):
                for gi in range(NG):
                    for bi in range(GB):
                        nc.vector.tensor_copy(by_tile_of(g.xn[:], gi)[:, bi], by_batch_of(g.x[:], gi)[:, bi])

        xt = st.sb("xt", [P, P])
        arena = st.sb("arena", [P, 9 * INNER])
        at = lambda n: arena[:, n * INNER:(n + 1) * INNER]
        kp, k0, qp, ez, ep, em = (at(n) for n in (0, 1, 2, 3, 5, 6))
        kn, q, sp_s, sp_r = (g.x[:, n * INNER:(n + 1) * INNER] for n in range(4))
        Y = arena[:, 0:4 * INNER].rearrange("p (f c n) -> p f c n", f=PAIRS, c=4)
        X, U, UR = at(4), at(5), at(6)
        OT = at(7).rearrange("p (f n) -> p f n", f=PAIRS)
        O = at(8)
        v = st.sb("v", [P, INNER])
        km, kmr = st.sb("km", [P, INNER]), st.sb("kmr", [P, INNER])
        TS = st.sb("TS", [P, PAIRS, 3, P])
        TR = st.sb("TR", [P, PAIRS, 2, P])
        KS, KR = st.sb("KS", [P, PAIRS, 2, P]), st.sb("KR", [P, PAIRS, 2, P])
        A, AR = st.sb("A", [P, HEADS, 2, P]), st.sb("AR", [P, HEADS, P])
        NL = st.sb("NL", [P, 2, 2, 4, P])
        SS, RR = st.sb("SS", [P, GB, PAIRS, HD]), st.sb("RR", [P, GB, PAIRS, HD])
        bgm, neg, bgm_next = (st.sb(n, [P, 2, HEADS]) for n in ("bgm", "neg", "bgm_next"))
        ss = st.sb("ss", [P, HEADS])
        er = st.sb("er", [P, 2, PAIRS, GB, 2])
        fac, last_ends = st.sb("fac", [P, 2, GB, PAIRS]), st.sb("last", [P, 2, GB, PAIRS])
        big = st.ps("big", [P, 8, BLK])
        wide = lambda a: big[:, a:a + 2, :].rearrange("p c n -> p (c n)")
        heads = lambda ap: ap.rearrange("p (h d) -> p h d", h=HEADS)
        by_head = lambda ap: ap.unsqueeze(2).to_broadcast([P, HEADS, HD])
        keep = W("keep").bitcast(I32).rearrange("p (m n) -> p m n", m=4)
        keep_r = W("keep_r").bitcast(I32).rearrange("p (m n) -> p m n", m=3)
        names = ("xt_ready", "early_ready", "early_used", "early_step", "proj_ready", "act_used", "dve_used", "squared", "summed", "root",
                 "kn_ready", "exp_done", "ln_ready", "e_ready", "ends_ready", "ends_used", "dve_made", "pool_made", "flipped", "flip_used",
                 "mats_ready", "masked", "y_start", "lev_ready", "nl_moved", "y_added", "scaled", "s1", "x_ready", "s2", "u_ready",
                 "s3", "r_ready", "s4", "xr_ready", "s5", "ur_ready", "s6", "o_ready", "s7", "s_added", "s8", "r_added",
                 "o_flipped", "ot_ready", "y_ready", "added", "dve_step", "zeroed", "pe_go", "dve_go")
        S = {n: st.sem(n) for n in names}
        split = lambda ap: ap.rearrange("p (f q d) -> p q f d", q=2, d=HD)
        even_odd = lambda a: big[:, a:a + 2, :].rearrange("p q (f d) -> p q f d", d=HD)
        time = lambda tile_, gi, ci: tile_.rearrange("p (b t) -> p b t", t=T)[:, bass.ds(gi * GB, GB), bass.ds(ci * CH, CH)]

        def tensor_early(pe, t, n):
            if n == 0:
                wait_for(pe, S["xt_ready"], t + 1)
            wait_for(pe, S["early_used"], 5 * t + n)
            if n == 0:
                nc.tensor.matmul(big[:, 6, 0:2 * HEADS], xt[:], W("wbg"), start=True, stop=False)
                mm = nc.tensor.matmul(big[:, 6, 0:2 * HEADS], g.ones_row, W("bbg"), start=False, stop=True)
            else:
                wn, bias = ((W("wk"), None), (W("wq"), None), (W("wa"), 0), (W("war"), 1))[n - 1]
                for c in range(2):
                    cols = slice(c * BLK, (c + 1) * BLK)
                    mm = nc.tensor.matmul(big[:, 6 + c, :], xt[:], wn[:, cols], start=True, stop=bias is None)
                    if bias is not None:
                        mm = nc.tensor.matmul(big[:, 6 + c, :], g.c("pick8")[:, bias * P:(bias + 1) * P], W("ba")[:, cols], start=False, stop=True)
            mm.then_inc(S["early_ready"], 1)

        def tensor_tile(pe, t, last=False):
            def early(n):
                if not last:
                    tensor_early(pe, t + 1, n)

            def wide_product(u, lhs, wn):
                for c in range(2):
                    out, cols = big[:, 2 * (u % 2) + c, :], slice(c * BLK, (c + 1) * BLK)
                    mm = nc.tensor.matmul(out, lhs, wn[:, cols], start=True, stop=True)
                mm.then_inc(S["proj_ready"], 1)

            def ends(s):
                for f in range(PAIRS):
                    for odd in range(2):
                        cols = slice(f * P + odd * HD, f * P + (odd + 1) * HD)
                        mm = nc.tensor.matmul(big[odd * HD:(odd + 1) * HD, 7, 64 * s + 8 * f:64 * s + 8 * f + 8], (sp_s, sp_r)[s][:, cols],
                                              W("ends"), start=True, stop=True)
                mm.then_inc(S["ends_ready"], 1)

            def flip(n, made, count, src):
                pe.wait_ge(S[made], count)
                pe.wait_ge(S["flip_used"], 7 * t + n + 1)
                for f in range(PAIRS):
                    mm = nc.tensor.transpose(big[:, 4 + f // 4, (f % 4) * P:(f % 4 + 1) * P], src[:, f * P:(f + 1) * P], g.c("ident"))
                mm.then_inc(S["flipped"], 1)

            pe.wait_ge(S["added"], t + 1)
            pe.wait_ge(S["xt_ready"], t + 1)
            wide_product(0, xt[:], W("wv"))
            pe.wait_ge(S["ln_ready"], 2 * t + 2)
            wide_product(1, W("cum"), sp_s)
            ends(0)
            ends(1)
            pe.wait_ge(S["act_used"], t + 1)
            wide_product(2, W("cum"), sp_r)
            flip(0, "dve_made", 3 * t + 1, k0)
            flip(1, "dve_made", 3 * t + 2, kp)
            flip(2, "pool_made", 4 * t + 1, km[:])
            flip(3, "pool_made", 4 * t + 2, qp)
            flip(4, "dve_made", 3 * t + 3, kp)
            flip(5, "pool_made", 4 * t + 3, kmr[:])
            flip(6, "pool_made", 4 * t + 4, qp)

            pe.wait_ge(S["flip_used"], 7 * t + 8)
            pe.wait_ge(S["ends_used"], 2 * t + 2)
            for p_ in range(PAIRS // 2):
                if p_:
                    pe.wait_ge(S["y_added"], 32 * t + 8 * p_)
                    pe.wait_ge(S["nl_moved"], 32 * t + 8 * p_)
                for wv in range(2):
                    f = 2 * p_ + wv
                    for par in range(2):
                        ks, kr = KS[:, f, par, :], KR[:, f, par, :]
                        a, b = big[:, 4 * wv + par, :], big[:, 4 * wv + 2 + par, :]
                        nc.tensor.matmul(a[:, 0:3 * P], ks, TS[:, f, 0:3, :], start=True, stop=True)
                        nc.tensor.matmul(a[:, 3 * P:4 * P], TS[:, f, 0, :], ks, start=True, stop=True)
                        nc.tensor.matmul(b[:, 0:2 * P], kr, TR[:, f, 0:2, :], start=True, stop=True)
                        mm = nc.tensor.matmul(b[:, 2 * P:3 * P], TR[:, f, 0, :], kr, start=True, stop=True)
                    mm.then_inc(S["mats_ready"], 1)
                pe.wait_ge(S["masked"], 8 * t + 2 * p_ + 2)
                for l in range(5):
                    for wv in range(2):
                        f = 2 * p_ + wv
                        if l >= 1:
                            pe.wait_ge(S["nl_moved"], 32 * t + 8 * p_ + 2 * (l - 1) + wv + 1)
                            if l == 1:
                                pe.wait_ge(S["y_start"], 8 * t + 2 * p_ + wv + 1)
                            else:
                                pe.wait_ge(S["y_added"], 32 * t + 8 * p_ + 2 * (l - 2) + wv + 1)
                        for ch in range(4):
                            Nm, Lm = NL[:, wv, 0, ch, :], NL[:, wv, 1, ch, :]
                            cols = slice(ch * P, (ch + 1) * P)
                            if l <= 2:
                                mm = nc.tensor.matmul(big[:, 3 * wv, cols], Lm, Nm, start=True, stop=True)
                            if l >= 1:
                                mm = nc.tensor.matmul(big[:, 3 * wv + 2, cols], Lm, Y[:, f, ch, :], start=True, stop=True)
                            if l <= 3:
                                mm = nc.tensor.matmul(big[:, 3 * wv + 1, cols], Nm, Lm, start=True, stop=True)
                        mm.then_inc(S["lev_ready"], 1)

            def by_batch(bank0, h, src, m, state, stop):
                f, par = divmod(h, 2)
                rows = slice(par * HD, (par + 1) * HD)
                for b in range(GB):
                    mm = nc.tensor.matmul(big[32 * b:32 * b + 32, bank0 + par, f * HD:(f + 1) * HD], src[rows, f, m, 32 * b:32 * b + 32],
                                          state[rows, b, f, :], start=stop != "add", stop=stop == "alone")
                return mm

            HALVES = (slice(0, HD), slice(HD, P))

            def whole(bank0, h, lhs, rhs, stop):
                f, par = divmod(h, 2)
                for rows in HALVES:
                    mm = nc.tensor.matmul(big[rows, bank0 + par, f * HD:(f + 1) * HD], lhs[:, rows], rhs[:, h * HD:(h + 1) * HD],
                                          start=False, stop=stop)
                return mm

            def solve(chain0, out):
                for h in range(HEADS):
                    f, par = divmod(h, 2)
                    for rows in HALVES:
                        mm = nc.tensor.matmul(big[rows, 2 + h // 8, (h % 8) * HD:(h % 8 + 1) * HD], Y[:, f, chain0 + par, rows],
                                              X[:, h * HD:(h + 1) * HD], start=True, stop=True)
                mm.then_inc(S[out], 1)

            pe.wait_ge(S["y_added"], 32 * t + 32)
            pe.wait_ge(S["scaled"], t + 1)
            early(0)
            nc.tensor.sem_inc(S["pe_go"], 1)
            for h in range(HEADS):
                mm = by_batch(0, h, TS, 0, SS, "alone")
            mm.then_inc(S["s1"], 1)
            early(1)
            pe.wait_ge(S["x_ready"], t + 1)
            solve(0, "s2")
            early(2)
            pe.wait_ge(S["u_ready"], t + 1)
            nc.tensor.sem_inc(S["pe_go"], 1)
            for h in range(HEADS):
                by_batch(4, h, TS, 2, SS, "open")
                mm = whole(4, h, A[:, h, 1, :], U, True)
            mm.then_inc(S["s3"], 1)
            for h in range(HEADS):
                mm = by_batch(0, h, TR, 0, RR, "alone")
            mm.then_inc(S["s4"], 1)
            early(3)
            pe.wait_ge(S["xr_ready"], t + 1)
            solve(2, "s5")
            early(4)
            pe.wait_ge(S["ur_ready"], t + 1)
            nc.tensor.sem_inc(S["pe_go"], 1)
            for h in range(HEADS):
                by_batch(4, h, TS, 1, SS, "open")
                whole(4, h, A[:, h, 0, :], U, False)
                by_batch(4, h, TR, 1, RR, "add")
                mm = whole(4, h, AR[:, h, :], UR, True)
            mm.then_inc(S["s6"], 1)

            def update(k_, u_, out):
                for h in range(HEADS):
                    f, par = divmod(h, 2)
                    for b in range(GB):
                        rows, cols = slice(32 * b, 32 * b + 32), slice(h * HD, (h + 1) * HD)
                        mm = nc.tensor.matmul(big[par * HD:(par + 1) * HD, b, f * HD:(f + 1) * HD], k_[rows, cols], u_[rows, cols],
                                              start=True, stop=True)
                mm.then_inc(S[out], 1)

            update(km, U, "s7")
            pe.wait_ge(S["s_added"], t + 1)
            nc.tensor.sem_inc(S["pe_go"], 1)
            update(kmr, UR, "s8")
            pe.wait_ge(S["o_ready"], t + 1)
            if not last:
                pe.wait_ge(S["early_used"], 5 * (t + 1) + 5)
            for f in range(PAIRS):
                mm = nc.tensor.transpose(big[:, 6 + f // 4, (f % 4) * P:(f % 4 + 1) * P], O[:, f * P:(f + 1) * P], g.c("ident"))
            mm.then_inc(S["o_flipped"], 1)
            pe.wait_ge(S["ot_ready"], t + 1)
            for f in range(PAIRS):
                mm = nc.tensor.matmul(big[:, 6, 0:P], W("wo")[:, f * D:(f + 1) * D], OT[:, f, :], start=(f == 0), stop=(f == PAIRS - 1))
            mm.then_inc(S["y_ready"], 1)

        def scalar_early(act, t, part):
            if part == 0:
                wait_for(act, S["proj_ready"], 3 * t)
                wait_for(act, S["dve_made"], 3 * t)
                wait_for(act, S["pool_made"], 4 * t)
                nc.scalar.activation(xt[:], g.xn[:, bass.ds(t * P, P)], ACT.Copy).then_inc(S["xt_ready"], 1)
                wait_for(act, S["early_ready"], 5 * t + 1)
                nc.scalar.activation(bgm_next[:].rearrange("p a h -> p (a h)"), big[:, 6, 0:2 * HEADS], ACT.Sigmoid).then_inc(S["early_used"], 1)
                wait_for(act, S["early_ready"], 5 * t + 2)
                nc.scalar.activation(kn, wide(6), ACT.Copy).then_inc(S["early_used"], 1)
                wait_for(act, S["early_used"], 5 * t + 2)
                nc.scalar.activation(q, kn, ACT.Square).then_inc(S["squared"], 1)
            elif part == 1:
                wait_for(act, S["summed"], t + 1)
                nc.scalar.activation(ss[:], ss[:], ACT.Sqrt).then_inc(S["root"], 1)
                wait_for(act, S["early_ready"], 5 * t + 3)
                nc.scalar.activation(q, wide(6), ACT.Copy).then_inc(S["early_used"], 1)
            elif part in (2, 3):
                z = (sp_s, sp_r)[part - 2]
                wait_for(act, S["early_used"], 5 * t + 2 + part)
                nc.scalar.activation(z, z, ACT.Exp).then_inc(S["exp_done"], 1)
            else:
                for n, z in enumerate((sp_s, sp_r)):
                    wait_for(act, S["exp_done"], 2 * t + n + 1)
                    nc.scalar.activation(z, z, ACT.Ln, bias=1.0).then_inc(S["ln_ready"], 1)

        def scalar_tile(act, t, last=False):
            def early(part):
                if not last:
                    scalar_early(act, t + 1, part)

            act.wait_ge(S["added"], t + 1)
            act.wait_ge(S["ln_ready"], 2 * t + 2)
            nc.scalar.activation(ez, sp_s, ACT.Exp)
            act.wait_ge(S["proj_ready"], 3 * t + 1)
            nc.scalar.activation(v[:], wide(0), ACT.Copy).then_inc(S["act_used"], 1)

            def decays(s):
                act.wait_ge(S["dve_used"], 2 * t + s + 1)
                nc.scalar.activation(em, ep, ACT.Exp, scale=-1.0)
                nc.scalar.activation(ep, ep, ACT.Exp).then_inc(S["e_ready"], 1)
                act.wait_ge(S["ends_ready"], 2 * t + 2)
                nc.scalar.activation(er[:, s].rearrange("p f b k -> p (f b k)"), big[:, 7, 64 * s:64 * s + 64], ACT.Exp,
                                     scale=-1.0).then_inc(S["ends_used"], 1)

            def flips(n0, dsts):
                for n, dst in enumerate(dsts):
                    act.wait_ge(S["flipped"], 7 * t + n0 + n + 1)
                    turned = big[:, 4:6, :].rearrange("p c (f n) -> p (c f) n", n=P)
                    if dst is KS or dst is KR:
                        nc.scalar.activation(dst[0:HD, :, 0, :], turned[0:HD], ACT.Copy)
                        nc.scalar.activation(dst[HD:P, :, 1, :], turned[HD:P], ACT.Copy).then_inc(S["flip_used"], 1)
                    else:
                        nc.scalar.activation(dst, turned, ACT.Copy).then_inc(S["flip_used"], 1)

            decays(0)
            flips(0, (TS[:, :, 2, :], TS[:, :, 0, :], KS, TS[:, :, 1, :]))
            decays(1)
            flips(4, (TR[:, :, 0, :], KR, TR[:, :, 1, :]))
            for p_ in range(PAIRS // 2):
                for l in range(4):
                    for wv in range(2):
                        act.wait_ge(S["lev_ready"], 40 * t + 10 * p_ + 2 * l + wv + 1)
                        if l == 0:
                            act.wait_ge(S["y_start"], 8 * t + 2 * p_ + wv + 1)
                        if l < 3:
                            src, dst = big[:, 3 * wv:3 * wv + 2, :], NL[:, wv].rearrange("p m c n -> p m (c n)")
                        else:
                            src, dst = big[:, 3 * wv + 1, :], NL[:, wv, 1].rearrange("p c n -> p (c n)")
                        nc.scalar.activation(dst, src, ACT.Copy).then_inc(S["nl_moved"], 1)
            early(0)
            act.wait_ge(S["s2"], t + 1)
            nc.scalar.activation(U, wide(2), ACT.Copy).then_inc(S["u_ready"], 1)
            early(1)
            early(2)
            act.wait_ge(S["s5"], t + 1)
            nc.scalar.activation(UR, wide(2), ACT.Copy).then_inc(S["ur_ready"], 1)
            early(3)
            early(4)
            act.wait_ge(S["s6"], t + 1)
            for par in range(2):
                ins = nc.scalar.activation(split(O)[:, par], even_odd(4)[:, par], ACT.Copy)
            ins.then_inc(S["o_ready"], 1)
            act.wait_ge(S["o_flipped"], t + 1)
            nc.scalar.activation(OT, big[:, 6:8, :].rearrange("p c (f n) -> p (c f) n", n=P), ACT.Copy).then_inc(S["ot_ready"], 1)

        def pool_tile(pool, t):
            pool.wait_ge(S["kn_ready"], t + 1)
            for s, (k_, wait_flip) in enumerate(((km, None), (kmr, 7 * t + 4))):
                pool.wait_ge(S["e_ready"], 2 * t + s + 1)
                nc.gpsimd.tensor_tensor(k_[:], kn, em, ALU.mult).then_inc(S["pool_made"], 1)
                if s == 1:
                    pool.wait_ge(S["flipped"], wait_flip)
                nc.gpsimd.tensor_tensor(qp, q, ep, ALU.mult).then_inc(S["pool_made"], 1)

        def vector_early(dve, t, part):
            if part == 0:
                c = Chain(dve, S["early_step"], 3, t)
                wait_for(dve, S["squared"], t + 1)
                nc.vector.tensor_reduce(ss[:], heads(q), AX, ALU.add).then_inc(S["summed"], 1)
                wait_for(dve, S["root"], t + 1)
                c.link(nc.vector.tensor_scalar(ss[:], ss[:], 1e-12, None, ALU.max))
                c.link(nc.vector.reciprocal(ss[:], ss[:]))
                c.link(nc.vector.tensor_tensor(heads(kn), heads(kn), by_head(ss[:]), ALU.mult))
                c.close()
                nc.vector.sem_inc(S["kn_ready"], 1)
            else:
                wait_for(dve, S["early_ready"], 5 * t + 3 + part)
                wait_for(dve, S["e_ready"], 2 * t)
                wait_for(dve, S["ends_ready"], 2 * t)
                nc.vector.tensor_scalar((sp_s, sp_r)[part - 1], wide(6), -1.0, 40.0, ALU.mult, ALU.min).then_inc(S["early_used"], 1)

        def vector_tile(dve, t, last=False):
            def early(part):
                if not last:
                    vector_early(dve, t + 1, part)

            c = Chain(dve, S["dve_step"], LINKS, t)
            dve.wait_ge(S["early_used"], 5 * t + 1)
            c.link(nc.vector.tensor_copy(bgm[:], bgm_next[:]))
            c.link(nc.vector.tensor_scalar(neg[:], bgm[:], -1.0, None, ALU.mult))
            for s in range(2):
                dve.wait_ge(S["proj_ready"], 3 * t + 2 + s)
                if s == 1:
                    dve.wait_ge(S["pool_made"], 4 * t + 2)
                nc.vector.tensor_scalar(ep, wide(2 - 2 * s), 80.0, -80.0, ALU.min, ALU.max).then_inc(S["dve_used"], 1)
                dve.wait_ge(S["e_ready"], 2 * t + s + 1)
                if s == 1:
                    dve.wait_ge(S["flipped"], 7 * t + 2)
                c.link(nc.vector.tensor_tensor(kp, kn, ep, ALU.mult))
                if s == 0:
                    nc.vector.tensor_tensor(k0, ez, kp, ALU.mult).then_inc(S["dve_made"], 1)
                    dve.wait_ge(S["dve_made"], 3 * t + 1)
                nc.vector.tensor_tensor(heads(kp), heads(kp), by_head(neg[:, s, :]), ALU.mult).then_inc(S["dve_made"], 1)
            dve.wait_ge(S["ends_used"], 2 * t + 2)
            for s, state in enumerate((SS, RR)):
                er_b = er[:, s].rearrange("p f b k -> p b f k")
                c.link(nc.vector.tensor_tensor(fac[:, s], last_ends[:, s], er_b[:, :, :, 0], ALU.mult))
                c.link(nc.vector.tensor_copy(last_ends[:, s], er_b[:, :, :, 1]))
                flat = state[:].rearrange("p b f d -> p (b f) d")
                ins = nc.vector.tensor_tensor(flat, flat, fac[:, s].rearrange("p b f -> p (b f)").unsqueeze(2).to_broadcast([P, 32, HD]), ALU.mult)
            ins.then_inc(S["scaled"], 1)
            nc.vector.tensor_tensor(heads(X), heads(v[:]), by_head(bgm[:, 0, :]), ALU.mult)
            for p_ in range(PAIRS // 2):
                for wv in range(2):
                    f = 2 * p_ + wv
                    dve.wait_ge(S["mats_ready"], 8 * t + f + 1)
                    nc.vector.sem_inc(S["dve_go"], 1)
                    for par in range(2):
                        h = 2 * f + par
                        a = big[:, 4 * wv + par, :].rearrange("p (m n) -> p m n", n=P)
                        b = big[:, 4 * wv + 2 + par, 0:3 * P].rearrange("p (m n) -> p m n", n=P)
                        nc.vector.copy_predicated(NL[:, wv, :, par, :], keep[:, 0:4:3, :], a[:, 0:4:3, :])
                        nc.vector.copy_predicated(NL[:, wv, :, 2 + par, :], keep_r[:, 0:3:2, :], b[:, 0:3:2, :])
                        nc.vector.copy_predicated(A[:, h], keep[:, 1:3, :], a[:, 1:3, :])
                        ins = nc.vector.copy_predicated(AR[:, h, :], keep_r[:, 1, :], b[:, 1, :])
                    ins.then_inc(S["masked"], 1)
                    dve.wait_ge(S["masked"], 8 * t + f + 1)
                    nc.vector.tensor_tensor(Y[:, f], NL[:, wv, 0], g.c("ident").unsqueeze(1).to_broadcast([P, 4, P]), ALU.add).then_inc(S["y_start"], 1)
                for l in range(1, 5):
                    for wv in range(2):
                        f = 2 * p_ + wv
                        dve.wait_ge(S["lev_ready"], 40 * t + 10 * p_ + 2 * l + wv + 1)
                        yf = Y[:, f].rearrange("p c n -> p (c n)")
                        nc.vector.tensor_tensor(yf, yf, big[:, 3 * wv + 2, :], ALU.add).then_inc(S["y_added"], 1)
            dve.wait_ge(S["s1"], t + 1)
            nc.vector.tensor_tensor(split(X), split(X), even_odd(0), ALU.add).then_inc(S["x_ready"], 1)
            early(0)
            dve.wait_ge(S["s3"], t + 1)
            c.link(nc.vector.tensor_tensor(split(X), split(v[:]), even_odd(4), ALU.subtract))
            c.link(nc.vector.tensor_scalar(X, X, 1.0, -1.0, ALU.min, ALU.max))
            c.link(nc.vector.tensor_tensor(heads(X), heads(X), by_head(bgm[:, 1, :]), ALU.mult))
            dve.wait_ge(S["s4"], t + 1)
            nc.vector.tensor_tensor(split(X), split(X), even_odd(0), ALU.add).then_inc(S["xr_ready"], 1)
            early(1)
            early(2)
            for state, ready, done in ((SS, "s7", "s_added"), (RR, "s8", "r_added")):
                dve.wait_ge(S[ready], t + 1)
                flat = state[:].rearrange("p b f d -> p (b f d)")
                nc.vector.tensor_tensor(flat, flat, big[:, 0:4, :].rearrange("p c n -> p (c n)"), ALU.add).then_inc(S[done], 1)
            dve.wait_ge(S["y_ready"], t + 1)
            c.link(nc.vector.tensor_copy(g.xn[:, bass.ds(t * P, P)], big[:, 6, 0:P]))
            nc.vector.sem_inc(S["added"], 1)
            c.close()

        LINKS = 2 + 2 + 4 + 3 + 1
        with nc.Block() as blk:
            @blk.tensor
            def _(pe):
                pe.wait_ge(S["zeroed"], 1)
                for n in range(5):
                    tensor_early(pe, 0, n)
                with pe.Fori(0, NG * NCH - 1) as t:
                    tensor_tile(pe, t)
                tensor_tile(pe, NG * NCH - 1, last=True)

            @blk.scalar
            def _(act):
                nc.scalar.sem_inc(S["flip_used"], 1)
                for part in range(5):
                    scalar_early(act, 0, part)
                with act.Fori(0, NG * NCH - 1) as t:
                    scalar_tile(act, t)
                scalar_tile(act, NG * NCH - 1, last=True)

            @blk.gpsimd
            def _(pool):
                with pool.Fori(0, NG * NCH) as t:
                    pool_tile(pool, t)

            @blk.vector
            def _(dve):
                for buf in (A, AR, NL, KS, KR):
                    ins = nc.vector.memset(buf[:], 0.0)
                nc.vector.sem_inc(S["added"], 1)
                ins.then_inc(S["zeroed"], 1)
                for part in range(3):
                    vector_early(dve, 0, part)

                def start_states():
                    nc.vector.memset(SS[:], 0.0)
                    nc.vector.memset(RR[:], 0.0)
                    nc.vector.memset(last_ends[:], 1.0)

                with dve.Fori(0, NG - 1) as gi:
                    start_states()
                    with dve.Fori(0, NCH) as ci:
                        vector_tile(dve, gi * NCH + ci)
                start_states()
                with dve.Fori((NG - 1) * NCH, NG * NCH - 1) as t:
                    vector_tile(dve, t)
                vector_tile(dve, NG * NCH - 1, last=True)
        back, results_added = st.sem("back"), st.sem("results_added")
        with nc.Block() as blk:
            @blk.sync
            def _(sp):
                sp.dma_start(g.x[:], x_kept).then_inc(back, 16)
                sp.wait_ge(back, 16)
                sp.wait_ge(results_added, 1)
                sp.dma_start(g.xn[:], kept).then_inc(back, 16)
                sp.wait_ge(back, 32)

            @blk.vector
            def _(dve):
                dve.wait_ge(back, 16)
                for gi in range(NG):
                    for bi in range(GB):
                        x_b = by_batch_of(g.x[:], gi)[:, bi]
                        ins = nc.vector.tensor_tensor(x_b, x_b, by_tile_of(g.xn[:], gi)[:, bi], ALU.add)
                ins.then_inc(results_added, 1)


L2F = layout([("n1", P, 1), ("n2", P, 1), ("wq", P, 4 * P), ("wk", P, 4 * P), ("wv", P, D), ("qn", P, 1), ("kn", P, 1),
              ("wo", P, 4 * D), ("gate", P, 4), ("e0u", P, 2 * P), ("e0d", P, 2 * D), ("e1a", P, 2 * P), ("e1b", P, 2 * P),
              ("e1d", P, 2 * D), ("e2a", P, 2 * P), ("e2b", P, 4 * P), ("e2c", P, 4 * P), ("e2d", P, 2 * D),
              ("e3a", P, P), ("e3b", P, 2 * P), ("e3d", P, 2 * D)])
QUADS = HEADS // 4


def rms_norm(nc, name, src, dst, mean_w, eps_col, weight):
    with Stage(nc, name) as st:
        sq, root = st.sb("sq", [P, 2, BLK]), st.sb("root", [P, 2, BLK])
        ms_ps = st.ps("ms", [P, 2, BLK])
        squared, ms_ready, root_ready, normed, step = (st.sem(n) for n in ("squared", "ms_ready", "root_ready", "normed", "step"))
        with nc.Block() as blk:
            @blk.tensor
            def _(pe):
                with pe.Fori(0, NBLK // 2) as i:
                    for k in range(2):
                        pe.wait_ge(squared, 2 * i + k + 1)
                        pe.wait_ge(root_ready, 2 * i + k + 1)
                        nc.tensor.matmul(ms_ps[:, k, :], mean_w, sq[:, k, :], start=True, stop=True).then_inc(ms_ready, 1)

            @blk.scalar
            def _(act):
                nc.scalar.sem_inc(root_ready, 2)
                with act.Fori(0, NBLK // 2) as i:
                    for k in range(2):
                        nc.scalar.activation(sq[:, k, :], src[:, block(2 * i + k)], ACT.Square).then_inc(squared, 1)
                    for k in range(2):
                        act.wait_ge(ms_ready, 2 * i + k + 1)
                        act.wait_ge(normed, 2 * i + k + 1)
                        nc.scalar.activation(root[:, k, :], ms_ps[:, k, :], ACT.Sqrt, bias=eps_col).then_inc(root_ready, 1)

            @blk.vector
            def _(dve):
                nc.vector.sem_inc(normed, 2)
                with dve.Fori(0, NBLK // 2) as i:
                    c = Chain(dve, step, 2, i)
                    for k in range(2):
                        dve.wait_ge(root_ready, 2 * i + k + 3)
                        c.link(nc.vector.reciprocal(root[:, k, :], root[:, k, :]))
                        nc.vector.scalar_tensor_tensor(out=dst[:, block(2 * i + k)], in0=src[:, block(2 * i + k)], scalar=weight,
                                                       in1=root[:, k, :], op0=ALU.mult, op1=ALU.mult).then_inc(normed, 1)
                    c.close()


def causal_attention(nc, g, w, h):
    W = lambda n: L2F.of(w, n)
    with Stage(nc, "l2h") as st:
        hb = st.sb("hb", [P, T])
        raw = st.sb("raw", [P, 2, 2 * T])
        sq, root = st.sb("sq", [P, 2, 2 * T]), st.sb("root", [P, 2, 2 * T])
        qk = st.sb("qk", [P, QUADS, 2, T])
        v = st.sb("v", [P, 2, HEADS, 32])
        mx = st.sb("mx", [P, 4, 2])
        e = st.sb("e", [P, 4, 3 * P])
        et = st.sb("et", [P, 2, 3 * P])
        raw_o, rden = st.sb("raw_o", [P, T]), st.sb("rden", [P, T])
        ctxt = st.sb("ctxt", [P, QUADS, T])
        identb, maskb = st.sb("identb", [P, P], mybir.dt.bfloat16), st.sb("maskb", [P, P], mybir.dt.bfloat16)
        big = st.ps("big", [P, 8, BLK])
        names = ("setup", "hb_ready", "v_ready", "v_moved", "raw_ready", "squared", "ms_ready", "root_ready", "normed", "moved",
                 "s_ready", "max_ready", "exp_ready", "e_turned", "et_ready", "mixed", "o_moved", "den_ready", "ctx_ready",
                 "y_ready", "added", "dve_step")
        S = {n: st.sem(n) for n in names}
        with nc.Block() as blk:
            @blk.tensor
            def _(pe):
                pe.wait_ge(S["setup"], 1)
                with pe.Fori(0, B) as b:
                    pe.wait_ge(S["hb_ready"], b + 1)
                    for t in range(2):
                        mm = nc.tensor.matmul(big[:, 7, t * P:(t + 1) * P], hb[:, t * P:(t + 1) * P], W("wv"), start=True, stop=True)
                    mm.then_inc(S["v_ready"], 1)
                    for j in range(QUADS):
                        if j >= 2:
                            pe.wait_ge(S["moved"], QUADS * b + j - 1)
                        for n, wn in enumerate(("wq", "wk")):
                            mm = nc.tensor.matmul(big[:, j % 2, n * T:(n + 1) * T], W(wn)[:, j * P:(j + 1) * P], hb[:], start=True, stop=True)
                        mm.then_inc(S["raw_ready"], 1)
                        pe.wait_ge(S["squared"], QUADS * b + j + 1)
                        if j >= 2:
                            pe.wait_ge(S["root_ready"], QUADS * b + j - 1)
                        nc.tensor.matmul(big[:, 2 + j % 2, :], g.c("mean32"), sq[:, j % 2, :], start=True, stop=True).then_inc(S["ms_ready"], 1)
                    pe.wait_ge(S["normed"], QUADS * b + QUADS)
                    pe.wait_ge(S["v_moved"], b + 1)

                    def scores(n):
                        j, r = divmod(n, 4)
                        rows = slice(32 * r, 32 * r + 32)
                        if n >= 4:
                            pe.wait_ge(S["exp_ready"], HEADS * b + n - 3)
                        nc.tensor.matmul(big[:, r, 0:P], qk[rows, j, 0, 0:P], qk[rows, j, 1, 0:P], start=True, stop=False, tile_position=(32 * r, 0))
                        nc.tensor.matmul(big[:, r, 0:P], identb[:], maskb[:], start=False, stop=True)
                        nc.tensor.matmul(big[:, r, P:2 * P], qk[rows, j, 0, P:T], qk[rows, j, 1, 0:P], start=True, stop=True, tile_position=(32 * r, 0))
                        nc.tensor.matmul(big[:, r, 2 * P:3 * P], qk[rows, j, 0, P:T], qk[rows, j, 1, P:T], start=True, stop=False, tile_position=(32 * r, 0))
                        nc.tensor.matmul(big[:, r, 2 * P:3 * P], identb[:], maskb[:], start=False, stop=True).then_inc(S["s_ready"], 1)

                    def turn(n):
                        pe.wait_ge(S["exp_ready"], HEADS * b + n + 1)
                        if n >= 2:
                            pe.wait_ge(S["et_ready"], HEADS * b + n - 1)
                        for k in range(3):
                            mm = nc.tensor.transpose(big[:, 4 + n % 2, k * P:(k + 1) * P], e[:, n % 4, k * P:(k + 1) * P], g.c("ident"))
                        mm.then_inc(S["e_turned"], 1)

                    def mix(n):
                        j, r = divmod(n, 4)
                        out = big[32 * r:32 * r + 32, 6, :]
                        if n >= 4 and r == 0:
                            pe.wait_ge(S["ctx_ready"], QUADS * b + j)
                        pe.wait_ge(S["et_ready"], HEADS * b + n + 1)
                        nc.tensor.matmul(out[:, 0:T], v[:, 0, n, :], et[:, n % 2, 0:T], start=True, stop=False)
                        mm = nc.tensor.matmul(out[:, P:T], v[:, 1, n, :], et[:, n % 2, T:3 * P], start=False, stop=True)
                        mm.then_inc(S["mixed"], 1)
                        if r == 3:
                            pe.wait_ge(S["o_moved"], QUADS * b + j + 1)
                            nc.tensor.matmul(big[:, 6, T:2 * T], g.c("sum32"), raw_o[:], start=True, stop=True).then_inc(S["den_ready"], 1)

                    scores(0)
                    for n in range(HEADS):
                        if n + 1 < HEADS:
                            scores(n + 1)
                        turn(n)
                        if n >= 1:
                            mix(n - 1)
                    mix(HEADS - 1)
                    pe.wait_ge(S["ctx_ready"], QUADS * b + QUADS)
                    for j in range(QUADS):
                        mm = nc.tensor.matmul(big[:, 7, 0:T], W("wo")[:, j * D:(j + 1) * D], ctxt[:, j, :], start=(j == 0), stop=(j == QUADS - 1))
                    mm.then_inc(S["y_ready"], 1)

            @blk.scalar
            def _(act):
                with act.Fori(0, B) as b:
                    act.wait_ge(S["added"], b + 1)
                    nc.scalar.activation(hb[:], h[:, bass.ds(b * T, T)], ACT.Copy).then_inc(S["hb_ready"], 1)
                    act.wait_ge(S["v_ready"], b + 1)
                    nc.scalar.activation(v[:, :, :, 0:8], big[:, 7, 0:2 * P].rearrange("p (t h d) -> p t h d", t=2, d=8),
                                         ACT.Copy).then_inc(S["v_moved"], 1)
                    for j in range(QUADS):
                        act.wait_ge(S["raw_ready"], QUADS * b + j + 1)
                        if j >= 2:
                            act.wait_ge(S["normed"], QUADS * b + j - 1)
                        nc.scalar.activation(raw[:, j % 2, :], big[:, j % 2, :], ACT.Copy).then_inc(S["moved"], 1)
                        act.wait_ge(S["moved"], QUADS * b + j + 1)
                        nc.scalar.activation(sq[:, j % 2, :], raw[:, j % 2, :], ACT.Square).then_inc(S["squared"], 1)
                        act.wait_ge(S["ms_ready"], QUADS * b + j + 1)
                        nc.scalar.activation(root[:, j % 2, :], big[:, 2 + j % 2, :], ACT.Sqrt, bias=g.c("eps_rms")).then_inc(S["root_ready"], 1)
                    for n in range(HEADS):
                        act.wait_ge(S["max_ready"], HEADS * b + n + 1)
                        if n >= 4:
                            act.wait_ge(S["e_turned"], HEADS * b + n - 3)
                        nc.scalar.activation(e[:, n % 4, 0:P], big[:, n % 4, 0:P], ACT.Exp, bias=mx[:, n % 4, 0:1], scale=8 ** -0.5)
                        nc.scalar.activation(e[:, n % 4, P:3 * P], big[:, n % 4, P:3 * P], ACT.Exp, bias=mx[:, n % 4, 1:2],
                                             scale=8 ** -0.5).then_inc(S["exp_ready"], 1)
                        act.wait_ge(S["e_turned"], HEADS * b + n + 1)
                        if n >= 2:
                            act.wait_ge(S["mixed"], HEADS * b + n - 1)
                        nc.scalar.activation(et[:, n % 2, :], big[:, 4 + n % 2, 0:3 * P], ACT.Copy).then_inc(S["et_ready"], 1)

            @blk.vector
            def _(dve):
                nc.vector.sem_inc(S["added"], 1)
                nc.vector.memset(v[:, :, :, 9:32], 0.0)
                nc.vector.memset(v[:, :, :, 8:9], 1.0)
                nc.vector.tensor_copy(identb[:], g.c("ident"))
                nc.vector.tensor_copy(maskb[:], g.c("causal")).then_inc(S["setup"], 1)
                with dve.Fori(0, B) as b:
                    c = Chain(dve, S["dve_step"], QUADS + 2 * HEADS + QUADS + 1, b)
                    for j in range(QUADS):
                        dve.wait_ge(S["root_ready"], QUADS * b + j + 1)
                        c.link(nc.vector.reciprocal(root[:, j % 2, :], root[:, j % 2, :]))
                        for n, wn in enumerate(("qn", "kn")):
                            cols = slice(n * T, (n + 1) * T)
                            ins = nc.vector.scalar_tensor_tensor(out=qk[:, j, n, :], in0=raw[:, j % 2, cols], scalar=W(wn),
                                                                 in1=root[:, j % 2, cols], op0=ALU.mult, op1=ALU.mult)
                        ins.then_inc(S["normed"], 1)

                    def finish(j):
                        dve.wait_ge(S["mixed"], HEADS * b + 4 * j + 4)
                        nc.vector.tensor_copy(raw_o[:], big[:, 6, 0:T]).then_inc(S["o_moved"], 1)
                        dve.wait_ge(S["den_ready"], QUADS * b + j + 1)
                        c.link(nc.vector.reciprocal(rden[:], big[:, 6, T:2 * T]))
                        nc.vector.tensor_tensor(ctxt[:, j, :], raw_o[:], rden[:], ALU.mult).then_inc(S["ctx_ready"], 1)

                    for n in range(HEADS):
                        r = n % 4
                        dve.wait_ge(S["s_ready"], HEADS * b + n + 1)
                        if n >= 4:
                            dve.wait_ge(S["exp_ready"], HEADS * b + n - 3)
                        nc.vector.tensor_reduce(mx[:, r, 0:1], big[:, r, 0:P], AX, ALU.max)
                        c.link(nc.vector.tensor_reduce(mx[:, r, 1:2], big[:, r, P:3 * P], AX, ALU.max))
                        c.link(nc.vector.tensor_scalar(mx[:, r, :], mx[:, r, :], -(8 ** -0.5), None, ALU.mult))
                        nc.vector.sem_inc(S["max_ready"], 1)
                        if n % 4 == 1 and n > 4:
                            finish(n // 4 - 1)
                    finish(QUADS - 1)
                    dve.wait_ge(S["y_ready"], b + 1)
                    for r in range(32, P, 32):
                        xs = g.xn[r:r + 32, bass.ds(b * T, T)]
                        ins = nc.vector.tensor_tensor(xs, xs, big[r:r + 32, 7, 0:T], ALU.add)
                    c.link(ins)
                    nc.vector.sem_inc(S["added"], 1)
                    c.close()


def l2_weigh(nc, g):
    def weigh(dve, c, s_ps, s, mask, prob, t_gt, t_eq, rank, one, exp_in, exp_out):
        sh = [P, TILES, 4]
        c.link(nc.vector.tensor_scalar(s[:], s_ps[:], 3.4028235e38, -3.4028235e38, ALU.min, ALU.max))
        c.link(nc.vector.tensor_reduce(one[:], s[:].unsqueeze(2), AX, ALU.max))
        c.link(nc.vector.tensor_tensor(s[:], s[:], one[:].to_broadcast(sh), ALU.subtract))
        nc.vector.sem_inc(exp_in, 1)
        dve.wait_ge(exp_out, 1)
        c.link(nc.vector.tensor_reduce(one[:], s[:].unsqueeze(2), AX, ALU.add))
        c.link(nc.vector.reciprocal(one[:], one[:]))
        c.link(nc.vector.tensor_tensor(s[:], s[:], one[:].to_broadcast(sh), ALU.mult))
        top2(nc, g, c, s[:], mask, 4, t_gt, t_eq, rank)
        c.link(nc.vector.tensor_tensor(prob[:], s[:], mask[:], ALU.mult))
        c.link(nc.vector.tensor_reduce(one[:], prob[:].unsqueeze(2), AX, ALU.add))
        c.link(nc.vector.tensor_scalar(one[:], one[:], 1e-8, None, ALU.add))
        c.link(nc.vector.reciprocal(one[:], one[:]))
        c.link(nc.vector.tensor_tensor(prob[:], prob[:], one[:].to_broadcast(sh), ALU.mult))
    return weigh


def mixed_experts(nc, g, w, xf, prob_t):
    W = lambda n: L2F.of(w, n)
    part = lambda n, k: W(n)[:, k * P:(k + 1) * P]
    CHUNKS = [
        ("a0", [("e0u", 0, None)], 0, ("e0d", 0)), ("a1", [("e0u", 1, None)], 0, ("e0d", 1)),
        ("b0", [("e1a", 0, None)], 1, ("e1d", 0)), ("b1", [("e1a", 1, None)], 1, ("e1d", 1)),
        ("c0", [("e2a", 0, None)], None, None), ("c1", [("e2a", 1, None)], None, None),
        ("d0", [("e3a", 0, None)], None, None),
        ("f0", [("e2b", 0, "c0"), ("e2b", 2, "c1")], None, None), ("f1", [("e2b", 1, "c0"), ("e2b", 3, "c1")], None, None),
        ("h0", [("e3b", 0, "d0")], 3, ("e3d", 0)), ("h1", [("e3b", 1, "d0")], 3, ("e3d", 1)),
        ("i0", [("e2c", 0, "f0"), ("e2c", 2, "f1")], 2, ("e2d", 0)), ("i1", [("e2c", 1, "f0"), ("e2c", 3, "f1")], 2, ("e2d", 1)),
    ]
    at = {c[0]: n for n, c in enumerate(CHUNKS)}
    OUTS = [n for n, c in enumerate(CHUNKS) if c[3]]
    NC, NO = len(CHUNKS), len(OUTS)
    RING = 4
    with Stage(nc, "l2m") as st:
        hid = st.sb("hid", [P, NC, BLK])
        big = st.ps("big", [P, 8, BLK])
        up_ready, hid_ready, scaled, used, spread, out_used, step = (
            st.sem(n) for n in ("up_ready", "hid_ready", "scaled", "used", "spread", "out_used", "step"))
        with nc.Block() as blk:
            @blk.tensor
            def _(pe):
                with pe.Fori(0, NBLK) as i:
                    def up(n):
                        name, products, expert, out = CHUNKS[n]
                        pe.wait_ge(hid_ready, NC * i + n + 1)
                        if name == "b0":
                            nc.tensor.matmul(big[:, 4, :], part("e1b", 0), xf[:, block(i)], start=True, stop=True)
                        if name == "b1":
                            pe.wait_ge(scaled, NO * i + 3)
                            nc.tensor.matmul(big[:, 4, :], part("e1b", 1), xf[:, block(i)], start=True, stop=True)
                        for m, (wn, k, source) in enumerate(products):
                            if source:
                                pe.wait_ge(hid_ready, NC * i + at[source] + 5)
                            rhs = hid[:, at[source], :] if source else xf[:, block(i)]
                            mm = nc.tensor.matmul(big[:, n % RING, :], part(wn, k), rhs, start=(m == 0), stop=(m == len(products) - 1))
                        mm.then_inc(up_ready, 1)
                        if n in OUTS and OUTS.index(n) % 2 == 0:
                            e = OUTS.index(n) // 2
                            if e >= 2:
                                pe.wait_ge(scaled, NO * i + 2 * (e - 1))
                            nc.tensor.matmul(big[:, 6 + e % 2, :], g.c("pick8").rearrange("k (e m) -> k e m", e=8)[:, expert, :],
                                             prob_t[:, block(i)], start=True, stop=True).then_inc(spread, 1)

                    def down(m):
                        wn, k = CHUNKS[OUTS[m]][3]
                        if m == 0:
                            pe.wait_ge(out_used, i + 1)
                        pe.wait_ge(scaled, NO * i + m + 1)
                        nc.tensor.matmul(big[:, 5, :], part(wn, k), hid[:, OUTS[m], :], start=(m == 0), stop=(m == NO - 1)).then_inc(used, 1)

                    m = 0
                    for n in range(NC):
                        up(n)
                        while m < NO and OUTS[m] < n:
                            down(m)
                            m += 1
                    while m < NO:
                        down(m)
                        m += 1

            @blk.scalar
            def _(act):
                nc.scalar.sem_inc(hid_ready, RING)
                with act.Fori(0, NBLK) as i:
                    for n, (name, products, expert, out) in enumerate(CHUNKS):
                        act.wait_ge(up_ready, NC * i + n + 1)
                        if n == 0:
                            act.wait_ge(out_used, i + 1)
                        nc.scalar.activation(hid[:, n, :], big[:, n % RING, :], ACT.Silu if expert == 1 else ACT.Gelu).then_inc(hid_ready, 1)

            @blk.vector
            def _(dve):
                nc.vector.sem_inc(out_used, 1)
                with dve.Fori(0, NBLK) as i:
                    c = Chain(dve, step, 2 + 1 + 1, i)
                    xs = g.x[:, block(i)]
                    for m, n in enumerate(OUTS):
                        dve.wait_ge(hid_ready, NC * i + n + 1 + RING)
                        dve.wait_ge(spread, 4 * i + m // 2 + 1)
                        if CHUNKS[n][2] == 1:
                            c.link(nc.vector.tensor_tensor(hid[:, n, :], hid[:, n, :], big[:, 4, :], ALU.mult))
                        nc.vector.tensor_tensor(hid[:, n, :], hid[:, n, :], big[:, 6 + m // 2 % 2, :], ALU.mult).then_inc(scaled, 1)
                    c.link(nc.vector.tensor_tensor(xs, xs, g.xn[:, block(i)], ALU.add))
                    dve.wait_ge(used, NO * i + NO)
                    for r in range(32, P, 32):
                        xr = g.x[r:r + 32, block(i)]
                        ins = nc.vector.tensor_tensor(xr, xr, big[r:r + 32, 5, :], ALU.add)
                    c.link(ins)
                    nc.vector.sem_inc(out_used, 1)
                    c.close()


DEPTH = 6
WINDOW = 32
HALF = 341
L3A = layout([("wq", P, INNER), ("wk", P, INNER), ("wv", P, INNER), ("wf", P, INNER), ("wg", P, INNER),
              ("wb", P, HEADS), ("wo", P, PAIRS * D), ("dt", P, PAIRS), ("bg", P, PAIRS), ("a_log", P, HEADS),
              ("norm_w", P, 1)])
L3W = layout([("wq", P, INNER), ("wqr", P, INNER), ("wk", P, INNER), ("wkr", P, INNER), ("wv", P, INNER),
              ("wo", P, PAIRS * D), ("qs", P, 2), ("ks", P, 2)])
L3F = layout([("w1", P, 6 * P), ("b1", P, 6), ("w2", P, 3 * D), ("b2", P, 1), ("g", P, 1), ("b", P, 1)])


def decay_attention(nc, g, w):
    W = lambda n: L3A.of(w, n)
    PARTS = (0, 1, 4, 8)
    with Stage(nc, "l3a") as st:
        dmask = st.sb("dmask", [P, HEADS, T])
        ealog = st.sb("ealog", [P, HEADS])
        minus_dt = st.sb("minus_dt", [P, PAIRS])
        xb = st.sb("xb", [P, 2, T])
        qk = st.sb("qk", [P, PAIRS, 2, T])
        sq = st.sb("sq", [P, 2, 2, T])
        ms, inv = st.sb("ms", [P, PAIRS, 3, T]), st.sb("inv", [P, PAIRS, 3, T])
        kf, qz = st.sb("kf", [P, 2, T]), st.sb("qz", [P, 2, 2, T])
        sc = st.sb("sc", [P, 2, 2, 3 * P])
        v, beta = st.sb("v", [P, 2, INNER]), st.sb("beta", [P, 2, HEADS])
        decay, gate_s = st.sb("decay", [P, PAIRS, T]), st.sb("gate", [P, PAIRS, T])
        og, osq, on = st.sb("og", [P, PAIRS, T]), st.sb("osq", [P, 2, T]), st.sb("on", [P, 2, T])
        big = st.ps("big", [P, 8, BLK])
        names = ("mask_arg", "mask_exp", "mask_done", "setup_done", "xb_ready", "qk_ready", "silu_ready", "sq_ready", "norm_ready",
                 "clamped", "rooted", "inv_ready", "scaled", "s_ready", "masked", "av_ready", "gated", "osq_ready", "ms_ready",
                 "ms_kept", "v_ready", "v_moved", "v_scaled", "beta_ready", "beta_moved", "g_ready", "g_moved", "o_gated",
                 "ln_ready", "unit_step", "unit_ready",
                 "o_final", "out_used", "added")
        S = {n: st.sem(n) for n in names}

        def pe_qk(pe, b, par, f):
            if f == 0:
                wait_for(pe, S["xb_ready"], b + 1)
            if f < 2:
                wait_for(pe, S["g_moved"], PAIRS * b)
            else:
                wait_for(pe, S["silu_ready"], PAIRS * b + f - 1)
            for n, wn in enumerate(("wq", "wk")):
                mm = nc.tensor.matmul(big[:, f % 2, n * T:(n + 1) * T], W(wn)[:, f * P:(f + 1) * P], xb[:, par, :], start=True, stop=True)
            mm.then_inc(S["qk_ready"], 1)

        def pe_norm(pe, b, f):
            wait_for(pe, S["sq_ready"], PAIRS * b + f + 1)
            wait_for(pe, S["clamped"], PAIRS * b + f)
            nc.tensor.matmul(big[:, 2, :], g.c("head64"), sq[:, f % 2].rearrange("p n t -> p (n t)"),
                             start=True, stop=True).then_inc(S["norm_ready"], 1)

        def pe_tokens(pe, b, par):
            wait_for(pe, S["ms_kept"], PAIRS * b)
            for t in range(2):
                mm = nc.tensor.matmul(big[:, 6, t * HEADS:(t + 1) * HEADS], xb[:, par, t * P:(t + 1) * P], W("wb"), start=True, stop=True)
            mm.then_inc(S["beta_ready"], 1)
            for n in range(4):
                t, c = divmod(n, 2)
                if n < 2:
                    wait_for(pe, S["silu_ready"], PAIRS * b + PAIRS)
                else:
                    wait_for(pe, S["v_moved"], 4 * b + n - 1)
                nc.tensor.matmul(big[:, c, :], xb[:, par, t * P:(t + 1) * P], W("wv")[:, c * BLK:(c + 1) * BLK],
                                 start=True, stop=True).then_inc(S["v_ready"], 1)

        def pe_gates(pe, b, par):
            for f in range(PAIRS):
                if f < 2:
                    wait_for(pe, S["v_moved"], 4 * b + 3 + f)
                else:
                    wait_for(pe, S["g_moved"], PAIRS * b + f - 1)
                for n, wn in enumerate(("wf", "wg")):
                    mm = nc.tensor.matmul(big[:, f % 2, n * T:(n + 1) * T], W(wn)[:, f * P:(f + 1) * P], xb[:, par, :], start=True, stop=True)
                mm.then_inc(S["g_ready"], 1)

        def pe_scores(pe, a, f):
            wait_for(pe, S["scaled"], PAIRS * a + f + 1)
            wait_for(pe, S["masked"], PAIRS * a + f)
            nc.tensor.matmul(big[:, 3, :], kf[:, f % 2, 0:P], qz[:, f % 2].rearrange("p h t -> p (h t)"), start=True, stop=True)
            nc.tensor.matmul(big[:, 4, 0:2 * P], kf[:, f % 2, P:T], qz[:, f % 2, :, P:T], start=True, stop=True).then_inc(S["s_ready"], 1)

        def pe_sums(pe, a, par, f):
            if f == 0:
                wait_for(pe, S["v_scaled"], a + 1)
            wait_for(pe, S["masked"], PAIRS * a + f + 1)
            wait_for(pe, S["gated"], PAIRS * a + f)
            for key, at, start, stop in ((0, 0, True, True), (0, 1, True, False), (1, 2, False, True)):
                for odd in range(2):
                    h, q = 2 * f + odd, min(at, 1)
                    mm = nc.tensor.matmul(big[odd * HD:(odd + 1) * HD, 5, q * P:(q + 1) * P], v[:, key, h * HD:(h + 1) * HD],
                                          sc[:, f % 2, odd, at * P:(at + 1) * P], start=start, stop=stop)
            mm.then_inc(S["av_ready"], 1)

        def pe_ms(pe, a, f):
            wait_for(pe, S["osq_ready"], PAIRS * a + f + 1)
            if f == 0:
                wait_for(pe, S["beta_moved"], a + 1)
            wait_for(pe, S["ms_kept"], PAIRS * a + f)
            nc.tensor.matmul(big[:, 6, 0:T], g.c("head64"), osq[:, f % 2, :], start=True, stop=True).then_inc(S["ms_ready"], 1)

        def pe_out(pe, a, f):
            wait_for(pe, S["o_final"], PAIRS * a + f + 1)
            if f == 0:
                wait_for(pe, S["added"], a + 1)
            nc.tensor.matmul(big[:, 7, 0:T], W("wo")[:, f * D:(f + 1) * D], on[:, f % 2, :],
                             start=(f == 0), stop=(f == PAIRS - 1)).then_inc(S["out_used"], 1)

        def pe_turn(pe, a, par, first=False, last=False):
            for f in range(PAIRS):
                pe_scores(pe, a, f)
                if not last:
                    pe_qk(pe, a + 1, 1 - par, f)
                    if f >= 1:
                        pe_norm(pe, a + 1, f - 1)
                pe_sums(pe, a, par, f)
                if f >= 1:
                    pe_ms(pe, a, f - 1)
                if f >= 1 and not first:
                    pe_out(pe, a - 1, f - 1)
            if not first:
                pe_out(pe, a - 1, PAIRS - 1)
            if not last:
                pe_norm(pe, a + 1, PAIRS - 1)
            pe_ms(pe, a, PAIRS - 1)
            if not last:
                pe_tokens(pe, a + 1, 1 - par)
                pe_gates(pe, a + 1, 1 - par)

        def act_input(act, b, par):
            nc.scalar.activation(xb[:, par, :], g.xn[:, bass.ds(b * T, T)], ACT.Copy).then_inc(S["xb_ready"], 1)

        def act_qk(act, b, f):
            wait_for(act, S["qk_ready"], PAIRS * b + f + 1)
            wait_for(act, S["scaled"], PAIRS * (b - 1) + f + 1)
            nc.scalar.activation(qk[:, f].rearrange("p n t -> p (n t)"), big[:, f % 2, :], ACT.Silu).then_inc(S["silu_ready"], 1)
            wait_for(act, S["silu_ready"], PAIRS * b + f + 1)
            wait_for(act, S["norm_ready"], PAIRS * b + f - 1)
            nc.scalar.activation(sq[:, f % 2], qk[:, f], ACT.Square).then_inc(S["sq_ready"], 1)

        def act_osq(act, a, f):
            wait_for(act, S["gated"], PAIRS * a + f + 1)
            wait_for(act, S["ms_ready"], PAIRS * a + f - 1)
            nc.scalar.activation(osq[:, f % 2, :], og[:, f, :], ACT.Square).then_inc(S["osq_ready"], 1)

        def act_v(act, b):
            wait_for(act, S["av_ready"], PAIRS * b)
            for n in range(4):
                wait_for(act, S["v_ready"], 4 * b + n + 1)
                nc.scalar.activation(v[:, n // 2, (n % 2) * BLK:(n % 2 + 1) * BLK], big[:, n % 2, :],
                                     ACT.Silu).then_inc(S["v_moved"], 1)

        def act_roots(act, made, done, which):
            nc.scalar.preload_act_table_set("natural_log_exp_and_others")
            wait_for(act, S["clamped"], PAIRS * made)
            wait_for(act, S["ms_kept"], PAIRS * done)
            wait_for(act, S["scaled"], PAIRS * (made - 1))
            wait_for(act, S["o_final"], PAIRS * (done - 1))
            for n in range(len(PARTS) - 1):
                some = slice(PARTS[n], PARTS[n + 1])
                nc.scalar.activation(inv[:, some, which, :], ms[:, some, which, :], ACT.Ln).then_inc(S["ln_ready"], 1)
                wait_for(act, S["ln_ready"], (len(PARTS) - 1) * done + n + 1)
                nc.scalar.activation(inv[:, some, which, :], inv[:, some, which, :], ACT.Exp, scale=-0.5).then_inc(S["rooted"], 1)

        def act_gates(act, b):
            wait_for(act, S["beta_ready"], b + 1)
            wait_for(act, S["v_scaled"], b)
            nc.scalar.activation(beta[:].rearrange("p t h -> p (t h)"), big[:, 6, 0:2 * HEADS], ACT.Sigmoid).then_inc(S["beta_moved"], 1)
            wait_for(act, S["gated"], PAIRS * b)
            wait_for(act, S["o_gated"], PAIRS * b)
            for f in range(PAIRS):
                wait_for(act, S["g_ready"], PAIRS * b + f + 1)
                nc.scalar.activation(decay[:, f, :], big[:, f % 2, 0:T], ACT.Sigmoid, bias=minus_dt[:, f:f + 1])
                nc.scalar.activation(gate_s[:, f, :], big[:, f % 2, T:2 * T], ACT.Sigmoid, bias=W("bg")[:, f:f + 1]).then_inc(S["g_moved"], 1)

        def act_turn(act, a, par, last=False):
            if not last:
                act_input(act, a + 1, 1 - par)
            for f in range(PAIRS):
                if not last:
                    act_qk(act, a + 1, f)
                act_osq(act, a, f)
            if last:
                act_roots(act, a + 1, a + 1, slice(2, 3))
            else:
                act_v(act, a + 1)
                act_gates(act, a + 1)
                act_roots(act, a + 2, a + 1, slice(0, 3))

        def dve_refine(dve, a, f, which):
            wait_for(dve, S["unit_ready"], PAIRS * a + f + 1)
            nc.vector.scalar_tensor_tensor(out=inv[:, f, which, :], in0=ms[:, f, which, :], scalar=-3.0, in1=inv[:, f, which, :],
                                           op0=ALU.add, op1=ALU.mult).then_inc(S["inv_ready"], 1)

        def dve_prepare(dve, a, f, first=False):
            dve_refine(dve, a, f, slice(0, 2 if first else 3))
            wait_for(dve, S["inv_ready"], PAIRS * a + f + 1)
            wait_for(dve, S["s_ready"], PAIRS * a + f - 1)
            nc.vector.scalar_tensor_tensor(out=kf[:, f % 2, :], in0=qk[:, f, 1, :], scalar=-128.0, in1=inv[:, f, 1, :],
                                           op0=ALU.mult, op1=ALU.mult)
            for odd in range(2):
                rows = slice(odd * HD, (odd + 1) * HD)
                ins = nc.vector.scalar_tensor_tensor(out=qz[rows, f % 2, odd, :], in0=qk[rows, f, 0, :], scalar=-128.0,
                                                     in1=inv[rows, f, 0, :], op0=ALU.mult, op1=ALU.mult)
            ins.then_inc(S["scaled"], 1)

        def dve_mask(dve, a, f):
            wait_for(dve, S["s_ready"], PAIRS * a + f + 1)
            wait_for(dve, S["av_ready"], PAIRS * a + f - 1)
            nc.vector.tensor_tensor(sc[:, f % 2, :, 0:T], big[:, 3, :].rearrange("p (h t) -> p h t", h=2), dmask[:, 2 * f:2 * f + 2, 0:T], ALU.mult)
            nc.vector.tensor_tensor(sc[:, f % 2, :, T:3 * P], big[:, 4, 0:2 * P].rearrange("p (h t) -> p h t", h=2),
                                    dmask[:, 2 * f:2 * f + 2, 0:P], ALU.mult).then_inc(S["masked"], 1)

        def dve_clamp(dve, b, f):
            wait_for(dve, S["norm_ready"], PAIRS * b + f + 1)
            wait_for(dve, S["scaled"], PAIRS * (b - 1) + f + 1)
            nc.vector.tensor_scalar(ms[:, f, 0:2, :], big[:, 2, :].rearrange("p (n t) -> p n t", n=2), 1e-24, 65536.0,
                                    ALU.max, ALU.mult).then_inc(S["clamped"], 1)

        def dve_gate(dve, a, f):
            if f == 0:
                wait_for(dve, S["g_moved"], PAIRS * a + PAIRS)
            wait_for(dve, S["av_ready"], PAIRS * a + f + 1)
            wait_for(dve, S["o_final"], PAIRS * (a - 1) + f + 1)
            nc.vector.tensor_tensor(og[:, f, :], big[:, 5, 0:T], decay[:, f, :], ALU.mult).then_inc(S["gated"], 1)

        def dve_keep_ms(dve, a, f):
            wait_for(dve, S["ms_ready"], PAIRS * a + f + 1)
            wait_for(dve, S["inv_ready"], PAIRS * a + f + 1)
            nc.vector.tensor_scalar(ms[:, f, 2, :], big[:, 6, 0:T], 1.0 / HD, 1e-5, ALU.mult, ALU.add).then_inc(S["ms_kept"], 1)

        def dve_add(dve, a):
            wait_for(dve, S["out_used"], PAIRS * a + PAIRS)
            xs = g.x[:, bass.ds(a * T, T)]
            nc.vector.tensor_tensor(xs, xs, big[:, 7, 0:T], ALU.add).then_inc(S["added"], 1)

        def dve_turn(dve, a, par, first=False, last=False):
            dve_prepare(dve, a, 0, first)
            for f in range(PAIRS):
                dve_mask(dve, a, f)
                if f + 1 < PAIRS:
                    dve_prepare(dve, a, f + 1, first)
                if f >= 1 and not last:
                    dve_clamp(dve, a + 1, f - 1)
                dve_gate(dve, a, f)
                if f >= 1:
                    dve_keep_ms(dve, a, f - 1)
            if not last:
                dve_clamp(dve, a + 1, PAIRS - 1)
            dve_keep_ms(dve, a, PAIRS - 1)
            if not first:
                dve_add(dve, a - 1)

        def pool_gate(pool, a, f):
            if f == 0:
                wait_for(pool, S["g_moved"], PAIRS * a + PAIRS)
            wait_for(pool, S["osq_ready"], PAIRS * a + f + 1)
            nc.gpsimd.tensor_tensor(og[:, f, :], og[:, f, :], gate_s[:, f, :], ALU.mult).then_inc(S["o_gated"], 1)

        def pool_final(pool, a, f):
            wait_for(pool, S["inv_ready"], PAIRS * (a + 1) + f + 1)
            wait_for(pool, S["out_used"], PAIRS * a + f - 1)
            wait_for(pool, S["o_gated"], PAIRS * a + f + 1)
            nc.gpsimd.tensor_tensor(on[:, f % 2, :], og[:, f, :], inv[:, f, 2, :], ALU.mult).then_inc(S["o_final"], 1)

        def pool_units(pool, a, f, which):
            wait_for(pool, S["rooted"], (len(PARTS) - 1) * a + [n for n in range(len(PARTS)) if PARTS[n] > f][0])
            s, r = ms[:, f, which, :], inv[:, f, which, :]
            nc.gpsimd.tensor_tensor(s, s, r, ALU.mult).then_inc(S["unit_step"], 1)
            wait_for(pool, S["unit_step"], PAIRS * a + f + 1)
            nc.gpsimd.tensor_tensor(s, s, r, ALU.mult).then_inc(S["unit_ready"], 1)

        def pool_turn(pool, a, first=False, last=False):
            which = slice(0, 2 if first else 3)
            pool_units(pool, a, 0, which)
            for f in range(PAIRS):
                if not first:
                    pool_final(pool, a - 1, f)
                if f + 1 < PAIRS:
                    pool_units(pool, a, f + 1, which)
                if f >= 1:
                    pool_gate(pool, a, f - 1)
            pool_gate(pool, a, PAIRS - 1)
            if not last:
                pool_v(pool, a + 1)

        def pool_v(pool, b):
            wait_for(pool, S["v_moved"], 4 * b + 4)
            wait_for(pool, S["beta_moved"], b + 1)
            vv = v[:].rearrange("p t (h d) -> p (t h) d", h=HEADS)
            nc.gpsimd.tensor_tensor(vv, vv, beta[:].rearrange("p t h -> p (t h)").unsqueeze(2).to_broadcast([P, 2 * HEADS, HD]),
                                    ALU.mult).then_inc(S["v_scaled"], 1)

        with nc.Block() as blk:
            @blk.tensor
            def _(pe):
                for f in range(PAIRS):
                    pe_qk(pe, 0, 0, f)
                    if f >= 1:
                        pe_norm(pe, 0, f - 1)
                pe_norm(pe, 0, PAIRS - 1)
                pe_tokens(pe, 0, 0)
                pe_gates(pe, 0, 0)
                pe_turn(pe, 0, 0, first=True)
                with pe.Fori(0, (B - 2) // 2) as i:
                    pe_turn(pe, 2 * i + 1, 1)
                    pe_turn(pe, 2 * i + 2, 0)
                pe_turn(pe, B - 1, 1, last=True)
                for f in range(PAIRS):
                    pe_out(pe, B - 1, f)

            @blk.scalar
            def _(act):
                nc.scalar.activation(ealog[:], W("a_log"), ACT.Exp).then_inc(S["mask_arg"], 1)
                for h in range(HEADS):
                    act.wait_ge(S["mask_exp"], h + 1)
                    nc.scalar.activation(dmask[:, h, :], dmask[:, h, :], ACT.Exp).then_inc(S["mask_done"], 1)
                act_input(act, 0, 0)
                for f in range(PAIRS):
                    act_qk(act, 0, f)
                act_v(act, 0)
                act_roots(act, 1, 0, slice(0, 2))
                act.wait_ge(S["setup_done"], 1)
                act_gates(act, 0)
                act_turn(act, 0, 0)
                with act.Fori(0, (B - 2) // 2) as i:
                    act_turn(act, 2 * i + 1, 1)
                    act_turn(act, 2 * i + 2, 0)
                act_turn(act, B - 1, 1, last=True)

            @blk.gpsimd
            def _(pool):
                pool_v(pool, 0)
                pool_turn(pool, 0, first=True)
                pool_turn(pool, 1)
                with pool.Fori(2, B - 1) as a:
                    pool_turn(pool, a)
                pool_turn(pool, B - 1, last=True)
                for f in range(PAIRS):
                    pool_units(pool, B, f, slice(2, 3))
                    pool_final(pool, B - 1, f)

            @blk.vector
            def _(dve):
                nc.vector.sem_inc(S["added"], 1)
                nc.vector.memset(qz[0:HD, :, 1, :], 0.0)
                nc.vector.memset(qz[HD:P, :, 0, :], 0.0)
                nc.vector.tensor_scalar(minus_dt[:], W("dt"), -1.0, None, ALU.mult)
                nc.vector.tensor_scalar(W("wo"), W("wo"), W("norm_w"), -0.5, ALU.mult, ALU.mult)
                dve.wait_ge(S["mask_arg"], 1)
                for h in range(HEADS):
                    nc.vector.tensor_scalar(dmask[:, h, :], g.c("lag"), ealog[:, h:h + 1], None, ALU.mult).then_inc(S["mask_exp"], 1)
                for h in range(HEADS):
                    dve.wait_ge(S["mask_done"], h + 1)
                    ins = nc.vector.tensor_tensor(dmask[:, h, :], dmask[:, h, :], g.c("earlier"), ALU.mult)
                ins.then_inc(S["setup_done"], 1)
                dve.wait_ge(S["setup_done"], 1)
                for f in range(PAIRS):
                    dve_clamp(dve, 0, f)
                dve_turn(dve, 0, 0, first=True)
                with dve.Fori(0, (B - 2) // 2) as i:
                    dve_turn(dve, 2 * i + 1, 1)
                    dve_turn(dve, 2 * i + 2, 0)
                dve_turn(dve, B - 1, 1, last=True)
                for f in range(PAIRS):
                    dve_refine(dve, B, f, slice(2, 3))
                dve_add(dve, B - 1)


QT = (0, 96, 160)
KT = (0, 64, 128)
QN = 96


def window_attention(nc, g, w, mlp_w, mlp_dram):
    W = lambda n: L3W.of(w, n)
    y = g.xn
    HG = 4
    GROUPS = 3 * HEADS // HG
    PER_TILE = HEADS // HG
    with Stage(nc, "l3w") as st:
        tab = st.sb("tab", [P, 2, 2, T])
        xb = st.sb("xb", [P, 2, T])
        rot = st.sb("rot", [P, 2, 2, 2, T])
        sq = st.sb("sq", [P, 2, 2, T])
        ss, rn, unit = (st.sb(n, [P, 2, 2, T]) for n in ("ss", "rn", "unit"))
        ks = st.sb("ks", [P, 4, T])
        qf, kz = st.sb("qf", [P, 2, PAIRS, T]), st.sb("kz", [P, 2, PAIRS, 2, T])
        v = st.sb("v", [P, 2, 3, INNER])
        nb, sm, rs = (st.sb(n, [P, 2, HG]) for n in ("nb", "sm", "rs"))
        pr, pt = st.sb("pr", [P, 2, HG, P]), st.sb("pt", [P, 2, HG, QN])
        ot = st.sb("ot", [P, PAIRS, T])
        identb, maskb = st.sb("identb", [P, QN], mybir.dt.bfloat16), st.sb("maskb", [P, 2, HG, P], mybir.dt.bfloat16)
        big = st.ps("big", [P, 8, BLK])
        names = ("tab_ready", "xb_ready", "qk_ready", "rot_done", "sq_ready", "norm_ready", "clamped", "ln_ready", "root_ready",
                 "summed", "scaled", "v_ready", "v_moved", "s_ready", "max_ready", "exp_done", "inv_ready", "p_ready", "p_turned",
                 "pt_ready", "pt_used", "ot_ready", "y_ready", "added",
                 "pool_step", "unit_ready", "refined")
        S = {n: st.sem(n) for n in names}

        def pe_qk(pe, b, par, f):
            if f == 0:
                wait_for(pe, S["xb_ready"], b + 1)
                wait_for(pe, S["v_moved"], 6 * b)
            wait_for(pe, S["sq_ready"], PAIRS * b + f)
            for n, (wa, wb) in enumerate((("wq", "wqr"), ("wk", "wkr"))):
                nc.tensor.matmul(big[:, n, 0:T], W(wa)[:, f * P:(f + 1) * P], xb[:, par, :], start=True, stop=True)
                mm = nc.tensor.matmul(big[:, n, T:2 * T], W(wb)[:, f * P:(f + 1) * P], xb[:, par, :], start=True, stop=True)
            mm.then_inc(S["qk_ready"], 1)

        def pe_norm(pe, b, f):
            wait_for(pe, S["sq_ready"], PAIRS * b + f + 1)
            wait_for(pe, S["clamped"], PAIRS * b + f)
            nc.tensor.matmul(big[:, 2, :], g.c("head64"), sq[:, f % 2].rearrange("p n t -> p (n t)"),
                             start=True, stop=True).then_inc(S["norm_ready"], 1)

        def pe_v(pe, b, par, n):
            t, c = divmod(n, 2)
            if n < 2:
                wait_for(pe, S["sq_ready"], PAIRS * b + PAIRS)
            else:
                wait_for(pe, S["v_moved"], 6 * b + n - 1)
            nc.tensor.matmul(big[:, c, :], xb[:, par, KT[t]:KT[t] + P], W("wv")[:, c * BLK:(c + 1) * BLK],
                             start=True, stop=True).then_inc(S["v_ready"], 1)

        def pe_scores(pe, a, par, u):
            t, grp = divmod(u, PER_TILE)
            if u == 0:
                wait_for(pe, S["scaled"], PAIRS * a + PAIRS)
            wait_for(pe, S["exp_done"], GROUPS * a + u - 1)
            bank = big[0:QN, 3 + u % 2, :]
            nc.tensor.matmul(bank, identb[:], maskb[:, min(t, 1)].rearrange("p i n -> p (i n)"), start=True, stop=False)
            for i in range(HG // 2):
                f = grp * HG // 2 + i
                mm = nc.tensor.matmul(bank[:, 2 * i * P:2 * (i + 1) * P], qf[:, par, f, QT[t]:QT[t] + QN],
                                      kz[:, par, f, :, KT[t]:KT[t] + P], start=False, stop=i == HG // 2 - 1)
            mm.then_inc(S["s_ready"], 1)

        def pe_turn(pe, a, u):
            wait_for(pe, S["p_ready"], GROUPS * a + u + 1)
            wait_for(pe, S["pt_ready"], GROUPS * a + u)
            for i in range(HG):
                mm = nc.tensor.matmul(big[:, 5, i * QN:(i + 1) * QN], pr[:, u % 2, i, :], g.c("ident")[:, 0:QN], start=True, stop=True)
            mm.then_inc(S["p_turned"], 1)

        def pe_mix(pe, a, par, u):
            t, grp = divmod(u, PER_TILE)
            j = grp // 2
            if u == 0:
                wait_for(pe, S["v_moved"], 6 * a + 6)
            if grp % 2 == 0:
                wait_for(pe, S["ot_ready"], 6 * a + 2 * t + j - 1)
                if t == 0 and j == 1:
                    wait_for(pe, S["added"], a)
            wait_for(pe, S["pt_ready"], GROUPS * a + u + 1)
            for i in range(HG):
                h = grp * HG + i
                f, odd = divmod(h, 2)
                mm = nc.tensor.matmul(big[odd * HD:(odd + 1) * HD, 6 + j, (f % 4) * QN:(f % 4 + 1) * QN],
                                      v[:, par, t, h * HD:(h + 1) * HD], pt[:, u % 2, i, :], start=True, stop=True)
            mm.then_inc(S["pt_used"], 1)

        def pe_out(pe, a):
            wait_for(pe, S["ot_ready"], 6 * a + 6)
            for f in range(PAIRS):
                mm = nc.tensor.matmul(big[:, 7, 0:T], W("wo")[:, f * D:(f + 1) * D], ot[:, f, :],
                                      start=(f == 0), stop=(f == PAIRS - 1))
            mm.then_inc(S["y_ready"], 1)

        def pe_project(pe, b, par, s):
            if s < PAIRS:
                pe_qk(pe, b, par, s)
            if 1 <= s <= PAIRS:
                pe_norm(pe, b, s - 1)
            if PAIRS <= s < PAIRS + 3:
                pe_v(pe, b, par, 2 * (s - PAIRS))
                pe_v(pe, b, par, 2 * (s - PAIRS) + 1)

        def pe_turn_of(pe, a, par, first=False, last=False):
            pe_scores(pe, a, par, 0)
            for u in range(GROUPS):
                if u + 1 < GROUPS:
                    pe_scores(pe, a, par, u + 1)
                if not last:
                    pe_project(pe, a + 1, 1 - par, u)
                if u == 1 and not first:
                    pe_out(pe, a - 1)
                pe_turn(pe, a, u)
                if u >= 1:
                    pe_mix(pe, a, par, u - 1)
            pe_mix(pe, a, par, GROUPS - 1)

        def act_input(act, b, par):
            nc.scalar.activation(xb[0:HD, par, :], y[0:HD, bass.ds(b * T, T)], ACT.Copy)
            nc.scalar.activation(xb[HD:P, par, 1:T], y[HD:P, bass.ds(b * T, T - 1)], ACT.Copy).then_inc(S["xb_ready"], 1)

        def act_square(act, b, f):
            wait_for(act, S["rot_done"], PAIRS * b + f + 1)
            wait_for(act, S["norm_ready"], PAIRS * b + f - 1)
            nc.scalar.activation(sq[:, f % 2], big[:, 0:2, 0:T], ACT.Square).then_inc(S["sq_ready"], 1)

        def act_root(act, b, f):
            wait_for(act, S["clamped"], PAIRS * b + f + 1)
            nc.scalar.activation(rn[:, f % 2], ss[:, f % 2], ACT.Ln).then_inc(S["ln_ready"], 1)
            wait_for(act, S["ln_ready"], PAIRS * b + f + 1)
            nc.scalar.activation(rn[:, f % 2], rn[:, f % 2], ACT.Exp, scale=-0.5).then_inc(S["root_ready"], 1)

        def act_v(act, b, par, n):
            if n == 0:
                wait_for(act, S["pt_used"], GROUPS * (b - 1))
            wait_for(act, S["v_ready"], 6 * b + n + 1)
            nc.scalar.activation(v[:, par, n // 2, (n % 2) * BLK:(n % 2 + 1) * BLK], big[:, n % 2, :],
                                 ACT.Copy).then_inc(S["v_moved"], 1)

        def act_exp(act, a, u):
            wait_for(act, S["max_ready"], GROUPS * a + u + 1)
            wait_for(act, S["p_turned"], GROUPS * a + u - 1)
            for i in range(HG):
                ins = nc.scalar.activation(pr[0:QN, u % 2, i, :], big[0:QN, 3 + u % 2, i * P:(i + 1) * P], ACT.Exp,
                                           bias=nb[0:QN, u % 2, i:i + 1], accum_out=sm[0:QN, u % 2, i:i + 1])
            ins.then_inc(S["exp_done"], 1)

        def act_turned(act, a, u):
            wait_for(act, S["p_turned"], GROUPS * a + u + 1)
            wait_for(act, S["pt_used"], GROUPS * a + u - 1)
            nc.scalar.activation(pt[:, u % 2], big[:, 5, 0:HG * QN].rearrange("p (i n) -> p i n", n=QN),
                                 ACT.Copy).then_inc(S["pt_ready"], 1)

        def act_sums(act, a, m):
            t, j = divmod(m, 2)
            skip = QT[1] + QN - QT[2] if t == 2 else 0
            wait_for(act, S["pt_used"], GROUPS * a + PER_TILE * t + 2 * j + 2)
            if m == 0:
                wait_for(act, S["y_ready"], a)
            nc.scalar.activation(ot[:, 4 * j:4 * j + 4, QT[t] + skip:QT[t] + QN],
                                 big[:, 6 + j, 0:4 * QN].rearrange("p (f n) -> p f n", f=4)[:, :, skip:QN],
                                 ACT.Copy).then_inc(S["ot_ready"], 1)

        def act_project_1(act, b, par, s):
            if s < PAIRS:
                act_square(act, b, s)
            if PAIRS <= s < PAIRS + 3:
                act_v(act, b, par, 2 * (s - PAIRS))
                act_v(act, b, par, 2 * (s - PAIRS) + 1)

        def act_project_2(act, b, s):
            if 1 <= s <= PAIRS:
                act_root(act, b, s - 1)

        def act_turn_of(act, a, par, last=False):
            for u in range(GROUPS):
                if u == 0 and not last:
                    act_input(act, a + 1, 1 - par)
                act_exp(act, a, u)
                if not last:
                    act_project_1(act, a + 1, 1 - par, u)
                act_turned(act, a, u)
                if not last:
                    act_project_2(act, a + 1, u)
                if u >= 2 and u % 2 == 0:
                    act_sums(act, a, u // 2 - 1)
            act_sums(act, a, 5)

        def dve_rotate(dve, b, f):
            wait_for(dve, S["qk_ready"], PAIRS * b + f + 1)
            wait_for(dve, S["summed"], PAIRS * b + f - 1)
            nc.vector.tensor_tensor(rot[:, f % 2].rearrange("p a b t -> p a (b t)"), big[:, 0:2, :],
                                    tab[:].rearrange("p a b t -> p a (b t)"), ALU.mult).then_inc(S["rot_done"], 1)

        def dve_clamp(dve, b, f):
            wait_for(dve, S["norm_ready"], PAIRS * b + f + 1)
            wait_for(dve, S["scaled"], PAIRS * b + f - 1)
            nc.vector.tensor_scalar(ss[:, f % 2].rearrange("p n t -> p (n t)"), big[:, 2, :], 1e-24, 65536.0,
                                    ALU.max, ALU.mult).then_inc(S["clamped"], 1)

        def dve_scale(dve, b, par, f):
            wait_for(dve, S["unit_ready"], PAIRS * b + f + 1)
            r = rn[:, f % 2]
            nc.vector.scalar_tensor_tensor(out=r, in0=unit[:, f % 2], scalar=-3.0, in1=r, op0=ALU.add, op1=ALU.mult).then_inc(S["refined"], 1)
            wait_for(dve, S["refined"], PAIRS * b + f + 1)
            if f == 0:
                wait_for(dve, S["s_ready"], GROUPS * (b - 1))
            nc.vector.scalar_tensor_tensor(out=qf[:, par, f, :], in0=qf[:, par, f, :], scalar=-128.0, in1=rn[:, f % 2, 0, :],
                                           op0=ALU.mult, op1=ALU.mult)
            for odd in range(2):
                rows = slice(odd * HD, (odd + 1) * HD)
                ins = nc.vector.scalar_tensor_tensor(out=kz[rows, par, f, odd, :], in0=ks[rows, f % 4, :], scalar=-128.0,
                                                     in1=rn[rows, f % 2, 1, :], op0=ALU.mult, op1=ALU.mult)
            ins.then_inc(S["scaled"], 1)

        def dve_max(dve, a, u):
            wait_for(dve, S["s_ready"], GROUPS * a + u + 1)
            wait_for(dve, S["exp_done"], GROUPS * a + u - 1)
            nc.vector.tensor_reduce(nb[0:QN, u % 2, :], big[0:QN, 3 + u % 2, :].rearrange("p (i n) -> p i n", n=P), AX, ALU.max,
                                    negate=True).then_inc(S["max_ready"], 1)

        def dve_probs(dve, a, u):
            wait_for(dve, S["exp_done"], GROUPS * a + u + 1)
            nc.vector.reciprocal(rs[0:QN, u % 2, :], sm[0:QN, u % 2, :]).then_inc(S["inv_ready"], 1)
            wait_for(dve, S["inv_ready"], GROUPS * a + u + 1)
            nc.vector.tensor_tensor(pr[0:QN, u % 2], pr[0:QN, u % 2], rs[0:QN, u % 2, :].unsqueeze(2).to_broadcast([QN, HG, P]),
                                    ALU.mult).then_inc(S["p_ready"], 1)

        def dve_add(dve, a):
            wait_for(dve, S["y_ready"], a + 1)
            ys = y[:, bass.ds(a * T, T)]
            nc.vector.tensor_tensor(ys, ys, big[:, 7, 0:T], ALU.add).then_inc(S["added"], 1)

        def dve_project(dve, b, par, s):
            if s < PAIRS:
                dve_rotate(dve, b, s)
            if 1 <= s <= PAIRS:
                dve_clamp(dve, b, s - 1)
            if 2 <= s <= PAIRS + 1:
                dve_scale(dve, b, par, s - 2)

        def dve_turn_of(dve, a, par, first=False, last=False):
            dve_max(dve, a, 0)
            for u in range(GROUPS):
                if u + 1 < GROUPS:
                    dve_max(dve, a, u + 1)
                dve_probs(dve, a, u)
                if not last:
                    dve_project(dve, a + 1, 1 - par, u)
                if u == 1 and not first:
                    dve_add(dve, a - 1)

        def pool_units(pool, b, f):
            wait_for(pool, S["root_ready"], PAIRS * b + f + 1)
            nc.gpsimd.tensor_tensor(unit[:, f % 2], ss[:, f % 2], rn[:, f % 2], ALU.mult).then_inc(S["pool_step"], 1)
            wait_for(pool, S["pool_step"], PAIRS * b + f + 1)
            nc.gpsimd.tensor_tensor(unit[:, f % 2], unit[:, f % 2], rn[:, f % 2], ALU.mult).then_inc(S["unit_ready"], 1)

        def pool_sums(pool, b, par):
            for f in range(PAIRS):
                wait_for(pool, S["rot_done"], PAIRS * b + f + 1)
                wait_for(pool, S["scaled"], PAIRS * b + f - 3)
                if f == 0:
                    wait_for(pool, S["s_ready"], GROUPS * (b - 1))
                nc.gpsimd.tensor_tensor(qf[:, par, f, :], rot[:, f % 2, 0, 0, :], rot[:, f % 2, 0, 1, :], ALU.add)
                nc.gpsimd.tensor_tensor(ks[:, f % 4, :], rot[:, f % 2, 1, 0, :], rot[:, f % 2, 1, 1, :], ALU.add).then_inc(S["summed"], 1)
                if f >= 1:
                    pool_units(pool, b, f - 1)
            pool_units(pool, b, PAIRS - 1)

        mlp_landed = st.sem("mlp_landed")
        with nc.Block() as blk:
            @blk.sync
            def _(sp):
                sp.dma_start(mlp_w[:], mlp_dram).then_inc(mlp_landed, 16)
                sp.wait_ge(mlp_landed, 16)

            @blk.tensor
            def _(pe):
                pe.wait_ge(S["tab_ready"], 1)
                for s in range(PAIRS + 3):
                    pe_project(pe, 0, 0, s)
                pe_turn_of(pe, 0, 0, first=True)
                with pe.Fori(0, (B - 2) // 2) as i:
                    pe_turn_of(pe, 2 * i + 1, 1)
                    pe_turn_of(pe, 2 * i + 2, 0)
                pe_turn_of(pe, B - 1, 1, last=True)
                pe_out(pe, B - 1)

            @blk.scalar
            def _(act):
                nc.scalar.preload_act_table_set("natural_log_exp_and_others")
                nc.scalar.preload_act_table_set("natural_log_exp_and_others")
                act_input(act, 0, 0)
                for s in range(PAIRS + 3):
                    act_project_1(act, 0, 0, s)
                    act_project_2(act, 0, s)
                act_turn_of(act, 0, 0)
                with act.Fori(0, (B - 2) // 2) as i:
                    act_turn_of(act, 2 * i + 1, 1)
                    act_turn_of(act, 2 * i + 2, 0)
                act_turn_of(act, B - 1, 1, last=True)

            @blk.gpsimd
            def _(pool):
                pool_sums(pool, 0, 0)
                pool_sums(pool, 1, 1)
                with pool.Fori(0, (B - 2) // 2) as i:
                    pool_sums(pool, 2 * i + 2, 0)
                    pool_sums(pool, 2 * i + 3, 1)

            @blk.vector
            def _(dve):
                nc.vector.memset(xb[HD:P, :, 0:1], 0.0)
                nc.vector.memset(kz[0:HD, :, :, 1, :], 0.0)
                nc.vector.memset(kz[HD:P, :, :, 0, :], 0.0)
                nc.vector.memset(pr[QN:P], 0.0)
                for n, s in enumerate(("qs", "ks")):
                    for m in range(2):
                        nc.vector.tensor_scalar(tab[:, n, m, :], g.c(("rot_q", "rot_k")[n])[:, m * T:(m + 1) * T], W(s)[:, m:m + 1], None, ALU.mult)
                nc.vector.tensor_copy(identb[:], g.c("ident")[:, 0:QN])
                for m in range(HG):
                    ins = nc.vector.tensor_copy(maskb[:, :, m, :], g.c("window").rearrange("p (a n) -> p a n", a=2))
                ins.then_inc(S["tab_ready"], 1)
                dve.wait_ge(S["tab_ready"], 1)
                for s in range(PAIRS + 2):
                    dve_project(dve, 0, 0, s)
                dve_turn_of(dve, 0, 0, first=True)
                with dve.Fori(0, (B - 2) // 2) as i:
                    dve_turn_of(dve, 2 * i + 1, 1)
                    dve_turn_of(dve, 2 * i + 2, 0)
                dve_turn_of(dve, B - 1, 1, last=True)
                dve_add(dve, B - 1)


def gated_mlp(nc, g, w, next_w, next_dram):
    W = lambda n: L3F.of(w, n)
    y = g.xn
    ROWS = (P, P, P)
    with Stage(nc, "l3f") as st:
        xs = st.sb("xs", [P, N])
        shifted, next_landed = st.sem("shifted"), st.sem("next_landed")
        with nc.Block() as blk:
            @blk.vector
            def _(dve):
                xs3, y3 = (ap.rearrange("p (b t) -> p b t", t=T) for ap in (xs[:], y[:]))
                nc.vector.tensor_copy(xs3[HD:P, :, 1:T], y3[HD:P, :, 0:T - 1])
                nc.vector.memset(xs3[HD:P, :, 0:1], 0.0).then_inc(shifted, 1)

            @blk.scalar
            def _(act):
                nc.scalar.activation(xs[0:HD, :], y[0:HD, :], ACT.Copy).then_inc(shifted, 1)
        layer_norm(nc, "l3n", xs, xs, g.c("mean"), g.c("eps5"), W("g"), W("b"))
        h_ps, o_ps = st.ps("h_ps", [P, 3, 2, BLK]), st.ps("o_ps", [P, BLK])
        ge, hid = st.sb("ge", [P, 3, BLK]), st.sb("hid", [P, 3, BLK])
        up_ready, gelu_ready, hid_ready, hid_used, out_used, step = (
            st.sem(n) for n in ("up_ready", "gelu_ready", "hid_ready", "hid_used", "out_used", "step"))
        def down(pe, i, c):
            if c == 0:
                pe.wait_ge(out_used, i + 1)
            pe.wait_ge(hid_ready, 3 * i + c + 4)
            nc.tensor.matmul(o_ps[:], W("w2")[0:ROWS[c], c * D:(c + 1) * D], hid[0:ROWS[c], c, :],
                             start=(c == 0), stop=(c == 2)).then_inc(hid_used, 1)

        with nc.Block() as blk:
            @blk.sync
            def _(sp):
                sp.dma_start(next_w[:], next_dram).then_inc(next_landed, 16)
                sp.wait_ge(next_landed, 16)

            @blk.tensor
            def _(pe):
                with pe.Fori(0, NBLK) as i:
                    def up(c):
                        pe.wait_ge(hid_ready, 3 * i + c + 1)
                        for m in range(2):
                            at = (3 * m + c) * P
                            mm = nc.tensor.matmul(h_ps[0:ROWS[c], c, m, :], W("w1")[:, at:at + ROWS[c]], xs[:, block(i)],
                                                  start=True, stop=True)
                        mm.then_inc(up_ready, 1)

                    for c in range(3):
                        up(c)
                        if c >= 1:
                            down(pe, i, c - 1)
                    down(pe, i, 2)

            @blk.scalar
            def _(act):
                with act.Fori(0, NBLK) as i:
                    for c in range(3):
                        act.wait_ge(up_ready, 3 * i + c + 1)
                        act.wait_ge(hid_ready, 3 * i + c + 1)
                        r = ROWS[c]
                        nc.scalar.activation(ge[0:r, c, :], h_ps[0:r, c, 1, :], ACT.Gelu,
                                             bias=W("b1")[0:r, 3 + c:4 + c]).then_inc(gelu_ready, 1)

            @blk.vector
            def _(dve):
                nc.vector.sem_inc(hid_ready, 3)
                nc.vector.sem_inc(out_used, 1)
                nc.vector.sem_inc(hid_used, 3)
                with dve.Fori(0, NBLK) as i:
                    c_ = Chain(dve, step, 1, i)
                    for c in range(3):
                        r = ROWS[c]
                        dve.wait_ge(gelu_ready, 3 * i + c + 1)
                        dve.wait_ge(hid_used, 3 * i + c + 1)
                        nc.vector.scalar_tensor_tensor(out=hid[0:r, c, :], in0=h_ps[0:r, c, 0, :], scalar=W("b1")[0:r, c:c + 1],
                                                       in1=ge[0:r, c, :], op0=ALU.add, op1=ALU.mult).then_inc(hid_ready, 1)
                    dve.wait_ge(hid_used, 3 * i + 3 + 3)
                    ys = y[:, block(i)]
                    c_.link(nc.vector.scalar_tensor_tensor(out=ys, in0=o_ps[:], scalar=W("b2"), in1=ys, op0=ALU.add, op1=ALU.add))
                    nc.vector.sem_inc(out_used, 1)
                    c_.close()


CONST = layout([("ident", P, P), ("mean", P, P), ("mask8", P, P), ("before8", P, 64), ("before4", P, 16),
                ("pick8", P, 8 * P), ("ones_row", P, P), ("eps5", P, 1),
                ("mean32", P, P), ("sum32", P, P), ("causal", P, P), ("eps_rms", P, 1)])
CONST3 = layout([("head64", P, P), ("lag", P, T), ("earlier", P, T),
                 ("rot_q", P, 2 * T), ("rot_k", P, 2 * T), ("window", P, 2 * P)])


def constants():
    i = np.arange(P)
    pick8 = np.zeros((P, 8, P), np.float32)
    pick8[np.arange(8), np.arange(8), :] = 1
    key, query = i[:, None], np.arange(T)[None]
    lag = query - 1 - key
    q96 = i[:, None]
    window0 = (i[None] <= q96) & (i[None] >= q96 - WINDOW)
    window1 = (i[None] <= q96 + WINDOW) & (i[None] >= q96)
    half = np.arange(0, HD, 2, dtype=np.float32)
    t = np.arange(T, dtype=np.float32)
    freqs = t[:, None] * (np.float32(1) / np.float32(10000) ** (half / np.float32(HD)))[None]
    base = (half + np.float32(0.4 * HD)) / np.float32(1.4 * HD)
    scale = base[None] ** ((t - T // 2) / np.float32(WINDOW // 2))[:, None]
    cos, sin = np.cos(freqs), np.sin(freqs)

    def rotation(s):
        c4 = np.concatenate([cos * s] * 4, 1).T
        s4 = np.concatenate([-sin * s, sin * s] * 2, 1).T
        return np.concatenate([c4, s4], 1)

    made = {
        "ident": np.eye(P), "mean": np.full((P, P), 1.0 / P), "mask8": (i[:, None] // 8 == i[None] // 8),
        "before8": np.tile(np.tril(np.ones((8, 8)), -1).reshape(1, 64), (P, 1)),
        "before4": np.tile(np.tril(np.ones((4, 4)), -1).reshape(1, 16), (P, 1)),
        "pick8": pick8.reshape(P, 8 * P), "ones_row": pad_rows(np.ones((1, P))), "eps5": np.full((P, 1), 1e-5),
        "head64": (i[:, None] // HD == i[None] // HD), "lag": np.where(lag >= 0, -lag, 0), "earlier": lag >= 0,
        "rot_q": rotation(8 * scale), "rot_k": rotation(np.float32(1) / scale),
        "mean32": (i[:, None] // 32 == i[None] // 32) / 8.0,
        "sum32": (i[:, None] // 32 == i[None] // 32) * (i[:, None] % 32 == 8),
        "causal": np.where(i[None] <= i[:, None], 0, NEG), "eps_rms": np.full((P, 1), 1.1920929e-07),
        "window": np.concatenate([np.where(window0, 0, NEG), np.where(window1, 0, NEG)], 1),
    }
    return made


class Shared:
    pass


def program(nc, dram, out):
    ctx = ExitStack()
    with ctx:
        g = Shared()
        g.x = ctx.enter_context(nc.sbuf_tensor("x", [P, N], F32))
        g.xn = ctx.enter_context(nc.sbuf_tensor("xn", [P, N], F32))
        const = ctx.enter_context(nc.sbuf_tensor("const", [P, CONST.n], F32))
        g.c = lambda n: CONST.of(const, n) if n in CONST.at else CONST3.of(g.const3, n)
        g.ones_row = CONST.of(const, "ones_row")[:, 0:P]
        in_landed = ctx.enter_context(nc.semaphore("in_landed"))
        with nc.Block() as blk:
            @blk.sync
            def _(sp):
                sp.dma_start(g.x[:], dram["x"]).then_inc(in_landed, 16)
                sp.dma_start(const[:], dram["const"]).then_inc(in_landed, 16)
                sp.wait_ge(in_landed, 32)
        with Stage(nc, "l0") as st:
            w, prob_t = st.sb("w", [P, L0.n]), st.sb("prob_t", [P, N])
            load_pack(nc, st, dram["l0"], w, "l0")
            layer_norm(nc, "ln0", g.x, g.xn, g.c("mean"), g.c("eps5"))
            linear_attention(nc, g, w)
            gate(nc, g, "l0g", g.xn, L0.of(w, "gate"), None, 8, l0_weigh(nc, g), prob_t)
            swiglu_experts(nc, g, w, prob_t)
        with Stage(nc, "l1") as st:
            w, prob_t = st.sb("w", [P, L1.n]), st.sb("prob_t", [P, N])
            load_pack(nc, st, dram["l1"], w, "l1")
            layer_norm(nc, "ln1", g.x, g.xn, g.c("mean"), g.c("eps5"))
            wkv_attention(nc, g, w)
            gate(nc, g, "l1g", g.xn, L1.of(w, "gate"), L1.of(w, "gate_b"), 8, l1_weigh(nc, g), prob_t)
            linear_experts(nc, g, w, prob_t)
        layer_norm(nc, "ln2", g.x, g.xn, g.c("mean"), g.c("eps5"))
        delta_attention(nc, g, dram)
        with Stage(nc, "l2") as st:
            w, prob_t = st.sb("w", [P, L2F.n]), st.sb("prob_t", [P, N])
            h = st.sb("h", [P, N])
            load_pack(nc, st, dram["l2f"], w, "l2f")
            rms_norm(nc, "l2n1", g.xn, h, g.c("mean"), g.c("eps_rms"), L2F.of(w, "n1"))
            causal_attention(nc, g, w, h)
            rms_norm(nc, "l2n2", g.xn, h, g.c("mean"), g.c("eps_rms"), L2F.of(w, "n2"))
            gate(nc, g, "l2g", h, L2F.of(w, "gate"), None, 4, l2_weigh(nc, g), prob_t)
            mixed_experts(nc, g, w, h, prob_t)
        g.const3 = ctx.enter_context(nc.sbuf_tensor("const3", [P, CONST3.n], F32))
        with Stage(nc, "c3") as st:
            load_pack(nc, st, dram["const3"], g.const3, "const3")
        layer_norm(nc, "ln3", g.x, g.xn, g.c("mean"), g.c("eps5"))
        with Stage(nc, "l3") as st:
            w = st.sb("w", [P, L3A.n])
            load_pack(nc, st, dram["l3a"], w, "l3a")
            decay_attention(nc, g, w)
        with Stage(nc, "l3deep") as st:
            wa, wf = st.sb("wa", [P, L3W.n]), st.sb("wf", [P, L3F.n])
            of = lambda name, layer: dram[name][bass.ds(layer, 1)].rearrange("l p n -> (l p) n")
            load_pack(nc, st, of("l3w", 0), wa, "l3w")
            with nc.Fori(0, DEPTH) as layer:
                window_attention(nc, g, wa, wf, of("l3f", layer))
                gated_mlp(nc, g, wf, wa, of("l3w", layer + 1))
            done = st.sem("done")
            with nc.Block() as blk:
                @blk.vector
                def _(dve):
                    nc.vector.tensor_tensor(g.x[:], g.x[:], g.xn[:], ALU.add).then_inc(done, 1)
        stored = ctx.enter_context(nc.semaphore("stored"))
        with nc.Block() as blk:
            @blk.sync
            def _(sp):
                sp.dma_start(out, g.x[:]).then_inc(stored, 16)
                sp.wait_ge(stored, 16)


def fill(pack, pieces):
    a = np.zeros((P, pack.n), np.float32)
    for name, (at, rows, cols) in pack.at.items():
        piece = np.asarray(pieces[name], np.float32)
        assert piece.shape == (rows, cols), (name, piece.shape, rows, cols)
        a[:rows, at:at + cols] = piece
    return a


def pad_rows(a):
    return np.concatenate([a, np.zeros((P - a.shape[0], a.shape[1]), a.dtype)], 0)


def col(v):
    return np.asarray(v).reshape(-1, 1)


def row(v):
    return np.asarray(v).reshape(1, -1)


def brow(v):
    return pad_rows(row(v))


def host_layout(i):
    i = {k: np.asarray(v) for k, v in i.items()}
    packs = {"x": np.ascontiguousarray(i["L0_attn_query"].reshape(N, D).T), "const": fill(CONST, constants()), "const3": fill(CONST3, constants())}
    a = "L0_attn_"
    packs["l0"] = fill(L0, {
        "wq": i[a + "Wq"].T, "wkv": np.concatenate([i[a + "Wk"].T, i[a + "Wv"].T], 1), "wo": i[a + "Wo"].T,
        "bq": col(i[a + "bq"]), "bo": col(i[a + "bo"]), "bkv": brow(np.concatenate([i[a + "bk"], i[a + "bv"]])),
        "gate": i["L0_ffn_gate_w"].T,
        "w12": i["L0_ffn_w12"].transpose(2, 0, 1).reshape(D, -1),
        "w3": i["L0_ffn_w3"].reshape(8, D, 2, P).transpose(3, 0, 2, 1).reshape(P, -1)})
    a, f = "L1_attn_", "L1_ffn_"
    packs["l1"] = fill(L1, {
        "wk": i[a + "Wk"].T, "wv": i[a + "Wv"].T, "wr": i[a + "Wr"].T, "wo": i[a + "Wo"].T,
        **{n: col(i[a + n]) for n in ("bo", "u", "w", "tmk", "tmv", "tmr")},
        "gate": i[f + "gate_W"], "gate_b": brow(i[f + "gate_b"]),
        "ew": i[f + "expert_W"].transpose(1, 0, 2).reshape(D, -1), "eb": pad_rows(i[f + "expert_b"])})
    a = "L2_attn_"
    by_pair = lambda wo: wo.reshape(PAIRS, P, D).transpose(1, 0, 2).reshape(P, -1)
    n = np.arange(P)
    b_, t_ = n // CH, n % CH
    same = b_[:, None] == b_[None]
    row_t, col_t = t_[:, None], t_[None]
    upto, before = same & (row_t <= col_t), same & (row_t < col_t)
    after = same & (row_t > col_t)
    first = same & (row_t < CH // 2)
    ends = np.stack([(b_[:, None] == np.arange(GB)) & (row_t < CH // 2), (b_[:, None] == np.arange(GB)) & (row_t >= CH // 2)], -1)
    packs["l2a"] = fill(L2A, {
        **{n_: i[a + "W" + n_[1:]].T for n_ in ("wk", "wq", "wv", "wa")}, "war": i[a + "WaR"].T,
        "wbg": np.concatenate([i[a + "Wb"].T, i[a + "Wg"].T], 1), "wo": by_pair(i[a + "Wo"].T),
        "lnw": col(i[a + "ln_w"]), "lnb": col(i[a + "ln_b"]), "ba": pad_rows(np.stack([i[a + "ba"], i[a + "baR"]])),
        "bbg": brow(np.concatenate([i[a + "bb"], i[a + "bg"]])),
        "cum": first.astype(np.float32) - upto, "ends": ends.reshape(P, 8),
        "keep": np.concatenate([before, upto, before, after], 1), "keep_r": np.concatenate([before, upto, after], 1)})
    f = "L2_ffn_"

    def spread32(wt):
        out = np.zeros((D, HEADS, 32), np.float32)
        out[:, :, :8] = wt.reshape(D, HEADS, 8)
        return out.reshape(D, -1)

    def head_col(v):
        out = np.zeros((4, 32), np.float32)
        out[:, :8] = v
        return out.reshape(P, 1)

    up = lambda n: i[f + n].T
    tall = lambda n: i[f + n].T.reshape(2, P, -1).transpose(1, 0, 2).reshape(P, -1)
    packs["l2f"] = fill(L2F, {
        "n1": col(i[f + "n1_w"]), "n2": col(i[f + "n2_w"]), "wq": spread32(up("wq")), "wk": spread32(up("wk")), "wv": up("wv"),
        "qn": head_col(i[f + "qn_w"]), "kn": head_col(i[f + "kn_w"]),
        "wo": spread32(i[f + "wo"]).T.reshape(4, P, D).transpose(1, 0, 2).reshape(P, -1), "gate": up("gate_w"),
        "e0u": up("e0_up"), "e0d": tall("e0_down"), "e1a": up("e1_w1"), "e1b": up("e1_w2"), "e1d": tall("e1_down"),
        "e2a": up("e2_l1"), "e2b": tall("e2_l2"), "e2c": tall("e2_l3"), "e2d": tall("e2_l4"),
        "e3a": up("e3_down"), "e3b": up("e3_up"), "e3d": tall("e3_out")})
    a = "L3_attn_"
    by_pair = lambda wo: wo.reshape(PAIRS, P, D).transpose(1, 0, 2).reshape(P, -1)
    packs["l3a"] = fill(L3A, {
        **{n: i[a + "W" + n[1:]] for n in ("wq", "wk", "wv", "wf", "wg", "wb")}, "wo": by_pair(i[a + "Wo"]),
        "dt": np.asarray(i[a + "dt_bias"]).reshape(PAIRS, P).T, "bg": np.asarray(i[a + "bg"]).reshape(PAIRS, P).T, "a_log": np.tile(row(i[a + "A_log"]), (P, 1)),
        "norm_w": col(np.tile(i[a + "norm_w"], 2))})
    a = "L3_ffn_"
    swap = np.arange(INNER).reshape(HEADS, 2, HD // 2)[:, ::-1].reshape(-1)
    deep_w, deep_f = [], []
    for l in range(DEPTH):
        wq, wk, wv = np.split(i[a + "Wqkv"][l], 3, -1)
        qs, ks = (np.tile(i[a + s][l], 2) for s in ("q_scale", "k_scale"))
        deep_w.append(fill(L3W, {
            "wq": wq, "wqr": wq[:, swap], "wk": wk, "wkr": wk[:, swap], "wv": wv, "wo": by_pair(i[a + "Wo"][l]),
            "qs": np.stack([qs, qs[swap[:P]]], 1), "ks": np.stack([ks, ks[swap[:P]]], 1)}))
        w1 = np.zeros((D, 2, 3 * P), np.float32)
        w1[:, :, :HALF] = i[a + "W1"][l].reshape(D, 2, HALF)
        b1 = np.zeros((2, 3 * P), np.float32)
        b1[:, :HALF] = i[a + "b1"][l].reshape(2, HALF)
        w2 = np.zeros((3 * P, D), np.float32)
        w2[:HALF] = i[a + "W2"][l]
        deep_f.append(fill(L3F, {
            "w1": w1.reshape(D, -1), "b1": b1.reshape(6, P).T, "w2": w2.reshape(3, P, D).transpose(1, 0, 2).reshape(P, -1),
            "b2": col(i[a + "b2"][l]), "g": col(i[a + "ln_g"][l]), "b": col(i[a + "ln_b"][l])}))
    packs["l3w"], packs["l3f"] = np.stack(deep_w + deep_w[:1]), np.stack(deep_f)
    return packs


def kernel(**inputs):
    import concourse.bacc as _bacc
    from concourse.bass_utils import run_bass_kernel_spmd as _run

    arrays = {k + "_dram": v for k, v in host_layout(inputs).items()}
    nc = _bacc.Bacc("TRN2", target_bir_lowering=False, num_devices=1)
    dram = {k[:-5]: nc.dram_tensor(k, v.shape, F32, kind="ExternalInput").ap() for k, v in arrays.items()}
    out = nc.dram_tensor("out_dram", (P, N), F32, kind="ExternalOutput").ap()
    program(nc, dram, out)
    r = _run(nc, [arrays], core_ids=[0])
    return np.ascontiguousarray(r.results[0]["out_dram"].T).reshape(B, T, D)
```
